# Optimizing a Trainium2 kernel written in Bass

```python
import numpy as np
import jax
import jax.numpy as jnp

def _softmax(x, axis=-1):
    return jax.nn.softmax(x, axis=axis)
def _gelu(x):
    return jax.nn.gelu(x, approximate=True)
def _silu(x):
    return jax.nn.silu(x)
def _sigmoid(x):
    return jax.nn.sigmoid(x)
def _layernorm(x, axis=-1, eps=1e-5):
    m = jnp.mean(x, axis=axis, keepdims=True)
    v = jnp.var(x, axis=axis, keepdims=True)
    return (x - m) / jnp.sqrt(v + eps)
def _scatter_add(tgt, idx, src, axis=0):
    return tgt.at[idx].add(src)
def _segment_sum(src, seg, n):
    return jax.ops.segment_sum(src, seg, n)

kernel_name = 'mk_metaformer_d4_conv_nhwc128_a414dc'

def setup_inputs(seed: int = 0):
    np.random.seed(seed)
    _w = jnp.asarray
    def _rec_inputs():
        import jax
        import jax.numpy as jnp
        _gk = jax.random.key(seed)
        x = -0.0009438 + 1 * jax.random.normal(jax.random.fold_in(_gk, 1), (4, 48, 48, 128), jnp.float32)
        return x
    x = _rec_inputs()
    def _L0_conv_setup():
        import jax, jax.numpy as jnp
        import numpy as np
        from jax import lax
        B, H, W, C = (4, 48, 48, 128)
        D_INNER, D_STATE, DT_RANK, K = (256, 16, 8, 4)
        key = jax.random.key(seed)
        ks = jax.random.split(key, 8)
        d, N, R = (D_INNER, D_STATE, DT_RANK)
        f32 = jnp.float32
        return {'x': jax.random.normal(ks[0], (B, H, W, C), f32), 'in_proj_w': jax.random.normal(ks[1], (2 * d, C), f32) * C ** (-0.5), 'conv_w': jax.random.normal(ks[2], (d, 1, 3, 3), f32) / 3.0, 'conv_b': jnp.zeros((d,), f32), 'x_proj_w': jax.random.normal(ks[3], (K, R + 2 * N, d), f32) * d ** (-0.5), 'dt_proj_w': jax.random.normal(ks[4], (K, d, R), f32) * R ** (-0.5), 'dt_proj_b': jax.random.uniform(ks[5], (K, d), f32, -4.0, -2.0), 'A_logs': jnp.broadcast_to(jnp.log(jnp.arange(1, N + 1, dtype=f32)), (K * d, N)).copy(), 'Ds': jnp.ones((K * d,), f32), 'norm_g': jnp.ones((d,), f32), 'norm_b': jnp.zeros((d,), f32), 'out_proj_w': jax.random.normal(ks[6], (C, d), f32) * d ** (-0.5)}
    _L0_conv_all = _L0_conv_setup()
    _L0_conv_in = {k: v for k, v in _L0_conv_all.items() if k in ('in_proj_w', 'conv_w', 'conv_b', 'x_proj_w', 'dt_proj_w', 'dt_proj_b', 'A_logs', 'Ds', 'norm_g', 'norm_b', 'out_proj_w', )}
    del _L0_conv_all

    def _L0_ffn_setup():
        import jax, jax.numpy as jnp
        import numpy as np
        PADDED_SL = 8192
        TEMPERATURE = 1.0
        SIGMA_POW = 0.25

        def _stu_conv(phi, u, n):
            b, sl, d = u.shape
            sgn = jnp.where(jnp.arange(sl) % 2 == 0, 1.0, -1.0).astype(u.dtype)
            sgn3 = sgn[None, :, None]
            Vf = jnp.fft.rfft(phi, n=n, axis=0)
            Uf_p = jnp.fft.rfft(u, n=n, axis=1)
            Uf_m = jnp.fft.rfft(u * sgn3, n=n, axis=1)
            U_plus = jnp.fft.irfft(Vf[None, :, :, None] * Uf_p[:, :, None, :], n=n, axis=1)[:, :sl]
            U_minus = jnp.fft.irfft(Vf[None, :, :, None] * Uf_m[:, :, None, :], n=n, axis=1)[:, :sl]
            U_minus = U_minus * sgn[None, :, None, None]
            return (U_plus, U_minus)

        def _compute_spectral(u, sigma, phi, Mpp, Mpm):
            U_plus, U_minus = _stu_conv(phi, u, PADDED_SL)
            s = sigma ** SIGMA_POW
            out = jnp.einsum('btkd,k,kde->bte', U_plus, s, Mpp)
            out = out + jnp.einsum('btkd,k,kde->bte', U_minus, s, Mpm)
            return out

        def _compute_ar_u(Mu, u):
            sl = u.shape[1]
            out = jnp.zeros(u.shape[:2] + (Mu.shape[-1],), dtype=u.dtype)
            for i in range(Mu.shape[0]):
                ui = jnp.pad(u, ((0, 0), (i, 0), (0, 0)))[:, :sl]
                out = out + jnp.einsum('btd,de->bte', ui, Mu[i])
            return out

        def _stu(u, sigma, phi, Mu, Mpp, Mpm):
            return _compute_spectral(u, sigma, phi, Mpp, Mpm) + _compute_ar_u(Mu, u)
        key = jax.random.key(seed)
        ks = jax.random.split(key, 8)
        b, sl, d, K, k_u = (2, 4096, 128, 16, 3)
        x = jax.random.normal(ks[0], (b, sl, d), dtype=jnp.float32)
        sigma = jax.random.uniform(ks[1], (K,), dtype=jnp.float32, minval=0.001, maxval=1.0)
        phi = jax.random.normal(ks[2], (sl, K), dtype=jnp.float32) / np.sqrt(sl)
        M_u = jax.random.normal(ks[3], (4, k_u, d, d), dtype=jnp.float32) * 0.02
        M_phi_plus = jax.random.normal(ks[4], (4, K, d, d), dtype=jnp.float32) * 0.02
        M_phi_minus = jax.random.normal(ks[5], (4, K, d, d), dtype=jnp.float32) * 0.02
        log_weights = jnp.ones((4,), dtype=jnp.float32)
        u01 = jax.random.uniform(ks[6], (4,), dtype=jnp.float32, minval=1e-06, maxval=1.0 - 1e-06)
        gumbel = -jnp.log(-jnp.log(u01))
        return {'x': x, 'sigma': sigma, 'phi': phi, 'M_u': M_u, 'M_phi_plus': M_phi_plus, 'M_phi_minus': M_phi_minus, 'log_weights': log_weights, 'gumbel': gumbel}
    _L0_ffn_all = _L0_ffn_setup()
    _L0_ffn_in = {k: v for k, v in _L0_ffn_all.items() if k in ('sigma', 'phi', 'M_u', 'M_phi_plus', 'M_phi_minus', 'log_weights', 'gumbel', )}
    del _L0_ffn_all

    def _L1_conv_setup():
        import jax, jax.numpy as jnp
        import numpy as np
        D = 128
        MODES = 32
        FACTOR = 4
        B, M, N = (16, 128, 128)

        def _forward_fourier(x, fw0, fw1):
            xt = jnp.transpose(x, (0, 3, 1, 2))
            b, i, m, n = xt.shape
            xfty = jnp.fft.rfft(xt, axis=-1, norm='ortho')
            my = min(MODES, n // 2 + 1)
            wy = jax.lax.complex(fw0[..., 0], fw0[..., 1])[..., :my]
            mixed_y = jnp.einsum('bixy,ioy->boxy', xfty[..., :my], wy)
            pad_y = jnp.zeros(mixed_y.shape[:3] + (n // 2 + 1 - my,), mixed_y.dtype)
            xy = jnp.fft.irfft(jnp.concatenate([mixed_y, pad_y], axis=-1), n=n, axis=-1, norm='ortho')
            xftx = jnp.fft.rfft(xt, axis=-2, norm='ortho')
            mx = min(MODES, m // 2 + 1)
            wx = jax.lax.complex(fw1[..., 0], fw1[..., 1])[..., :mx]
            mixed_x = jnp.einsum('bixy,iox->boxy', xftx[:, :, :mx, :], wx)
            pad_x = jnp.zeros((b, mixed_x.shape[1], m // 2 + 1 - mx, n), mixed_x.dtype)
            xx = jnp.fft.irfft(jnp.concatenate([mixed_x, pad_x], axis=-2), n=m, axis=-2, norm='ortho')
            return jnp.transpose(xx + xy, (0, 2, 3, 1))
        key = jax.random.key(seed)
        ks = jax.random.split(key, 7)
        xavier = float(np.sqrt(2.0 / (D + D)))
        x = jax.random.normal(ks[0], (B, M, N, D), dtype=jnp.float32)
        fw0 = jax.random.normal(ks[1], (D, D, MODES, 2), dtype=jnp.float32) * xavier
        fw1 = jax.random.normal(ks[2], (D, D, MODES, 2), dtype=jnp.float32) * xavier
        H = D * FACTOR
        lim1 = float(np.sqrt(1.0 / D))
        lim2 = float(np.sqrt(1.0 / H))
        w1 = jax.random.uniform(ks[3], (D, H), jnp.float32, -lim1, lim1)
        b1 = jax.random.uniform(ks[4], (H,), jnp.float32, -lim1, lim1)
        w2 = jax.random.uniform(ks[5], (H, D), jnp.float32, -lim2, lim2)
        b2 = jax.random.uniform(ks[6], (D,), jnp.float32, -lim2, lim2)
        return {'x': x, 'fw0': fw0, 'fw1': fw1, 'w1': w1, 'b1': b1, 'w2': w2, 'b2': b2}
    _L1_conv_all = _L1_conv_setup()
    _L1_conv_in = {k: v for k, v in _L1_conv_all.items() if k in ('fw0', 'fw1', 'w1', 'b1', 'w2', 'b2', )}
    del _L1_conv_all

    def _L1_ffn_setup():
        import jax, jax.numpy as jnp
        import numpy as np
        B, S, D, E, H, O, K = (512, 2048, 128, 64, 512, 128, 8)
        key = jax.random.key(seed)
        k0, k1, k2, k3 = jax.random.split(key, 4)
        x = jax.random.normal(k0, (B, S, D), dtype=jnp.float32)
        gate_w = jax.random.normal(k1, (E, D), dtype=jnp.float32) * (1.0 / np.sqrt(D))
        gate_b = jnp.zeros((E,), dtype=jnp.float32)
        weight1 = jax.random.uniform(k2, (E, D + 1, H), dtype=jnp.float32, minval=-1.0, maxval=1.0) * (1.0 / np.sqrt(D + 1))
        weight2 = jax.random.uniform(k3, (E, H + 1, O), dtype=jnp.float32, minval=-1.0, maxval=1.0) * (1.0 / np.sqrt(H + 1))
        return {'x': x, 'gate_w': gate_w, 'gate_b': gate_b, 'weight1': weight1, 'weight2': weight2}
    _L1_ffn_all = _L1_ffn_setup()
    _L1_ffn_in = {k: v for k, v in _L1_ffn_all.items() if k in ('gate_w', 'gate_b', 'weight1', 'weight2', )}
    del _L1_ffn_all

    def _L2_conv_setup():
        import jax, jax.numpy as jnp
        import numpy as np
        HEADS = 4
        DIM_HEAD = 32
        SCALE = 10.0
        EPS = 1e-12

        def l2norm_axis1(t):
            denom = jnp.clip(jnp.linalg.norm(t, ord=2, axis=1, keepdims=True), EPS)
            return t / denom
        key = jax.random.key(seed)
        k1, k2, k3 = jax.random.split(key, 3)
        B, H, W, C = (4, 64, 64, 128)
        dim = HEADS * DIM_HEAD
        x = jax.random.normal(k1, (B, H, W, C), dtype=jnp.float32)
        w_qkv = jax.random.normal(k2, (C, dim * 3), dtype=jnp.float32) * (1.0 / np.sqrt(C))
        w_out = jax.random.normal(k3, (dim, C), dtype=jnp.float32) * (1.0 / np.sqrt(dim))
        b_out = jnp.zeros((C,), dtype=jnp.float32)
        return {'x': x, 'w_qkv': w_qkv, 'w_out': w_out, 'b_out': b_out}
    _L2_conv_all = _L2_conv_setup()
    _L2_conv_in = {k: v for k, v in _L2_conv_all.items() if k in ('w_qkv', 'w_out', 'b_out', )}
    del _L2_conv_all

    def _L2_ffn_setup():
        import jax, jax.numpy as jnp
        import numpy as np
        B, S, D, E, H, O, K = (512, 2048, 128, 64, 512, 128, 8)
        key = jax.random.key(seed)
        k0, k1, k2, k3 = jax.random.split(key, 4)
        x = jax.random.normal(k0, (B, S, D), dtype=jnp.float32)
        gate_w = jax.random.normal(k1, (E, D), dtype=jnp.float32) * (1.0 / np.sqrt(D))
        gate_b = jnp.zeros((E,), dtype=jnp.float32)
        weight1 = jax.random.uniform(k2, (E, D + 1, H), dtype=jnp.float32, minval=-1.0, maxval=1.0) * (1.0 / np.sqrt(D + 1))
        weight2 = jax.random.uniform(k3, (E, H + 1, O), dtype=jnp.float32, minval=-1.0, maxval=1.0) * (1.0 / np.sqrt(H + 1))
        return {'x': x, 'gate_w': gate_w, 'gate_b': gate_b, 'weight1': weight1, 'weight2': weight2}
    _L2_ffn_all = _L2_ffn_setup()
    _L2_ffn_in = {k: v for k, v in _L2_ffn_all.items() if k in ('gate_w', 'gate_b', 'weight1', 'weight2', )}
    del _L2_ffn_all

    def _L3_conv_setup():
        import jax, jax.numpy as jnp
        import numpy as np
        EPS = 1e-05
        AXIS = 1

        def _sparse_norm(x, alpha, beta):
            m = jnp.mean(x)
            v = jnp.var(x)
            nv = jax.lax.stop_gradient((x - m) * jax.lax.rsqrt(v + EPS))
            return alpha * nv + beta

        def _lin(x, W, b):
            return jnp.einsum('bijc,oc->bijo', x, W) + b
        key = jax.random.key(seed)
        ks = jax.random.split(key, 8)
        L, Cin, Cd = (512, 128, 128)
        g = 1.0 / np.sqrt(2.0)
        std_proj = g * np.sqrt(2.0 / (Cin + Cd))
        std_gate = np.sqrt(2.0 / (Cin + Cd))

        def w(k, o, i, s):
            return (jax.random.normal(k, (o, i), jnp.float32) * s).astype(jnp.float32)
        return {'z': jax.random.normal(ks[0], (1, L, L, Cin), jnp.float32), 'alpha_in': jnp.ones((1,), jnp.float32), 'beta_in': jnp.zeros((1,), jnp.float32), 'W_la': w(ks[1], Cd, Cin, std_proj), 'b_la': jnp.zeros((Cd,), jnp.float32), 'W_ga': w(ks[2], Cd, Cin, std_gate), 'b_ga': jnp.zeros((Cd,), jnp.float32), 'W_lb': w(ks[3], Cd, Cin, std_proj), 'b_lb': jnp.zeros((Cd,), jnp.float32), 'W_gb': w(ks[4], Cd, Cin, std_gate), 'b_gb': jnp.zeros((Cd,), jnp.float32), 'alpha_o': jnp.ones((1,), jnp.float32), 'beta_o': jnp.zeros((1,), jnp.float32), 'W_go': w(ks[5], Cin, Cin, std_gate), 'b_go': jnp.zeros((Cin,), jnp.float32), 'W_lo': w(ks[6], Cin, Cd, std_proj), 'b_lo': jnp.zeros((Cin,), jnp.float32)}
    _L3_conv_all = _L3_conv_setup()
    _L3_conv_in = {k: v for k, v in _L3_conv_all.items() if k in ('alpha_in', 'beta_in', 'W_la', 'b_la', 'W_ga', 'b_ga', 'W_lb', 'b_lb', 'W_gb', 'b_gb', 'alpha_o', 'beta_o', 'W_go', 'b_go', 'W_lo', 'b_lo', )}
    del _L3_conv_all

    def _L3_ffn_setup():
        import jax, jax.numpy as jnp
        import numpy as np
        B, N, D, C, E, K = (8, 8192, 128, 128, 8, 2)
        key = jax.random.key(seed)
        k0, k1, k2 = jax.random.split(key, 3)
        x = jax.random.normal(k0, (B, N, D), dtype=jnp.float32)
        router_w = jax.random.normal(k1, (D, E), dtype=jnp.float32) * 0.05
        router_b = jnp.zeros((E,), dtype=jnp.float32)
        expert_w = jax.random.normal(k2, (E, D, C), dtype=jnp.float32) * (1.0 / np.sqrt(D))
        expert_b = jnp.zeros((E, C), dtype=jnp.float32)
        return {'x': x, 'router_w': router_w, 'router_b': router_b, 'expert_w': expert_w, 'expert_b': expert_b}
    _L3_ffn_all = _L3_ffn_setup()
    _L3_ffn_in = {k: v for k, v in _L3_ffn_all.items() if k in ('router_w', 'router_b', 'expert_w', 'expert_b', )}
    del _L3_ffn_all

    return {
        "x": x,
        "L0_conv_in_proj_w": _L0_conv_in["in_proj_w"],
        "L0_conv_conv_w": _L0_conv_in["conv_w"],
        "L0_conv_conv_b": _L0_conv_in["conv_b"],
        "L0_conv_x_proj_w": _L0_conv_in["x_proj_w"],
        "L0_conv_dt_proj_w": _L0_conv_in["dt_proj_w"],
        "L0_conv_dt_proj_b": _L0_conv_in["dt_proj_b"],
        "L0_conv_A_logs": _L0_conv_in["A_logs"],
        "L0_conv_Ds": _L0_conv_in["Ds"],
        "L0_conv_norm_g": _L0_conv_in["norm_g"],
        "L0_conv_norm_b": _L0_conv_in["norm_b"],
        "L0_conv_out_proj_w": _L0_conv_in["out_proj_w"],
        "L0_ffn_sigma": _L0_ffn_in["sigma"],
        "L0_ffn_phi": _L0_ffn_in["phi"],
        "L0_ffn_M_u": _L0_ffn_in["M_u"],
        "L0_ffn_M_phi_plus": _L0_ffn_in["M_phi_plus"],
        "L0_ffn_M_phi_minus": _L0_ffn_in["M_phi_minus"],
        "L0_ffn_log_weights": _L0_ffn_in["log_weights"],
        "L0_ffn_gumbel": _L0_ffn_in["gumbel"],
        "L1_conv_fw0": _L1_conv_in["fw0"],
        "L1_conv_fw1": _L1_conv_in["fw1"],
        "L1_conv_w1": _L1_conv_in["w1"],
        "L1_conv_b1": _L1_conv_in["b1"],
        "L1_conv_w2": _L1_conv_in["w2"],
        "L1_conv_b2": _L1_conv_in["b2"],
        "L1_ffn_gate_w": _L1_ffn_in["gate_w"],
        "L1_ffn_gate_b": _L1_ffn_in["gate_b"],
        "L1_ffn_weight1": _L1_ffn_in["weight1"],
        "L1_ffn_weight2": _L1_ffn_in["weight2"],
        "L2_conv_w_qkv": _L2_conv_in["w_qkv"],
        "L2_conv_w_out": _L2_conv_in["w_out"],
        "L2_conv_b_out": _L2_conv_in["b_out"],
        "L2_ffn_gate_w": _L2_ffn_in["gate_w"],
        "L2_ffn_gate_b": _L2_ffn_in["gate_b"],
        "L2_ffn_weight1": _L2_ffn_in["weight1"],
        "L2_ffn_weight2": _L2_ffn_in["weight2"],
        "L3_conv_alpha_in": _L3_conv_in["alpha_in"],
        "L3_conv_beta_in": _L3_conv_in["beta_in"],
        "L3_conv_W_la": _L3_conv_in["W_la"],
        "L3_conv_b_la": _L3_conv_in["b_la"],
        "L3_conv_W_ga": _L3_conv_in["W_ga"],
        "L3_conv_b_ga": _L3_conv_in["b_ga"],
        "L3_conv_W_lb": _L3_conv_in["W_lb"],
        "L3_conv_b_lb": _L3_conv_in["b_lb"],
        "L3_conv_W_gb": _L3_conv_in["W_gb"],
        "L3_conv_b_gb": _L3_conv_in["b_gb"],
        "L3_conv_alpha_o": _L3_conv_in["alpha_o"],
        "L3_conv_beta_o": _L3_conv_in["beta_o"],
        "L3_conv_W_go": _L3_conv_in["W_go"],
        "L3_conv_b_go": _L3_conv_in["b_go"],
        "L3_conv_W_lo": _L3_conv_in["W_lo"],
        "L3_conv_b_lo": _L3_conv_in["b_lo"],
        "L3_ffn_router_w": _L3_ffn_in["router_w"],
        "L3_ffn_router_b": _L3_ffn_in["router_b"],
        "L3_ffn_expert_w": _L3_ffn_in["expert_w"],
        "L3_ffn_expert_b": _L3_ffn_in["expert_b"],
    }

def reference(x, L0_conv_in_proj_w, L0_conv_conv_w, L0_conv_conv_b, L0_conv_x_proj_w, L0_conv_dt_proj_w, L0_conv_dt_proj_b, L0_conv_A_logs, L0_conv_Ds, L0_conv_norm_g, L0_conv_norm_b, L0_conv_out_proj_w, L0_ffn_sigma, L0_ffn_phi, L0_ffn_M_u, L0_ffn_M_phi_plus, L0_ffn_M_phi_minus, L0_ffn_log_weights, L0_ffn_gumbel, L1_conv_fw0, L1_conv_fw1, L1_conv_w1, L1_conv_b1, L1_conv_w2, L1_conv_b2, L1_ffn_gate_w, L1_ffn_gate_b, L1_ffn_weight1, L1_ffn_weight2, L2_conv_w_qkv, L2_conv_w_out, L2_conv_b_out, L2_ffn_gate_w, L2_ffn_gate_b, L2_ffn_weight1, L2_ffn_weight2, L3_conv_alpha_in, L3_conv_beta_in, L3_conv_W_la, L3_conv_b_la, L3_conv_W_ga, L3_conv_b_ga, L3_conv_W_lb, L3_conv_b_lb, L3_conv_W_gb, L3_conv_b_gb, L3_conv_alpha_o, L3_conv_beta_o, L3_conv_W_go, L3_conv_b_go, L3_conv_W_lo, L3_conv_b_lo, L3_ffn_router_w, L3_ffn_router_b, L3_ffn_expert_w, L3_ffn_expert_b):
    import jax
    import jax.numpy as jnp
    def _L0_conv_ref(x, in_proj_w, conv_w, conv_b, x_proj_w, dt_proj_w, dt_proj_b, A_logs, Ds, norm_g, norm_b, out_proj_w):
        import jax, jax.numpy as jnp
        import numpy as np
        from jax import lax
        B, H, W, C = (4, 48, 48, 128)
        D_INNER, D_STATE, DT_RANK, K = (256, 16, 8, 4)
        B, H, W, C = x.shape
        d = in_proj_w.shape[0] // 2
        K = x_proj_w.shape[0]
        N = A_logs.shape[1]
        R = x_proj_w.shape[1] - 2 * N
        L = H * W
        xz = jnp.einsum('bhwc,ec->bhwe', x, in_proj_w)
        xin, z = jnp.split(xz, 2, axis=-1)
        xc = jnp.transpose(xin, (0, 3, 1, 2))
        xc = lax.conv_general_dilated(xc, conv_w, (1, 1), [(1, 1), (1, 1)], feature_group_count=d, dimension_numbers=('NCHW', 'OIHW', 'NCHW'))
        xc = jax.nn.silu(xc + conv_b[None, :, None, None])
        x0 = xc.reshape(B, d, L)
        x1 = jnp.transpose(xc, (0, 1, 3, 2)).reshape(B, d, L)
        xs = jnp.stack([x0, x1, x0[..., ::-1], x1[..., ::-1]], axis=1)
        x_dbl = jnp.einsum('bkdl,kcd->bkcl', xs, x_proj_w)
        dts_r, Bs, Cs = (x_dbl[:, :, :R], x_dbl[:, :, R:R + N], x_dbl[:, :, R + N:])
        dts = jnp.einsum('bkrl,kdr->bkdl', dts_r, dt_proj_w)
        dt = jax.nn.softplus(dts + dt_proj_b[None, :, :, None])
        A = -jnp.exp(A_logs).reshape(K, d, N)
        dt_t = jnp.moveaxis(dt, -1, 0)
        u_t = jnp.moveaxis(xs, -1, 0)
        B_t = jnp.moveaxis(Bs, -1, 0)
        C_t = jnp.moveaxis(Cs, -1, 0)

        def step(h, inp):
            dt_l, u_l, B_l, C_l = inp
            dA = jnp.exp(dt_l[..., None] * A)
            h = h * dA + (dt_l * u_l)[..., None] * B_l[:, :, None, :]
            y = jnp.einsum('bkdn,bkn->bkd', h, C_l)
            return (h, y)
        h0 = jnp.zeros((B, K, d, N), x.dtype)
        _, ys = lax.scan(step, h0, (dt_t, u_t, B_t, C_t))
        ys = jnp.moveaxis(ys, 0, -1)
        ys = ys + Ds.reshape(1, K, d, 1) * xs
        y = ys[:, 0] + ys[:, 2][..., ::-1]
        y1 = ys[:, 1] + ys[:, 3][..., ::-1]
        y = y + jnp.transpose(y1.reshape(B, d, W, H), (0, 1, 3, 2)).reshape(B, d, L)
        y = jnp.transpose(y, (0, 2, 1))
        mu = jnp.mean(y, -1, keepdims=True)
        var = jnp.var(y, -1, keepdims=True)
        y = (y - mu) * lax.rsqrt(var + 1e-05) * norm_g + norm_b
        y = y.reshape(B, H, W, d) * jax.nn.silu(z)
        return jnp.einsum('bhwd,cd->bhwc', y, out_proj_w)

    def _L0_ffn_ref(x, sigma, phi, M_u, M_phi_plus, M_phi_minus, log_weights, gumbel):
        import jax, jax.numpy as jnp
        import numpy as np
        PADDED_SL = 8192
        TEMPERATURE = 1.0
        SIGMA_POW = 0.25

        def _stu_conv(phi, u, n):
            b, sl, d = u.shape
            sgn = jnp.where(jnp.arange(sl) % 2 == 0, 1.0, -1.0).astype(u.dtype)
            sgn3 = sgn[None, :, None]
            Vf = jnp.fft.rfft(phi, n=n, axis=0)
            Uf_p = jnp.fft.rfft(u, n=n, axis=1)
            Uf_m = jnp.fft.rfft(u * sgn3, n=n, axis=1)
            U_plus = jnp.fft.irfft(Vf[None, :, :, None] * Uf_p[:, :, None, :], n=n, axis=1)[:, :sl]
            U_minus = jnp.fft.irfft(Vf[None, :, :, None] * Uf_m[:, :, None, :], n=n, axis=1)[:, :sl]
            U_minus = U_minus * sgn[None, :, None, None]
            return (U_plus, U_minus)

        def _compute_spectral(u, sigma, phi, Mpp, Mpm):
            U_plus, U_minus = _stu_conv(phi, u, PADDED_SL)
            s = sigma ** SIGMA_POW
            out = jnp.einsum('btkd,k,kde->bte', U_plus, s, Mpp)
            out = out + jnp.einsum('btkd,k,kde->bte', U_minus, s, Mpm)
            return out

        def _compute_ar_u(Mu, u):
            sl = u.shape[1]
            out = jnp.zeros(u.shape[:2] + (Mu.shape[-1],), dtype=u.dtype)
            for i in range(Mu.shape[0]):
                ui = jnp.pad(u, ((0, 0), (i, 0), (0, 0)))[:, :sl]
                out = out + jnp.einsum('btd,de->bte', ui, Mu[i])
            return out

        def _stu(u, sigma, phi, Mu, Mpp, Mpm):
            return _compute_spectral(u, sigma, phi, Mpp, Mpm) + _compute_ar_u(Mu, u)
        T = x.shape[1]
        outs = []
        for i, frac in enumerate((1, 2, 4, 8)):
            xi = x[:, :T // frac]
            si = _stu(xi, sigma, phi, M_u[i], M_phi_plus[i], M_phi_minus[i])
            si = jnp.pad(si, ((0, 0), (0, T - si.shape[1]), (0, 0)))
            outs.append(si)
        y_soft = jax.nn.softmax((log_weights + gumbel) / TEMPERATURE)
        y_hard = jax.nn.one_hot(jnp.argmax(y_soft), 4, dtype=y_soft.dtype)
        weights = y_hard - jax.lax.stop_gradient(y_soft) + y_soft
        stacked = jnp.stack(outs, axis=-1)
        return jnp.sum(stacked * weights, axis=-1)

    def _L1_conv_ref(x, fw0, fw1, w1, b1, w2, b2):
        import jax, jax.numpy as jnp
        import numpy as np
        D = 128
        MODES = 32
        FACTOR = 4
        B, M, N = (16, 128, 128)

        def _forward_fourier(x, fw0, fw1):
            xt = jnp.transpose(x, (0, 3, 1, 2))
            b, i, m, n = xt.shape
            xfty = jnp.fft.rfft(xt, axis=-1, norm='ortho')
            my = min(MODES, n // 2 + 1)
            wy = jax.lax.complex(fw0[..., 0], fw0[..., 1])[..., :my]
            mixed_y = jnp.einsum('bixy,ioy->boxy', xfty[..., :my], wy)
            pad_y = jnp.zeros(mixed_y.shape[:3] + (n // 2 + 1 - my,), mixed_y.dtype)
            xy = jnp.fft.irfft(jnp.concatenate([mixed_y, pad_y], axis=-1), n=n, axis=-1, norm='ortho')
            xftx = jnp.fft.rfft(xt, axis=-2, norm='ortho')
            mx = min(MODES, m // 2 + 1)
            wx = jax.lax.complex(fw1[..., 0], fw1[..., 1])[..., :mx]
            mixed_x = jnp.einsum('bixy,iox->boxy', xftx[:, :, :mx, :], wx)
            pad_x = jnp.zeros((b, mixed_x.shape[1], m // 2 + 1 - mx, n), mixed_x.dtype)
            xx = jnp.fft.irfft(jnp.concatenate([mixed_x, pad_x], axis=-2), n=m, axis=-2, norm='ortho')
            return jnp.transpose(xx + xy, (0, 2, 3, 1))
        h = _forward_fourier(x, fw0, fw1)
        h = jax.nn.relu(jnp.einsum('bxyd,dh->bxyh', h, w1) + b1)
        b_out = jnp.einsum('bxyh,hd->bxyd', h, w2) + b2
        return b_out

    def _L1_ffn_ref(x, gate_w, gate_b, weight1, weight2):
        import jax, jax.numpy as jnp
        import numpy as np
        B, S, D, E, H, O, K = (512, 2048, 128, 64, 512, 128, 8)
        Bn, Sn, Dn = x.shape
        logits = jnp.einsum('bsd,ed->bse', x, gate_w) + gate_b
        probs = jax.nn.softmax(logits, axis=1)
        vals, idx = jax.lax.top_k(probs.transpose(0, 2, 1), K)
        topv = vals.transpose(0, 2, 1)
        topi = idx.transpose(0, 2, 1)
        flat_idx = topi.reshape(Bn, K * E)
        gathered = jnp.take_along_axis(x, flat_idx[:, :, None], axis=1)
        gathered = gathered.reshape(Bn, K, E, Dn)
        pooled = jnp.einsum('bked,bke->bed', gathered, topv)
        ones = jnp.ones((E, Bn, 1), dtype=x.dtype)
        h = jnp.concatenate([pooled.transpose(1, 0, 2), ones], axis=-1)
        h = jax.nn.gelu(jnp.einsum('ebd,edh->ebh', h, weight1), approximate=False)
        h = jnp.concatenate([h, ones], axis=-1)
        out = jnp.einsum('ebh,eho->ebo', h, weight2)
        out = out.transpose(1, 0, 2)
        weighted = jnp.einsum('beo,bke->bkeo', out, topv).reshape(Bn, K * E, O)
        outputs = jnp.zeros((Bn, Sn, O), dtype=x.dtype)
        outputs = outputs.at[jnp.arange(Bn)[:, None], flat_idx].add(weighted)
        return outputs

    def _L2_conv_ref(x, w_qkv, w_out, b_out):
        import jax, jax.numpy as jnp
        import numpy as np
        HEADS = 4
        DIM_HEAD = 32
        SCALE = 10.0
        EPS = 1e-12

        def l2norm_axis1(t):
            denom = jnp.clip(jnp.linalg.norm(t, ord=2, axis=1, keepdims=True), EPS)
            return t / denom
        B, H, W, C = x.shape
        dim = HEADS * DIM_HEAD
        qkv = jnp.einsum('bxyc,cf->bxyf', x, w_qkv)
        q, k, v = jnp.split(qkv, 3, axis=-1)

        def to_seq(t):
            return t.reshape(B, H * W, HEADS, DIM_HEAD)
        q, k, v = (to_seq(q), to_seq(k), to_seq(v))
        q = l2norm_axis1(q)
        k = l2norm_axis1(k)
        sim = jnp.einsum('bihd,bjhd->bhij', q, k) * SCALE
        attn = jax.nn.softmax(sim, axis=-1)
        out = jnp.einsum('bhij,bjhd->bhid', attn, v)
        out = out.transpose(0, 2, 1, 3).reshape(B, H, W, dim)
        out = jnp.einsum('bxyd,dc->bxyc', out, w_out) + b_out
        return out

    def _L2_ffn_ref(x, gate_w, gate_b, weight1, weight2):
        import jax, jax.numpy as jnp
        import numpy as np
        B, S, D, E, H, O, K = (512, 2048, 128, 64, 512, 128, 8)
        Bn, Sn, Dn = x.shape
        logits = jnp.einsum('bsd,ed->bse', x, gate_w) + gate_b
        probs = jax.nn.softmax(logits, axis=1)
        vals, idx = jax.lax.top_k(probs.transpose(0, 2, 1), K)
        topv = vals.transpose(0, 2, 1)
        topi = idx.transpose(0, 2, 1)
        flat_idx = topi.reshape(Bn, K * E)
        gathered = jnp.take_along_axis(x, flat_idx[:, :, None], axis=1)
        gathered = gathered.reshape(Bn, K, E, Dn)
        pooled = jnp.einsum('bked,bke->bed', gathered, topv)
        ones = jnp.ones((E, Bn, 1), dtype=x.dtype)
        h = jnp.concatenate([pooled.transpose(1, 0, 2), ones], axis=-1)
        h = jax.nn.gelu(jnp.einsum('ebd,edh->ebh', h, weight1), approximate=False)
        h = jnp.concatenate([h, ones], axis=-1)
        out = jnp.einsum('ebh,eho->ebo', h, weight2)
        out = out.transpose(1, 0, 2)
        weighted = jnp.einsum('beo,bke->bkeo', out, topv).reshape(Bn, K * E, O)
        outputs = jnp.zeros((Bn, Sn, O), dtype=x.dtype)
        outputs = outputs.at[jnp.arange(Bn)[:, None], flat_idx].add(weighted)
        return outputs

    def _L3_conv_ref(z, alpha_in, beta_in, W_la, b_la, W_ga, b_ga, W_lb, b_lb, W_gb, b_gb, alpha_o, beta_o, W_go, b_go, W_lo, b_lo):
        import jax, jax.numpy as jnp
        import numpy as np
        EPS = 1e-05
        AXIS = 1

        def _sparse_norm(x, alpha, beta):
            m = jnp.mean(x)
            v = jnp.var(x)
            nv = jax.lax.stop_gradient((x - m) * jax.lax.rsqrt(v + EPS))
            return alpha * nv + beta

        def _lin(x, W, b):
            return jnp.einsum('bijc,oc->bijo', x, W) + b
        zn = _sparse_norm(z, alpha_in, beta_in)
        a = jax.nn.sigmoid(_lin(zn, W_ga, b_ga)) * _lin(zn, W_la, b_la)
        b = jax.nn.sigmoid(_lin(zn, W_gb, b_gb)) * _lin(zn, W_lb, b_lb)
        if AXIS == 1:
            k = jnp.einsum('bitc,bjtc->bijc', a, b)
        else:
            k = jnp.einsum('btic,btjc->bijc', a, b)
        kn = _sparse_norm(k, alpha_o, beta_o)
        return jax.nn.sigmoid(_lin(zn, W_go, b_go)) * _lin(kn, W_lo, b_lo)

    def _L3_ffn_ref(x, router_w, router_b, expert_w, expert_b):
        import jax, jax.numpy as jnp
        import numpy as np
        B, N, D, C, E, K = (8, 8192, 128, 128, 8, 2)
        router_probs = jax.nn.softmax(x @ router_w + router_b, axis=-1)
        top_p, top_i = jax.lax.top_k(router_probs, K)
        top_p = top_p / jnp.sum(top_p, axis=-1, keepdims=True)
        expert_out = jnp.einsum('bnd,edc->bnec', x, expert_w) + expert_b
        gathered = jnp.take_along_axis(expert_out, top_i[..., None], axis=2)
        return jnp.einsum('bnk,bnkc->bnc', top_p, gathered)

    def _gn(v, G=32, eps=1e-5):
        B_, H_, W_, C_ = v.shape
        g = v.reshape(B_, H_, W_, G, C_ // G)
        m = jnp.mean(g, axis=(1, 2, 4), keepdims=True)
        s = jnp.var(g, axis=(1, 2, 4), keepdims=True)
        return ((g - m) / jnp.sqrt(s + eps)).reshape(v.shape)

    def _ln_c(v, eps=1e-6):
        m = jnp.mean(v, axis=-1, keepdims=True)
        s = jnp.var(v, axis=-1, keepdims=True)
        return (v - m) / jnp.sqrt(s + eps)

    def _ln_t(v, eps=1e-5):
        m = jnp.mean(v, axis=-1, keepdims=True)
        s = jnp.var(v, axis=-1, keepdims=True)
        return (v - m) / jnp.sqrt(s + eps)

    def _to_tokens(v):
        B_, H_, W_, C_ = v.shape
        return v.reshape(B_, H_ * W_, C_)
    def _from_tokens(t, like):
        return t.reshape(like.shape)

    x = x + _L0_conv_ref(_ln_c(x), L0_conv_in_proj_w, L0_conv_conv_w, L0_conv_conv_b, L0_conv_x_proj_w, L0_conv_dt_proj_w, L0_conv_dt_proj_b, L0_conv_A_logs, L0_conv_Ds, L0_conv_norm_g, L0_conv_norm_b, L0_conv_out_proj_w)
    t = _to_tokens(x)
    t = t + _L0_ffn_ref(_ln_t(t), L0_ffn_sigma, L0_ffn_phi, L0_ffn_M_u, L0_ffn_M_phi_plus, L0_ffn_M_phi_minus, L0_ffn_log_weights, L0_ffn_gumbel)
    x = _from_tokens(t, x)
    x = x + _L1_conv_ref(_ln_c(x), L1_conv_fw0, L1_conv_fw1, L1_conv_w1, L1_conv_b1, L1_conv_w2, L1_conv_b2)
    t = _to_tokens(x)
    t = t + _L1_ffn_ref(_ln_t(t), L1_ffn_gate_w, L1_ffn_gate_b, L1_ffn_weight1, L1_ffn_weight2)
    x = _from_tokens(t, x)
    x = x + _L2_conv_ref(_ln_c(x), L2_conv_w_qkv, L2_conv_w_out, L2_conv_b_out)
    t = _to_tokens(x)
    t = t + _L2_ffn_ref(_ln_t(t), L2_ffn_gate_w, L2_ffn_gate_b, L2_ffn_weight1, L2_ffn_weight2)
    x = _from_tokens(t, x)
    x = x + _L3_conv_ref(_ln_c(x), L3_conv_alpha_in, L3_conv_beta_in, L3_conv_W_la, L3_conv_b_la, L3_conv_W_ga, L3_conv_b_ga, L3_conv_W_lb, L3_conv_b_lb, L3_conv_W_gb, L3_conv_b_gb, L3_conv_alpha_o, L3_conv_beta_o, L3_conv_W_go, L3_conv_b_go, L3_conv_W_lo, L3_conv_b_lo)
    t = _to_tokens(x)
    t = t + _L3_ffn_ref(_ln_t(t), L3_ffn_router_w, L3_ffn_router_b, L3_ffn_expert_w, L3_ffn_expert_b)
    x = _from_tokens(t, x)
    return x


_drawn_inputs = setup_inputs


def setup_inputs(seed=0):
    import zlib

    import numpy as np

    out = dict(_drawn_inputs(seed))
    spreads = {'L0_conv_conv_b': (0.0, 0.1),
     'L0_conv_Ds': (1.0, 0.2),
     'L0_conv_norm_g': (1.0, 0.2),
     'L0_conv_norm_b': (0.0, 0.1),
     'L0_ffn_log_weights': (1.0, 0.2),
     'L1_ffn_gate_b': (0.0, 2.0),
     'L2_conv_b_out': (0.0, 0.1),
     'L2_ffn_gate_b': (0.0, 2.0),
     'L3_conv_b_la': (0.0, 0.1),
     'L3_conv_b_ga': (0.0, 0.299),
     'L3_conv_b_lb': (0.0, 0.1),
     'L3_conv_b_gb': (0.0, 0.272),
     'L3_conv_b_go': (0.0, 0.308),
     'L3_conv_b_lo': (0.0, 0.1),
     'L3_ffn_router_b': (0.0, 0.1),
     'L3_ffn_expert_b': (0.0, 0.274)}
    factors = {'L1_ffn_gate_w': 8.0,
     'L1_ffn_weight1': 6.972,
     'L1_ffn_weight2': 6.925,
     'L2_ffn_gate_w': 8.0,
     'L2_ffn_weight1': 7.844,
     'L2_ffn_weight2': 7.786}
    for name, (base, spread) in spreads.items():
        noise = np.random.default_rng([zlib.crc32(name.encode()), seed]).standard_normal(out[name].shape)
        drawn = base * np.exp(spread * noise) if base else spread * noise
        out[name] = jnp.asarray(drawn.astype(out[name].dtype))
    for name, factor in factors.items():
        out[name] = (out[name] * factor).astype(out[name].dtype)
    return out
```

```python
from contextlib import ExitStack

import numpy as np
import concourse.bass as bass
from concourse import mybir

P = 128
B, H, W, C = 4, 48, 48, 128
S = H * W
T = B * S
G = T // 256
GB = G // B
HALF = S // 2

F32 = mybir.dt.float32
BF16 = mybir.dt.bfloat16
ALU = mybir.AluOpType
ACT = mybir.ActivationFunctionType
AX = mybir.AxisListType


class Chain:

    def __init__(self, eng, sem):
        self.eng, self.sem, self.base, self.n = eng, sem, 0, 0

    def link(self, ins):
        self.n += 1
        ins.then_inc(self.sem, 1)
        self.eng.wait_ge(self.sem, self.base + self.n)

    def enter(self, i, per):
        self.start, self.per, self.outer = self.base + self.n, per, (self.base, self.n)
        self.base, self.n = self.start + i * per, 0

    def leave(self, passes):
        assert self.n == self.per, (self.n, self.per)
        self.base, self.n = self.outer[0], self.outer[1] + passes * self.per


class Signals:

    def __init__(self, nc, stage, names):
        self.nc = nc
        self.named = {n: nc.alloc_semaphore(f"{stage}_{n}") for n in names.split()}
        self.all = list(self.named.values())

    def __getitem__(self, name):
        return self.named[name]

    def clear(self):
        for s in self.all:
            self.nc.gpsimd.sem_clear(s)
        self.nc.all_engine_barrier()

    def release(self):
        for s in self.all:
            self.nc.release_semaphore(s)

    def end(self):
        self.clear()
        self.release()


def bc(ap, shape):
    return ap.to_broadcast(shape)


def layer_norm(nc, name, X, XN, eps):
    NT = 2 * G
    with ExitStack() as ctx:
        st = ctx.enter_context(nc.sbuf_tensor(name + "_stats", [P, NT, 6], F32))
        mean = ctx.enter_context(nc.sbuf_tensor(name + "_mean", [P, NT], F32))
        var = ctx.enter_context(nc.sbuf_tensor(name + "_var", [P, NT], F32))
        std = ctx.enter_context(nc.sbuf_tensor(name + "_std", [P, NT], F32))
        rstd = ctx.enter_context(nc.sbuf_tensor(name + "_rstd", [P, NT], F32))
        epst = ctx.enter_context(nc.sbuf_tensor(name + "_eps", [P, 1], F32))
        s = Signals(nc, name, "own var_ready std_ready")
        xf = X[:, :, :, :].rearrange("p g t c -> p (g t) c")
        nf = XN[:, :, :, :].rearrange("p g t c -> p (g t) c")
        block = ctx.enter_context(nc.Block())

        @block.vector
        def _(dve):
            ch = Chain(dve, s["own"])
            ch.link(dve.memset(epst[:, :], eps))
            with dve.Fori(0, NT // 4) as i:
                for u in range(4):
                    ins = dve.bn_stats(st[:, i * 4 + u, :], xf[:, i * 4 + u, :])
                ch.enter(i, 1)
                ch.link(ins)
            ch.leave(NT // 4)
            me, mo, ve, vo = (st[:, :, k] for k in (1, 4, 2, 5))
            ch.link(dve.tensor_tensor(mean[:, :], me, mo, ALU.add))
            ch.link(dve.tensor_tensor(std[:, :], me, mo, ALU.subtract))
            ch.link(dve.tensor_tensor(std[:, :], std[:, :], std[:, :], ALU.mult))
            ch.link(dve.tensor_tensor(var[:, :], ve, vo, ALU.add))
            ch.link(dve.tensor_scalar(mean[:, :], mean[:, :], 0.5, None, ALU.mult))
            ch.link(dve.tensor_scalar(var[:, :], var[:, :], 1.0 / C, None, ALU.mult))
            dve.scalar_tensor_tensor(var[:, :], std[:, :], 0.25, var[:, :], ALU.mult, ALU.add).then_inc(s["var_ready"], 1)
            ch.link(dve.tensor_tensor(nf, xf, bc(mean[:, :, None], [P, NT, C]), ALU.subtract))
            dve.wait_ge(s["std_ready"], 1)
            ch.link(dve.reciprocal(rstd[:, :], std[:, :]))
            ch.link(dve.tensor_tensor(nf, nf, bc(rstd[:, :, None], [P, NT, C]), ALU.mult))

        @block.scalar
        def _(act):
            act.wait_ge(s["var_ready"], 1)
            act.activation(std[:, :], var[:, :], ACT.Sqrt, bias=epst[:, :]).then_inc(s["std_ready"], 1)
    s.end()


def transpose_tokens(nc, name, XN, out_of, ident):
    with ExitStack() as ctx:
        stage = ctx.enter_context(nc.sbuf_tensor(name + "_stage", [P, 2, 4, C], F32))
        ps = ctx.enter_context(nc.psum_tensor(name + "_ps", [P, 2, 512], F32))
        s = Signals(nc, name, "staged turned stored")
        staged, turned, stored = s.all
        block = ctx.enter_context(nc.Block())

        @block.vector
        def _(dve):
            with dve.Fori(0, G // 4) as i:
                for u in range(2):
                    dve.wait_ge(turned, i * 2 + u + 1)
                    src = XN[:, bass.ds(i * 4 + 2 * u, 2), :, :].rearrange("p g t c -> p (g t) c")
                    dve.tensor_copy(stage[:, u, :, :], src).then_inc(staged, 1)

        @block.tensor
        def _(pe):
            pe.sem_inc(turned, 2)
            with pe.Fori(0, G // 4) as i:
                for u in range(2):
                    pe.wait_ge(staged, i * 2 + u + 1)
                    pe.wait_ge(stored, i * 2 + u + 1)
                    for t in range(4):
                        ins = pe.transpose(ps[:, u, t * 128:(t + 1) * 128], stage[:, u, t, :], ident[:, :])
                    ins.then_inc(turned, 1)

        @block.scalar
        def _(act):
            act.sem_inc(stored, 2)
            with act.Fori(0, G // 4) as i:
                for u in range(2):
                    act.wait_ge(turned, i * 2 + u + 3)
                    for g in range(2):
                        src = ps[:, u, g * 256:(g + 1) * 256].rearrange("c (t p) -> c t p", t=2)
                        ins = act.activation(out_of(i * 4 + 2 * u + g), src, ACT.Copy)
                    ins.then_inc(stored, 1)
    s.end()


def load_all(nc, name, pairs):
    s = Signals(nc, name, "loaded")
    with nc.Block() as block:
        @block.sync
        def _(sp):
            for dst, src in pairs:
                sp.dma_start(dst, src).then_inc(s["loaded"], 16)
            sp.wait_ge(s["loaded"], 16 * len(pairs))
    s.end()


R_ORDER = 384
NCH = S // R_ORDER
D2 = 2
NST = 16
DTR = 8
L2 = S // 2
SC = L2 // R_ORDER


def selective_scan_mixer(nc, XT, x_in, x_out, w):
    with ExitStack() as ctx:
        def sb(name, shape, dt=F32):
            return ctx.enter_context(nc.sbuf_tensor("ss_" + name, shape, dt))

        win = sb("win", [P, 512])
        convw = sb("convw", [P, D2, 9])
        convb = sb("convb", [P, D2])
        xpw = sb("xpw", [P, D2, 4, 40])
        dtw = sb("dtw", [DTR, 4, 256])
        dtb = sb("dtb", [P, 4, D2])
        a_log = sb("a_log", [P, 4, D2, NST])
        a_neg = sb("a_neg", [P, 4, D2, NST])
        ds = sb("ds", [P, 4, D2])
        dsum = sb("dsum", [P, D2])
        ng = sb("ng", [P, D2])
        nb = sb("nb", [P, D2])
        wout = sb("wout", [P, D2, P])
        ident = sb("ident", [P, P])
        sel = sb("sel", [96, 32, P], BF16)
        zero = sb("zero", [P, R_ORDER], BF16)
        over = sb("over", [P, P])
        eps = sb("eps", [P, 1])
        xb = sb("xb", [P, 18, C])
        xc = sb("xc", [P, 2, D2, S])
        y = sb("y", [P, D2, S])
        work = sb("work", [P, 16 * L2])
        bc3 = sb("bc3", [96, L2], BF16)
        rest = sb("rest", [32, L2])
        mid = sb("mid", [32, L2], BF16)
        dtr = sb("dtr", [DTR, L2])
        last = sb("last", [P, D2, NST])
        ps = ctx.enter_context(nc.psum_tensor("ss_ps", [P, 8, 512], F32))

        def part(at, shape):
            n = int(np.prod(shape))
            names = "abcd"[:len(shape)]
            kw = {c: s for c, s in zip(names, shape)}
            return work[:, at * L2:at * L2 + n].rearrange(f"p ({' '.join(names)}) -> p {' '.join(names)}", **kw)

        xpad = part(0, [D2, 50, 50])
        decay, drive, hid, rep = part(0, [D2, L2]), part(2, [D2, L2]), part(4, [2, D2, L2]), part(8, [2, 2, L2])
        dt, dtu = part(12, [D2, L2]), part(14, [D2, L2])
        sq, sd, sz = part(0, [D2, S]), part(4, [S]), part(6, [D2, S])

        load_all(nc, "ss_weights", [
            (win[:, :], w["win"]), (convw[:, :, :], w["convw"]), (convb[:, :], w["convb"]),
            (xpw[:, :, :, :], w["xpw"]), (dtw[:, :, :], w["dtw"]), (dtb[:, :, :], w["dtb"]),
            (a_log[:, :, :, :], w["a_log"]), (ds[:, :, :], w["ds"]), (ng[:, :], w["ng"]), (nb[:, :], w["nb"]),
            (wout[:, :, :], w["wout"]), (ident[:, :], w["ident"]), (sel[:, :, :], w["sel"])])

        s0 = Signals(nc, "ss0", "own exp_ready")
        own, exp_ready = s0["own"], s0["exp_ready"]
        with nc.Block() as block:

            @block.scalar
            def _(act):
                act.activation(a_neg[:, :, :, :], a_log[:, :, :, :], ACT.Exp).then_inc(exp_ready, 1)

            @block.vector
            def _(dve):
                ch = Chain(dve, own)
                dve.memset(zero[:, :], 0.0)
                dve.memset(over[:, :], 1.0 / 256)
                dve.memset(eps[:, :], 1e-5)
                ch.link(dve.tensor_tensor(dsum[:, :], ds[:, 0, :], ds[:, 1, :], ALU.add))
                for k in (2, 3):
                    ch.link(dve.tensor_tensor(dsum[:, :], dsum[:, :], ds[:, k, :], ALU.add))
                dve.wait_ge(exp_ready, 1)
                ch.link(dve.tensor_scalar(a_neg[:, :, :, :], a_neg[:, :, :, :], -1.0, None, ALU.mult))

        s0.end()
        s1 = Signals(nc, "ss1", "loaded projected padded cleared conv_own conv_done gated")
        s2 = Signals(nc, "ss2", "xdbl dtr_ready bank_free split own dts prep own_act soft dt_ready decay_ready "
                                "rep_banks rep_ready scanned weighted summed zeroed last_own y_free pool_own")
        s3 = Signals(nc, "ss3", "mean centred squared varied sd_ready own normed affine zed zgated gated summed stored own_act")
        TOK = S
        held = dict(ps=ps, xc=xc, y=y, xpw=xpw, dtw=dtw, dtb=dtb, a_neg=a_neg, sel=sel, zero=zero, ident=ident, decay=decay, drive=drive, hid=hid, rep=rep, dt=dt, dtu=dtu, bc3=bc3, rest=rest, mid=mid, dtr=dtr, last=last, xb=xb, over=over, eps=eps, ng=ng, nb=nb, win=win, wout=wout, XT=XT, x_out=x_out, sq=sq, sd=sd, sz=sz)

        with nc.Fori(0, B) as b:
            with nc.Block() as block:
                @block.sync
                def _(sp):
                    sp.dma_start(xb[:, :, :].rearrange("p n c -> p (n c)"), x_in[bass.ds(b * S, S), :].rearrange("(p n) c -> p (n c)", p=P)).then_inc(s1["loaded"], 16)
                    sp.wait_ge(s1["loaded"], 16)

                @block.gpsimd
                def _(pool):
                    pool.memset(xpad, 0.0).then_inc(s1["cleared"], 1)

                @block.tensor
                def _(pe):
                    for n in range(D2 * NCH):
                        d, c = n // NCH, n % NCH
                        if n >= 8:
                            pe.wait_ge(s1["padded"], n - 7)
                        pe.matmul(ps[:, n % 8, 0:R_ORDER], win[:, d * P:(d + 1) * P],
                                  XT[:, bass.ds(b * TOK + c * R_ORDER, R_ORDER)], start=True, stop=True).then_inc(s1["projected"], 1)

                @block.scalar
                def _(act):
                    act.wait_ge(s1["cleared"], 1)
                    for n in range(D2 * NCH):
                        d, c = n // NCH, n % NCH
                        act.wait_ge(s1["projected"], n + 1)
                        act.activation(xpad[:, d, 1 + 8 * c:9 + 8 * c, 1:49],
                                       ps[:, n % 8, 0:R_ORDER].rearrange("p (h w) -> p h w", w=W), ACT.Copy).then_inc(s1["padded"], 1)
                    for d in range(D2):
                        act.wait_ge(s1["conv_done"], d + 1)
                        act.activation(xc[:, 0, d, :], y[:, d, :], ACT.Silu, bias=convb[:, d:d + 1]).then_inc(s1["gated"], 1)
                        act.wait_ge(s1["gated"], 2 * d + 1)
                        act.activation(xc[:, 1, d, :].rearrange("p (w h) -> p h w", h=H),
                                       xc[:, 0, d, :].rearrange("p (h w) -> p h w", w=W), ACT.Copy).then_inc(s1["gated"], 1)

                @block.vector
                def _(dve):
                    ch = Chain(dve, s1["conv_own"])
                    for d in range(D2):
                        dve.wait_ge(s1["padded"], NCH * (d + 1))
                        out = y[:, d, :].rearrange("p (h w) -> p h w", w=W)
                        for t in range(9):
                            tap = xpad[:, d, t // 3:t // 3 + H, t % 3:t % 3 + W]
                            if t == 0:
                                ch.link(dve.tensor_scalar(out, tap, convw[:, d, 0:1], None, ALU.mult))
                            else:
                                ins = dve.scalar_tensor_tensor(out, tap, convw[:, d, t:t + 1], out, ALU.mult, ALU.add)
                                if t < 8:
                                    ch.link(ins)
                        ins.then_inc(s1["conv_done"], 1)
                    for d in range(D2):
                        dve.wait_ge(s1["gated"], 2 * d + 1)
                        ins = dve.tensor_scalar(y[:, d, :], xc[:, 0, d, :], dsum[:, d:d + 1], None, ALU.mult)
            s1.clear()

            for k in range(4):
                for half in ((0, 1) if k < 2 else (1, 0)):
                    scan_section(nc, s2, k, half, half == (0 if k < 2 else 1), held)
                    s2.clear()

            norm_gate_project(nc, s3, b, held)
            s3.clear()
        for s in (s1, s2, s3):
            s.release()


def scan_section(nc, s, k, half, first, v):
    ps, xc, y, xpw, dtw, dtb, a_neg, sel, zero, ident = (v[n] for n in "ps xc y xpw dtw dtb a_neg sel zero ident".split())
    decay, drive, hid, rep, dt, dtu = (v[n] for n in "decay drive hid rep dt dtu".split())
    bc3, rest, mid, dtr, last = (v[n] for n in "bc3 rest mid dtr last".split())
    lo = half * L2
    src = xc[:, k % 2, :, lo:lo + L2]
    step = -1 if k >= 2 else 1
    R = R_ORDER
    acc = ps[:, 0:6, 0:R]
    bank = ps[:, 6:8, 0:R]

    with nc.Block() as block:
        @block.tensor
        def _(pe):
            for c in range(SC):
                if c >= 2:
                    pe.wait_ge(s["split"], c - 1)
                    pe.wait_ge(s["dtr_ready"], c - 1)
                for d in range(D2):
                    ins = pe.matmul(bank[0:40, c % 2, :], xpw[:, d, k, :], src[:, d, c * R:(c + 1) * R], start=d == 0, stop=d == 1)
                ins.then_inc(s["xdbl"], 1)
            pe.wait_ge(s["dtr_ready"], SC)
            pe.wait_ge(s["split"], SC)
            for m in range(2 * SC):
                d, c = m // SC, m % SC
                if m >= 2:
                    pe.wait_ge(s["bank_free"], m - 1)
                pe.matmul(bank[:, m % 2, :], dtw[:, k, d * P:(d + 1) * P], dtr[:, c * R:(c + 1) * R], start=True, stop=True).then_inc(s["dts"], 1)
            for m in range(6):
                pe.matmul(acc[:, m, :], sel[:, 0, :], zero[0:96, :], start=True, stop=False, skip_group_check=True)
            pe.wait_ge(s["prep"], 1)

            def rep_state(n, u):
                for m in range(6):
                    pe.wait_ge(s["bank_free"], n * 6 + (2 * SC + m - 1))
                    pe.matmul(bank[:, m % 2, :], sel[:, bass.ds(n + 16 * (m // 3), 1), :].rearrange("p a c -> p (a c)"),
                              bc3[:, (m % 3) * R:(m % 3 + 1) * R], start=True, stop=True).then_inc(s["rep_banks"], 1)

            def sum_state(n, u):
                for d in range(D2):
                    pe.wait_ge(s["weighted"], n * 2 + (d + 1))
                    for c in range(SC):
                        ins = pe.matmul(acc[:, d * SC + c, :], ident[:, :], hid[:, u, d, c * R:(c + 1) * R], start=False, stop=False, skip_group_check=True)
                    ins.then_inc(s["summed"], 1)

            rep_state(0, 0)
            with pe.Fori(0, NST // 2 - 1) as i:
                for u in range(2):
                    rep_state(i * 2 + (u + 1), 1 - u)
                    sum_state(i * 2 + u, u)
            rep_state(NST - 1, 1)
            sum_state(NST - 2, 0)
            sum_state(NST - 1, 1)
            for m in range(6):
                ins = pe.matmul(acc[:, m, :], sel[:, 0, :], zero[0:96, :], start=False, stop=True, skip_group_check=True)
            ins.then_inc(s["summed"], 1)

        @block.scalar
        def _(act):
            for c in range(SC):
                act.wait_ge(s["xdbl"], c + 1)
                act.activation(dtr[:, c * R:(c + 1) * R], bank[32:40, c % 2, :], ACT.Copy).then_inc(s["dtr_ready"], 1)
            for m in range(2 * SC):
                d, c = m // SC, m % SC
                act.wait_ge(s["dts"], m + 1)
                act.activation(decay[:, d, c * R:(c + 1) * R], bank[:, m % 2, :], ACT.Abs, bias=dtb[:, k, d:d + 1])
                act.activation(dt[:, d, c * R:(c + 1) * R], bank[:, m % 2, :], ACT.Relu, bias=dtb[:, k, d:d + 1]).then_inc(s["bank_free"], 1)
            act.wait_ge(s["bank_free"], 2 * SC)
            act.activation(decay, decay, ACT.Exp, scale=-1.0).then_inc(s["own_act"], 1)
            act.wait_ge(s["own_act"], 1)
            act.activation(decay, decay, ACT.Ln, bias=1.0).then_inc(s["soft"], 1)
            act.wait_ge(s["dt_ready"], 1)

            def rep_store(n, u):
                if not isinstance(n, int) or n >= 2:
                    act.wait_ge(s["weighted"], n * 2 - 2)
                for m in range(6):
                    act.wait_ge(s["rep_banks"], n * 6 + (m + 1))
                    act.activation(rep[:, u, m // 3, (m % 3) * R:(m % 3 + 1) * R], bank[:, m % 2, :], ACT.Copy).then_inc(s["bank_free"], 1)

            def decays(n, u):
                for d in range(D2):
                    if not isinstance(n, int) or n >= 1:
                        act.wait_ge(s["scanned"], n * 2 + (d - 1))
                    act.activation(decay[:, d, :], dt[:, d, :], ACT.Exp, scale=a_neg[:, k, d, bass.ds(n, 1)]).then_inc(s["decay_ready"], 1)

            for n in range(2):
                rep_store(n, n)
                decays(n, n)
            with act.Fori(1, NST // 2) as i:
                for u in range(2):
                    rep_store(i * 2 + u, u)
                    decays(i * 2 + u, u)

        @block.vector
        def _(dve):
            ch = Chain(dve, s["own"])
            if first:
                ch.link(dve.memset(last[:, :, :], 0.0))
            for c in range(SC):
                at = slice(c * R, (c + 1) * R)
                dve.wait_ge(s["xdbl"], c + 1)
                ch.link(dve.tensor_copy(bc3[0:32, at], bank[0:32, c % 2, :]))
                dve.tensor_tensor(rest[:, at], bank[0:32, c % 2, :], bc3[0:32, at], ALU.subtract).then_inc(s["split"], 1)
            dve.wait_ge(s["split"], SC)
            ch.link(dve.tensor_copy(mid[:, :], rest[:, :]))
            ch.link(dve.tensor_copy(bc3[32:64, :], mid[:, :]))
            dve.tensor_tensor(bc3[64:96, :], rest[:, :], mid[:, :], ALU.subtract).then_inc(s["prep"], 1)
            dve.wait_ge(s["soft"], 1)
            ch.link(dve.tensor_tensor(dt, dt, decay, ALU.add))
            dve.tensor_tensor(dtu, dt, src, ALU.mult).then_inc(s["dt_ready"], 1)
            dve.wait_ge(s["dt_ready"], 1)

            def scan_state(n, u):
                for d in range(D2):
                    dve.wait_ge(s["bank_free"], n * 6 + (2 * SC + 3))
                    ch.link(dve.tensor_tensor(drive[:, d, :], dtu[:, d, :], rep[:, u, 0, :], ALU.mult))
                    dve.wait_ge(s["decay_ready"], n * 2 + (d + 1))
                    if not isinstance(n, int) or n >= 2:
                        dve.wait_ge(s["summed"], n * 2 + (d - 3))
                    dve.tensor_tensor_scan(hid[:, u, d, ::step], decay[:, d, ::step], drive[:, d, ::step],
                                           last[:, d, bass.ds(n, 1)], ALU.mult, ALU.add).then_inc(s["own"], 1)
                    ch.n += 1
                    dve.wait_ge(s["own"], ch.base + ch.n)
                    end = 0 if step < 0 else L2 - 1
                    dve.tensor_scalar(last[:, d, bass.ds(n, 1)], hid[:, u, d, end:end + 1], 1.0, None, ALU.mult).then_inc(s["scanned"], 1)

            for n in range(2):
                scan_state(n, n)
            per = 8
            with dve.Fori(1, NST // 2) as i:
                ch.enter(i - 1, per)
                for u in range(2):
                    scan_state(i * 2 + u, u)
            ch.leave(NST // 2 - 1)
            dve.wait_ge(s["summed"], 2 * NST + 1)
            for d in range(D2):
                for c in range(SC):
                    src_c = acc[:, d * SC + c, :].rearrange("p (a b) -> p a b", b=48)
                    if k % 2 == 0:
                        out = y[:, d, lo + c * R:lo + (c + 1) * R].rearrange("p (a b) -> p a b", b=48)
                    else:
                        w0 = (lo + c * R) // 48
                        out = y[:, d, :].rearrange("p (h w) -> p w h", w=W)[:, w0:w0 + 8, :]
                    dve.tensor_tensor(out, out, src_c, ALU.add)

        @block.gpsimd
        def _(pool):
            def weigh(n, u):
                pool.wait_ge(s["bank_free"], n * 6 + (2 * SC + 6))
                for d in range(D2):
                    pool.wait_ge(s["scanned"], n * 2 + (d + 1))
                    pool.tensor_tensor(hid[:, u, d, :], hid[:, u, d, :], rep[:, u, 1, :], ALU.mult).then_inc(s["weighted"], 1)
            with pool.Fori(0, NST // 2) as i:
                for u in range(2):
                    weigh(i * 2 + u, u)


def norm_gate_project(nc, s, b, v):
    ps, y, xb, over, eps, ng, nb, win, wout, XT, x_out = (v[n] for n in "ps y xb over eps ng nb win wout XT x_out".split())
    sq, sd, sz = v["sq"], v["sd"], v["sz"]
    R = R_ORDER
    flat = ps[:, 0:NCH, 0:R]

    def chunks(ap):
        return ap.rearrange("p (n r) -> p n r", r=R)

    with nc.Block() as block:
        @block.tensor
        def _(pe):
            for c in range(NCH):
                for d in range(D2):
                    ins = pe.matmul(flat[:, c, :], over[:, :], y[:, d, c * R:(c + 1) * R], start=d == 0, stop=d == 1)
            ins.then_inc(s["mean"], 1)
            pe.wait_ge(s["squared"], D2)
            for c in range(NCH):
                for d in range(D2):
                    ins = pe.matmul(flat[:, c, :], over[:, :], sq[:, d, c * R:(c + 1) * R], start=d == 0, stop=d == 1)
            ins.then_inc(s["varied"], 1)
            for d in range(D2):
                pe.wait_ge(s["sd_ready"], 1)
                if d:
                    pe.wait_ge(s["zgated"], 1)
                for c in range(NCH):
                    ins = pe.matmul(flat[:, c, :], win[:, (2 + d) * P:(3 + d) * P], XT[:, bass.ds(b * S + c * R, R)], start=True, stop=True)
                ins.then_inc(s["zed"], 1)
            pe.wait_ge(s["zgated"], 2)
            pe.wait_ge(s["gated"], 2)
            for n in range(18):
                for d in range(D2):
                    ins = pe.matmul(ps[:, n // 4, (n % 4) * P:(n % 4 + 1) * P], y[:, d, n::18], wout[:, d, :], start=d == 0, stop=d == 1)
            ins.then_inc(s["summed"], 1)

        @block.vector
        def _(dve):
            ch = Chain(dve, s["own"])
            dve.wait_ge(s["mean"], 1)
            for d in range(D2):
                dve.tensor_tensor(chunks(y[:, d, :]), chunks(y[:, d, :]), flat, ALU.subtract).then_inc(s["centred"], 1)
            dve.wait_ge(s["sd_ready"], 1)
            ch.link(dve.reciprocal(sd, sd))
            for d in range(D2):
                dve.tensor_tensor(y[:, d, :], y[:, d, :], sd, ALU.mult).then_inc(s["normed"], 1)
            for d in range(D2):
                dve.wait_ge(s["zgated"], d + 1)
                dve.wait_ge(s["affine"], d + 1)
                dve.tensor_tensor(y[:, d, :], y[:, d, :], sz[:, d, :], ALU.mult).then_inc(s["gated"], 1)
            dve.wait_ge(s["summed"], 1)
            for n in range(5):
                m = min(4, 18 - 4 * n)
                out = xb[:, 4 * n:4 * n + m, :]
                ins = dve.tensor_tensor(out, out, ps[:, n, 0:m * P].rearrange("p (n c) -> p n c", c=C), ALU.add)
                ins.then_inc(s["stored"], 1)

        @block.scalar
        def _(act):
            for d in range(D2):
                act.wait_ge(s["centred"], d + 1)
                act.activation(sq[:, d, :], y[:, d, :], ACT.Square).then_inc(s["squared"], 1)
            act.wait_ge(s["varied"], 1)
            act.activation(chunks(sd), flat, ACT.Sqrt, bias=eps[:, :]).then_inc(s["sd_ready"], 1)
            for d in range(D2):
                act.wait_ge(s["zed"], d + 1)
                act.activation(chunks(sz[:, d, :]), flat, ACT.Silu).then_inc(s["zgated"], 1)
            for d in range(D2):
                act.wait_ge(s["normed"], d + 1)
                act.activation(y[:, d, :], y[:, d, :], ACT.Identity, scale=ng[:, d:d + 1], bias=nb[:, d:d + 1]).then_inc(s["affine"], 1)

        @block.sync
        def _(sp):
            sp.wait_ge(s["stored"], 5)
            sp.dma_start(x_out[bass.ds(b * S, S), :].rearrange("(p n) c -> p (n c)", p=P), xb[:, :, :].rearrange("p n c -> p (n c)")).then_inc(s["mean"], 16)
            sp.wait_ge(s["mean"], 17)


def spread(ap, n):
    return bass.AP(ap.tensor, 0, [[0, P], [1, n]])


def add_channel_major(nc, name, X, Y, ident):
    with ExitStack() as ctx:
        stage = ctx.enter_context(nc.sbuf_tensor(name + "_stage", [P, 2, 4, P], F32))
        ps = ctx.enter_context(nc.psum_tensor(name + "_ps", [P, 2, 512], F32))
        s = Signals(nc, name, "staged turned added")
        with nc.Block() as block:
            @block.scalar
            def _(act):
                with act.Fori(0, G // 4) as i:
                    for u in range(2):
                        act.wait_ge(s["turned"], i * 2 + (u + 1))
                        act.activation(stage[:, u, :, :].rearrange("c (g t) p -> c t g p", t=2),
                                       Y[:, :, bass.ds((i * 4 + 2 * u) * P, 2 * P)].rearrange("c t (g p) -> c t g p", p=P),
                                       ACT.Copy).then_inc(s["staged"], 1)

            @block.tensor
            def _(pe):
                pe.sem_inc(s["turned"], 2)
                with pe.Fori(0, G // 4) as i:
                    for u in range(2):
                        pe.wait_ge(s["staged"], i * 2 + (u + 1))
                        pe.wait_ge(s["added"], i * 2 + (u + 1))
                        for t in range(4):
                            ins = pe.transpose(ps[:, u, t * P:(t + 1) * P], stage[:, u, t, :], ident[:, :])
                        ins.then_inc(s["turned"], 1)

            @block.vector
            def _(dve):
                dve.sem_inc(s["added"], 2)
                with dve.Fori(0, G // 4) as i:
                    for u in range(2):
                        dve.wait_ge(s["turned"], i * 2 + (u + 3))
                        out = X[:, bass.ds(i * 4 + 2 * u, 2), :, :].rearrange("p g t c -> p (g t c)")
                        dve.tensor_tensor(out, out, ps[:, u, :], ALU.add).then_inc(s["added"], 1)
        s.end()


NK = 16
CW = 288
NCW = HALF // CW
NEDGE = 4


def pieces(c):
    return [(0, CW // 2, 0), (CW // 2, CW, 1)] if c == 0 else [(0, CW, {1: 2, 2: 3, 3: 3}[c])]


def spectral_unit(nc, X, w):
    with ExitStack() as ctx:
        def sb(name, shape, dt=F32):
            return ctx.enter_context(nc.sbuf_tensor("stu_" + name, shape, dt))

        ident = sb("ident", [P, P])
        wgt = sb("wgt", [P, NEDGE])
        wk = sb("wk", [P, NK, NEDGE])
        U = sb("U", [P, G, 2, C])
        YT = sb("YT", [P, 2, G * P])
        load_all(nc, "stu_ident", [(ident[:, :], w["ident"])])
        layer_norm(nc, "stu_ln", X, U, 1e-5)
        with nc.sbuf_tensor("stu_XT", [P, 2, G * P], F32) as XT:
            transpose_tokens(nc, "stu_tr", U, lambda g: XT[:, :, bass.ds(g * P, P)], ident)
            branch_weights(nc, w, wgt, wk)
            autoregress(nc, w, XT, YT, wgt)
        convolve(nc, w, U, YT, wk)
        add_channel_major(nc, "stu_add", X, YT, ident)


def branch_weights(nc, w, wgt, wk):
    with ExitStack() as ctx:
        def sb(name, shape):
            return ctx.enter_context(nc.sbuf_tensor("bw_" + name, shape, F32))
        lw, gum, sig, e = sb("lw", [P, 4]), sb("gum", [P, 4]), sb("sig", [P, NK]), sb("e", [P, 4])
        mx, total, hard, count = sb("mx", [P, 1]), sb("total", [P, 1]), sb("hard", [P, 4]), sb("count", [P, 4])
        ones = sb("ones", [P, 4])
        load_all(nc, "bw_load", [(lw[:, :], spread(w["log_weights"], 4)), (gum[:, :], spread(w["gumbel"], 4)),
                                 (sig[:, :], spread(w["sigma"], NK))])
        s = Signals(nc, "bw", "own max_ready exp_ready root")
        with nc.Block() as block:
            @block.vector
            def _(dve):
                ch = Chain(dve, s["own"])
                dve.memset(ones[:, :], 1.0)
                ch.link(dve.tensor_tensor(lw[:, :], lw[:, :], gum[:, :], ALU.add))
                dve.tensor_reduce(mx[:, :], lw[:, :], AX.X, ALU.max, negate=True).then_inc(s["max_ready"], 1)
                dve.wait_ge(s["exp_ready"], 1)
                ch.link(dve.reciprocal(total[:, :], total[:, :]))
                ch.link(dve.tensor_scalar(e[:, :], e[:, :], total[:, :], None, ALU.mult))
                ch.link(dve.tensor_reduce(mx[:, :], e[:, :], AX.X, ALU.max))
                ch.link(dve.tensor_scalar(hard[:, :], e[:, :], mx[:, :], None, ALU.is_equal))
                ch.link(dve.tensor_tensor_scan(count[:, :], ones[:, :], hard[:, :], 0.0, ALU.mult, ALU.add))
                ch.link(dve.tensor_scalar(count[:, :], count[:, :], 1.0, None, ALU.is_equal))
                ch.link(dve.tensor_tensor(hard[:, :], hard[:, :], count[:, :], ALU.mult))
                ch.link(dve.tensor_tensor(wgt[:, :], hard[:, :], e[:, :], ALU.subtract))
                ch.link(dve.tensor_tensor(wgt[:, :], wgt[:, :], e[:, :], ALU.add))
                dve.wait_ge(s["root"], 2)
                for n in range(NEDGE):
                    dve.tensor_scalar(wk[:, :, n], sig[:, :], wgt[:, n:n + 1], None, ALU.mult)

            @block.scalar
            def _(act):
                act.wait_ge(s["max_ready"], 1)
                act.activation(e[:, :], lw[:, :], ACT.Exp, bias=mx[:, :], accum_out=total[:, :]).then_inc(s["exp_ready"], 1)
                act.activation(sig[:, :], sig[:, :], ACT.Sqrt).then_inc(s["root"], 1)
                act.wait_ge(s["root"], 1)
                act.activation(sig[:, :], sig[:, :], ACT.Sqrt).then_inc(s["root"], 1)
        s.end()


def autoregress(nc, w, XT, YT, wgt):
    with ExitStack() as ctx:
        mu = ctx.enter_context(nc.sbuf_tensor("ar_mu", [P, 3, NEDGE, P], F32))
        eff = ctx.enter_context(nc.sbuf_tensor("ar_eff", [P, 3, NEDGE, P], F32))
        ps = ctx.enter_context(nc.psum_tensor("ar_ps", [P, 8, 512], F32))
        load_all(nc, "ar_load", [(mu[:, n, :, :], w["M_u"][n]) for n in range(3)])
        s = Signals(nc, "ar", "own ready made kept")
        with nc.Block() as block:
            @block.vector
            def _(dve):
                ch = Chain(dve, s["own"])
                ch.link(dve.tensor_scalar(eff[:, :, 3, :], mu[:, :, 0, :], wgt[:, 0:1], None, ALU.mult))
                for n in (1, 2, 3):
                    ch.link(dve.scalar_tensor_tensor(eff[:, :, 3 - n, :], mu[:, :, n, :], wgt[:, n:n + 1], eff[:, :, 4 - n, :], ALU.mult, ALU.add))
                dve.sem_inc(s["ready"], 1)

            @block.tensor
            def _(pe):
                pe.wait_ge(s["ready"], 1)
                with pe.Fori(0, B) as b:
                    for n in range(2 * NCW):
                        q, c = n % 2, n // 2
                        pe.wait_ge(s["kept"], b * 8 + (n + 1))
                        for lo, hi, seg in pieces(c):
                            for back in range(3):
                                parity, shift = (q - back) % 2, -((q - back) // 2)
                                skip = shift if c == 0 and lo == 0 else 0
                                at = b * HALF + (c * CW + lo - shift + skip)
                                ins = pe.matmul(ps[:, n, lo + skip:hi], eff[:, back, seg, :],
                                                XT[:, parity, bass.ds(at, hi - lo - skip)],
                                                start=back == 0, stop=back == 2, skip_group_check=True)
                        ins.then_inc(s["made"], 1)

            @block.scalar
            def _(act):
                act.sem_inc(s["kept"], 8)
                with act.Fori(0, B) as b:
                    for n in range(2 * NCW):
                        act.wait_ge(s["made"], b * 8 + (n + 1))
                        act.activation(YT[:, n % 2, bass.ds(b * HALF + (n // 2) * CW, CW)], ps[:, n, 0:CW], ACT.Copy).then_inc(s["kept"], 1)
        s.end()


def convolve(nc, w, U, YT, wk):
    UNITS = B * NCW * 2
    with ExitStack() as ctx:
        def sb(name, shape):
            return ctx.enter_context(nc.sbuf_tensor("cv_" + name, shape, F32))
        even, odd = sb("even", [P, 2, HALF]), sb("odd", [P, 2, HALF + 1])
        mp, mm = sb("mp", [P, 2, NEDGE, P]), sb("mm", [P, 2, NEDGE, P])
        total = sb("total", [P, NEDGE, P])
        eff = sb("eff", [P, 2, 2, NEDGE, P])
        uk = sb("uk", [P, 2, 2, CW])
        ps = ctx.enter_context(nc.psum_tensor("cv_ps", [P, 8, 512], F32))
        s = Signals(nc, "cv", "filter0 filter1 matrix0 matrix1 filter_used matrix_used eff_ready own convolved kept mixed added")
        filt, matr = (s["filter0"], s["filter1"]), (s["matrix0"], s["matrix1"])
        rows = P + HALF
        units = [(b, c, q) for b in range(B) for c in reversed(range(NCW)) for q in range(2)]

        with nc.Block() as block:
            @block.sync
            def _(sp):
                with sp.Fori(0, NK // 2) as i:
                    for u in range(2):
                        k = i * 2 + u
                        sp.wait_ge(s["filter_used"], k + 1)
                        sp.dma_start(even[:, u, :], bass.AP(w["phi_even"].tensor, k * rows, [[1, P], [1, HALF]])).then_inc(filt[u], 16)
                        sp.dma_start(odd[:, u, :], bass.AP(w["phi_odd"].tensor, k * rows, [[1, P], [1, HALF + 1]])).then_inc(filt[u], 16)
                        sp.wait_ge(s["matrix_used"], k + 1)
                        sp.dma_start(mp[:, u, :, :].rearrange("d n e -> d (n e)"), w["M_plus"][bass.ds(k, 1)].rearrange("k d n e -> (k d) (n e)")).then_inc(matr[u], 16)
                        sp.dma_start(mm[:, u, :, :].rearrange("d n e -> d (n e)"), w["M_minus"][bass.ds(k, 1)].rearrange("k d n e -> (k d) (n e)")).then_inc(matr[u], 16)

            @block.tensor
            def _(pe):
                pe.sem_inc(s["filter_used"], 2)
                pe.sem_inc(s["mixed"], 2)
                with pe.Fori(0, NK // 2) as i:
                    for u in range(2):
                        k = i * 2 + u
                        pe.wait_ge(filt[u], i * 32 + 32)

                        def conv(n):
                            b, c, q = units[n]
                            pe.wait_ge(s["kept"], k * UNITS + (n + 1))
                            blocks = [g for g in range(GB) if g * P < (c + 1) * CW]
                            for kind in range(2):
                                for g in blocks:
                                    off = max(0, g * P - c * CW)
                                    lag = c * CW + off - g * P
                                    rhs = (even[:, u, ::-1][:, lag:lag + CW - off] if kind == 0
                                           else odd[:, u, ::-1][:, lag + q:lag + q + CW - off])
                                    ins = pe.matmul(ps[:, 2 * (n % 2) + kind, off:CW], U[:, b * GB + g, q if kind == 0 else 1 - q, :],
                                                    rhs, start=g == 0, stop=g == blocks[-1], skip_group_check=True)
                            ins.then_inc(s["convolved"], 1)

                        def mix(n):
                            b, c, q = units[n]
                            if n == 0:
                                pe.wait_ge(s["eff_ready"], k + 1)
                            pe.wait_ge(s["kept"], k * UNITS + (n + 3))
                            pe.wait_ge(s["added"], k * UNITS + (n + 1))
                            for lo, hi, seg in pieces(c):
                                for kind in range(2):
                                    ins = pe.matmul(ps[:, 4 + n % 2, lo:hi], eff[:, u, kind, seg, :], uk[:, n % 2, kind, lo:hi],
                                                    start=kind == 0, stop=kind == 1, skip_group_check=True)
                            ins.then_inc(s["mixed"], 1)
                            return ins

                        for n in range(UNITS):
                            conv(n)
                            if n:
                                mix(n - 1)
                        mix(UNITS - 1)
                        pe.wait_ge(s["mixed"], k * UNITS + (UNITS + 2))
                        pe.sem_inc(s["filter_used"], 1)

            @block.scalar
            def _(act):
                act.sem_inc(s["kept"], 2)
                with act.Fori(0, NK) as k:
                    for n in range(UNITS):
                        act.wait_ge(s["convolved"], k * UNITS + (n + 1))
                        act.wait_ge(s["mixed"], k * UNITS + (n + 1))
                        at = 2 * (n % 2)
                        act.activation(uk[:, n % 2, :, :], ps[:, at:at + 2, 0:CW], ACT.Copy).then_inc(s["kept"], 1)

            @block.vector
            def _(dve):
                dve.sem_inc(s["matrix_used"], 2)
                dve.sem_inc(s["added"], 2)
                ch = Chain(dve, s["own"])
                with dve.Fori(0, NK // 2) as i:
                    ch.enter(i, 16)
                    for u in range(2):
                        k = i * 2 + u
                        dve.wait_ge(matr[u], i * 32 + 32)
                        dve.wait_ge(s["filter_used"], k + 1)
                        dve.tensor_tensor(total[:, :, :], mp[:, u, :, :], mm[:, u, :, :], ALU.add)
                        ch.link(dve.tensor_tensor(mm[:, u, :, :], mp[:, u, :, :], mm[:, u, :, :], ALU.subtract))
                        for kind, m in enumerate((total[:, :, :], mm[:, u, :, :])):
                            ins = dve.tensor_scalar(eff[:, u, kind, 3, :], m[:, 0, :], wk[:, bass.ds(k, 1), 0], None, ALU.mult)
                        ch.link(ins)
                        for n in (1, 2, 3):
                            for kind, m in enumerate((total[:, :, :], mm[:, u, :, :])):
                                ins = dve.scalar_tensor_tensor(eff[:, u, kind, 3 - n, :], m[:, n, :], wk[:, bass.ds(k, 1), n],
                                                               eff[:, u, kind, 4 - n, :], ALU.mult, ALU.add)
                                ch.link(ins)
                        dve.sem_inc(s["eff_ready"], 1)
                        dve.sem_inc(s["matrix_used"], 1)
                        dve.wait_ge(s["added"], k * UNITS + 2)
                        for n in range(UNITS):
                            b, c, q = units[n]
                            dve.wait_ge(s["mixed"], k * UNITS + (n + 3))
                            out = YT[:, q, b * HALF + c * CW:b * HALF + (c + 1) * CW]
                            dve.tensor_tensor(out, out, ps[:, 4 + n % 2, 0:CW], ALU.add).then_inc(s["added"], 1)
                ch.leave(NK // 2)
        s.end()


NF = H // 2 + 1
NR = B * H
NW = 5


def fourier_mixer(nc, X, xn_dram, w):
    with ExitStack() as ctx:
        def sb(name, shape, dt=F32):
            return ctx.enter_context(nc.sbuf_tensor("ff_" + name, shape, dt))

        with nc.sbuf_tensor("ff_xn", [P, G, 2, C], F32) as XN:
            layer_norm(nc, "ff_ln", X, XN, 1e-6)
            load_all(nc, "ff_store", [(xn_dram.rearrange("(g p t) c -> p g t c", p=P, t=2), XN[:, :, :, :])])
        ident = sb("ident", [P, P])
        dft = sb("dft", [W, 3 * NF])
        idft = sb("idft", [2 * NF, W])
        HT = sb("HT", [P, T])
        load_all(nc, "ff_load", [(ident[:, :], w["ident"]), (dft[:, :], w["dft"]), (idft[:, :], w["idft"])])
        with nc.sbuf_tensor("ff_mx", [P, NR, 2 * NF], F32) as mixed:
            for axis in range(2):
                with nc.sbuf_tensor(f"ff_fx{axis}", [P, 3, NF, NR], F32) as spectrum:
                    transform_rows(nc, f"ffa{axis}", axis, xn_dram, dft, spectrum)
                    mix_modes(nc, f"ffb{axis}", w["fw"][axis], spectrum, mixed)
                inverse_rows(nc, f"ffc{axis}", axis, idft, ident, mixed, HT)
        row_mlp(nc, w, HT, X)


def transform_rows(nc, name, axis, xn_dram, dft, spectrum):
    with ExitStack() as ctx:
        rows = ctx.enter_context(nc.sbuf_tensor(name + "_rows", [W, H, C], F32))
        ps = ctx.enter_context(nc.psum_tensor(name + "_ps", [P, 8, 512], F32))
        s = Signals(nc, name, "loaded made kept")
        flat = spectrum[:, :, :, :].rearrange("c m f r -> c (m f) r")
        with nc.Block() as block:
            @block.sync
            def _(sp):
                for b in range(B):
                    if b:
                        sp.wait_ge(s["made"], 8 * b)
                    img = xn_dram[b * S:(b + 1) * S, :]
                    src = img.rearrange("(h w) c -> w h c", w=W) if axis == 0 else img.rearrange("(h w) c -> h w c", w=W)
                    sp.dma_start(rows[:, :, :], src).then_inc(s["loaded"], 16)

            @block.tensor
            def _(pe):
                with pe.Fori(0, B) as b:
                    pe.wait_ge(s["loaded"], b * 16 + 16)
                    for n in range(8):
                        pe.wait_ge(s["kept"], b * 8 + (n + 1))
                        for r in range(6):
                            ins = pe.matmul(ps[:, n, r * 3 * NF:(r + 1) * 3 * NF], rows[:, 6 * n + r, :], dft[:, :], start=True, stop=True)
                        ins.then_inc(s["made"], 1)

            @block.scalar
            def _(act):
                act.sem_inc(s["kept"], 8)
                with act.Fori(0, B) as b:
                    for n in range(8):
                        act.wait_ge(s["made"], b * 8 + (n + 1))
                        act.activation(flat[:, :, bass.ds(b * H + 6 * n, 6)],
                                       ps[:, n, 0:18 * NF].rearrange("c (r m) -> c m r", r=6), ACT.Copy).then_inc(s["kept"], 1)
        s.end()


def mix_modes(nc, name, fw, spectrum, mixed):
    with ExitStack() as ctx:
        wt = ctx.enter_context(nc.sbuf_tensor(name + "_w", [P, NW, 2, C], F32))
        ps = ctx.enter_context(nc.psum_tensor(name + "_ps", [P, NW, 512], F32))
        s = Signals(nc, name, " ".join(f"loaded{u}" for u in range(NW)) + " made kept")
        loaded = s.all[:NW]
        with nc.Block() as block:
            @block.sync
            def _(sp):
                with sp.Fori(0, NF // NW) as i:
                    for u in range(NW):
                        sp.wait_ge(s["made"], i * NW + (u + 1))
                        sp.dma_start(wt[:, u, :, :].rearrange("c m o -> c (m o)"), fw[bass.ds((i * NW + u) * P, P), :]).then_inc(loaded[u], 16)

            @block.tensor
            def _(pe):
                pe.sem_inc(s["made"], NW)
                with pe.Fori(0, NF // NW) as i:
                    for u in range(NW):
                        pe.wait_ge(loaded[u], i * 16 + 16)
                        pe.wait_ge(s["kept"], i * NW + (u + 1))
                        for m in range(2):
                            rhs = spectrum[:, 1 - m:3 - m, bass.ds(i * NW + u, 1), :].rearrange("c m f r -> c m (f r)")
                            ins = pe.matmul(ps[:, u, 0:2 * NR].rearrange("c (m r) -> c m r", m=2), wt[:, u, m, :], rhs, start=m == 0, stop=m == 1)
                        ins.then_inc(s["made"], 1)

            @block.vector
            def _(dve):
                dve.sem_inc(s["kept"], NW)
                with dve.Fori(0, NF // NW) as i:
                    for u in range(NW):
                        dve.wait_ge(s["made"], i * NW + (NW + u + 1))
                        out = mixed[:, :, :].rearrange("c r (m f) -> c m f r", m=2)[:, :, bass.ds(i * NW + u, 1), :].rearrange("c m f r -> c m (f r)")
                        dve.tensor_copy(out, ps[:, u, 0:2 * NR].rearrange("c (m r) -> c m r", m=2)).then_inc(s["kept"], 1)
        s.end()


def inverse_rows(nc, name, axis, idft, ident, mixed, HT):
    with ExitStack() as ctx:
        stage = ctx.enter_context(nc.sbuf_tensor(name + "_stage", [P, H, P], F32))
        modes = ctx.enter_context(nc.sbuf_tensor(name + "_modes", [2 * NF, H, C], F32))
        ps = ctx.enter_context(nc.psum_tensor(name + "_ps", [P, 8, 512], F32))
        s = Signals(nc, name, "padded staged turned kept made added")
        with nc.Block() as block:
            @block.gpsimd
            def _(pool):
                pool.memset(stage[:, :, 2 * NF:], 0.0).then_inc(s["padded"], 1)

            @block.scalar
            def _(act):
                act.sem_inc(s["kept"], 2)
                with act.Fori(0, B) as b:
                    act.wait_ge(s["turned"], b * 12 + 1)
                    act.activation(stage[:, :, 0:2 * NF], mixed[:, bass.ds(b * H, H), :], ACT.Copy).then_inc(s["staged"], 1)
                    act.wait_ge(s["made"], b * 6 + 1)
                    for n in range(12):
                        act.wait_ge(s["turned"], b * 12 + (n + 2))
                        act.activation(modes[:, 4 * n:4 * n + 4, :], ps[0:2 * NF, n % 2, :].rearrange("m (r c) -> m r c", c=C), ACT.Copy).then_inc(s["kept"], 1)

            @block.tensor
            def _(pe):
                pe.sem_inc(s["turned"], 1)
                pe.sem_inc(s["made"], 1)
                pe.wait_ge(s["padded"], 1)
                with pe.Fori(0, B) as b:
                    pe.wait_ge(s["staged"], b + 1)
                    for n in range(13):
                        if n < 12:
                            pe.wait_ge(s["kept"], b * 12 + (n + 1))
                            for r in range(4):
                                ins = pe.transpose(ps[:, n % 2, r * P:(r + 1) * P], stage[:, 4 * n + r, :], ident[:, :])
                            ins.then_inc(s["turned"], 1)
                        if n >= 2 and n % 2 == 0:
                            j = n // 2 - 1
                            pe.wait_ge(s["kept"], b * 12 + (2 * j + 4))
                            pe.wait_ge(s["added"], b * 6 + (j + 1))
                            for r in range(8):
                                ins = pe.matmul(ps[:, 2 + j, r * W:(r + 1) * W], modes[:, 8 * j + r, :], idft[:, :], start=True, stop=True)
                            ins.then_inc(s["made"], 1)

            @block.vector
            def _(dve):
                dve.sem_inc(s["added"], 6)
                with dve.Fori(0, B) as b:
                    for j in range(6):
                        dve.wait_ge(s["made"], b * 6 + (j + 2))
                        if axis == 0:
                            dve.tensor_copy(HT[:, bass.ds(b * S + j * 384, 384)], ps[:, 2 + j, 0:384]).then_inc(s["added"], 1)
                        else:
                            out = HT[:, bass.ds(b * S, S)].rearrange("c (h w) -> c w h", w=W)[:, 8 * j:8 * j + 8, :]
                            dve.tensor_tensor(out, out, ps[:, 2 + j, 0:384].rearrange("c (w h) -> c w h", h=H), ALU.add).then_inc(s["added"], 1)
        s.end()


def row_mlp(nc, w, HT, X):
    with ExitStack() as ctx:
        def sb(name, shape):
            return ctx.enter_context(nc.sbuf_tensor("mlp_" + name, shape, F32))
        w1, w2, b1, b2, ones = sb("w1", [P, 512]), sb("w2", [P, 4, C]), sb("b1", [P, 4]), sb("b2", [1, C]), sb("ones", [1, P])
        hid = sb("hid", [P, 2, 4, 256])
        ps = ctx.enter_context(nc.psum_tensor("mlp_ps", [P, 8, 512], F32))
        load_all(nc, "mlp_load", [(w1[:, :], w["w1"]), (w2[:, :, :], w["w2"]), (b1[:, :], w["b1"]), (b2[:, :], w["b2"])])
        s = Signals(nc, "mlp", "ones_ready made hid_ready done added")
        with nc.Block() as block:
            @block.tensor
            def _(pe):
                pe.sem_inc(s["done"], 2)
                pe.wait_ge(s["ones_ready"], 1)
                with pe.Fori(0, G // 2) as i:
                    for u in range(2):
                        pe.wait_ge(s["hid_ready"], i * 2 + (u + 1))
                        for n in range(4):
                            ins = pe.matmul(ps[:, 2 * u + n // 2, (n % 2) * 256:(n % 2) * 256 + 256], w1[:, n * P:(n + 1) * P],
                                            HT[:, bass.ds((i * 2 + u) * 256, 256)], start=True, stop=True)
                        ins.then_inc(s["made"], 1)
                    for u in range(2):
                        pe.wait_ge(s["hid_ready"], i * 2 + (u + 3))
                        pe.wait_ge(s["added"], i * 2 + (u + 1))
                        for t in range(2):
                            for n in range(4):
                                pe.matmul(ps[:, 4 + u, t * C:(t + 1) * C], hid[:, u, n, t::2], w2[:, n, :], start=n == 0, stop=False)
                            ins = pe.matmul(ps[:, 4 + u, t * C:(t + 1) * C], ones[:, :], b2[:, :], start=False, stop=True)
                        ins.then_inc(s["done"], 1)

            @block.scalar
            def _(act):
                act.sem_inc(s["hid_ready"], 2)
                with act.Fori(0, G // 2) as i:
                    for u in range(2):
                        act.wait_ge(s["made"], i * 2 + (u + 1))
                        act.wait_ge(s["done"], i * 2 + (u + 1))
                        for n in range(4):
                            ins = act.activation(hid[:, u, n, :], ps[:, 2 * u + n // 2, (n % 2) * 256:(n % 2) * 256 + 256], ACT.Relu, bias=b1[:, n:n + 1])
                        ins.then_inc(s["hid_ready"], 1)

            @block.vector
            def _(dve):
                dve.memset(ones[:, :], 1.0).then_inc(s["ones_ready"], 1)
                dve.sem_inc(s["added"], 2)
                with dve.Fori(0, G // 2) as i:
                    for u in range(2):
                        dve.wait_ge(s["done"], i * 2 + (u + 3))
                        out = X[:, bass.ds(i * 2 + u, 1), :, :].rearrange("p g t c -> p (g t c)")
                        dve.tensor_tensor(out, out, ps[:, 4 + u, 0:256], ALU.add).then_inc(s["added"], 1)
        s.end()


NE = 64
GE = 4
LOWEST = -3.0e38


def expert_choice(nc, name, X, w):
    with ExitStack() as ctx:
        def sb(n, shape, dt=F32):
            return ctx.enter_context(nc.sbuf_tensor(f"{name}_{n}", shape, dt))

        ident = sb("ident", [P, P])
        weights = sb("weights", [NE, T])
        pooled = sb("pooled", [P, NE, B])
        outs = sb("outs", [P, B, P])
        load_all(nc, name + "_load", [(ident[:, :], w["ident"])])
        with nc.sbuf_tensor(name + "_xn", [P, G, 2, C], F32) as XN:
            layer_norm(nc, name + "_ln", X, XN, 1e-5)
            with nc.sbuf_tensor(name + "_xt", [P, T], F32) as XT:
                transpose_tokens(nc, name + "_tr", XN, lambda g: XT[:, bass.ds(g * 256, 256)].rearrange("c (p t) -> c t p", t=2), ident)
                expert_weights(nc, name + "w", w, XT, weights)
            pool_tokens(nc, name + "p", XN, weights, ident, pooled)
        expert_layers(nc, name + "e", w, pooled, outs)
        scatter_tokens(nc, name + "s", w, weights, ident, outs, X)


def expert_weights(nc, name, w, XT, weights):
    with ExitStack() as ctx:
        def sb(n, shape):
            return ctx.enter_context(nc.sbuf_tensor(f"{name}_{n}", shape, F32))
        gate, gate_b = sb("gate", [P, NE]), sb("gate_b", [NE, 1])
        top, neg, total, probs, kept = sb("top", [NE, B, 8]), sb("neg", [NE, B]), sb("total", [NE, B]), sb("probs", [NE, B, S]), sb("kept", [NE, S])
        ps = ctx.enter_context(nc.psum_tensor(name + "_ps", [NE, 8, 512], F32))
        load_all(nc, name + "_load", [(gate[:, :], w["gate"]), (gate_b[:, :], w["gate_b"])])
        s = Signals(nc, name, "made stored own max_ready exp_ready")
        R = R_ORDER
        with nc.Block() as block:
            @block.tensor
            def _(pe):
                with pe.Fori(0, B * NCH // 8) as i:
                    for u in range(8):
                        pe.wait_ge(s["stored"], i * 8 + (u + 1))
                        pe.matmul(ps[:, u, 0:R], gate[:, :], XT[:, bass.ds((i * 8 + u) * R, R)], start=True, stop=True).then_inc(s["made"], 1)

            @block.scalar
            def _(act):
                act.sem_inc(s["stored"], 8)
                with act.Fori(0, B * NCH // 8) as i:
                    for u in range(8):
                        act.wait_ge(s["made"], i * 8 + (u + 1))
                        act.activation(weights[:, bass.ds((i * 8 + u) * R, R)], ps[:, u, 0:R], ACT.Identity, bias=gate_b[:, :]).then_inc(s["stored"], 1)
                for b in range(B):
                    act.wait_ge(s["max_ready"], b + 1)
                    act.activation(probs[:, b, :], weights[:, b * S:(b + 1) * S], ACT.Exp, bias=neg[:, b:b + 1],
                                   accum_out=total[:, b:b + 1]).then_inc(s["exp_ready"], 1)

            @block.vector
            def _(dve):
                ch = Chain(dve, s["own"])
                dve.wait_ge(s["stored"], 8 + B * NCH)
                for b in range(B):
                    logit = weights[:, b * S:(b + 1) * S]
                    ch.link(dve.max(top[:, b, :], logit))
                    dve.tensor_scalar(neg[:, b:b + 1], top[:, b, 0:1], -1.0, None, ALU.mult).then_inc(s["max_ready"], 1)
                for b in range(B):
                    logit = weights[:, b * S:(b + 1) * S]
                    ch.link(dve.match_replace(kept[:, :], top[:, b, :], logit, LOWEST))
                    ch.link(dve.tensor_tensor(kept[:, :], kept[:, :], logit, ALU.not_equal))
                    dve.wait_ge(s["exp_ready"], b + 1)
                    ch.link(dve.reciprocal(total[:, b:b + 1], total[:, b:b + 1]))
                    ch.link(dve.scalar_tensor_tensor(logit, probs[:, b, :], total[:, b:b + 1], kept[:, :], ALU.mult, ALU.mult))
        s.end()


def tile_of(stage, n):
    return stage[:, (n // 2) * 256 + n % 2:(n // 2 + 1) * 256:2]


def pool_tokens(nc, name, XN, weights, ident, pooled):
    with ExitStack() as ctx:
        def sb(n, shape):
            return ctx.enter_context(nc.sbuf_tensor(f"{name}_{n}", shape, F32))
        stage, wt, sums = sb("stage", [P, S]), sb("wt", [P, 20, P]), sb("sums", [P, C])
        ps = ctx.enter_context(nc.psum_tensor(name + "_ps", [P, 8, 512], F32))
        s = Signals(nc, name, "padded staged turned kept summed sums_ready sums_turned pooled")
        with nc.Block() as block:
            @block.gpsimd
            def _(pool):
                pool.memset(stage[NE:, :], 0.0).then_inc(s["padded"], 1)

            @block.scalar
            def _(act):
                with act.Fori(0, B) as b:
                    act.wait_ge(s["turned"], b * 5 + 1)
                    act.activation(stage[0:NE, :], weights[:, bass.ds(b * S, S)], ACT.Copy).then_inc(s["staged"], 1)
                    for n in range(5):
                        act.wait_ge(s["turned"], b * 5 + (n + 2))
                        m = 4 if n < 4 else 2
                        act.activation(wt[:, 4 * n:4 * n + m, :], ps[:, n, 0:m * P].rearrange("s (m e) -> s m e", e=P), ACT.Copy).then_inc(s["kept"], 1)

            @block.tensor
            def _(pe):
                pe.sem_inc(s["turned"], 1)
                pe.wait_ge(s["padded"], 1)
                with pe.Fori(0, B) as b:
                    pe.wait_ge(s["staged"], b + 1)
                    for n in range(18):
                        if n % 4 == 0:
                            pe.wait_ge(s["kept"], b * 5 + (n // 4 + 1))
                        ins = pe.transpose(ps[:, n // 4, (n % 4) * P:(n % 4 + 1) * P], tile_of(stage, n), ident[:, :])
                        if n % 4 == 3 or n == 17:
                            ins.then_inc(s["turned"], 1)
                    pe.wait_ge(s["kept"], b * 5 + 10)
                    pe.wait_ge(s["sums_ready"], b + 1)
                    for n in range(18):
                        ins = pe.matmul(ps[:, 5, 0:C], wt[:, n, :], XN[:, bass.ds(b * GB + n // 2, 1), n % 2, :].rearrange("p g c -> p (g c)"), start=n == 0, stop=n == 17)
                    ins.then_inc(s["summed"], 1)
                    pe.wait_ge(s["sums_ready"], b + 2)
                    pe.wait_ge(s["pooled"], b + 1)
                    pe.transpose(ps[:, 6, 0:P], sums[:, :], ident[:, :]).then_inc(s["sums_turned"], 1)

            @block.vector
            def _(dve):
                dve.sem_inc(s["kept"], 5)
                dve.sem_inc(s["sums_ready"], 1)
                dve.sem_inc(s["pooled"], 1)
                with dve.Fori(0, B) as b:
                    dve.wait_ge(s["summed"], b + 1)
                    dve.tensor_copy(sums[:, :], ps[:, 5, 0:C]).then_inc(s["sums_ready"], 1)
                    dve.wait_ge(s["sums_turned"], b + 1)
                    dve.tensor_copy(pooled[:, :, bass.ds(b, 1)].rearrange("d e b -> d (e b)"), ps[:, 6, 0:NE]).then_inc(s["pooled"], 1)
        s.end()


def expert_layers(nc, name, w, pooled, outs):
    with ExitStack() as ctx:
        def sb(n, shape):
            return ctx.enter_context(nc.sbuf_tensor(f"{name}_{n}", shape, F32))
        w1, w2 = sb("w1", [P, 2, GE, 512]), sb("w2", [P, 2, GE, 512])
        b1, pre, hid = sb("b1", [P, NE * 4]), sb("pre", [P, 2, GE * 4, B]), sb("hid", [P, 2, GE * 4, B])
        ps = ctx.enter_context(nc.psum_tensor(name + "_ps", [P, 4, 512], F32))
        load_all(nc, name + "_load", [(b1[:, :], w["b1"])])
        s = Signals(nc, name, "loaded0 loaded1 made biased hid_ready done stored cleared")
        loaded = (s["loaded0"], s["loaded1"])
        NG = NE // GE
        with nc.Block() as block:
            @block.sync
            def _(sp):
                with sp.Fori(0, NG // 2) as i:
                    for u in range(2):
                        sp.wait_ge(s["done"], i * 2 + (u + 1))
                        for n in range(GE):
                            e = i * (2 * GE) + (u * GE + n)
                            sp.dma_start(w1[:, u, n, :], w["w1"][bass.ds(e * 129, P), :]).then_inc(loaded[u], 16)
                            sp.dma_start(w2[:, u, n, :], w["w2"][bass.ds(e * 513, 512), :].rearrange("(p r) o -> p (r o)", r=4)).then_inc(loaded[u], 16)

            @block.tensor
            def _(pe):
                pe.sem_inc(s["done"], 2)
                with pe.Fori(0, NG // 2) as i:
                    for u in range(2):
                        pe.wait_ge(loaded[u], i * (32 * GE) + 32 * GE)
                        pe.wait_ge(s["biased"], i * 2 + (u + 1))
                        for n in range(GE):
                            for r in range(4):
                                ins = pe.matmul(ps[:, u, (n * 4 + r) * B:(n * 4 + r + 1) * B], w1[:, u, n, r::4],
                                                pooled[:, bass.ds(i * (2 * GE) + (u * GE + n), 1), :].rearrange("d e b -> d (e b)"), start=True, stop=True)
                        ins.then_inc(s["made"], 1)
                        pe.wait_ge(s["hid_ready"], i * 2 + (u + 1))
                        pe.wait_ge(s["stored"], i * 2 + (u + 1))
                        for n in range(GE):
                            for r in range(4):
                                ins = pe.matmul(ps[:, 2 + u, n * B:(n + 1) * B], w2[:, u, n, r * C:(r + 1) * C], hid[:, u, n * 4 + r, :], start=r == 0, stop=r == 3)
                        ins.then_inc(s["done"], 1)

            @block.vector
            def _(dve):
                dve.sem_inc(s["biased"], 2)
                dve.sem_inc(s["stored"], 2)
                dve.memset(outs[:, :, :], 0.0).then_inc(s["cleared"], 1)
                dve.wait_ge(s["cleared"], 1)
                with dve.Fori(0, NG // 2) as i:
                    for u in range(2):
                        dve.wait_ge(s["made"], i * 2 + (u + 1))
                        dve.wait_ge(s["done"], i * 2 + (u + 1))
                        bias = b1[:, bass.ds((i * 2 + u) * (GE * 4), GE * 4)]
                        dve.tensor_tensor(pre[:, u, :, :], ps[:, u, 0:GE * 4 * B].rearrange("p (n b) -> p n b", b=B),
                                          bc(bias[:, :, None], [P, GE * 4, B]), ALU.add).then_inc(s["biased"], 1)
                        dve.wait_ge(s["done"], i * 2 + (u + 3))
                        dve.tensor_copy(outs[:, :, bass.ds((i * 2 + u) * GE, GE)],
                                        ps[:, 2 + u, 0:GE * B].rearrange("o (n b) -> o b n", b=B)).then_inc(s["stored"], 1)

            @block.scalar
            def _(act):
                with act.Fori(0, NG // 2) as i:
                    for u in range(2):
                        act.wait_ge(s["biased"], i * 2 + (u + 3))
                        act.activation(hid[:, u, :, :], pre[:, u, :, :], ACT.Gelu).then_inc(s["hid_ready"], 1)
        s.end()


def scatter_tokens(nc, name, w, weights, ident, outs, X):
    with ExitStack() as ctx:
        def sb(n, shape):
            return ctx.enter_context(nc.sbuf_tensor(f"{name}_{n}", shape, F32))
        stage, rows, b2 = sb("stage", [P, S]), sb("rows", [P, B, C]), sb("b2", [NE, C])
        ps = ctx.enter_context(nc.psum_tensor(name + "_ps", [P, 8, 512], F32))
        load_all(nc, name + "_load", [(b2[:, :], w["b2"])])
        s = Signals(nc, name, "padded turned rows_ready staged made added")
        with nc.Block() as block:
            @block.gpsimd
            def _(pool):
                pool.memset(stage[NE:, :], 0.0).then_inc(s["padded"], 1)
                pool.memset(rows[NE:, :, :], 0.0).then_inc(s["padded"], 1)

            @block.scalar
            def _(act):
                with act.Fori(0, B) as b:
                    act.wait_ge(s["made"], b * 5 + 1)
                    act.activation(stage[0:NE, :], weights[:, bass.ds(b * S, S)], ACT.Copy).then_inc(s["staged"], 1)

            @block.tensor
            def _(pe):
                pe.sem_inc(s["made"], 1)
                for b in range(B):
                    ins = pe.transpose(ps[:, 7, b * P:(b + 1) * P], outs[:, b, :], ident[:, :])
                ins.then_inc(s["turned"], 1)
                pe.wait_ge(s["padded"], 2)
                pe.wait_ge(s["rows_ready"], 1)
                with pe.Fori(0, B) as b:
                    pe.wait_ge(s["staged"], b + 1)
                    for n in range(18):
                        if n % 4 == 0:
                            pe.wait_ge(s["added"], b * 5 + (n // 4 + 1))
                        ins = pe.matmul(ps[:, n // 4, (n % 4) * C:(n % 4 + 1) * C], tile_of(stage, n),
                                        rows[:, bass.ds(b, 1), :].rearrange("e b c -> e (b c)"), start=True, stop=True)
                        if n % 4 == 3 or n == 17:
                            ins.then_inc(s["made"], 1)

            @block.vector
            def _(dve):
                dve.sem_inc(s["added"], 5)
                dve.wait_ge(s["turned"], 1)
                for b in range(B):
                    ins = dve.tensor_tensor(rows[0:NE, b, :], ps[0:NE, 7, b * P:(b + 1) * P], b2[:, :], ALU.add)
                ins.then_inc(s["rows_ready"], 1)
                with dve.Fori(0, B) as b:
                    for n in range(5):
                        dve.wait_ge(s["made"], b * 5 + (n + 2))
                        m = 2 if n < 4 else 1
                        out = X[:, bass.ds(b * GB + 2 * n, m), :, :].rearrange("p g t c -> p (g t c)")
                        dve.tensor_tensor(out, out, ps[:, n, 0:m * 256], ALU.add).then_inc(s["added"], 1)
        s.end()


NH = 4
DH = 32
NT_ = S // P
NJP = NT_ // 2


def attention(nc, X, xt_dram, max_dram, w):
    with ExitStack() as ctx:
        def sb(n, shape, dt=F32):
            return ctx.enter_context(nc.sbuf_tensor("at_" + n, shape, dt))

        ident = sb("ident", [P, P])
        load_all(nc, "at_ident", [(ident[:, :], w["ident"])])
        with nc.sbuf_tensor("at_xn", [P, G, 2, C], F32) as XN, nc.sbuf_tensor("at_xt", [P, T], F32) as XT:
            layer_norm(nc, "at_ln", X, XN, 1e-6)
            transpose_tokens(nc, "at_tr", XN, lambda g: XT[:, bass.ds(g * 256, 256)].rearrange("c (t p) -> c t p", t=2), ident)
            load_all(nc, "at_store", [(xt_dram, XT[:, :])])
        wqkv, wout, bout = sb("wqkv", [P, 3 * P]), sb("wout", [P, C]), sb("bout", [1, C])
        ones, pick = sb("ones", [1, P]), sb("pick", [P, P])
        xb, qk = sb("xb", [P, S]), sb("qk", [P, 2, S])
        heads = sb("heads", [P, 2, NH, S])
        low = sb("low", [P, 2, S], BF16)
        kept = sb("kept", [P, R_ORDER])
        v = sb("v", [P, NT_, NH, DH + 1])
        ssq, scale = sb("ssq", [P, 2]), sb("scale", [P, 2])
        top, topT = sb("top", [P, NH * NT_, 2]), sb("topT", [P, P])
        neg = sb("neg", [P, P])
        OT = sb("OT", [P, S])
        load_all(nc, "at_load", [(wqkv[:, :], w["wqkv"]), (wout[:, :], w["wout"]), (bout[:, :], w["bout"])])
        R = R_ORDER

        ps = ctx.enter_context(nc.psum_tensor("at_ps", [P, 8, 512], F32))
        c0 = Signals(nc, "at0", "own cleared")
        with nc.Block() as block:
            @block.vector
            def _(dve):
                ch = Chain(dve, c0["own"])
                dve.memset(heads[:, 0, :, :], 0.0)
                dve.memset(v[:, :, :, :], 1.0)
                dve.memset(ones[:, :], 1.0)
                ch.link(dve.memset(neg[:, :], 0.0))
                dve.memset(low[:, :, :], 0.0)
                dve.memset(kept[:, :], 0.0)
                ch.link(dve.memset(pick[:, :], 0.0))
                dve.memset(pick[DH:DH + 1, :], 1.0)

            @block.gpsimd
            def _(pool):
                pool.memset(heads[:, 1, :, :], 0.0).then_inc(c0["cleared"], 1)
                pool.wait_ge(c0["cleared"], 1)
                pool.memset(heads[DH:DH + 1, 1, :, :], 1.0)
        c0.end()

        s1 = Signals(nc, "at1", "loaded made kept own squared rooted scaled")
        s2 = Signals(nc, "at2", "lowered lowered2 made reduced negated turned copied stored placed own")
        s3 = Signals(nc, "at3", "scored weighed used accumulated kept spread own placed")
        s4 = Signals(nc, "at4", "made")
        held = dict(ps=ps, heads=heads, low=low, top=top, neg=neg, topT=topT, ident=ident, max_dram=max_dram, v=v, pick=pick, OT=OT, kept=kept)

        with nc.Fori(0, B) as b:
            with nc.Block() as block:
                @block.sync
                def _(sp):
                    sp.dma_start(xb[:, :], xt_dram[:, bass.ds(b * S, S)]).then_inc(s1["loaded"], 16)

                @block.tensor
                def _(pe):
                    pe.wait_ge(s1["loaded"], 16)
                    for n in range(12):
                        m, c = n // NCH, n % NCH
                        if n >= 4:
                            pe.wait_ge(s1["kept"], n - 3)
                        pe.matmul(ps_bank(ps, n % 4)[:, 0:R], wqkv[:, m * P:(m + 1) * P], xb[:, c * R:(c + 1) * R], start=True, stop=True).then_inc(s1["made"], 1)
                    for n in range(NT_):
                        if n < 4:
                            pe.wait_ge(s1["kept"], 9 + n)
                        else:
                            pe.wait_ge(s1["own"], n - 3)
                        pe.matmul(ps_bank(ps, n % 4)[:, 0:P], xb[:, n * P:(n + 1) * P], wqkv[:, 2 * P:3 * P], start=True, stop=True).then_inc(s1["made"], 1)

                @block.scalar
                def _(act):
                    for n in range(12):
                        act.wait_ge(s1["made"], n + 1)
                        act.activation(qk[:, n // NCH, (n % NCH) * R:(n % NCH + 1) * R], ps_bank(ps, n % 4)[:, 0:R], ACT.Copy).then_inc(s1["kept"], 1)
                    act.wait_ge(s1["kept"], 12)
                    for m in range(2):
                        act.activation(OT[:, :], qk[:, m, :], ACT.Square, accum_out=ssq[:, m:m + 1]).then_inc(s1["squared"], 1)
                        act.wait_ge(s1["squared"], m + 1)
                    act.activation(scale[:, :], ssq[:, :], ACT.Sqrt).then_inc(s1["rooted"], 1)
                    act.wait_ge(s1["scaled"], 2)
                    for h in range(NH):
                        act.activation(heads[0:DH, 1, h, :], qk[h * DH:(h + 1) * DH, 1, :], ACT.Copy)

                @block.vector
                def _(dve):
                    for n in range(NT_):
                        dve.wait_ge(s1["made"], 13 + n)
                        dve.tensor_copy(v[:, n, :, 0:DH], ps_bank(ps, n % 4)[:, 0:P].rearrange("p (h d) -> p h d", h=NH)).then_inc(s1["own"], 1)
                    ch = Chain(dve, s1["own"])
                    ch.n = NT_
                    dve.wait_ge(s1["rooted"], 1)
                    ch.link(dve.tensor_scalar(scale[:, :], scale[:, :], 1e-12, None, ALU.max))
                    ch.link(dve.reciprocal(scale[:, :], scale[:, :]))
                    for m in range(2):
                        dve.tensor_scalar(qk[:, m, :], qk[:, m, :], scale[:, m:m + 1], 10.0 if m == 0 else 1.0, ALU.mult, ALU.mult).then_inc(s1["scaled"], 1)
                    dve.wait_ge(s1["scaled"], 2)
                    for h in range(NH):
                        dve.tensor_copy(heads[0:DH, 0, h, :], qk[h * DH:(h + 1) * DH, 0, :])
            s1.clear()
            row_maxima(nc, s2, held)
            s2.clear()
            attend(nc, s3, held)
            s3.clear()
            with nc.Block() as block:
                @block.tensor
                def _(pe):
                    for n in range(NT_):
                        out = ps_bank(ps, n // 4)[:, (n % 4) * C:(n % 4 + 1) * C]
                        pe.matmul(out, OT[:, n * P:(n + 1) * P], wout[:, :], start=True, stop=False)
                        ins = pe.matmul(out, ones[:, :], bout[:, :], start=False, stop=True)
                        if n % 4 == 3 or n == NT_ - 1:
                            ins.then_inc(s4["made"], 1)

                @block.vector
                def _(dve):
                    for n in range(5):
                        dve.wait_ge(s4["made"], n + 1)
                        m = 2 if n < 4 else 1
                        out = X[:, bass.ds(b * GB + 2 * n, m), :, :].rearrange("p g t c -> p (g t c)")
                        dve.tensor_tensor(out, out, ps_bank(ps, n)[:, 0:m * 256], ALU.add)
            s4.clear()
        for s in (s1, s2, s3, s4):
            s.release()


def ps_bank(ps, n):
    return ps[:, n, :]


def row_maxima(nc, s, vv):
    ps, heads, low, top, neg, topT, ident, max_dram = (vv[n] for n in "ps heads low top neg topT ident max_dram".split())
    R = R_ORDER
    NHALF = 2
    with nc.Block() as block:
        @block.scalar
        def _(act):
            for h in range(NH):
                if h:
                    act.wait_ge(s["made"], h * NT_ * NHALF)
                act.activation(low[0:DH, 0, :], heads[0:DH, 0, h, :], ACT.Copy)
                act.activation(low[0:DH, 1, :], heads[0:DH, 1, h, :], ACT.Copy).then_inc(s["lowered"], 1)

        @block.tensor
        def _(pe):
            for h in range(NH):
                pe.wait_ge(s["lowered"], h + 1)
                with pe.Fori(0, NT_) as n:
                    for u in range(NHALF):
                        pe.wait_ge(s["reduced"], n * 2 + (h * 2 * NT_ + u + 1))
                        for c in range(SC):
                            at = u * L2 + c * R
                            ins = pe.matmul(ps_bank(ps, 3 * u + c)[:, 0:R], low[:, 0, bass.ds(n * P, P)], low[:, 1, at:at + R], start=True, stop=True)
                        ins.then_inc(s["made"], 1)
            pe.wait_ge(s["negated"], 1)
            pe.transpose(ps_bank(ps, 6)[:, 0:P], neg[:, :], ident[:, :]).then_inc(s["turned"], 1)

        @block.vector
        def _(dve):
            dve.sem_inc(s["reduced"], 2)
            for h in range(NH):
                with dve.Fori(0, NT_) as n:
                    for u in range(NHALF):
                        dve.wait_ge(s["made"], n * 2 + (h * 2 * NT_ + u + 1))
                        dve.tensor_reduce(top[:, bass.ds(n + h * NT_, 1), u], ps[:, 3 * u:3 * u + 3, 0:R], AX.XY, ALU.max).then_inc(s["reduced"], 1)
            dve.wait_ge(s["reduced"], 2 * NH * NT_ + 2)
            dve.tensor_reduce(neg[:, 0:NH * NT_], top[:, :, :], AX.X, ALU.max, negate=True).then_inc(s["negated"], 1)
            dve.wait_ge(s["turned"], 1)
            dve.tensor_copy(topT[:, :], ps_bank(ps, 6)[:, 0:P]).then_inc(s["copied"], 1)

        @block.sync
        def _(sp):
            sp.wait_ge(s["copied"], 1)
            sp.dma_start(max_dram, topT[0:NH * NT_, :]).then_inc(s["stored"], 16)
            sp.wait_ge(s["stored"], 16)
            sp.dma_start(heads[DH:DH + 1, 0, :, :].rearrange("a h s -> a (h s)"), max_dram.rearrange("(a m) p -> a (m p)", a=1)).then_inc(s["placed"], 16)
            sp.wait_ge(s["placed"], 16)


def attend(nc, s, vv):
    ps, heads, v, pick, OT, kept = (vv[n] for n in "ps heads v pick OT kept".split())
    R = R_ORDER
    NB = 3
    acc, tot = ps_bank(ps, 6)[0:DH + 1, 0:R], ps_bank(ps, 7)[0:DH, 0:R]
    with ExitStack() as ctx:
        probs = ctx.enter_context(nc.sbuf_tensor("at_probs", [P, NB, 2, R], F32))
        inv = ctx.enter_context(nc.sbuf_tensor("at_inv", [DH, R], F32))
        block = ctx.enter_context(nc.Block())

        @block.tensor
        def _(pe):
            pe.sem_inc(s["used"], NB)
            for h in range(NH):
                with pe.Fori(0, NCH) as c:
                    base = c * NJP + h * NCH * NJP

                    def score(j):
                        pe.wait_ge(s["weighed"], base + (j + 1))
                        for t in range(2):
                            ins = pe.matmul(ps_bank(ps, 2 * (j % NB) + t)[:, 0:R], heads[:, 1, h, (2 * j + t) * P:(2 * j + t + 1) * P],
                                            heads[:, 0, h, bass.ds(c * R, R)], start=True, stop=True)
                        ins.then_inc(s["scored"], 1)

                    def apply(j):
                        pe.wait_ge(s["weighed"], base + (j + 1 + NB))
                        for t in range(2):
                            ins = pe.matmul(acc, v[:, 2 * j + t, h, :], probs[:, j % NB, t, :], start=j == 0 and t == 0, stop=j == NJP - 1 and t == 1)
                        ins.then_inc(s["used"], 1)

                    score(0)
                    score(1)
                    pe.wait_ge(s["kept"], c + (h * NCH + 1))
                    for j in range(NJP):
                        apply(j)
                        if j + 2 < NJP:
                            score(j + 2)
                    pe.wait_ge(s["kept"], c + (h * NCH + 2))
                    pe.wait_ge(s["placed"], c + (h * NCH + 1))
                    pe.matmul(ps_bank(ps, 7)[:, 0:R], pick[:, :], kept[:, :], start=True, stop=True).then_inc(s["spread"], 1)

        @block.scalar
        def _(act):
            act.sem_inc(s["weighed"], NB)
            for h in range(NH):
                with act.Fori(0, NCH) as c:
                    base = c * NJP + h * NCH * NJP
                    for j in range(NJP):
                        act.wait_ge(s["scored"], base + (j + 1))
                        act.wait_ge(s["used"], base + (j + 1))
                        at = 2 * (j % NB)
                        act.activation(probs[:, j % NB, :, :], ps[:, at:at + 2, 0:R], ACT.Exp).then_inc(s["weighed"], 1)

        @block.vector
        def _(dve):
            dve.sem_inc(s["kept"], 1)
            dve.sem_inc(s["placed"], 1)
            ch = Chain(dve, s["own"])
            for h in range(NH):
                with dve.Fori(0, NCH) as c:
                    ch.enter(c, 1)
                    dve.wait_ge(s["used"], c * NJP + (h * NCH * NJP + NJP + NB))
                    dve.wait_ge(s["placed"], c + (h * NCH + 1))
                    dve.tensor_copy(kept[0:DH + 1, :], acc).then_inc(s["kept"], 1)
                    dve.wait_ge(s["spread"], c + (h * NCH + 1))
                    ch.link(dve.reciprocal(inv[:, :], tot))
                    dve.tensor_tensor(OT[h * DH:(h + 1) * DH, bass.ds(c * R, R)], kept[0:DH, :], inv[:, :], ALU.mult).then_inc(s["placed"], 1)
                ch.leave(NCH)


def global_norm(nc, name, V, alpha, beta, scale, shift):
    with ExitStack() as ctx:
        def sb(n, shape):
            return ctx.enter_context(nc.sbuf_tensor(f"{name}_{n}", shape, F32))
        a, bt, sums, sq, total = sb("a", [P, 1]), sb("bt", [P, 1]), sb("sums", [P, 1]), sb("sq", [P, 4]), sb("total", [P, 1])
        mean, var, over, junk, eps = sb("mean", [P, 1]), sb("var", [P, 1]), sb("over", [P, P]), sb("junk", [P, T // 4]), sb("eps", [P, 1])
        neg = sb("neg", [P, 1])
        ps = ctx.enter_context(nc.psum_tensor(name + "_ps", [P, 2, 512], F32))
        load_all(nc, name + "_load", [(a[:, :], spread(alpha, 1)), (bt[:, :], spread(beta, 1))])
        s = Signals(nc, name, "own summed mean_ready squared total_ready var_ready rooted")
        flat = V[:, :, :, :].rearrange("p g t c -> p (g t c)")
        with nc.Block() as block:
            @block.vector
            def _(dve):
                ch = Chain(dve, s["own"])
                dve.memset(over[:, :], 1.0 / (T * C))
                dve.memset(eps[:, :], 1e-5)
                ch.link(dve.tensor_reduce(sums[:, :], flat, AX.X, ALU.add))
                dve.sem_inc(s["summed"], 1)
                dve.wait_ge(s["mean_ready"], 1)
                ch.link(dve.tensor_copy(mean[:, :], ps[:, 0, 0:1]))
                dve.tensor_scalar(neg[:, :], mean[:, :], -1.0, None, ALU.mult).then_inc(s["summed"], 1)
                dve.wait_ge(s["squared"], 4)
                dve.tensor_reduce(total[:, :], sq[:, :], AX.X, ALU.add).then_inc(s["total_ready"], 1)
                dve.wait_ge(s["var_ready"], 1)
                ch.link(dve.tensor_copy(var[:, :], ps[:, 1, 0:1]))
                dve.sem_inc(s["total_ready"], 1)
                dve.wait_ge(s["rooted"], 1)
                ch.link(dve.reciprocal(var[:, :], var[:, :]))
                ch.link(dve.tensor_tensor(scale[:, :], var[:, :], a[:, :], ALU.mult))
                ch.link(dve.scalar_tensor_tensor(shift[:, :], neg[:, :], scale[:, :], bt[:, :], ALU.mult, ALU.add))

            @block.tensor
            def _(pe):
                pe.wait_ge(s["summed"], 1)
                pe.matmul(ps[:, 0, 0:1], over[:, :], sums[:, :], start=True, stop=True).then_inc(s["mean_ready"], 1)
                pe.wait_ge(s["total_ready"], 1)
                pe.matmul(ps[:, 1, 0:1], over[:, :], total[:, :], start=True, stop=True).then_inc(s["var_ready"], 1)

            @block.scalar
            def _(act):
                act.wait_ge(s["summed"], 2)
                for n in range(4):
                    act.activation(junk[:, :], flat[:, n * (T // 4):(n + 1) * (T // 4)], ACT.Square, bias=neg[:, :], accum_out=sq[:, n:n + 1]).then_inc(s["squared"], 1)
                    act.wait_ge(s["squared"], n + 1)
                act.wait_ge(s["total_ready"], 2)
                act.activation(var[:, :], var[:, :], ACT.Sqrt, bias=eps[:, :]).then_inc(s["rooted"], 1)
        s.end()


def triangle(nc, X, k_dram, w):
    with ExitStack() as ctx:
        def sb(n, shape):
            return ctx.enter_context(nc.sbuf_tensor("tr_" + n, shape, F32))

        ident, ones = sb("ident", [P, P]), sb("ones", [1, P])
        wab, bab, wo, bo = sb("wab", [P, 512]), sb("bab", [1, 512]), sb("wo", [P, 2, C]), sb("bo", [1, 2, C])
        zs, zb, ks, kb = sb("zs", [P, 1]), sb("zb", [P, 1]), sb("ks", [P, 1]), sb("kb", [P, 1])
        Z = sb("Z", [P, G, 2, C])
        load_all(nc, "tr_load", [(ident[:, :], w["ident"]), (wab[:, :], w["wab"]), (bab[:, :], w["bab"]), (wo[:, :, :], w["wo"]), (bo[:, :, :], w["bo"])])
        layer_norm(nc, "tr_ln", X, Z, 1e-6)
        global_norm(nc, "tr_gz", Z, w["alpha_in"], w["beta_in"], zs, zb)
        with nc.Block() as block:
            @block.vector
            def _(dve):
                zf = Z[:, :, :, :].rearrange("p g t c -> p (g t c)")
                dve.tensor_scalar(zf, zf, zs[:, :], zb[:, :], ALU.mult, ALU.add)
                dve.memset(ones[:, :], 1.0)
        with nc.sbuf_tensor("tr_zt", [P, T], F32) as ZT:
            transpose_tokens(nc, "tr_tr", Z, lambda g: ZT[:, bass.ds(g * 256, 256)].rearrange("c (p t) -> c t p", t=2), ident)
            triangle_products(nc, ZT, wab, bab, ones, k_dram)
        with nc.sbuf_tensor("tr_k", [P, G, 2, C], F32) as K:
            load_all(nc, "tr_kload", [(K[:, :, :, :], k_dram.rearrange("(g p t) c -> p g t c", p=P, t=2))])
            global_norm(nc, "tr_gk", K, w["alpha_o"], w["beta_o"], ks, kb)
            triangle_output(nc, Z, K, ks, kb, wo, bo, ones, ident, X)


def triangle_products(nc, ZT, wab, bab, ones, k_dram):
    with ExitStack() as ctx:
        def sb(n, shape):
            return ctx.enter_context(nc.sbuf_tensor("tp_" + n, shape, F32))
        zimg, gates = sb("zimg", [P, S]), sb("gates", [W, 4, 2, C])
        ab, kimg = sb("ab", [W, 2, H, C]), sb("kimg", [H, H, C])
        ps = ctx.enter_context(nc.psum_tensor("tp_ps", [P, 8, 512], F32))
        s = Signals(nc, "tp", "staged projected gated multiplied made kept_act kept_dve stored")
        with nc.Fori(0, B) as b:
            with nc.Block() as block:
                @block.scalar
                def _(act):
                    act.activation(zimg[:, :], ZT[:, bass.ds(b * S, S)], ACT.Copy).then_inc(s["staged"], 1)
                    for r in range(H):
                        act.wait_ge(s["projected"], r + 1)
                        if r >= 4:
                            act.wait_ge(s["multiplied"], r - 3)
                        act.activation(gates[:, r % 4, :, :], ps[0:W, r % 4, :].rearrange("w (n m c) -> w n m c", n=2, m=2)[:, :, 0, :],
                                       ACT.Sigmoid).then_inc(s["gated"], 1)
                    for n in range(0, 16, 2):
                        act.wait_ge(s["made"], n + 1)
                        act.activation(kimg[:, :, 8 * n:8 * n + 8], ps[0:H, 4 + n % 4, 0:384].rearrange("i (c j) -> i j c", c=8), ACT.Copy).then_inc(s["kept_act"], 1)

                @block.vector
                def _(dve):
                    for r in range(H):
                        dve.wait_ge(s["gated"], r + 1)
                        dve.tensor_tensor(ab[:, :, r, :], gates[:, r % 4, :, :],
                                          ps[0:W, r % 4, :].rearrange("w (n m c) -> w n m c", n=2, m=2)[:, :, 1, :], ALU.mult).then_inc(s["multiplied"], 1)
                    for n in range(1, 16, 2):
                        dve.wait_ge(s["made"], n + 1)
                        dve.tensor_copy(kimg[:, :, 8 * n:8 * n + 8], ps[0:H, 4 + n % 4, 0:384].rearrange("i (c j) -> i j c", c=8)).then_inc(s["kept_dve"], 1)

                @block.tensor
                def _(pe):
                    pe.wait_ge(s["staged"], 1)
                    for r in range(H):
                        if r >= 4:
                            pe.wait_ge(s["multiplied"], r - 3)
                        pe.matmul(ps[0:W, r % 4, :], zimg[:, r * W:(r + 1) * W], wab[:, :], start=True, stop=False)
                        pe.matmul(ps[0:W, r % 4, :], ones[:, 0:W], bab[:, :], start=False, stop=True).then_inc(s["projected"], 1)
                    pe.wait_ge(s["multiplied"], H)
                    for n in range(16):
                        if n >= 4:
                            pe.wait_ge(s["kept_act"] if n % 2 == 0 else s["kept_dve"], n // 2 - 1)
                        for c in range(8):
                            ins = pe.matmul(ps[0:H, 4 + n % 4, c * H:(c + 1) * H], ab[:, 0, :, 8 * n + c], ab[:, 1, :, 8 * n + c], start=True, stop=True)
                        ins.then_inc(s["made"], 1)

                @block.sync
                def _(sp):
                    sp.wait_ge(s["kept_act"], 8)
                    sp.wait_ge(s["kept_dve"], 8)
                    sp.dma_start(k_dram[bass.ds(b * S, S), :].rearrange("(i j) c -> i (j c)", i=H), kimg[:, :, :].rearrange("i j c -> i (j c)")).then_inc(s["stored"], 16)
                    sp.wait_ge(s["stored"], 16)
            s.clear()
        s.release()


def triangle_output(nc, Z, K, ks, kb, wo, bo, ones, ident, X):
    with ExitStack() as ctx:
        def sb(n, shape):
            return ctx.enter_context(nc.sbuf_tensor("to_" + n, shape, F32))
        stage, turned, gate, prod = sb("stage", [P, 2, 4, C]), sb("turned", [P, 2, 4, P]), sb("gate", [P, 2, 256]), sb("prod", [P, 2, 256])
        ps = ctx.enter_context(nc.psum_tensor("to_ps", [P, 4, 512], F32))
        s = Signals(nc, "to", "staged turned kept made gated own added")

        def tiles(V, g):
            return V[:, bass.ds(g, 1), :, :].rearrange("p g t c -> p (g t) c")

        with nc.Block() as block:
            @block.vector
            def _(dve):
                ch = Chain(dve, s["own"])
                dve.sem_inc(s["added"], 2)
                with dve.Fori(0, G // 2) as i:
                    ch.enter(i, 2)
                    for u in range(2):
                        dve.wait_ge(s["turned"], i * 2 + (u + 1))
                        dve.tensor_copy(stage[:, u, 0:2, :], tiles(Z, i * 2 + u))
                        dve.tensor_scalar(stage[:, u, 2:4, :], tiles(K, i * 2 + u), ks[:, :], kb[:, :], ALU.mult, ALU.add).then_inc(s["staged"], 1)
                    for u in range(2):
                        dve.wait_ge(s["gated"], i * 2 + (u + 1))
                        ch.link(dve.tensor_tensor(prod[:, u, :], gate[:, u, :], ps[:, 2 + u, 256:512], ALU.mult))
                        out = X[:, bass.ds(i * 2 + u, 1), :, :].rearrange("p g t c -> p (g t c)")
                        dve.tensor_tensor(out, out, prod[:, u, :], ALU.add).then_inc(s["added"], 1)

            @block.tensor
            def _(pe):
                pe.sem_inc(s["turned"], 2)
                with pe.Fori(0, G // 2) as i:
                    for u in range(2):
                        pe.wait_ge(s["staged"], i * 2 + (u + 1))
                        pe.wait_ge(s["kept"], i * 2 + (u + 1))
                        for t in range(4):
                            ins = pe.transpose(ps[:, u, t * P:(t + 1) * P], stage[:, u, t, :], ident[:, :])
                        ins.then_inc(s["turned"], 1)
                    for u in range(2):
                        pe.wait_ge(s["kept"], i * 2 + (u + 3))
                        pe.wait_ge(s["added"], i * 2 + (u + 1))
                        for t in range(4):
                            out = ps[:, 2 + u, t * C:(t + 1) * C]
                            pe.matmul(out, turned[:, u, t, :], wo[:, t // 2, :], start=True, stop=False)
                            ins = pe.matmul(out, ones[:, :], bo[:, t // 2, :], start=False, stop=True)
                        ins.then_inc(s["made"], 1)

            @block.scalar
            def _(act):
                act.sem_inc(s["kept"], 2)
                with act.Fori(0, G // 2) as i:
                    for u in range(2):
                        act.wait_ge(s["turned"], i * 2 + (u + 3))
                        act.wait_ge(s["added"], i * 2 + (u + 1))
                        act.activation(turned[:, u, :, :].rearrange("c t p -> c (t p)"), ps[:, u, :], ACT.Copy).then_inc(s["kept"], 1)
                    for u in range(2):
                        act.wait_ge(s["made"], i * 2 + (u + 1))
                        act.activation(gate[:, u, :], ps[:, 2 + u, 0:256], ACT.Sigmoid).then_inc(s["gated"], 1)
        s.end()


NX = 8


def top2_experts(nc, X, w):
    with ExitStack() as ctx:
        def sb(n, shape):
            return ctx.enter_context(nc.sbuf_tensor("moe_" + n, shape, F32))

        ident, ones = sb("ident", [P, P]), sb("ones", [1, P])
        router, router_b, ew, eb = sb("router", [P, NX]), sb("router_b", [1, NX]), sb("ew", [P, NX * C]), sb("eb", [1, NX * C])
        gates = sb("gates", [P, 2 * G, NX])
        XT = sb("xt", [P, T])
        stage = sb("stage", [P, 2, 4, P])
        load_all(nc, "moe_load", [(ident[:, :], w["ident"]), (router[:, :], w["router"]), (router_b[:, :], w["router_b"]), (ew[:, :], w["ew"]), (eb[:, :], w["eb"])])
        with nc.sbuf_tensor("moe_xn", [P, G, 2, C], F32) as XN:
            layer_norm(nc, "moe_ln", X, XN, 1e-5)
            transpose_tokens(nc, "moe_tr", XN, lambda g: XT[:, bass.ds(g * 256, 256)].rearrange("c (t p) -> c t p", t=2), ident)
        ps = ctx.enter_context(nc.psum_tensor("moe_ps", [P, 8, 512], F32))

        s = Signals(nc, "mr", "ones_ready staged made kept")
        with nc.Block() as block:
            @block.scalar
            def _(act):
                with act.Fori(0, G // 4) as i:
                    for u in range(2):
                        act.wait_ge(s["made"], i * 2 + (u + 1))
                        act.activation(stage[:, u, :, :].rearrange("c t p -> c (t p)"), XT[:, bass.ds((i * 2 + u) * 512, 512)], ACT.Copy).then_inc(s["staged"], 1)

            @block.tensor
            def _(pe):
                pe.sem_inc(s["made"], 2)
                pe.wait_ge(s["ones_ready"], 1)
                with pe.Fori(0, G // 4) as i:
                    for u in range(2):
                        pe.wait_ge(s["staged"], i * 2 + (u + 1))
                        pe.wait_ge(s["kept"], i * 2 + (u + 1))
                        for t in range(4):
                            pe.matmul(ps[:, u, t * NX:(t + 1) * NX], stage[:, u, t, :], router[:, :], start=True, stop=False)
                            ins = pe.matmul(ps[:, u, t * NX:(t + 1) * NX], ones[:, :], router_b[:, :], start=False, stop=True)
                        ins.then_inc(s["made"], 1)

            @block.vector
            def _(dve):
                dve.sem_inc(s["kept"], 2)
                dve.memset(ones[:, :], 1.0).then_inc(s["ones_ready"], 1)
                with dve.Fori(0, G // 4) as i:
                    for u in range(2):
                        dve.wait_ge(s["made"], i * 2 + (u + 3))
                        dve.tensor_copy(gates[:, bass.ds((i * 2 + u) * 4, 4), :], ps[:, u, 0:4 * NX].rearrange("p (t e) -> p t e", e=NX)).then_inc(s["kept"], 1)
        s.end()
        route(nc, gates)

        s = Signals(nc, "me", "staged made own added")
        with nc.Block() as block:
            @block.scalar
            def _(act):
                with act.Fori(0, G // 2) as i:
                    for u in range(2):
                        act.wait_ge(s["made"], i * 4 + (2 * u + 1))
                        act.activation(stage[:, u, 0:2, :].rearrange("c t p -> c (t p)"), XT[:, bass.ds((i * 2 + u) * 256, 256)], ACT.Copy).then_inc(s["staged"], 1)

            @block.tensor
            def _(pe):
                pe.sem_inc(s["made"], 3)
                with pe.Fori(0, G // 2) as i:
                    for u in range(2):
                        pe.wait_ge(s["staged"], i * 2 + (u + 1))
                        for t in range(2):
                            pe.wait_ge(s["added"], i * 4 + (2 * u + t + 1))
                            for n in range(2):
                                out = ps[:, 4 * u + 2 * t + n, :]
                                pe.matmul(out, stage[:, u, t, :], ew[:, n * 512:(n + 1) * 512], start=True, stop=False)
                                ins = pe.matmul(out, ones[:, :], eb[:, n * 512:(n + 1) * 512], start=False, stop=True)
                            ins.then_inc(s["made"], 1)

            @block.vector
            def _(dve):
                dve.sem_inc(s["added"], 4)
                ch = Chain(dve, s["own"])
                with dve.Fori(0, G // 2) as i:
                    ch.enter(i, 2 * (NX - 1))
                    for u in range(2):
                        dve.wait_ge(s["made"], i * 4 + (2 * u + 5))
                        for e in range(NX):
                            for t in range(2):
                                out = X[:, bass.ds(i * 2 + u, 1), t, :].rearrange("p g c -> p (g c)")
                                gate = gates[:, bass.ds(i * 4 + (2 * u + t), 1), e]
                                ins = dve.scalar_tensor_tensor(out, ps[:, 4 * u + 2 * t + e // 4, (e % 4) * C:(e % 4 + 1) * C], gate, out, ALU.mult, ALU.add)
                                if e == NX - 1:
                                    ins.then_inc(s["added"], 1)
                                elif t == 1:
                                    ch.link(ins)
        s.end()


def route(nc, gates):
    n = 2 * G
    with ExitStack() as ctx:
        def sb(name, shape):
            return ctx.enter_context(nc.sbuf_tensor("rt_" + name, shape, F32))
        rest, equal, count, mask, top, second = sb("rest", [P, n, NX]), sb("equal", [P, n, NX]), sb("count", [P, n, NX]), sb("mask", [P, n, NX]), sb("top", [P, n]), sb("second", [P, n])
        s = Signals(nc, "rt", "own centred exp_ready")

        def wide(ap):
            return bc(ap[:, :, None], [P, n, NX])

        with nc.Block() as block:
            @block.vector
            def _(dve):
                ch = Chain(dve, s["own"])

                def first_of(logits, peak):
                    ch.link(dve.tensor_tensor(equal[:, :, :], logits, wide(peak), ALU.is_equal))
                    ch.link(dve.tensor_copy(count[:, :, :], equal[:, :, :]))
                    for e in range(1, NX):
                        ch.link(dve.tensor_tensor(count[:, :, e], count[:, :, e], count[:, :, e - 1], ALU.add))
                    ch.link(dve.tensor_scalar(count[:, :, :], count[:, :, :], 1.0, None, ALU.is_equal))
                    ch.link(dve.tensor_tensor(equal[:, :, :], equal[:, :, :], count[:, :, :], ALU.mult))

                ch.link(dve.tensor_reduce(top[:, :], gates[:, :, :], AX.X, ALU.max))
                first_of(gates[:, :, :], top)
                ch.link(dve.tensor_copy(mask[:, :, :], equal[:, :, :]))
                ch.link(dve.scalar_tensor_tensor(rest[:, :, :], mask[:, :, :], LOWEST, gates[:, :, :], ALU.mult, ALU.add))
                ch.link(dve.tensor_reduce(second[:, :], rest[:, :, :], AX.X, ALU.max))
                first_of(rest[:, :, :], second)
                ch.link(dve.tensor_tensor(mask[:, :, :], mask[:, :, :], equal[:, :, :], ALU.add))
                dve.tensor_tensor(gates[:, :, :], gates[:, :, :], wide(top), ALU.subtract).then_inc(s["centred"], 1)
                dve.wait_ge(s["exp_ready"], 1)
                ch.link(dve.tensor_tensor(gates[:, :, :], gates[:, :, :], mask[:, :, :], ALU.mult))
                ch.link(dve.tensor_reduce(top[:, :], gates[:, :, :], AX.X, ALU.add))
                ch.link(dve.reciprocal(top[:, :], top[:, :]))
                ch.link(dve.tensor_tensor(gates[:, :, :], gates[:, :, :], wide(top), ALU.mult))

            @block.scalar
            def _(act):
                act.wait_ge(s["centred"], 1)
                act.activation(gates[:, :, :], gates[:, :, :], ACT.Exp).then_inc(s["exp_ready"], 1)
        s.end()


def metaformer(nc, w, out):
    def scratch(name, shape):
        return nc.dram_tensor(name, shape, F32, kind="Internal").ap()

    def tokens(ap):
        return ap.rearrange("(g p t) c -> p g t c", p=P, t=2)

    x1, rows, channels, maxima = scratch("x1", [T, C]), scratch("rows", [T, C]), scratch("channels", [P, T]), scratch("maxima", [NH * NT_, P])
    with nc.sbuf_tensor("m0_xt", [P, T], F32) as XT:
        with nc.sbuf_tensor("m0_x", [P, G, 2, C], F32) as X0, nc.sbuf_tensor("m0_xn", [P, G, 2, C], F32) as XN, nc.sbuf_tensor("m0_ident", [P, P], F32) as ident:
            load_all(nc, "m0_load", [(X0[:, :, :, :], tokens(w["x"])), (ident[:, :], w["ident"])])
            layer_norm(nc, "m0_ln", X0, XN, 1e-6)
            transpose_tokens(nc, "m0_tr", XN, lambda g: XT[:, bass.ds(g * 256, 256)].rearrange("c (p t) -> c t p", t=2), ident)
        selective_scan_mixer(nc, XT, w["x"], x1, w["l0_conv"])
    with nc.sbuf_tensor("x", [P, G, 2, C], F32) as X:
        load_all(nc, "m1_load", [(X[:, :, :, :], tokens(x1))])
        spectral_unit(nc, X, w["l0_ffn"])
        fourier_mixer(nc, X, rows, w["l1_conv"])
        expert_choice(nc, "c1", X, w["l1_ffn"])
        attention(nc, X, channels, maxima, w["l2_conv"])
        expert_choice(nc, "c2", X, w["l2_ffn"])
        triangle(nc, X, rows, w["l3_conv"])
        top2_experts(nc, X, w["l3_ffn"])
        load_all(nc, "m_store", [(tokens(out), X[:, :, :, :])])



def layout(inputs):
    def of(prefix):
        return lambda n: np.asarray(inputs[prefix + n])

    def turned(a, order, *shape):
        return np.ascontiguousarray(a.transpose(order)).reshape(shape)

    ident = np.eye(P, dtype=np.float32)
    out = {"x": np.asarray(inputs["x"]).reshape(T, C), "ident": ident}
    stage = {}

    f = of("L0_conv_")
    xp = f("x_proj_w")
    sel = np.zeros((3, 2 * NST, 2 * NST, P), np.float32)
    for n in range(2 * NST):
        sel[:, n, n] = 1
    stage["l0_conv"] = {
        "win": np.ascontiguousarray(f("in_proj_w").T),
        "convw": turned(f("conv_w").reshape(D2, P, 9), (1, 0, 2), P, D2, 9),
        "convb": np.ascontiguousarray(f("conv_b").reshape(D2, P).T),
        "xpw": turned(np.concatenate([xp[:, DTR:], xp[:, :DTR]], 1).reshape(4, 40, D2, P), (3, 2, 0, 1), P, D2, 4, 40),
        "dtw": turned(f("dt_proj_w"), (2, 0, 1), DTR, 4, 256),
        "dtb": turned(f("dt_proj_b").reshape(4, D2, P), (2, 0, 1), P, 4, D2),
        "a_log": turned(f("A_logs").reshape(4, D2, P, NST), (2, 0, 1, 3), P, 4, D2, NST),
        "ds": turned(f("Ds").reshape(4, D2, P), (2, 0, 1), P, 4, D2),
        "ng": np.ascontiguousarray(f("norm_g").reshape(D2, P).T),
        "nb": np.ascontiguousarray(f("norm_b").reshape(D2, P).T),
        "wout": turned(f("out_proj_w").T.reshape(D2, P, C), (1, 0, 2), P, D2, C),
        "sel": sel.reshape(96, 2 * NST, P).astype(mybir.dt.np(BF16)),
    }

    f = of("L0_ffn_")
    none = np.zeros((NK, P), np.float32)
    phi = f("phi")[:S].T
    stage["l0_ffn"] = {
        "phi_even": np.concatenate([phi[:, 0::2][:, ::-1], none], 1),
        "phi_odd": np.concatenate([phi[:, 1::2][:, ::-1], none], 1),
        "M_plus": turned(f("M_phi_plus"), (1, 2, 0, 3), NK, P, NEDGE, P),
        "M_minus": turned(f("M_phi_minus"), (1, 2, 0, 3), NK, P, NEDGE, P),
        "M_u": turned(f("M_u"), (1, 2, 0, 3), 3, P, NEDGE, P),
        "log_weights": f("log_weights"), "gumbel": f("gumbel"), "sigma": f("sigma"),
    }

    f = of("L1_conv_")
    turn = 2 * np.pi * (np.outer(np.arange(W), np.arange(NF)) % W) / W
    cos, sin = np.cos(turn), np.sin(turn)
    sin[:, [0, NF - 1]] = 0
    both = np.full(NF, 2.0)
    both[[0, NF - 1]] = 1
    stage["l1_conv"] = {
        "fw0": turned(f("fw0")[:, :, :NF], (2, 0, 3, 1), NF * P, 2 * C),
        "fw1": turned(f("fw1")[:, :, :NF], (2, 0, 3, 1), NF * P, 2 * C),
        "dft": (np.concatenate([sin, cos, -sin], 1) / np.sqrt(W)).astype(np.float32),
        "idft": np.ascontiguousarray((np.concatenate([cos * both, -sin * both], 1).T / np.sqrt(W)).astype(np.float32)),
        "w1": f("w1"), "w2": turned(f("w2").reshape(4, P, C), (1, 0, 2), P, 4, C),
        "b1": np.ascontiguousarray(f("b1").reshape(4, P).T), "b2": f("b2").reshape(1, C),
    }

    for layer in (1, 2):
        f = of(f"L{layer}_ffn_")
        w1, w2 = f("weight1"), f("weight2")
        stage[f"l{layer}_ffn"] = {
            "gate": np.ascontiguousarray(f("gate_w").T), "gate_b": f("gate_b").reshape(NE, 1),
            "w1": w1.reshape(NE * 129, 512), "w2": w2.reshape(NE * 513, C),
            "b1": turned(w1[:, P].reshape(NE, P, 4), (1, 0, 2), P, NE * 4), "b2": np.ascontiguousarray(w2[:, 512]),
        }

    f = of("L2_conv_")
    stage["l2_conv"] = {"wqkv": f("w_qkv"), "wout": f("w_out"), "bout": f("b_out").reshape(1, C)}

    f = of("L3_conv_")
    four = ("ga", "la", "gb", "lb")
    stage["l3_conv"] = {
        "wab": np.concatenate([f("W_" + n).T for n in four], 1), "bab": np.concatenate([f("b_" + n) for n in four]).reshape(1, 512),
        "wo": np.stack([f("W_go").T, f("W_lo").T], 1), "bo": np.stack([f("b_go"), f("b_lo")]).reshape(1, 2, C),
        "alpha_in": f("alpha_in"), "beta_in": f("beta_in"), "alpha_o": f("alpha_o"), "beta_o": f("beta_o"),
    }

    f = of("L3_ffn_")
    stage["l3_ffn"] = {
        "router": f("router_w"), "router_b": f("router_b").reshape(1, NX),
        "ew": turned(f("expert_w"), (1, 0, 2), P, NX * C), "eb": f("expert_b").reshape(1, NX * C),
    }
    for name, arrays in stage.items():
        for n, a in arrays.items():
            out[f"{name}.{n}"] = np.ascontiguousarray(a)
    return out


def kernel(**inputs):
    import concourse.bacc as bacc
    from concourse.bass_utils import run_bass_kernel_spmd

    nc = bacc.Bacc("TRN2", target_bir_lowering=False, num_devices=1)
    arrays, w = {}, {}
    for name, a in layout(inputs).items():
        dram = "in_" + name.replace(".", "_")
        arrays[dram] = a
        ap = nc.dram_tensor(dram, a.shape, mybir.dt.from_np(a.dtype), kind="ExternalInput").ap()
        if "." in name:
            group, n = name.split(".")
            w.setdefault(group, {})[n] = ap
        else:
            w[name] = ap
    for group in list(w):
        if group[0] == "l":
            w[group]["ident"] = w["ident"]
    w["l1_conv"]["fw"] = [w["l1_conv"]["fw0"], w["l1_conv"]["fw1"]]
    out = nc.dram_tensor("out", [T, C], F32, kind="ExternalOutput").ap()
    metaformer(nc, w, out)
    result = run_bass_kernel_spmd(nc, [arrays], core_ids=[0])
    return result.results[0]["out"].reshape(B, H, W, C)
```

```python
from contextlib import ExitStack

import numpy as np
import concourse.bass as bass
from concourse import mybir

P = 128
B, H, W, C = 4, 48, 48, 128
S = H * W
T = B * S
G = T // 256
GB = G // B
HALF = S // 2

F32 = mybir.dt.float32
BF16 = mybir.dt.bfloat16
F32R = mybir.dt.float32r
ALU = mybir.AluOpType
ACT = mybir.ActivationFunctionType
AX = mybir.AxisListType


class Chain:

    def __init__(self, eng, sem):
        self.eng, self.sem, self.base, self.n = eng, sem, 0, 0

    def link(self, ins):
        self.n += 1
        ins.then_inc(self.sem, 1)
        self.eng.wait_ge(self.sem, self.base + self.n)

    def enter(self, i, per):
        self.start, self.per, self.outer = self.base + self.n, per, (self.base, self.n)
        self.base, self.n = self.start + i * per, 0

    def leave(self, passes):
        assert self.n == self.per, (self.n, self.per)
        self.base, self.n = self.outer[0], self.outer[1] + passes * self.per


class Signals:

    def __init__(self, nc, stage, names):
        self.nc = nc
        self.named = {n: nc.alloc_semaphore(f"{stage}_{n}") for n in names.split()}
        self.all = list(self.named.values())

    def __getitem__(self, name):
        return self.named[name]

    def clear(self):
        for s in self.all:
            self.nc.gpsimd.sem_clear(s)
        self.nc.all_engine_barrier()

    def release(self):
        for s in self.all:
            self.nc.release_semaphore(s)

    def end(self):
        self.clear()
        self.release()


def bc(ap, shape):
    return ap.to_broadcast(shape)


def layer_norm(nc, name, X, XN, eps):
    NT = 2 * G
    with ExitStack() as ctx:
        st = ctx.enter_context(nc.sbuf_tensor(name + "_stats", [P, NT, 6], F32))
        mean = ctx.enter_context(nc.sbuf_tensor(name + "_mean", [P, NT], F32))
        var = ctx.enter_context(nc.sbuf_tensor(name + "_var", [P, NT], F32))
        std = ctx.enter_context(nc.sbuf_tensor(name + "_std", [P, NT], F32))
        rstd = ctx.enter_context(nc.sbuf_tensor(name + "_rstd", [P, NT], F32))
        epst = ctx.enter_context(nc.sbuf_tensor(name + "_eps", [P, 1], F32))
        s = Signals(nc, name, "own var_ready std_ready")
        xf = X[:, :, :, :].rearrange("p g t c -> p (g t) c")
        nf = XN[:, :, :, :].rearrange("p g t c -> p (g t) c")
        block = ctx.enter_context(nc.Block())

        @block.vector
        def _(dve):
            ch = Chain(dve, s["own"])
            ch.link(dve.memset(epst[:, :], eps))
            with dve.Fori(0, NT // 4) as i:
                for u in range(4):
                    ins = dve.bn_stats(st[:, i * 4 + u, :], xf[:, i * 4 + u, :])
                ch.enter(i, 1)
                ch.link(ins)
            ch.leave(NT // 4)
            me, mo, ve, vo = (st[:, :, k] for k in (1, 4, 2, 5))
            ch.link(dve.tensor_tensor(mean[:, :], me, mo, ALU.add))
            ch.link(dve.tensor_tensor(std[:, :], me, mo, ALU.subtract))
            ch.link(dve.tensor_tensor(std[:, :], std[:, :], std[:, :], ALU.mult))
            ch.link(dve.tensor_tensor(var[:, :], ve, vo, ALU.add))
            ch.link(dve.tensor_scalar(mean[:, :], mean[:, :], 0.5, None, ALU.mult))
            ch.link(dve.tensor_scalar(var[:, :], var[:, :], 1.0 / C, None, ALU.mult))
            dve.scalar_tensor_tensor(var[:, :], std[:, :], 0.25, var[:, :], ALU.mult, ALU.add).then_inc(s["var_ready"], 1)
            ch.link(dve.tensor_tensor(nf, xf, bc(mean[:, :, None], [P, NT, C]), ALU.subtract))
            dve.wait_ge(s["std_ready"], 1)
            ch.link(dve.reciprocal(rstd[:, :], std[:, :]))
            ch.link(dve.tensor_tensor(nf, nf, bc(rstd[:, :, None], [P, NT, C]), ALU.mult))

        @block.scalar
        def _(act):
            act.wait_ge(s["var_ready"], 1)
            act.activation(std[:, :], var[:, :], ACT.Sqrt, bias=epst[:, :]).then_inc(s["std_ready"], 1)
    s.end()


def transpose_tokens(nc, name, XN, out_of, ident):
    with ExitStack() as ctx:
        stage = ctx.enter_context(nc.sbuf_tensor(name + "_stage", [P, 2, 4, C], F32))
        ps = ctx.enter_context(nc.psum_tensor(name + "_ps", [P, 2, 512], F32))
        s = Signals(nc, name, "staged turned stored")
        staged, turned, stored = s.all
        block = ctx.enter_context(nc.Block())

        @block.vector
        def _(dve):
            with dve.Fori(0, G // 4) as i:
                for u in range(2):
                    dve.wait_ge(turned, i * 2 + u + 1)
                    src = XN[:, bass.ds(i * 4 + 2 * u, 2), :, :].rearrange("p g t c -> p (g t) c")
                    dve.tensor_copy(stage[:, u, :, :], src).then_inc(staged, 1)

        @block.tensor
        def _(pe):
            pe.sem_inc(turned, 2)
            with pe.Fori(0, G // 4) as i:
                for u in range(2):
                    pe.wait_ge(staged, i * 2 + u + 1)
                    pe.wait_ge(stored, i * 2 + u + 1)
                    for t in range(4):
                        ins = pe.transpose(ps[:, u, t * 128:(t + 1) * 128], stage[:, u, t, :], ident[:, :])
                    ins.then_inc(turned, 1)

        @block.scalar
        def _(act):
            act.sem_inc(stored, 2)
            with act.Fori(0, G // 4) as i:
                for u in range(2):
                    act.wait_ge(turned, i * 2 + u + 3)
                    for g in range(2):
                        src = ps[:, u, g * 256:(g + 1) * 256].rearrange("c (t p) -> c t p", t=2)
                        ins = act.activation(out_of(i * 4 + 2 * u + g), src, ACT.Copy)
                    ins.then_inc(stored, 1)
    s.end()


def load_all(nc, name, pairs):
    s = Signals(nc, name, "loaded")
    with nc.Block() as block:
        @block.sync
        def _(sp):
            for dst, src in pairs:
                sp.dma_start(dst, src).then_inc(s["loaded"], 16)
            sp.wait_ge(s["loaded"], 16 * len(pairs))
    s.end()


def bias_rows(nc, ctx, name, biases):
    widths = [int(np.prod(b.shape)) for b in biases]
    total = sum(widths)
    rows = ctx.enter_context(nc.sbuf_tensor(name + "_bias", [P, total], F32R))
    ones = ctx.enter_context(nc.sbuf_tensor(name + "_ones", [P, P], F32R))
    with nc.sbuf_tensor(name + "_raw", [33, 2, total], F32) as raw, nc.sbuf_tensor(name + "_plain", [P, total], F32) as plain:
        at = [sum(widths[:i]) for i in range(len(widths))]
        load_all(nc, name + "_load", [(raw[r:r + 1, 0, a:a + n], b) for a, n, b in zip(at, widths, biases) for r in (0, 32)])
        s = Signals(nc, name, "cleared high kept")
        with nc.Block() as block:
            @block.vector
            def _(dve):
                dve.memset(plain[:, :], 0.0).then_inc(s["cleared"], 1)
                dve.wait_ge(s["cleared"], 1)
                dve.tensor_copy(rows[:, :], plain[:, :]).then_inc(s["cleared"], 1)
                dve.wait_ge(s["high"], 2)
                dve.tensor_tensor(rows[32:33, :], raw[32:33, 0, :], raw[32:33, 1, :].bitcast(F32R), ALU.subtract)
                n = min(P, total)
                for i in range(P // n):
                    dve.tensor_scalar(ones[:, i * n:(i + 1) * n], plain[:, 0:n], 1.0, None, ALU.add)

            @block.scalar
            def _(act):
                act.wait_ge(s["cleared"], 2)
                act.activation(rows[0:1, :], raw[0:1, 0, :], ACT.Copy).then_inc(s["high"], 1)
                act.activation(raw[32:33, 1, :].bitcast(F32R), raw[32:33, 0, :], ACT.Copy).then_inc(s["high"], 1)
        s.end()
    return ones, [rows[:, a:a + n] for a, n in zip(at, widths)]


R_ORDER = 384
NCH = S // R_ORDER
D2 = 2
NST = 16
DTR = 8
L2 = S // 2
SC = L2 // R_ORDER


def selective_scan_mixer(nc, XT, x_in, x_out, w):
    with ExitStack() as ctx:
        def sb(name, shape, dt=F32):
            return ctx.enter_context(nc.sbuf_tensor("ss_" + name, shape, dt))

        win = sb("win", [P, 512])
        convw = sb("convw", [P, D2, 9])
        convb = sb("convb", [P, D2])
        xpw = sb("xpw", [P, D2, 4, 40])
        dtw = sb("dtw", [DTR, 4, 256])
        dtb = sb("dtb", [P, 4, D2])
        a_log = sb("a_log", [P, 4, D2, NST])
        a_neg = sb("a_neg", [P, 4, D2, NST])
        ds = sb("ds", [P, 4, D2])
        dsum = sb("dsum", [P, D2])
        ng = sb("ng", [P, D2])
        nb = sb("nb", [P, D2])
        wout = sb("wout", [P, D2, P])
        ident = sb("ident", [P, P])
        sel = sb("sel", [96, 32, P], BF16)
        zero = sb("zero", [P, R_ORDER], BF16)
        over = sb("over", [P, P])
        eps = sb("eps", [P, 1])
        xb = sb("xb", [P, 18, C])
        xc = sb("xc", [P, 2, D2, S])
        y = sb("y", [P, D2, S])
        work = sb("work", [P, 16 * L2])
        bc3 = sb("bc3", [96, L2], BF16)
        rest = sb("rest", [32, L2])
        mid = sb("mid", [32, L2], BF16)
        dtr = sb("dtr", [DTR, L2])
        last = sb("last", [P, D2, NST])
        ps = ctx.enter_context(nc.psum_tensor("ss_ps", [P, 8, 512], F32))

        def part(at, shape):
            n = int(np.prod(shape))
            names = "abcd"[:len(shape)]
            kw = {c: s for c, s in zip(names, shape)}
            return work[:, at * L2:at * L2 + n].rearrange(f"p ({' '.join(names)}) -> p {' '.join(names)}", **kw)

        xpad = part(0, [D2, 50, 50])
        decay, drive, hid, rep = part(0, [D2, L2]), part(2, [D2, L2]), part(4, [2, D2, L2]), part(8, [2, 2, L2])
        dt, dtu = part(12, [D2, L2]), part(14, [D2, L2])
        sq, sd, sz = part(0, [D2, S]), part(4, [S]), part(6, [D2, S])

        load_all(nc, "ss_weights", [
            (win[:, :], w["win"]), (convw[:, :, :], w["convw"]), (convb[:, :], w["convb"]),
            (xpw[:, :, :, :], w["xpw"]), (dtw[:, :, :], w["dtw"]), (dtb[:, :, :], w["dtb"]),
            (a_log[:, :, :, :], w["a_log"]), (ds[:, :, :], w["ds"]), (ng[:, :], w["ng"]), (nb[:, :], w["nb"]),
            (wout[:, :, :], w["wout"]), (ident[:, :], w["ident"]), (sel[:, :, :], w["sel"])])

        s0 = Signals(nc, "ss0", "own exp_ready")
        own, exp_ready = s0["own"], s0["exp_ready"]
        with nc.Block() as block:

            @block.scalar
            def _(act):
                act.activation(a_neg[:, :, :, :], a_log[:, :, :, :], ACT.Exp).then_inc(exp_ready, 1)

            @block.vector
            def _(dve):
                ch = Chain(dve, own)
                dve.memset(zero[:, :], 0.0)
                dve.memset(over[:, :], 1.0 / 256)
                dve.memset(eps[:, :], 1e-5)
                ch.link(dve.tensor_tensor(dsum[:, :], ds[:, 0, :], ds[:, 1, :], ALU.add))
                for k in (2, 3):
                    ch.link(dve.tensor_tensor(dsum[:, :], dsum[:, :], ds[:, k, :], ALU.add))
                dve.wait_ge(exp_ready, 1)
                ch.link(dve.tensor_scalar(a_neg[:, :, :, :], a_neg[:, :, :, :], -1.0, None, ALU.mult))

        s0.end()
        s1 = Signals(nc, "ss1", "loaded projected padded cleared conv_own conv_done gated")
        s2 = Signals(nc, "ss2", "xdbl dtr_ready bank_free split own dts prep own_act soft dt_ready decay_ready "
                                "rep_banks rep_ready scanned weighted summed zeroed last_own y_free pool_own")
        s3 = Signals(nc, "ss3", "mean centred squared varied sd_ready own normed affine zed zgated gated summed stored own_act")
        TOK = S
        held = dict(ps=ps, xc=xc, y=y, xpw=xpw, dtw=dtw, dtb=dtb, a_neg=a_neg, sel=sel, zero=zero, ident=ident, decay=decay, drive=drive, hid=hid, rep=rep, dt=dt, dtu=dtu, bc3=bc3, rest=rest, mid=mid, dtr=dtr, last=last, xb=xb, over=over, eps=eps, ng=ng, nb=nb, win=win, wout=wout, XT=XT, x_out=x_out, sq=sq, sd=sd, sz=sz)

        with nc.Fori(0, B) as b:
            with nc.Block() as block:
                @block.sync
                def _(sp):
                    sp.dma_start(xb[:, :, :].rearrange("p n c -> p (n c)"), x_in[bass.ds(b * S, S), :].rearrange("(p n) c -> p (n c)", p=P)).then_inc(s1["loaded"], 16)
                    sp.wait_ge(s1["loaded"], 16)

                @block.gpsimd
                def _(pool):
                    pool.memset(xpad, 0.0).then_inc(s1["cleared"], 1)

                @block.tensor
                def _(pe):
                    for n in range(D2 * NCH):
                        d, c = n // NCH, n % NCH
                        if n >= 8:
                            pe.wait_ge(s1["padded"], n - 7)
                        pe.matmul(ps[:, n % 8, 0:R_ORDER], win[:, d * P:(d + 1) * P],
                                  XT[:, bass.ds(b * TOK + c * R_ORDER, R_ORDER)], start=True, stop=True).then_inc(s1["projected"], 1)

                @block.scalar
                def _(act):
                    act.wait_ge(s1["cleared"], 1)
                    for n in range(D2 * NCH):
                        d, c = n // NCH, n % NCH
                        act.wait_ge(s1["projected"], n + 1)
                        act.activation(xpad[:, d, 1 + 8 * c:9 + 8 * c, 1:49],
                                       ps[:, n % 8, 0:R_ORDER].rearrange("p (h w) -> p h w", w=W), ACT.Copy).then_inc(s1["padded"], 1)
                    for d in range(D2):
                        act.wait_ge(s1["conv_done"], d + 1)
                        act.activation(xc[:, 0, d, :], y[:, d, :], ACT.Silu, bias=convb[:, d:d + 1]).then_inc(s1["gated"], 1)
                        act.wait_ge(s1["gated"], 2 * d + 1)
                        act.activation(xc[:, 1, d, :].rearrange("p (w h) -> p h w", h=H),
                                       xc[:, 0, d, :].rearrange("p (h w) -> p h w", w=W), ACT.Copy).then_inc(s1["gated"], 1)

                @block.vector
                def _(dve):
                    ch = Chain(dve, s1["conv_own"])
                    for d in range(D2):
                        dve.wait_ge(s1["padded"], NCH * (d + 1))
                        out = y[:, d, :].rearrange("p (h w) -> p h w", w=W)
                        for t in range(9):
                            tap = xpad[:, d, t // 3:t // 3 + H, t % 3:t % 3 + W]
                            if t == 0:
                                ch.link(dve.tensor_scalar(out, tap, convw[:, d, 0:1], None, ALU.mult))
                            else:
                                ins = dve.scalar_tensor_tensor(out, tap, convw[:, d, t:t + 1], out, ALU.mult, ALU.add)
                                if t < 8:
                                    ch.link(ins)
                        ins.then_inc(s1["conv_done"], 1)
                    for d in range(D2):
                        dve.wait_ge(s1["gated"], 2 * d + 1)
                        ins = dve.tensor_scalar(y[:, d, :], xc[:, 0, d, :], dsum[:, d:d + 1], None, ALU.mult)
            s1.clear()

            for k in range(4):
                for half in ((0, 1) if k < 2 else (1, 0)):
                    scan_section(nc, s2, k, half, half == (0 if k < 2 else 1), held)
                    s2.clear()

            norm_gate_project(nc, s3, b, held)
            s3.clear()
        for s in (s1, s2, s3):
            s.release()


def scan_section(nc, s, k, half, first, v):
    ps, xc, y, xpw, dtw, dtb, a_neg, sel, zero, ident = (v[n] for n in "ps xc y xpw dtw dtb a_neg sel zero ident".split())
    decay, drive, hid, rep, dt, dtu = (v[n] for n in "decay drive hid rep dt dtu".split())
    bc3, rest, mid, dtr, last = (v[n] for n in "bc3 rest mid dtr last".split())
    lo = half * L2
    src = xc[:, k % 2, :, lo:lo + L2]
    step = -1 if k >= 2 else 1
    R = R_ORDER
    acc = ps[:, 0:6, 0:R]
    bank = ps[:, 6:8, 0:R]

    with nc.Block() as block:
        @block.tensor
        def _(pe):
            for c in range(SC):
                if c >= 2:
                    pe.wait_ge(s["split"], c - 1)
                    pe.wait_ge(s["dtr_ready"], c - 1)
                for d in range(D2):
                    ins = pe.matmul(bank[0:40, c % 2, :], xpw[:, d, k, :], src[:, d, c * R:(c + 1) * R], start=d == 0, stop=d == 1)
                ins.then_inc(s["xdbl"], 1)
            pe.wait_ge(s["dtr_ready"], SC)
            pe.wait_ge(s["split"], SC)
            for m in range(2 * SC):
                d, c = m // SC, m % SC
                if m >= 2:
                    pe.wait_ge(s["bank_free"], m - 1)
                pe.matmul(bank[:, m % 2, :], dtw[:, k, d * P:(d + 1) * P], dtr[:, c * R:(c + 1) * R], start=True, stop=True).then_inc(s["dts"], 1)
            for m in range(6):
                pe.matmul(acc[:, m, :], sel[:, 0, :], zero[0:96, :], start=True, stop=False, skip_group_check=True)
            pe.wait_ge(s["prep"], 1)

            def rep_state(n, u):
                for m in range(6):
                    pe.wait_ge(s["bank_free"], n * 6 + (2 * SC + m - 1))
                    pe.matmul(bank[:, m % 2, :], sel[:, bass.ds(n + 16 * (m // 3), 1), :].rearrange("p a c -> p (a c)"),
                              bc3[:, (m % 3) * R:(m % 3 + 1) * R], start=True, stop=True).then_inc(s["rep_banks"], 1)

            def sum_state(n, u):
                for d in range(D2):
                    pe.wait_ge(s["weighted"], n * 2 + (d + 1))
                    for c in range(SC):
                        ins = pe.matmul(acc[:, d * SC + c, :], ident[:, :], hid[:, u, d, c * R:(c + 1) * R], start=False, stop=False, skip_group_check=True)
                    ins.then_inc(s["summed"], 1)

            rep_state(0, 0)
            rep_state(1, 1)
            with pe.Fori(0, NST // 2 - 1) as i:
                for u in range(2):
                    rep_state(i * 2 + (u + 2), u)
                    sum_state(i * 2 + u, u)
            sum_state(NST - 2, 0)
            sum_state(NST - 1, 1)
            for m in range(6):
                ins = pe.matmul(acc[:, m, :], sel[:, 0, :], zero[0:96, :], start=False, stop=True, skip_group_check=True)
            ins.then_inc(s["summed"], 1)

        @block.scalar
        def _(act):
            for c in range(SC):
                act.wait_ge(s["xdbl"], c + 1)
                act.activation(dtr[:, c * R:(c + 1) * R], bank[32:40, c % 2, :], ACT.Copy).then_inc(s["dtr_ready"], 1)
            for m in range(2 * SC):
                d, c = m // SC, m % SC
                act.wait_ge(s["dts"], m + 1)
                act.activation(decay[:, d, c * R:(c + 1) * R], bank[:, m % 2, :], ACT.Abs, bias=dtb[:, k, d:d + 1])
                act.activation(dt[:, d, c * R:(c + 1) * R], bank[:, m % 2, :], ACT.Relu, bias=dtb[:, k, d:d + 1]).then_inc(s["bank_free"], 1)
            act.wait_ge(s["bank_free"], 2 * SC)
            act.activation(decay, decay, ACT.Exp, scale=-1.0).then_inc(s["own_act"], 1)
            act.wait_ge(s["own_act"], 1)
            act.activation(decay, decay, ACT.Ln, bias=1.0).then_inc(s["soft"], 1)
            act.wait_ge(s["dt_ready"], 1)

            def rep_store(n, u):
                for m in range(6):
                    if m % 3 == 0 and (not isinstance(n, int) or n >= 2):
                        act.wait_ge(s["weighted" if m else "scanned"], n * 2 - 2)
                    act.wait_ge(s["rep_banks"], n * 6 + (m + 1))
                    act.activation(rep[:, u, m // 3, (m % 3) * R:(m % 3 + 1) * R], bank[:, m % 2, :], ACT.Copy).then_inc(s["bank_free"], 1)

            def decays(n, u):
                for d in range(D2):
                    if not isinstance(n, int) or n >= 1:
                        act.wait_ge(s["scanned"], n * 2 + (d - 1))
                    act.activation(decay[:, d, :], dt[:, d, :], ACT.Exp, scale=a_neg[:, k, d, bass.ds(n, 1)]).then_inc(s["decay_ready"], 1)

            for n in range(2):
                rep_store(n, n)
                decays(n, n)
            with act.Fori(1, NST // 2) as i:
                for u in range(2):
                    rep_store(i * 2 + u, u)
                    decays(i * 2 + u, u)

        @block.vector
        def _(dve):
            ch = Chain(dve, s["own"])
            if first:
                ch.link(dve.memset(last[:, :, :], 0.0))
            for c in range(SC):
                at = slice(c * R, (c + 1) * R)
                dve.wait_ge(s["xdbl"], c + 1)
                ch.link(dve.tensor_copy(bc3[0:32, at], bank[0:32, c % 2, :]))
                dve.tensor_tensor(rest[:, at], bank[0:32, c % 2, :], bc3[0:32, at], ALU.subtract).then_inc(s["split"], 1)
            dve.wait_ge(s["split"], SC)
            ch.link(dve.tensor_copy(mid[:, :], rest[:, :]))
            ch.link(dve.tensor_copy(bc3[32:64, :], mid[:, :]))
            dve.tensor_tensor(bc3[64:96, :], rest[:, :], mid[:, :], ALU.subtract).then_inc(s["prep"], 1)
            dve.wait_ge(s["soft"], 1)
            ch.link(dve.tensor_tensor(dt, dt, decay, ALU.add))
            dve.tensor_tensor(dtu, dt, src, ALU.mult).then_inc(s["dt_ready"], 1)
            dve.wait_ge(s["dt_ready"], 1)

            def scan_state(n, u):
                for d in range(D2):
                    dve.wait_ge(s["bank_free"], n * 6 + (2 * SC + 3))
                    ch.link(dve.tensor_tensor(drive[:, d, :], dtu[:, d, :], rep[:, u, 0, :], ALU.mult))
                    dve.wait_ge(s["decay_ready"], n * 2 + (d + 1))
                    if not isinstance(n, int) or n >= 2:
                        dve.wait_ge(s["summed"], n * 2 + (d - 3))
                    dve.tensor_tensor_scan(hid[:, u, d, ::step], decay[:, d, ::step], drive[:, d, ::step],
                                           last[:, d, bass.ds(n, 1)], ALU.mult, ALU.add).then_inc(s["own"], 1)
                    ch.n += 1
                    dve.wait_ge(s["own"], ch.base + ch.n)
                    end = 0 if step < 0 else L2 - 1
                    dve.tensor_scalar(last[:, d, bass.ds(n, 1)], hid[:, u, d, end:end + 1], 1.0, None, ALU.mult).then_inc(s["scanned"], 1)

            for n in range(2):
                scan_state(n, n)
            per = 8
            with dve.Fori(1, NST // 2) as i:
                ch.enter(i - 1, per)
                for u in range(2):
                    scan_state(i * 2 + u, u)
            ch.leave(NST // 2 - 1)
            dve.wait_ge(s["summed"], 2 * NST + 1)
            for d in range(D2):
                for c in range(SC):
                    src_c = acc[:, d * SC + c, :].rearrange("p (a b) -> p a b", b=48)
                    if k % 2 == 0:
                        out = y[:, d, lo + c * R:lo + (c + 1) * R].rearrange("p (a b) -> p a b", b=48)
                    else:
                        w0 = (lo + c * R) // 48
                        out = y[:, d, :].rearrange("p (h w) -> p w h", w=W)[:, w0:w0 + 8, :]
                    dve.tensor_tensor(out, out, src_c, ALU.add)

        @block.gpsimd
        def _(pool):
            def weigh(n, u):
                pool.wait_ge(s["bank_free"], n * 6 + (2 * SC + 6))
                for d in range(D2):
                    pool.wait_ge(s["scanned"], n * 2 + (d + 1))
                    pool.tensor_tensor(hid[:, u, d, :], hid[:, u, d, :], rep[:, u, 1, :], ALU.mult).then_inc(s["weighted"], 1)
            with pool.Fori(0, NST // 2) as i:
                for u in range(2):
                    weigh(i * 2 + u, u)


def norm_gate_project(nc, s, b, v):
    ps, y, xb, over, eps, ng, nb, win, wout, XT, x_out = (v[n] for n in "ps y xb over eps ng nb win wout XT x_out".split())
    sq, sd, sz = v["sq"], v["sd"], v["sz"]
    R = R_ORDER
    flat = ps[:, 0:NCH, 0:R]

    def chunks(ap):
        return ap.rearrange("p (n r) -> p n r", r=R)

    with nc.Block() as block:
        @block.tensor
        def _(pe):
            for c in range(NCH):
                for d in range(D2):
                    ins = pe.matmul(flat[:, c, :], over[:, :], y[:, d, c * R:(c + 1) * R], start=d == 0, stop=d == 1)
            ins.then_inc(s["mean"], 1)
            pe.wait_ge(s["squared"], D2)
            for c in range(NCH):
                for d in range(D2):
                    ins = pe.matmul(flat[:, c, :], over[:, :], sq[:, d, c * R:(c + 1) * R], start=d == 0, stop=d == 1)
            ins.then_inc(s["varied"], 1)
            for d in range(D2):
                pe.wait_ge(s["sd_ready"], 1)
                if d:
                    pe.wait_ge(s["zgated"], 1)
                for c in range(NCH):
                    ins = pe.matmul(flat[:, c, :], win[:, (2 + d) * P:(3 + d) * P], XT[:, bass.ds(b * S + c * R, R)], start=True, stop=True)
                ins.then_inc(s["zed"], 1)
            pe.wait_ge(s["zgated"], 2)
            pe.wait_ge(s["gated"], 2)
            for n in range(18):
                for d in range(D2):
                    ins = pe.matmul(ps[:, n // 4, (n % 4) * P:(n % 4 + 1) * P], y[:, d, n::18], wout[:, d, :], start=d == 0, stop=d == 1)
            ins.then_inc(s["summed"], 1)

        @block.vector
        def _(dve):
            ch = Chain(dve, s["own"])
            dve.wait_ge(s["mean"], 1)
            for d in range(D2):
                dve.tensor_tensor(chunks(y[:, d, :]), chunks(y[:, d, :]), flat, ALU.subtract).then_inc(s["centred"], 1)
            dve.wait_ge(s["sd_ready"], 1)
            ch.link(dve.reciprocal(sd, sd))
            for d in range(D2):
                dve.tensor_tensor(y[:, d, :], y[:, d, :], sd, ALU.mult).then_inc(s["normed"], 1)
            for d in range(D2):
                dve.wait_ge(s["zgated"], d + 1)
                dve.wait_ge(s["affine"], d + 1)
                dve.tensor_tensor(y[:, d, :], y[:, d, :], sz[:, d, :], ALU.mult).then_inc(s["gated"], 1)
            dve.wait_ge(s["summed"], 1)
            for n in range(5):
                m = min(4, 18 - 4 * n)
                out = xb[:, 4 * n:4 * n + m, :]
                ins = dve.tensor_tensor(out, out, ps[:, n, 0:m * P].rearrange("p (n c) -> p n c", c=C), ALU.add)
                ins.then_inc(s["stored"], 1)

        @block.scalar
        def _(act):
            for d in range(D2):
                act.wait_ge(s["centred"], d + 1)
                act.activation(sq[:, d, :], y[:, d, :], ACT.Square).then_inc(s["squared"], 1)
            act.wait_ge(s["varied"], 1)
            act.activation(chunks(sd), flat, ACT.Sqrt, bias=eps[:, :]).then_inc(s["sd_ready"], 1)
            for d in range(D2):
                act.wait_ge(s["zed"], d + 1)
                act.activation(chunks(sz[:, d, :]), flat, ACT.Silu).then_inc(s["zgated"], 1)
            for d in range(D2):
                act.wait_ge(s["normed"], d + 1)
                act.activation(y[:, d, :], y[:, d, :], ACT.Identity, scale=ng[:, d:d + 1], bias=nb[:, d:d + 1]).then_inc(s["affine"], 1)

        @block.sync
        def _(sp):
            sp.wait_ge(s["stored"], 5)
            sp.dma_start(x_out[bass.ds(b * S, S), :].rearrange("(p n) c -> p (n c)", p=P), xb[:, :, :].rearrange("p n c -> p (n c)")).then_inc(s["mean"], 16)
            sp.wait_ge(s["mean"], 17)


def spread(ap, n):
    return bass.AP(ap.tensor, 0, [[0, P], [1, n]])


def add_channel_major(nc, name, X, Y, ident):
    with ExitStack() as ctx:
        stage = ctx.enter_context(nc.sbuf_tensor(name + "_stage", [P, 2, 4, P], F32))
        ps = ctx.enter_context(nc.psum_tensor(name + "_ps", [P, 2, 512], F32))
        s = Signals(nc, name, "staged turned added")
        with nc.Block() as block:
            @block.scalar
            def _(act):
                with act.Fori(0, G // 4) as i:
                    for u in range(2):
                        act.wait_ge(s["turned"], i * 2 + (u + 1))
                        act.activation(stage[:, u, :, :].rearrange("c (g t) p -> c t g p", t=2),
                                       Y[:, :, bass.ds((i * 4 + 2 * u) * P, 2 * P)].rearrange("c t (g p) -> c t g p", p=P),
                                       ACT.Copy).then_inc(s["staged"], 1)

            @block.tensor
            def _(pe):
                pe.sem_inc(s["turned"], 2)
                with pe.Fori(0, G // 4) as i:
                    for u in range(2):
                        pe.wait_ge(s["staged"], i * 2 + (u + 1))
                        pe.wait_ge(s["added"], i * 2 + (u + 1))
                        for t in range(4):
                            ins = pe.transpose(ps[:, u, t * P:(t + 1) * P], stage[:, u, t, :], ident[:, :])
                        ins.then_inc(s["turned"], 1)

            @block.vector
            def _(dve):
                dve.sem_inc(s["added"], 2)
                with dve.Fori(0, G // 4) as i:
                    for u in range(2):
                        dve.wait_ge(s["turned"], i * 2 + (u + 3))
                        out = X[:, bass.ds(i * 4 + 2 * u, 2), :, :].rearrange("p g t c -> p (g t c)")
                        dve.tensor_tensor(out, out, ps[:, u, :], ALU.add).then_inc(s["added"], 1)
        s.end()


NK = 16
CW = 384
NCW = HALF // CW
NEDGE = 4


def pieces(c):
    at, ends = c * CW, [HALF // 8, HALF // 4, HALF // 2, HALF]
    return [(max(lo, at) - at, min(hi, at + CW) - at, seg) for seg, (lo, hi) in enumerate(zip([0] + ends, ends)) if lo < at + CW and hi > at]


def spectral_unit(nc, x_dram, out_dram, w):
    def tokens(ap):
        return ap.rearrange("(g p t) c -> p g t c", p=P, t=2)

    with ExitStack() as ctx:
        def sb(name, shape, dt=F32):
            return ctx.enter_context(nc.sbuf_tensor("stu_" + name, shape, dt))

        ident = sb("ident", [P, P])
        wgt = sb("wgt", [P, NEDGE])
        wk = sb("wk", [P, NK, NEDGE])
        YT = sb("YT", [P, 2, G * P])
        with nc.sbuf_tensor("stu_u_high", [P, G, 2, C], F32R) as u_high, nc.sbuf_tensor("stu_u_low", [P, G, 2, C], F32R) as u_low:
            with nc.sbuf_tensor("stu_u", [P, G, 2, C], F32) as U:
                with nc.sbuf_tensor("stu_x", [P, G, 2, C], F32) as X:
                    load_all(nc, "stu_load", [(ident[:, :], w["ident"]), (X[:, :, :, :], tokens(x_dram))])
                    layer_norm(nc, "stu_ln", X, U, 1e-5)
                with nc.sbuf_tensor("stu_XT", [P, 2, G * P], F32) as XT:
                    transpose_tokens(nc, "stu_tr", U, lambda g: XT[:, :, bass.ds(g * P, P)], ident)
                    branch_weights(nc, w, wgt, wk)
                    autoregress(nc, w, XT, YT, wgt, U, u_high, u_low)
            convolve(nc, w, u_high, u_low, YT, wk)
        with nc.sbuf_tensor("stu_sum", [P, G, 2, C], F32) as X:
            load_all(nc, "stu_again", [(X[:, :, :, :], tokens(x_dram))])
            add_channel_major(nc, "stu_add", X, YT, ident)
            load_all(nc, "stu_store", [(tokens(out_dram), X[:, :, :, :])])


def branch_weights(nc, w, wgt, wk):
    with ExitStack() as ctx:
        def sb(name, shape):
            return ctx.enter_context(nc.sbuf_tensor("bw_" + name, shape, F32))
        lw, gum, sig, e = sb("lw", [P, 4]), sb("gum", [P, 4]), sb("sig", [P, NK]), sb("e", [P, 4])
        mx, total, hard, count = sb("mx", [P, 1]), sb("total", [P, 1]), sb("hard", [P, 4]), sb("count", [P, 4])
        ones = sb("ones", [P, 4])
        load_all(nc, "bw_load", [(lw[:, :], spread(w["log_weights"], 4)), (gum[:, :], spread(w["gumbel"], 4)),
                                 (sig[:, :], spread(w["sigma"], NK))])
        s = Signals(nc, "bw", "own max_ready exp_ready root")
        with nc.Block() as block:
            @block.vector
            def _(dve):
                ch = Chain(dve, s["own"])
                dve.memset(ones[:, :], 1.0)
                ch.link(dve.tensor_tensor(lw[:, :], lw[:, :], gum[:, :], ALU.add))
                dve.tensor_reduce(mx[:, :], lw[:, :], AX.X, ALU.max, negate=True).then_inc(s["max_ready"], 1)
                dve.wait_ge(s["exp_ready"], 1)
                ch.link(dve.reciprocal(total[:, :], total[:, :]))
                ch.link(dve.tensor_scalar(e[:, :], e[:, :], total[:, :], None, ALU.mult))
                ch.link(dve.tensor_reduce(mx[:, :], e[:, :], AX.X, ALU.max))
                ch.link(dve.tensor_scalar(hard[:, :], e[:, :], mx[:, :], None, ALU.is_equal))
                ch.link(dve.tensor_tensor_scan(count[:, :], ones[:, :], hard[:, :], 0.0, ALU.mult, ALU.add))
                ch.link(dve.tensor_scalar(count[:, :], count[:, :], 1.0, None, ALU.is_equal))
                ch.link(dve.tensor_tensor(hard[:, :], hard[:, :], count[:, :], ALU.mult))
                ch.link(dve.tensor_tensor(wgt[:, :], hard[:, :], e[:, :], ALU.subtract))
                ch.link(dve.tensor_tensor(wgt[:, :], wgt[:, :], e[:, :], ALU.add))
                dve.wait_ge(s["root"], 2)
                for n in range(NEDGE):
                    dve.tensor_scalar(wk[:, :, n], sig[:, :], wgt[:, n:n + 1], None, ALU.mult)

            @block.scalar
            def _(act):
                act.wait_ge(s["max_ready"], 1)
                act.activation(e[:, :], lw[:, :], ACT.Exp, bias=mx[:, :], accum_out=total[:, :]).then_inc(s["exp_ready"], 1)
                act.activation(sig[:, :], sig[:, :], ACT.Sqrt).then_inc(s["root"], 1)
                act.wait_ge(s["root"], 1)
                act.activation(sig[:, :], sig[:, :], ACT.Sqrt).then_inc(s["root"], 1)
        s.end()


def autoregress(nc, w, XT, YT, wgt, U, u_high, u_low):
    with ExitStack() as ctx:
        mu = ctx.enter_context(nc.sbuf_tensor("ar_mu", [P, 3, NEDGE, P], F32))
        eff = ctx.enter_context(nc.sbuf_tensor("ar_eff", [P, 3, NEDGE, P], F32))
        ps = ctx.enter_context(nc.psum_tensor("ar_ps", [P, 8, 512], F32))
        load_all(nc, "ar_load", [(mu[:, n, :, :], w["M_u"][n]) for n in range(3)])
        s = Signals(nc, "ar", "own ready made kept cut")
        with nc.Block() as block:
            @block.gpsimd
            def _(pool):
                pool.wait_ge(s["cut"], 1)
                pool.tensor_tensor(u_low[:, 0:G // 2, :, :], U[:, 0:G // 2, :, :], u_high[:, 0:G // 2, :, :], ALU.subtract)

            @block.vector
            def _(dve):
                ch = Chain(dve, s["own"])
                ch.link(dve.tensor_scalar(eff[:, :, 3, :], mu[:, :, 0, :], wgt[:, 0:1], None, ALU.mult))
                for n in (1, 2, 3):
                    ch.link(dve.scalar_tensor_tensor(eff[:, :, 3 - n, :], mu[:, :, n, :], wgt[:, n:n + 1], eff[:, :, 4 - n, :], ALU.mult, ALU.add))
                dve.sem_inc(s["ready"], 1)
                dve.wait_ge(s["cut"], 1)
                dve.tensor_tensor(u_low[:, G // 2:, :, :], U[:, G // 2:, :, :], u_high[:, G // 2:, :, :], ALU.subtract)

            @block.tensor
            def _(pe):
                pe.wait_ge(s["ready"], 1)
                with pe.Fori(0, B) as b:
                    for n in range(2 * NCW):
                        q, c = n % 2, n // 2
                        pe.wait_ge(s["kept"], b * (2 * NCW) + (n + 1))
                        for lo, hi, seg in pieces(c):
                            for back in range(3):
                                parity, shift = (q - back) % 2, -((q - back) // 2)
                                skip = shift if c == 0 and lo == 0 else 0
                                at = b * HALF + (c * CW + lo - shift + skip)
                                ins = pe.matmul(ps[:, n, lo + skip:hi], eff[:, back, seg, :],
                                                XT[:, parity, bass.ds(at, hi - lo - skip)],
                                                start=back == 0, stop=back == 2, skip_group_check=True)
                        ins.then_inc(s["made"], 1)

            @block.scalar
            def _(act):
                act.activation(u_high[:, :, :, :], U[:, :, :, :], ACT.Copy).then_inc(s["cut"], 1)
                act.sem_inc(s["kept"], 2 * NCW)
                with act.Fori(0, B) as b:
                    for n in range(2 * NCW):
                        act.wait_ge(s["made"], b * (2 * NCW) + (n + 1))
                        act.activation(YT[:, n % 2, bass.ds(b * HALF + (n // 2) * CW, CW)], ps[:, n, 0:CW], ACT.Copy).then_inc(s["kept"], 1)
        s.end()


def convolve(nc, w, u_high, u_low, YT, wk):
    UNITS = B * NCW * 2
    with ExitStack() as ctx:
        def sb(name, shape):
            return ctx.enter_context(nc.sbuf_tensor("cv_" + name, shape, F32))
        def sbr(name, shape):
            return ctx.enter_context(nc.sbuf_tensor("cv_" + name, shape, F32R))
        even, odd = sb("even", [P, HALF]), sb("odd", [P, HALF + 1])
        mp, mm = sb("mp", [P, 2, NEDGE, P]), sb("mm", [P, 2, NEDGE, P])
        even_high, odd_high = sbr("even_high", [P, 2, HALF]), sbr("odd_high", [P, 2, HALF + 1])
        even_low, odd_low = sbr("even_low", [P, 2, HALF]), sbr("odd_low", [P, 2, HALF + 1])
        total = sb("total", [P, NEDGE, P])
        one = sb("one", [P, 1])
        eff = sb("eff", [P, 2, NEDGE, P])
        eff_high, eff_low = sbr("eff_high", [P, 2, 2, NEDGE, P]), sbr("eff_low", [P, 2, 2, NEDGE, P])
        uk_high, uk_low = sbr("uk_high", [P, 3, 2, CW]), sbr("uk_low", [P, 3, 2, CW])
        ps = ctx.enter_context(nc.psum_tensor("cv_ps", [P, 8, 512], F32))
        s = Signals(nc, "cv", "filter0 filter1 matrix0 matrix1 filter_used matrix_used eff_ready own convolved kept lowered mixed added filter_halved filter_split filled")
        filt, matr = (s["filter0"], s["filter1"]), (s["matrix0"], s["matrix1"])
        rows = P + HALF
        units = [(b, c, q) for b in range(B) for c in reversed(range(NCW)) for q in range(2)]

        with nc.Block() as block:
            @block.sync
            def _(sp):
                with sp.Fori(0, NK // 2) as i:
                    for u in range(2):
                        k = i * 2 + u
                        sp.wait_ge(s["filter_split"], k * 2 + 2)
                        sp.dma_start(even[:, :], bass.AP(w["phi_even"].tensor, k * rows, [[1, P], [1, HALF]])).then_inc(filt[u], 16)
                        sp.dma_start(odd[:, :], bass.AP(w["phi_odd"].tensor, k * rows, [[1, P], [1, HALF + 1]])).then_inc(filt[u], 16)
                        sp.wait_ge(s["matrix_used"], k + 1)
                        sp.dma_start(mp[:, u, :, :].rearrange("d n e -> d (n e)"), w["M_plus"][bass.ds(k, 1)].rearrange("k d n e -> (k d) (n e)")).then_inc(matr[u], 16)
                        sp.dma_start(mm[:, u, :, :].rearrange("d n e -> d (n e)"), w["M_minus"][bass.ds(k, 1)].rearrange("k d n e -> (k d) (n e)")).then_inc(matr[u], 16)

            @block.tensor
            def _(pe):
                pe.sem_inc(s["filter_used"], 2)
                pe.sem_inc(s["mixed"], 3)
                with pe.Fori(0, NK // 2) as i:
                    for u in range(2):
                        k = i * 2 + u
                        pe.wait_ge(s["filter_split"], k * 2 + 4)

                        def conv(n):
                            b, c, q = units[n]
                            pe.wait_ge(s["kept"], k * UNITS + (n + 1))
                            pe.wait_ge(s["lowered"], k * UNITS + (n + 1))
                            blocks = [g for g in range(GB) if g * P < (c + 1) * CW]
                            for kind in range(2):
                                for g in blocks:
                                    off = max(0, g * P - c * CW)
                                    lag = c * CW + off - g * P
                                    filters = ((even_high, even_low), (odd_high, odd_low))[kind]
                                    from_, parity = (lag, q) if kind == 0 else (lag + q, 1 - q)
                                    for turn, (a, f) in enumerate(((0, 0), (0, 1), (1, 0))):
                                        ins = pe.matmul(ps[:, 2 * (n % 3) + kind, off:CW], (u_high, u_low)[a][:, b * GB + g, parity, :],
                                                        filters[f][:, u, ::-1][:, from_:from_ + CW - off],
                                                        start=g == 0 and turn == 0, stop=g == blocks[-1] and turn == 2, skip_group_check=True)
                            ins.then_inc(s["convolved"], 1)

                        def mix(n):
                            b, c, q = units[n]
                            if n == 0:
                                pe.wait_ge(s["eff_ready"], k + 1)
                            pe.wait_ge(s["kept"], k * UNITS + (n + 4))
                            pe.wait_ge(s["lowered"], k * UNITS + (n + 4))
                            pe.wait_ge(s["added"], k * UNITS + (n + 1))
                            for lo, hi, seg in pieces(c):
                                for kind in range(2):
                                    for turn, (m, x) in enumerate(((eff_high, uk_high), (eff_high, uk_low), (eff_low, uk_high))):
                                        ins = pe.matmul(ps[:, 6 + n % 2, lo:hi], m[:, u, kind, seg, :], x[:, n % 3, kind, lo:hi],
                                                        start=kind == 0 and turn == 0, stop=kind == 1 and turn == 2, skip_group_check=True)
                            ins.then_inc(s["mixed"], 1)
                            return ins

                        for n in range(UNITS):
                            conv(n)
                            if n >= 2:
                                mix(n - 2)
                        mix(UNITS - 2)
                        mix(UNITS - 1)
                        pe.wait_ge(s["mixed"], k * UNITS + (UNITS + 3))
                        pe.sem_inc(s["filter_used"], 1)

            @block.scalar
            def _(act):
                act.sem_inc(s["kept"], 3)
                with act.Fori(0, NK) as k:
                    for n in range(UNITS):
                        act.wait_ge(s["convolved"], k * UNITS + (n + 1))
                        act.wait_ge(s["mixed"], k * UNITS + (n + 1))
                        at = 2 * (n % 3)
                        act.activation(uk_high[:, n % 3, :, :], ps[:, at:at + 2, 0:CW], ACT.Copy).then_inc(s["kept"], 1)

            @block.gpsimd
            def _(pool):
                pool.memset(one[:, :], 1.0).then_inc(s["filled"], 1)
                pool.wait_ge(s["filled"], 1)
                pool.sem_inc(s["filter_split"], 2)
                with pool.Fori(0, NK // 2) as i:
                    for u in range(2):
                        k = i * 2 + u
                        pool.wait_ge(filt[u], i * 32 + 32)
                        pool.wait_ge(s["filter_used"], k + 1)
                        for n, (raw, high, low) in enumerate(((even, even_high, even_low), (odd, odd_high, odd_low))):
                            pool.tensor_tensor(high[:, u, :], raw[:, :], bc(one[:, :], [P, HALF + n]), ALU.mult).then_inc(s["filter_halved"], 1)
                            pool.wait_ge(s["filter_halved"], k * 2 + (n + 1))
                            pool.tensor_tensor(low[:, u, :], raw[:, :], high[:, u, :], ALU.subtract).then_inc(s["filter_split"], 1)

            @block.vector
            def _(dve):
                dve.sem_inc(s["matrix_used"], 2)
                dve.sem_inc(s["added"], 2)
                dve.sem_inc(s["lowered"], 3)
                ch = Chain(dve, s["own"])

                def sum_matrices(step, k, slot, loads):
                    both = tuple(enumerate((total[:, :, :], mm[:, slot, :, :])))
                    if step == 0:
                        dve.wait_ge(matr[slot], loads)
                        dve.wait_ge(s["filter_used"], k + 1)
                        dve.tensor_tensor(total[:, :, :], mp[:, slot, :, :], mm[:, slot, :, :], ALU.add)
                        ch.link(dve.tensor_tensor(mm[:, slot, :, :], mp[:, slot, :, :], mm[:, slot, :, :], ALU.subtract))
                    elif step == 1:
                        for kind, m in both:
                            ins = dve.tensor_scalar(eff[:, kind, 3, :], m[:, 0, :], wk[:, bass.ds(k, 1), 0], None, ALU.mult)
                        ch.link(ins)
                    elif step <= 4:
                        n = step - 1
                        for kind, m in both:
                            ins = dve.scalar_tensor_tensor(eff[:, kind, 3 - n, :], m[:, n, :], wk[:, bass.ds(k, 1), n],
                                                           eff[:, kind, 4 - n, :], ALU.mult, ALU.add)
                        ch.link(ins)
                    elif step == 5:
                        ch.link(dve.tensor_copy(eff_high[:, slot, :, :, :], eff[:, :, :, :]))
                    else:
                        ch.link(dve.tensor_tensor(eff_low[:, slot, :, :, :], eff[:, :, :, :], eff_high[:, slot, :, :, :], ALU.subtract))
                        dve.sem_inc(s["eff_ready"], 1)
                        dve.sem_inc(s["matrix_used"], 1)

                def add_units(k, u, following):
                    def lower(n):
                        dve.wait_ge(s["kept"], k * UNITS + (n + 4))
                        at = 2 * (n % 3)
                        dve.tensor_tensor(uk_low[:, n % 3, :, :], ps[:, at:at + 2, 0:CW], uk_high[:, n % 3, :, :], ALU.subtract).then_inc(s["lowered"], 1)

                    dve.wait_ge(s["added"], k * UNITS + 2)
                    lower(0)
                    lower(1)
                    for n in range(UNITS):
                        if n + 2 < UNITS:
                            lower(n + 2)
                        b, c, q = units[n]
                        dve.wait_ge(s["mixed"], k * UNITS + (n + 4))
                        out = YT[:, q, b * HALF + c * CW:b * HALF + (c + 1) * CW]
                        dve.tensor_tensor(out, out, ps[:, 6 + n % 2, 0:CW], ALU.add).then_inc(s["added"], 1)
                        if following is not None and n >= 8 and n % 2 == 0 and (n - 8) // 2 < 7:
                            sum_matrices((n - 8) // 2, k + 1, 1 - u, following)

                for step in range(7):
                    sum_matrices(step, 0, 0, 32)
                with dve.Fori(0, NK // 2 - 1) as i:
                    ch.enter(i, 14)
                    add_units(i * 2, 0, i * 32 + 32)
                    add_units(i * 2 + 1, 1, i * 32 + 64)
                ch.leave(NK // 2 - 1)
                add_units(NK - 2, 0, (NK // 2) * 32)
                add_units(NK - 1, 1, None)
        s.end()


NF = H // 2 + 1
NR = B * H
NW = 5


def fourier_mixer(nc, X, xn_dram, w):
    with ExitStack() as ctx:
        def sb(name, shape, dt=F32):
            return ctx.enter_context(nc.sbuf_tensor("ff_" + name, shape, dt))

        with nc.sbuf_tensor("ff_xn", [P, G, 2, C], F32) as XN:
            layer_norm(nc, "ff_ln", X, XN, 1e-6)
            load_all(nc, "ff_store", [(xn_dram.rearrange("(g p t) c -> p g t c", p=P, t=2), XN[:, :, :, :])])
        ident = sb("ident", [P, P])
        dft = sb("dft", [W, 3 * NF])
        idft = sb("idft", [2 * NF, W])
        HT = sb("HT", [P, T])
        load_all(nc, "ff_load", [(ident[:, :], w["ident"]), (dft[:, :], w["dft"]), (idft[:, :], w["idft"])])
        with nc.sbuf_tensor("ff_mx", [P, NR, 2 * NF], F32) as mixed:
            for axis in range(2):
                with nc.sbuf_tensor(f"ff_fx{axis}", [P, 3, NF, NR], F32) as spectrum:
                    transform_rows(nc, f"ffa{axis}", axis, xn_dram, dft, spectrum)
                    mix_modes(nc, f"ffb{axis}", w["fw"][axis], spectrum, mixed)
                inverse_rows(nc, f"ffc{axis}", axis, idft, ident, mixed, HT)
        row_mlp(nc, w, HT, X)


def transform_rows(nc, name, axis, xn_dram, dft, spectrum):
    with ExitStack() as ctx:
        rows = ctx.enter_context(nc.sbuf_tensor(name + "_rows", [W, H, C], F32))
        ps = ctx.enter_context(nc.psum_tensor(name + "_ps", [P, 8, 512], F32))
        s = Signals(nc, name, "loaded made kept")
        flat = spectrum[:, :, :, :].rearrange("c m f r -> c (m f) r")
        with nc.Block() as block:
            @block.sync
            def _(sp):
                for b in range(B):
                    if b:
                        sp.wait_ge(s["made"], 8 * b)
                    img = xn_dram[b * S:(b + 1) * S, :]
                    src = img.rearrange("(h w) c -> w h c", w=W) if axis == 0 else img.rearrange("(h w) c -> h w c", w=W)
                    sp.dma_start(rows[:, :, :], src).then_inc(s["loaded"], 16)

            @block.tensor
            def _(pe):
                with pe.Fori(0, B) as b:
                    pe.wait_ge(s["loaded"], b * 16 + 16)
                    for n in range(8):
                        pe.wait_ge(s["kept"], b * 8 + (n + 1))
                        for r in range(6):
                            ins = pe.matmul(ps[:, n, r * 3 * NF:(r + 1) * 3 * NF], rows[:, 6 * n + r, :], dft[:, :], start=True, stop=True)
                        ins.then_inc(s["made"], 1)

            @block.scalar
            def _(act):
                act.sem_inc(s["kept"], 8)
                with act.Fori(0, B) as b:
                    for n in range(8):
                        act.wait_ge(s["made"], b * 8 + (n + 1))
                        act.activation(flat[:, :, bass.ds(b * H + 6 * n, 6)],
                                       ps[:, n, 0:18 * NF].rearrange("c (r m) -> c m r", r=6), ACT.Copy).then_inc(s["kept"], 1)
        s.end()


def mix_modes(nc, name, fw, spectrum, mixed):
    with ExitStack() as ctx:
        wt = ctx.enter_context(nc.sbuf_tensor(name + "_w", [P, NW, 2, C], F32))
        ps = ctx.enter_context(nc.psum_tensor(name + "_ps", [P, NW, 512], F32))
        s = Signals(nc, name, " ".join(f"loaded{u}" for u in range(NW)) + " made kept")
        loaded = s.all[:NW]
        with nc.Block() as block:
            @block.sync
            def _(sp):
                with sp.Fori(0, NF // NW) as i:
                    for u in range(NW):
                        sp.wait_ge(s["made"], i * NW + (u + 1))
                        sp.dma_start(wt[:, u, :, :].rearrange("c m o -> c (m o)"), fw[bass.ds((i * NW + u) * P, P), :]).then_inc(loaded[u], 16)

            @block.tensor
            def _(pe):
                pe.sem_inc(s["made"], NW)
                with pe.Fori(0, NF // NW) as i:
                    for u in range(NW):
                        pe.wait_ge(loaded[u], i * 16 + 16)
                        pe.wait_ge(s["kept"], i * NW + (u + 1))
                        for m in range(2):
                            rhs = spectrum[:, 1 - m:3 - m, bass.ds(i * NW + u, 1), :].rearrange("c m f r -> c m (f r)")
                            ins = pe.matmul(ps[:, u, 0:2 * NR].rearrange("c (m r) -> c m r", m=2), wt[:, u, m, :], rhs, start=m == 0, stop=m == 1)
                        ins.then_inc(s["made"], 1)

            @block.vector
            def _(dve):
                dve.sem_inc(s["kept"], NW)
                with dve.Fori(0, NF // NW) as i:
                    for u in range(NW):
                        dve.wait_ge(s["made"], i * NW + (NW + u + 1))
                        out = mixed[:, :, :].rearrange("c r (m f) -> c m f r", m=2)[:, :, bass.ds(i * NW + u, 1), :].rearrange("c m f r -> c m (f r)")
                        dve.tensor_copy(out, ps[:, u, 0:2 * NR].rearrange("c (m r) -> c m r", m=2)).then_inc(s["kept"], 1)
        s.end()


def inverse_rows(nc, name, axis, idft, ident, mixed, HT):
    with ExitStack() as ctx:
        stage = ctx.enter_context(nc.sbuf_tensor(name + "_stage", [P, H, P], F32))
        modes = ctx.enter_context(nc.sbuf_tensor(name + "_modes", [2 * NF, H, C], F32))
        ps = ctx.enter_context(nc.psum_tensor(name + "_ps", [P, 8, 512], F32))
        s = Signals(nc, name, "padded staged turned kept made added")
        with nc.Block() as block:
            @block.gpsimd
            def _(pool):
                pool.memset(stage[:, :, 2 * NF:], 0.0).then_inc(s["padded"], 1)

            @block.scalar
            def _(act):
                act.sem_inc(s["kept"], 2)
                with act.Fori(0, B) as b:
                    act.wait_ge(s["turned"], b * 12 + 1)
                    act.activation(stage[:, :, 0:2 * NF], mixed[:, bass.ds(b * H, H), :], ACT.Copy).then_inc(s["staged"], 1)
                    act.wait_ge(s["made"], b * 6 + 1)
                    for n in range(12):
                        act.wait_ge(s["turned"], b * 12 + (n + 2))
                        act.activation(modes[:, 4 * n:4 * n + 4, :], ps[0:2 * NF, n % 2, :].rearrange("m (r c) -> m r c", c=C), ACT.Copy).then_inc(s["kept"], 1)

            @block.tensor
            def _(pe):
                pe.sem_inc(s["turned"], 1)
                pe.sem_inc(s["made"], 1)
                pe.wait_ge(s["padded"], 1)
                with pe.Fori(0, B) as b:
                    pe.wait_ge(s["staged"], b + 1)
                    for n in range(13):
                        if n < 12:
                            pe.wait_ge(s["kept"], b * 12 + (n + 1))
                            for r in range(4):
                                ins = pe.transpose(ps[:, n % 2, r * P:(r + 1) * P], stage[:, 4 * n + r, :], ident[:, :])
                            ins.then_inc(s["turned"], 1)
                        if n >= 2 and n % 2 == 0:
                            j = n // 2 - 1
                            pe.wait_ge(s["kept"], b * 12 + (2 * j + 4))
                            pe.wait_ge(s["added"], b * 6 + (j + 1))
                            for r in range(8):
                                ins = pe.matmul(ps[:, 2 + j, r * W:(r + 1) * W], modes[:, 8 * j + r, :], idft[:, :], start=True, stop=True)
                            ins.then_inc(s["made"], 1)

            @block.vector
            def _(dve):
                dve.sem_inc(s["added"], 6)
                with dve.Fori(0, B) as b:
                    for j in range(6):
                        dve.wait_ge(s["made"], b * 6 + (j + 2))
                        if axis == 0:
                            dve.tensor_copy(HT[:, bass.ds(b * S + j * 384, 384)], ps[:, 2 + j, 0:384]).then_inc(s["added"], 1)
                        else:
                            out = HT[:, bass.ds(b * S, S)].rearrange("c (h w) -> c w h", w=W)[:, 8 * j:8 * j + 8, :]
                            dve.tensor_tensor(out, out, ps[:, 2 + j, 0:384].rearrange("c (w h) -> c w h", h=H), ALU.add).then_inc(s["added"], 1)
        s.end()


def row_mlp(nc, w, HT, X):
    with ExitStack() as ctx:
        def sb(name, shape):
            return ctx.enter_context(nc.sbuf_tensor("mlp_" + name, shape, F32))
        w1, w2, b1 = sb("w1", [P, 512]), sb("w2", [P, 4, C]), sb("b1", [P, 4])
        ones, (b2,) = bias_rows(nc, ctx, "mlp_b", [w["b2"]])
        hid = sb("hid", [P, 2, 4, 256])
        ps = ctx.enter_context(nc.psum_tensor("mlp_ps", [P, 8, 512], F32))
        load_all(nc, "mlp_load", [(w1[:, :], w["w1"]), (w2[:, :, :], w["w2"]), (b1[:, :], w["b1"])])
        s = Signals(nc, "mlp", "made hid_ready done added")
        with nc.Block() as block:
            @block.tensor
            def _(pe):
                pe.sem_inc(s["done"], 2)
                with pe.Fori(0, G // 2) as i:
                    for u in range(2):
                        pe.wait_ge(s["hid_ready"], i * 2 + (u + 1))
                        for n in range(4):
                            ins = pe.matmul(ps[:, 2 * u + n // 2, (n % 2) * 256:(n % 2) * 256 + 256], w1[:, n * P:(n + 1) * P],
                                            HT[:, bass.ds((i * 2 + u) * 256, 256)], start=True, stop=True)
                        ins.then_inc(s["made"], 1)
                    for u in range(2):
                        pe.wait_ge(s["hid_ready"], i * 2 + (u + 3))
                        pe.wait_ge(s["added"], i * 2 + (u + 1))
                        for t in range(2):
                            for n in range(4):
                                pe.matmul(ps[:, 4 + u, t * C:(t + 1) * C], hid[:, u, n, t::2], w2[:, n, :], start=n == 0, stop=False)
                            ins = pe.matmul(ps[:, 4 + u, t * C:(t + 1) * C], ones[:, :], b2, start=False, stop=True)
                        ins.then_inc(s["done"], 1)

            @block.scalar
            def _(act):
                act.sem_inc(s["hid_ready"], 2)
                with act.Fori(0, G // 2) as i:
                    for u in range(2):
                        act.wait_ge(s["made"], i * 2 + (u + 1))
                        act.wait_ge(s["done"], i * 2 + (u + 1))
                        for n in range(4):
                            ins = act.activation(hid[:, u, n, :], ps[:, 2 * u + n // 2, (n % 2) * 256:(n % 2) * 256 + 256], ACT.Relu, bias=b1[:, n:n + 1])
                        ins.then_inc(s["hid_ready"], 1)

            @block.vector
            def _(dve):
                dve.sem_inc(s["added"], 2)
                with dve.Fori(0, G // 2) as i:
                    for u in range(2):
                        dve.wait_ge(s["done"], i * 2 + (u + 3))
                        out = X[:, bass.ds(i * 2 + u, 1), :, :].rearrange("p g t c -> p (g t c)")
                        dve.tensor_tensor(out, out, ps[:, 4 + u, 0:256], ALU.add).then_inc(s["added"], 1)
        s.end()


NE = 64
GE = 4
LOWEST = -3.0e38


def expert_choice(nc, name, X, w):
    with ExitStack() as ctx:
        def sb(n, shape, dt=F32):
            return ctx.enter_context(nc.sbuf_tensor(f"{name}_{n}", shape, dt))

        ident = sb("ident", [P, P])
        weights = sb("weights", [NE, T])
        pooled = sb("pooled", [P, NE, B])
        outs = sb("outs", [P, B, P])
        load_all(nc, name + "_load", [(ident[:, :], w["ident"])])
        with nc.sbuf_tensor(name + "_xn", [P, G, 2, C], F32) as XN:
            layer_norm(nc, name + "_ln", X, XN, 1e-5)
            with nc.sbuf_tensor(name + "_xt", [P, T], F32) as XT:
                transpose_tokens(nc, name + "_tr", XN, lambda g: XT[:, bass.ds(g * 256, 256)].rearrange("c (p t) -> c t p", t=2), ident)
                expert_weights(nc, name + "w", w, XT, weights)
            pool_tokens(nc, name + "p", XN, weights, ident, pooled)
        expert_layers(nc, name + "e", w, pooled, outs)
        scatter_tokens(nc, name + "s", w, weights, ident, outs, X)


def expert_weights(nc, name, w, XT, weights):
    with ExitStack() as ctx:
        def sb(n, shape):
            return ctx.enter_context(nc.sbuf_tensor(f"{name}_{n}", shape, F32))
        gate, gate_b = sb("gate", [P, NE]), sb("gate_b", [NE, 1])
        top, neg, total, probs, kept = sb("top", [NE, B, 8]), sb("neg", [NE, B]), sb("total", [NE, B]), sb("probs", [NE, B, S]), sb("kept", [NE, S])
        ps = ctx.enter_context(nc.psum_tensor(name + "_ps", [NE, 8, 512], F32))
        load_all(nc, name + "_load", [(gate[:, :], w["gate"]), (gate_b[:, :], w["gate_b"])])
        s = Signals(nc, name, "made stored own max_ready exp_ready")
        R = R_ORDER
        with nc.Block() as block:
            @block.tensor
            def _(pe):
                with pe.Fori(0, B * NCH // 8) as i:
                    for u in range(8):
                        pe.wait_ge(s["stored"], i * 8 + (u + 1))
                        pe.matmul(ps[:, u, 0:R], gate[:, :], XT[:, bass.ds((i * 8 + u) * R, R)], start=True, stop=True).then_inc(s["made"], 1)

            @block.scalar
            def _(act):
                act.sem_inc(s["stored"], 8)
                with act.Fori(0, B * NCH // 8) as i:
                    for u in range(8):
                        act.wait_ge(s["made"], i * 8 + (u + 1))
                        act.activation(weights[:, bass.ds((i * 8 + u) * R, R)], ps[:, u, 0:R], ACT.Identity, bias=gate_b[:, :]).then_inc(s["stored"], 1)
                for b in range(B):
                    act.wait_ge(s["max_ready"], b + 1)
                    act.activation(probs[:, b, :], weights[:, b * S:(b + 1) * S], ACT.Exp, bias=neg[:, b:b + 1],
                                   accum_out=total[:, b:b + 1]).then_inc(s["exp_ready"], 1)

            @block.vector
            def _(dve):
                ch = Chain(dve, s["own"])
                dve.wait_ge(s["stored"], 8 + B * NCH)
                for b in range(B):
                    logit = weights[:, b * S:(b + 1) * S]
                    ch.link(dve.max(top[:, b, :], logit))
                    dve.tensor_scalar(neg[:, b:b + 1], top[:, b, 0:1], -1.0, None, ALU.mult).then_inc(s["max_ready"], 1)
                for b in range(B):
                    logit = weights[:, b * S:(b + 1) * S]
                    ch.link(dve.match_replace(kept[:, :], top[:, b, :], logit, LOWEST))
                    ch.link(dve.tensor_tensor(kept[:, :], kept[:, :], logit, ALU.not_equal))
                    dve.wait_ge(s["exp_ready"], b + 1)
                    ch.link(dve.reciprocal(total[:, b:b + 1], total[:, b:b + 1]))
                    ch.link(dve.scalar_tensor_tensor(logit, probs[:, b, :], total[:, b:b + 1], kept[:, :], ALU.mult, ALU.mult))
        s.end()


def tile_of(stage, n):
    return stage[:, (n // 2) * 256 + n % 2:(n // 2 + 1) * 256:2]


def pool_tokens(nc, name, XN, weights, ident, pooled):
    with ExitStack() as ctx:
        def sb(n, shape):
            return ctx.enter_context(nc.sbuf_tensor(f"{name}_{n}", shape, F32))
        stage, wt, sums = sb("stage", [P, S]), sb("wt", [P, 20, P]), sb("sums", [P, C])
        ps = ctx.enter_context(nc.psum_tensor(name + "_ps", [P, 8, 512], F32))
        s = Signals(nc, name, "padded staged turned kept summed sums_ready sums_turned pooled")
        with nc.Block() as block:
            @block.gpsimd
            def _(pool):
                pool.memset(stage[NE:, :], 0.0).then_inc(s["padded"], 1)

            @block.scalar
            def _(act):
                with act.Fori(0, B) as b:
                    act.wait_ge(s["turned"], b * 5 + 1)
                    act.activation(stage[0:NE, :], weights[:, bass.ds(b * S, S)], ACT.Copy).then_inc(s["staged"], 1)
                    for n in range(5):
                        act.wait_ge(s["turned"], b * 5 + (n + 2))
                        m = 4 if n < 4 else 2
                        act.activation(wt[:, 4 * n:4 * n + m, :], ps[:, n, 0:m * P].rearrange("s (m e) -> s m e", e=P), ACT.Copy).then_inc(s["kept"], 1)

            @block.tensor
            def _(pe):
                pe.sem_inc(s["turned"], 1)
                pe.wait_ge(s["padded"], 1)
                with pe.Fori(0, B) as b:
                    pe.wait_ge(s["staged"], b + 1)
                    for n in range(18):
                        if n % 4 == 0:
                            pe.wait_ge(s["kept"], b * 5 + (n // 4 + 1))
                        ins = pe.transpose(ps[:, n // 4, (n % 4) * P:(n % 4 + 1) * P], tile_of(stage, n), ident[:, :])
                        if n % 4 == 3 or n == 17:
                            ins.then_inc(s["turned"], 1)
                    pe.wait_ge(s["kept"], b * 5 + 10)
                    pe.wait_ge(s["sums_ready"], b + 1)
                    for n in range(18):
                        ins = pe.matmul(ps[:, 5, 0:C], wt[:, n, :], XN[:, bass.ds(b * GB + n // 2, 1), n % 2, :].rearrange("p g c -> p (g c)"), start=n == 0, stop=n == 17)
                    ins.then_inc(s["summed"], 1)
                    pe.wait_ge(s["sums_ready"], b + 2)
                    pe.wait_ge(s["pooled"], b + 1)
                    pe.transpose(ps[:, 6, 0:P], sums[:, :], ident[:, :]).then_inc(s["sums_turned"], 1)

            @block.vector
            def _(dve):
                dve.sem_inc(s["kept"], 5)
                dve.sem_inc(s["sums_ready"], 1)
                dve.sem_inc(s["pooled"], 1)
                with dve.Fori(0, B) as b:
                    dve.wait_ge(s["summed"], b + 1)
                    dve.tensor_copy(sums[:, :], ps[:, 5, 0:C]).then_inc(s["sums_ready"], 1)
                    dve.wait_ge(s["sums_turned"], b + 1)
                    dve.tensor_copy(pooled[:, :, bass.ds(b, 1)].rearrange("d e b -> d (e b)"), ps[:, 6, 0:NE]).then_inc(s["pooled"], 1)
        s.end()


def expert_layers(nc, name, w, pooled, outs):
    with ExitStack() as ctx:
        def sb(n, shape):
            return ctx.enter_context(nc.sbuf_tensor(f"{name}_{n}", shape, F32))
        w1, w2 = sb("w1", [P, 2, GE, 512]), sb("w2", [P, 2, GE, 512])
        b1, pre, hid = sb("b1", [P, NE * 4]), sb("pre", [P, 2, GE * 4, B]), sb("hid", [P, 2, GE * 4, B])
        ps = ctx.enter_context(nc.psum_tensor(name + "_ps", [P, 4, 512], F32))
        load_all(nc, name + "_load", [(b1[:, :], w["b1"])])
        s = Signals(nc, name, "loaded0 loaded1 made biased hid_ready done stored cleared")
        loaded = (s["loaded0"], s["loaded1"])
        NG = NE // GE
        with nc.Block() as block:
            @block.sync
            def _(sp):
                with sp.Fori(0, NG // 2) as i:
                    for u in range(2):
                        sp.wait_ge(s["done"], i * 2 + (u + 1))
                        for n in range(GE):
                            e = i * (2 * GE) + (u * GE + n)
                            sp.dma_start(w1[:, u, n, :], w["w1"][bass.ds(e * 129, P), :]).then_inc(loaded[u], 16)
                            sp.dma_start(w2[:, u, n, :], w["w2"][bass.ds(e * 513, 512), :].rearrange("(p r) o -> p (r o)", r=4)).then_inc(loaded[u], 16)

            @block.tensor
            def _(pe):
                pe.sem_inc(s["done"], 2)
                with pe.Fori(0, NG // 2) as i:
                    for u in range(2):
                        pe.wait_ge(loaded[u], i * (32 * GE) + 32 * GE)
                        pe.wait_ge(s["biased"], i * 2 + (u + 1))
                        for n in range(GE):
                            for r in range(4):
                                ins = pe.matmul(ps[:, u, (n * 4 + r) * B:(n * 4 + r + 1) * B], w1[:, u, n, r::4],
                                                pooled[:, bass.ds(i * (2 * GE) + (u * GE + n), 1), :].rearrange("d e b -> d (e b)"), start=True, stop=True)
                        ins.then_inc(s["made"], 1)
                        pe.wait_ge(s["hid_ready"], i * 2 + (u + 1))
                        pe.wait_ge(s["stored"], i * 2 + (u + 1))
                        for n in range(GE):
                            for r in range(4):
                                ins = pe.matmul(ps[:, 2 + u, n * B:(n + 1) * B], w2[:, u, n, r * C:(r + 1) * C], hid[:, u, n * 4 + r, :], start=r == 0, stop=r == 3)
                        ins.then_inc(s["done"], 1)

            @block.vector
            def _(dve):
                dve.sem_inc(s["biased"], 2)
                dve.sem_inc(s["stored"], 2)
                dve.memset(outs[:, :, :], 0.0).then_inc(s["cleared"], 1)
                dve.wait_ge(s["cleared"], 1)
                with dve.Fori(0, NG // 2) as i:
                    for u in range(2):
                        dve.wait_ge(s["made"], i * 2 + (u + 1))
                        dve.wait_ge(s["done"], i * 2 + (u + 1))
                        bias = b1[:, bass.ds((i * 2 + u) * (GE * 4), GE * 4)]
                        dve.tensor_tensor(pre[:, u, :, :], ps[:, u, 0:GE * 4 * B].rearrange("p (n b) -> p n b", b=B),
                                          bc(bias[:, :, None], [P, GE * 4, B]), ALU.add).then_inc(s["biased"], 1)
                        dve.wait_ge(s["done"], i * 2 + (u + 3))
                        dve.tensor_copy(outs[:, :, bass.ds((i * 2 + u) * GE, GE)],
                                        ps[:, 2 + u, 0:GE * B].rearrange("o (n b) -> o b n", b=B)).then_inc(s["stored"], 1)

            @block.scalar
            def _(act):
                with act.Fori(0, NG // 2) as i:
                    for u in range(2):
                        act.wait_ge(s["biased"], i * 2 + (u + 3))
                        act.activation(hid[:, u, :, :], pre[:, u, :, :], ACT.Gelu).then_inc(s["hid_ready"], 1)
        s.end()


def scatter_tokens(nc, name, w, weights, ident, outs, X):
    with ExitStack() as ctx:
        def sb(n, shape):
            return ctx.enter_context(nc.sbuf_tensor(f"{name}_{n}", shape, F32))
        stage, rows, b2 = sb("stage", [P, S]), sb("rows", [P, B, C]), sb("b2", [NE, C])
        ps = ctx.enter_context(nc.psum_tensor(name + "_ps", [P, 8, 512], F32))
        load_all(nc, name + "_load", [(b2[:, :], w["b2"])])
        s = Signals(nc, name, "padded turned rows_ready staged made added")
        with nc.Block() as block:
            @block.gpsimd
            def _(pool):
                pool.memset(stage[NE:, :], 0.0).then_inc(s["padded"], 1)
                pool.memset(rows[NE:, :, :], 0.0).then_inc(s["padded"], 1)

            @block.scalar
            def _(act):
                with act.Fori(0, B) as b:
                    act.wait_ge(s["made"], b * 5 + 1)
                    act.activation(stage[0:NE, :], weights[:, bass.ds(b * S, S)], ACT.Copy).then_inc(s["staged"], 1)

            @block.tensor
            def _(pe):
                pe.sem_inc(s["made"], 1)
                for b in range(B):
                    ins = pe.transpose(ps[:, 7, b * P:(b + 1) * P], outs[:, b, :], ident[:, :])
                ins.then_inc(s["turned"], 1)
                pe.wait_ge(s["padded"], 2)
                pe.wait_ge(s["rows_ready"], 1)
                with pe.Fori(0, B) as b:
                    pe.wait_ge(s["staged"], b + 1)
                    for n in range(18):
                        if n % 4 == 0:
                            pe.wait_ge(s["added"], b * 5 + (n // 4 + 1))
                        ins = pe.matmul(ps[:, n // 4, (n % 4) * C:(n % 4 + 1) * C], tile_of(stage, n),
                                        rows[:, bass.ds(b, 1), :].rearrange("e b c -> e (b c)"), start=True, stop=True)
                        if n % 4 == 3 or n == 17:
                            ins.then_inc(s["made"], 1)

            @block.vector
            def _(dve):
                dve.sem_inc(s["added"], 5)
                dve.wait_ge(s["turned"], 1)
                for b in range(B):
                    ins = dve.tensor_tensor(rows[0:NE, b, :], ps[0:NE, 7, b * P:(b + 1) * P], b2[:, :], ALU.add)
                ins.then_inc(s["rows_ready"], 1)
                with dve.Fori(0, B) as b:
                    for n in range(5):
                        dve.wait_ge(s["made"], b * 5 + (n + 2))
                        m = 2 if n < 4 else 1
                        out = X[:, bass.ds(b * GB + 2 * n, m), :, :].rearrange("p g t c -> p (g t c)")
                        dve.tensor_tensor(out, out, ps[:, n, 0:m * 256], ALU.add).then_inc(s["added"], 1)
        s.end()


NH = 4
DH = 32
NT_ = S // P


def attention(nc, X, xt_dram, max_dram, w):
    with ExitStack() as ctx:
        def sb(n, shape, dt=F32):
            return ctx.enter_context(nc.sbuf_tensor("at_" + n, shape, dt))

        ident = sb("ident", [P, P])
        load_all(nc, "at_ident", [(ident[:, :], w["ident"])])
        with nc.sbuf_tensor("at_xn", [P, G, 2, C], F32) as XN, nc.sbuf_tensor("at_xt", [P, T], F32) as XT:
            layer_norm(nc, "at_ln", X, XN, 1e-6)
            transpose_tokens(nc, "at_tr", XN, lambda g: XT[:, bass.ds(g * 256, 256)].rearrange("c (t p) -> c t p", t=2), ident)
            load_all(nc, "at_store", [(xt_dram, XT[:, :])])
        wqkv, wout = sb("wqkv", [P, 3 * P]), sb("wout", [P, C])
        ones, (bout,) = bias_rows(nc, ctx, "at_b", [w["bout"]])
        packs = sb("packs", [P, 2, 4, 2, S], BF16)
        parts = sb("parts", [P, 2, 3, S], BF16)
        qk = sb("qk", [P, 2, S])
        probs = sb("probs", [P, 3, 2, R_ORDER])
        vn = sb("vn", [P, NT_, NH, DH])
        v = sb("v", [P, NT_, NH, 2, DH])
        ssq, scale = sb("ssq", [P, 2]), sb("scale", [P, 2])
        top, topT = sb("top", [P, 2 * NT_, NCH]), sb("topT", [P, P], BF16)
        neg = sb("neg", [P, P])
        kept, inv = sb("kept", [P, R_ORDER]), sb("inv", [P, R_ORDER])
        OT = sb("OT", [P, S])
        xb = probs[:, :, :, :].rearrange("p a h r -> p (a h r)")
        load_all(nc, "at_load", [(wqkv[:, :], w["wqkv"]), (wout[:, :], w["wout"])])

        ps = ctx.enter_context(nc.psum_tensor("at_ps", [P, 8, 512], F32))
        c0 = Signals(nc, "at0", "cleared")
        with nc.Block() as block:
            @block.vector
            def _(dve):
                dve.memset(v[:, :, :, 1, :], 1.0)
                dve.memset(neg[:, :], 0.0)

            @block.gpsimd
            def _(pool):
                for p in range(2):
                    pool.memset(packs[64:P, p, Q_SECOND, :, :], 0.0)
                    pool.memset(packs[64:P, p, K_SECOND, :, :], 0.0).then_inc(c0["cleared"], 1)
                pool.wait_ge(c0["cleared"], 2)
                for p in range(2):
                    pool.memset(packs[64:65, p, K_SECOND, :, :], 1.0)
        c0.end()

        s1 = Signals(nc, "at1", "loaded made kept own squared rooted lowered centred")
        s3 = Signals(nc, "at3", "packed mmade reduced negated turned copied stored placed "
                                "scored weighed used kept divided own")
        s4 = Signals(nc, "at4", "made")
        held = dict(ps=ps, packs=packs, parts=parts, top=top, neg=neg, topT=topT, ident=ident, max_dram=max_dram, v=v,
                    OT=OT, kept=kept, inv=inv, probs=probs, xb=xb, qk=qk, vn=vn, ssq=ssq, scale=scale, wqkv=wqkv, xt_dram=xt_dram)

        def output(b):
            with nc.Block() as block:
                @block.tensor
                def _(pe):
                    for n in range(NT_):
                        out = ps_bank(ps, n // 4)[:, (n % 4) * C:(n % 4 + 1) * C]
                        pe.matmul(out, OT[:, n * P:(n + 1) * P], wout[:, :], start=True, stop=False)
                        ins = pe.matmul(out, ones[:, :], bout, start=False, stop=True)
                        if n % 4 == 3 or n == NT_ - 1:
                            ins.then_inc(s4["made"], 1)

                @block.vector
                def _(dve):
                    for n in range(5):
                        dve.wait_ge(s4["made"], n + 1)
                        m = 2 if n < 4 else 1
                        out = X[:, bass.ds(b * GB + 2 * n, m), :, :].rearrange("p g t c -> p (g t c)")
                        dve.tensor_tensor(out, out, ps_bank(ps, n)[:, 0:m * 256], ALU.add)

                @block.scalar
                def _(act):
                    act.activation(v[:, :, :, 0, :], vn[:, :, :, :], ACT.Copy)
            s4.clear()

        def attend_pair(p, build):
            pair_of_heads(nc, s3, p, build, held)
            s3.clear()

        project_heads(nc, s1, 0, held)
        s1.clear()
        with nc.Block() as block:
            @block.scalar
            def _(act):
                act.activation(v[:, :, :, 0, :], vn[:, :, :, :], ACT.Copy)
        attend_pair(None, 0)
        with nc.Fori(0, B - 1) as b:
            attend_pair(0, 1)
            project_heads(nc, s1, b + 1, held)
            s1.clear()
            attend_pair(1, 0)
            output(b)
        attend_pair(0, 1)
        attend_pair(1, None)
        output(B - 1)
        for s in (s1, s3, s4):
            s.release()


Q_FIRST, K_FIRST, Q_SECOND, K_SECOND = range(4)
ROWS = {Q_FIRST: [(0, 0), (1, 0), (2, 1), (3, 1)], K_FIRST: [(0, 0), (1, 1), (2, 0), (3, 1)],
        Q_SECOND: [(0, 0), (1, 2)], K_SECOND: [(0, 2), (1, 0)]}


def ps_bank(ps, n):
    return ps[:, n, :]


def project_heads(nc, s, b, vv):
    ps, parts, xb, qk, vn, ssq, scale, wqkv, xt_dram = (vv[n] for n in "ps parts xb qk vn ssq scale wqkv xt_dram".split())
    R = R_ORDER
    with nc.Block() as block:
        @block.sync
        def _(sp):
            sp.dma_start(xb, xt_dram[:, bass.ds(b * S, S)]).then_inc(s["loaded"], 16)

        @block.tensor
        def _(pe):
            pe.wait_ge(s["loaded"], 16)
            for n in range(12):
                m, c = n // NCH, n % NCH
                if n >= 4:
                    pe.wait_ge(s["kept"], n - 3)
                pe.matmul(ps_bank(ps, n % 4)[:, 0:R], wqkv[:, m * P:(m + 1) * P], xb[:, c * R:(c + 1) * R], start=True, stop=True).then_inc(s["made"], 1)
            for n in range(NT_):
                if n >= 4:
                    pe.wait_ge(s["own"], n - 3)
                pe.matmul(ps_bank(ps, 4 + n % 4)[:, 0:P], xb[:, n * P:(n + 1) * P], wqkv[:, 2 * P:3 * P], start=True, stop=True).then_inc(s["made"], 1)

        @block.scalar
        def _(act):
            for n in range(12):
                act.wait_ge(s["made"], n + 1)
                act.activation(qk[:, n // NCH, (n % NCH) * R:(n % NCH + 1) * R], ps_bank(ps, n % 4)[:, 0:R], ACT.Copy).then_inc(s["kept"], 1)
                if n % NCH == NCH - 1:
                    m = n // NCH
                    act.wait_ge(s["kept"], n + 1)
                    act.activation(parts[:, m, 2, :], qk[:, m, :], ACT.Square, accum_out=ssq[:, m:m + 1]).then_inc(s["squared"], 1)
            act.wait_ge(s["squared"], 2)
            act.activation(scale[:, :], ssq[:, :], ACT.Sqrt).then_inc(s["rooted"], 1)
            for m in range(2):
                act.wait_ge(s["centred"], m + 1)
                act.activation(parts[:, m, 1, :], qk[:, m, :], ACT.Copy).then_inc(s["lowered"], 1)

        @block.vector
        def _(dve):
            for n in range(NT_):
                dve.wait_ge(s["made"], 13 + n)
                dve.tensor_copy(vn[:, n, :, :].rearrange("p h d -> p (h d)"), ps_bank(ps, 4 + n % 4)[:, 0:P]).then_inc(s["own"], 1)
            ch = Chain(dve, s["own"])
            ch.n = NT_
            dve.wait_ge(s["rooted"], 1)
            ch.link(dve.tensor_scalar(scale[:, :], scale[:, :], 1e-12, None, ALU.max))
            ch.link(dve.reciprocal(scale[:, :], scale[:, :]))
            ch.link(dve.tensor_scalar(scale[:, 0:1], scale[:, 0:1], 10.0, None, ALU.mult))
            for m in range(2):
                ch.link(dve.tensor_scalar(parts[:, m, 0, :], qk[:, m, :], scale[:, m:m + 1], None, ALU.mult))
                dve.scalar_tensor_tensor(qk[:, m, :], qk[:, m, :], scale[:, m:m + 1], parts[:, m, 0, :], ALU.mult, ALU.subtract).then_inc(s["centred"], 1)
            for m in range(2):
                dve.wait_ge(s["lowered"], m + 1)
                dve.tensor_tensor(parts[:, m, 2, :], qk[:, m, :], parts[:, m, 1, :], ALU.subtract)


def pair_of_heads(nc, s, pair, build, vv):
    ps, packs, parts, top, neg, topT, ident, max_dram = (vv[n] for n in "ps packs parts top neg topT ident max_dram".split())
    v, OT, kept, inv, probs = (vv[n] for n in "v OT kept inv probs".split())
    R = R_ORDER
    acc = ps_bank(ps, 4)
    STEPS = 4 * len(ROWS[Q_FIRST]) + 4 * len(ROWS[Q_SECOND])
    tiles = {c: [] for c in range(NCH)}
    if build is not None:
        tiles = {0: [], 5: [16, 17]}

    def at_least(eng, sem, n):
        if not isinstance(n, int) or n > 0:
            eng.wait_ge(sem, n)

    def maxima_groups(c):
        if build is None or (isinstance(c, int) and c == 0):
            return []
        if isinstance(c, int) and c == NCH - 1:
            return [((32 + 2 * t + h) * NCH + u, 16 + t, h, u) for t in range(2) for h in range(2) for u in range(NCH)]
        return [(c * (8 * NCH) + ((2 * t + h - 8) * NCH + u), c * 4 + (t - 4), h, u) for t in range(4) for h in range(2) for u in range(NCH)]

    def chunks(eng, body):
        body(0)
        with eng.Fori(1, NCH - 1) as c:
            body(c)
        body(NCH - 1)

    with nc.Block() as block:
        @block.tensor
        def _(pe):
            def maxima(group):
                g, tile, h, u = group
                pe.wait_ge(s["reduced"], g + 1)
                q = packs[:, build, Q_FIRST, h, bass.ds(tile * P, P)] if not isinstance(tile, int) else packs[:, build, Q_FIRST, h, tile * P:(tile + 1) * P]
                pe.matmul(ps_bank(ps, 5 + u % 3)[:, 0:R], q, packs[:, build, K_FIRST, h, u * R:(u + 1) * R], start=True, stop=True).then_inc(s["mmade"], 1)

            def turn():
                pe.wait_ge(s["negated"], 1)
                pe.transpose(ps_bank(ps, 5)[:, 0:P], neg[:, :], ident[:, :]).then_inc(s["turned"], 1)

            def attend(c):
                base = c * NT_
                groups = maxima_groups(c)
                if build is not None and isinstance(c, int) and c == NCH - 1 or groups:
                    pe.wait_ge(s["packed"], 16 * STEPS)

                def score(j):
                    at_least(pe, s["weighed"], base + (j - 1))
                    for h in range(2):
                        for q, k in ((Q_FIRST, K_FIRST), (Q_SECOND, K_SECOND)):
                            ins = pe.matmul(ps_bank(ps, 2 * (j % 2) + h)[:, 0:R], packs[:, pair, k, h, j * P:(j + 1) * P],
                                            packs[:, pair, q, h, bass.ds(c * R, R)], start=q == Q_FIRST, stop=q == Q_SECOND)
                    ins.then_inc(s["scored"], 1)

                def apply(j):
                    pe.wait_ge(s["weighed"], base + (j + 1))
                    for h in range(2):
                        ins = pe.matmul(acc[64 * h:64 * h + 64, 0:R], v[:, j, 2 * pair + h, :, :].rearrange("p a d -> p (a d)"), probs[:, j % 3, h, :],
                                        start=j == 0, stop=j == NT_ - 1, skip_group_check=True)
                    ins.then_inc(s["used"], 1)

                score(0)
                score(1)
                at_least(pe, s["kept"], c)
                for j in range(NT_):
                    apply(j)
                    for group in groups[3 * j:3 * j + 1]:
                        maxima(group)
                    if j + 2 < NT_:
                        score(j + 2)
                    for group in groups[3 * j + 1:3 * j + 3]:
                        maxima(group)
                    if build is not None and isinstance(c, int) and c == NCH - 1 and j == 12:
                        turn()

            if pair is not None:
                chunks(pe, attend)
            else:
                pe.wait_ge(s["packed"], 16 * STEPS)
                for tile in range(NT_):
                    for h in range(2):
                        for u in range(NCH):
                            maxima(((2 * tile + h) * NCH + u, tile, h, u))
                turn()

        @block.scalar
        def _(act):
            def weigh(c):
                base = c * NT_
                for j in range(NT_):
                    act.wait_ge(s["scored"], base + (j + 1))
                    at_least(act, s["used"], base + (j - 2))
                    act.activation(probs[:, j % 3, :, :], ps[:, 2 * (j % 2):2 * (j % 2) + 2, 0:R], ACT.Exp).then_inc(s["weighed"], 1)
                act.wait_ge(s["used"], base + NT_)
                at_least(act, s["divided"], c)
                act.activation(kept[:, :], acc[:, 0:R], ACT.Copy).then_inc(s["kept"], 1)

            if pair is not None:
                chunks(act, weigh)

        @block.vector
        def _(dve):
            ch = Chain(dve, s["own"])

            dve.sem_inc(s["reduced"], 3)

            def reduce(group):
                g, tile, h, u = group
                dve.wait_ge(s["mmade"], g + 1)
                dve.tensor_reduce(top[:, bass.ds(tile + h * NT_, 1), u], ps_bank(ps, 5 + u % 3)[:, 0:R], AX.X, ALU.max).then_inc(s["reduced"], 1)

            def negate():
                dve.wait_ge(s["reduced"], 3 + 2 * NT_ * NCH)
                dve.tensor_reduce(neg[:, 0:2 * NT_], top[:, :, :], AX.X, ALU.max, negate=True).then_inc(s["negated"], 1)
                dve.wait_ge(s["turned"], 1)
                dve.tensor_copy(topT[:, :], ps_bank(ps, 5)[:, 0:P]).then_inc(s["copied"], 1)

            def divide(c):
                for group in maxima_groups(c):
                    reduce(group)
                if build is not None and isinstance(c, int) and c == NCH - 1:
                    negate()
                ch.enter(c, 1)
                dve.wait_ge(s["kept"], c + 1)
                for h in range(2):
                    ins = dve.reciprocal(inv[64 * h:64 * h + DH, :], kept[64 * h + DH:64 * h + 2 * DH, :])
                ch.link(ins)
                for h in range(2):
                    at = (2 * pair + h) * DH
                    ins = dve.tensor_tensor(OT[at:at + DH, bass.ds(c * R, R)], kept[64 * h:64 * h + DH, :], inv[64 * h:64 * h + DH, :], ALU.mult)
                ins.then_inc(s["divided"], 1)
                ch.base, ch.n = 0, 0

            if pair is not None:
                chunks(dve, divide)
            else:
                for tile in range(NT_):
                    for h in range(2):
                        for u in range(NCH):
                            reduce(((2 * tile + h) * NCH + u, tile, h, u))
                negate()

        @block.sync
        def _(sp):
            if build is not None:
                for h in range(2):
                    at = (2 * build + h) * DH
                    for kind, rows in ROWS.items():
                        for group, part in rows:
                            m = 0 if kind in (Q_FIRST, Q_SECOND) else 1
                            sp.dma_start(packs[32 * group:32 * group + DH, build, kind, h, :], parts[at:at + DH, m, part, :]).then_inc(s["packed"], 16)
                sp.wait_ge(s["copied"], 1)
                sp.dma_start(max_dram, topT[0:2 * NT_, :]).then_inc(s["stored"], 16)
                sp.wait_ge(s["stored"], 16)
                sp.dma_start(packs[64:65, build, Q_SECOND, :, :].rearrange("a h s -> a (h s)"), max_dram.rearrange("(a m) p -> a (m p)", a=1)).then_inc(s["placed"], 16)
                sp.wait_ge(s["placed"], 16)


def global_norm(nc, name, V, alpha, beta, scale, shift):
    with ExitStack() as ctx:
        def sb(n, shape):
            return ctx.enter_context(nc.sbuf_tensor(f"{name}_{n}", shape, F32))
        a, bt, sums, sq, total = sb("a", [P, 1]), sb("bt", [P, 1]), sb("sums", [P, 1]), sb("sq", [P, 4]), sb("total", [P, 1])
        mean, var, over, junk, eps = sb("mean", [P, 1]), sb("var", [P, 1]), sb("over", [P, P]), sb("junk", [P, T // 4]), sb("eps", [P, 1])
        neg = sb("neg", [P, 1])
        ps = ctx.enter_context(nc.psum_tensor(name + "_ps", [P, 2, 512], F32))
        load_all(nc, name + "_load", [(a[:, :], spread(alpha, 1)), (bt[:, :], spread(beta, 1))])
        s = Signals(nc, name, "own summed mean_ready squared total_ready var_ready rooted")
        flat = V[:, :, :, :].rearrange("p g t c -> p (g t c)")
        with nc.Block() as block:
            @block.vector
            def _(dve):
                ch = Chain(dve, s["own"])
                dve.memset(over[:, :], 1.0 / (T * C))
                dve.memset(eps[:, :], 1e-5)
                ch.link(dve.tensor_reduce(sums[:, :], flat, AX.X, ALU.add))
                dve.sem_inc(s["summed"], 1)
                dve.wait_ge(s["mean_ready"], 1)
                ch.link(dve.tensor_copy(mean[:, :], ps[:, 0, 0:1]))
                dve.tensor_scalar(neg[:, :], mean[:, :], -1.0, None, ALU.mult).then_inc(s["summed"], 1)
                dve.wait_ge(s["squared"], 4)
                dve.tensor_reduce(total[:, :], sq[:, :], AX.X, ALU.add).then_inc(s["total_ready"], 1)
                dve.wait_ge(s["var_ready"], 1)
                ch.link(dve.tensor_copy(var[:, :], ps[:, 1, 0:1]))
                dve.sem_inc(s["total_ready"], 1)
                dve.wait_ge(s["rooted"], 1)
                ch.link(dve.reciprocal(var[:, :], var[:, :]))
                ch.link(dve.tensor_tensor(scale[:, :], var[:, :], a[:, :], ALU.mult))
                ch.link(dve.scalar_tensor_tensor(shift[:, :], neg[:, :], scale[:, :], bt[:, :], ALU.mult, ALU.add))

            @block.tensor
            def _(pe):
                pe.wait_ge(s["summed"], 1)
                pe.matmul(ps[:, 0, 0:1], over[:, :], sums[:, :], start=True, stop=True).then_inc(s["mean_ready"], 1)
                pe.wait_ge(s["total_ready"], 1)
                pe.matmul(ps[:, 1, 0:1], over[:, :], total[:, :], start=True, stop=True).then_inc(s["var_ready"], 1)

            @block.scalar
            def _(act):
                act.wait_ge(s["summed"], 2)
                for n in range(4):
                    act.activation(junk[:, :], flat[:, n * (T // 4):(n + 1) * (T // 4)], ACT.Square, bias=neg[:, :], accum_out=sq[:, n:n + 1]).then_inc(s["squared"], 1)
                    act.wait_ge(s["squared"], n + 1)
                act.wait_ge(s["total_ready"], 2)
                act.activation(var[:, :], var[:, :], ACT.Sqrt, bias=eps[:, :]).then_inc(s["rooted"], 1)
        s.end()


def triangle(nc, X, k_dram, w):
    with ExitStack() as ctx:
        def sb(n, shape):
            return ctx.enter_context(nc.sbuf_tensor("tr_" + n, shape, F32))

        ident = sb("ident", [P, P])
        wab, wo = sb("wab", [P, 512]), sb("wo", [P, 2, C])
        zs, zb, ks, kb = sb("zs", [P, 1]), sb("zb", [P, 1]), sb("ks", [P, 1]), sb("kb", [P, 1])
        Z = sb("Z", [P, G, 2, C])
        load_all(nc, "tr_load", [(ident[:, :], w["ident"]), (wab[:, :], w["wab"]), (wo[:, :, :], w["wo"])])
        ones, (bab, bo) = bias_rows(nc, ctx, "tr_b", [w["bab"], w["bo"].rearrange("a n c -> a (n c)")])
        layer_norm(nc, "tr_ln", X, Z, 1e-6)
        global_norm(nc, "tr_gz", Z, w["alpha_in"], w["beta_in"], zs, zb)
        with nc.Block() as block:
            @block.vector
            def _(dve):
                zf = Z[:, :, :, :].rearrange("p g t c -> p (g t c)")
                dve.tensor_scalar(zf, zf, zs[:, :], zb[:, :], ALU.mult, ALU.add)
        with nc.sbuf_tensor("tr_zt", [P, T], F32) as ZT:
            transpose_tokens(nc, "tr_tr", Z, lambda g: ZT[:, bass.ds(g * 256, 256)].rearrange("c (p t) -> c t p", t=2), ident)
            triangle_products(nc, ZT, wab, bab, ones, k_dram)
        with nc.sbuf_tensor("tr_k", [P, G, 2, C], F32) as K:
            load_all(nc, "tr_kload", [(K[:, :, :, :], k_dram.rearrange("(g p t) c -> p g t c", p=P, t=2))])
            global_norm(nc, "tr_gk", K, w["alpha_o"], w["beta_o"], ks, kb)
            triangle_output(nc, Z, K, ks, kb, wo, bo, ones, ident, X)


def triangle_products(nc, ZT, wab, bab, ones, k_dram):
    with ExitStack() as ctx:
        def sb(n, shape):
            return ctx.enter_context(nc.sbuf_tensor("tp_" + n, shape, F32))
        zimg, gates = sb("zimg", [P, S]), sb("gates", [W, 4, 2, C])
        ab, kimg = sb("ab", [W, 2, H, C]), sb("kimg", [H, H, C])
        ps = ctx.enter_context(nc.psum_tensor("tp_ps", [P, 8, 512], F32))
        s = Signals(nc, "tp", "staged projected gated multiplied made kept_act kept_dve stored")
        with nc.Fori(0, B) as b:
            with nc.Block() as block:
                @block.scalar
                def _(act):
                    act.activation(zimg[:, :], ZT[:, bass.ds(b * S, S)], ACT.Copy).then_inc(s["staged"], 1)
                    for r in range(H):
                        act.wait_ge(s["projected"], r + 1)
                        if r >= 4:
                            act.wait_ge(s["multiplied"], r - 3)
                        act.activation(gates[:, r % 4, :, :], ps[0:W, r % 4, :].rearrange("w (n m c) -> w n m c", n=2, m=2)[:, :, 0, :],
                                       ACT.Sigmoid).then_inc(s["gated"], 1)
                    for n in range(0, 16, 2):
                        act.wait_ge(s["made"], n + 1)
                        act.activation(kimg[:, :, 8 * n:8 * n + 8], ps[0:H, 4 + n % 4, 0:384].rearrange("i (c j) -> i j c", c=8), ACT.Copy).then_inc(s["kept_act"], 1)

                @block.vector
                def _(dve):
                    for r in range(H):
                        dve.wait_ge(s["gated"], r + 1)
                        dve.tensor_tensor(ab[:, :, r, :], gates[:, r % 4, :, :],
                                          ps[0:W, r % 4, :].rearrange("w (n m c) -> w n m c", n=2, m=2)[:, :, 1, :], ALU.mult).then_inc(s["multiplied"], 1)
                    for n in range(1, 16, 2):
                        dve.wait_ge(s["made"], n + 1)
                        dve.tensor_copy(kimg[:, :, 8 * n:8 * n + 8], ps[0:H, 4 + n % 4, 0:384].rearrange("i (c j) -> i j c", c=8)).then_inc(s["kept_dve"], 1)

                @block.tensor
                def _(pe):
                    pe.wait_ge(s["staged"], 1)
                    for r in range(H):
                        if r >= 4:
                            pe.wait_ge(s["multiplied"], r - 3)
                        pe.matmul(ps[0:W, r % 4, :], zimg[:, r * W:(r + 1) * W], wab[:, :], start=True, stop=False)
                        pe.matmul(ps[0:W, r % 4, :], ones[:, 0:W], bab, start=False, stop=True).then_inc(s["projected"], 1)
                    pe.wait_ge(s["multiplied"], H)
                    for n in range(16):
                        if n >= 4:
                            pe.wait_ge(s["kept_act"] if n % 2 == 0 else s["kept_dve"], n // 2 - 1)
                        for c in range(8):
                            ins = pe.matmul(ps[0:H, 4 + n % 4, c * H:(c + 1) * H], ab[:, 0, :, 8 * n + c], ab[:, 1, :, 8 * n + c], start=True, stop=True)
                        ins.then_inc(s["made"], 1)

                @block.sync
                def _(sp):
                    sp.wait_ge(s["kept_act"], 8)
                    sp.wait_ge(s["kept_dve"], 8)
                    sp.dma_start(k_dram[bass.ds(b * S, S), :].rearrange("(i j) c -> i (j c)", i=H), kimg[:, :, :].rearrange("i j c -> i (j c)")).then_inc(s["stored"], 16)
                    sp.wait_ge(s["stored"], 16)
            s.clear()
        s.release()


def triangle_output(nc, Z, K, ks, kb, wo, bo, ones, ident, X):
    with ExitStack() as ctx:
        def sb(n, shape):
            return ctx.enter_context(nc.sbuf_tensor("to_" + n, shape, F32))
        stage, turned, gate, prod = sb("stage", [P, 2, 4, C]), sb("turned", [P, 2, 4, P]), sb("gate", [P, 2, 256]), sb("prod", [P, 2, 256])
        ps = ctx.enter_context(nc.psum_tensor("to_ps", [P, 4, 512], F32))
        s = Signals(nc, "to", "staged turned kept made gated own added")

        def tiles(V, g):
            return V[:, bass.ds(g, 1), :, :].rearrange("p g t c -> p (g t) c")

        with nc.Block() as block:
            @block.vector
            def _(dve):
                ch = Chain(dve, s["own"])
                dve.sem_inc(s["added"], 2)
                with dve.Fori(0, G // 2) as i:
                    ch.enter(i, 2)
                    for u in range(2):
                        dve.wait_ge(s["turned"], i * 2 + (u + 1))
                        dve.tensor_copy(stage[:, u, 0:2, :], tiles(Z, i * 2 + u))
                        dve.tensor_scalar(stage[:, u, 2:4, :], tiles(K, i * 2 + u), ks[:, :], kb[:, :], ALU.mult, ALU.add).then_inc(s["staged"], 1)
                    for u in range(2):
                        dve.wait_ge(s["gated"], i * 2 + (u + 1))
                        ch.link(dve.tensor_tensor(prod[:, u, :], gate[:, u, :], ps[:, 2 + u, 256:512], ALU.mult))
                        out = X[:, bass.ds(i * 2 + u, 1), :, :].rearrange("p g t c -> p (g t c)")
                        dve.tensor_tensor(out, out, prod[:, u, :], ALU.add).then_inc(s["added"], 1)

            @block.tensor
            def _(pe):
                pe.sem_inc(s["turned"], 2)
                with pe.Fori(0, G // 2) as i:
                    for u in range(2):
                        pe.wait_ge(s["staged"], i * 2 + (u + 1))
                        pe.wait_ge(s["kept"], i * 2 + (u + 1))
                        for t in range(4):
                            ins = pe.transpose(ps[:, u, t * P:(t + 1) * P], stage[:, u, t, :], ident[:, :])
                        ins.then_inc(s["turned"], 1)
                    for u in range(2):
                        pe.wait_ge(s["kept"], i * 2 + (u + 3))
                        pe.wait_ge(s["added"], i * 2 + (u + 1))
                        for t in range(4):
                            out = ps[:, 2 + u, t * C:(t + 1) * C]
                            pe.matmul(out, turned[:, u, t, :], wo[:, t // 2, :], start=True, stop=False)
                            ins = pe.matmul(out, ones[:, :], bo[:, (t // 2) * C:(t // 2 + 1) * C], start=False, stop=True)
                        ins.then_inc(s["made"], 1)

            @block.scalar
            def _(act):
                act.sem_inc(s["kept"], 2)
                with act.Fori(0, G // 2) as i:
                    for u in range(2):
                        act.wait_ge(s["turned"], i * 2 + (u + 3))
                        act.wait_ge(s["added"], i * 2 + (u + 1))
                        act.activation(turned[:, u, :, :].rearrange("c t p -> c (t p)"), ps[:, u, :], ACT.Copy).then_inc(s["kept"], 1)
                    for u in range(2):
                        act.wait_ge(s["made"], i * 2 + (u + 1))
                        act.activation(gate[:, u, :], ps[:, 2 + u, 0:256], ACT.Sigmoid).then_inc(s["gated"], 1)
        s.end()


NX = 8


def top2_experts(nc, X, w):
    with ExitStack() as ctx:
        def sb(n, shape):
            return ctx.enter_context(nc.sbuf_tensor("moe_" + n, shape, F32))

        ident = sb("ident", [P, P])
        router, ew = sb("router", [P, NX]), sb("ew", [P, NX * C])
        ew_high, ew_low = (ctx.enter_context(nc.sbuf_tensor("moe_ew_" + n, [P, NX * C], F32R)) for n in ("high", "low"))
        gates = sb("gates", [P, 2 * G, NX])
        XT = sb("xt", [P, T])
        stage = sb("stage", [P, 2, 4, P])
        load_all(nc, "moe_load", [(ident[:, :], w["ident"]), (router[:, :], w["router"]), (ew[:, :], w["ew"])])
        ones, (router_b, eb) = bias_rows(nc, ctx, "moe_b", [w["router_b"], w["eb"]])
        with nc.sbuf_tensor("moe_xn", [P, G, 2, C], F32) as XN:
            layer_norm(nc, "moe_ln", X, XN, 1e-5)
            transpose_tokens(nc, "moe_tr", XN, lambda g: XT[:, bass.ds(g * 256, 256)].rearrange("c (t p) -> c t p", t=2), ident)
        ps = ctx.enter_context(nc.psum_tensor("moe_ps", [P, 8, 512], F32))

        s = Signals(nc, "mr", "staged made kept")
        with nc.Block() as block:
            @block.scalar
            def _(act):
                with act.Fori(0, G // 4) as i:
                    for u in range(2):
                        act.wait_ge(s["made"], i * 2 + (u + 1))
                        act.activation(stage[:, u, :, :].rearrange("c t p -> c (t p)"), XT[:, bass.ds((i * 2 + u) * 512, 512)], ACT.Copy).then_inc(s["staged"], 1)

            @block.tensor
            def _(pe):
                pe.sem_inc(s["made"], 2)
                with pe.Fori(0, G // 4) as i:
                    for u in range(2):
                        pe.wait_ge(s["staged"], i * 2 + (u + 1))
                        pe.wait_ge(s["kept"], i * 2 + (u + 1))
                        for t in range(4):
                            pe.matmul(ps[:, u, t * NX:(t + 1) * NX], stage[:, u, t, :], router[:, :], start=True, stop=False)
                            ins = pe.matmul(ps[:, u, t * NX:(t + 1) * NX], ones[:, :], router_b, start=False, stop=True)
                        ins.then_inc(s["made"], 1)

            @block.vector
            def _(dve):
                dve.sem_inc(s["kept"], 2)
                with dve.Fori(0, G // 4) as i:
                    for u in range(2):
                        dve.wait_ge(s["made"], i * 2 + (u + 3))
                        dve.tensor_copy(gates[:, bass.ds((i * 2 + u) * 4, 4), :], ps[:, u, 0:4 * NX].rearrange("p (t e) -> p t e", e=NX)).then_inc(s["kept"], 1)
        s.end()
        route(nc, gates)

        s = Signals(nc, "me", "cut weights_ready staged lowered made own added")
        high, low = (ctx.enter_context(nc.sbuf_tensor("moe_stage_" + n, [P, 2, 2, P], F32R)) for n in ("high", "low"))
        with nc.Block() as block:
            @block.gpsimd
            def _(pool):
                pool.wait_ge(s["cut"], 1)
                pool.tensor_tensor(ew_low[:, :], ew[:, :], ew_high[:, :], ALU.subtract).then_inc(s["weights_ready"], 1)
                with pool.Fori(0, G // 2) as i:
                    for u in range(2):
                        pool.wait_ge(s["staged"], i * 2 + (u + 1))
                        source = XT[:, bass.ds((i * 2 + u) * 256, 256)].rearrange("c (t p) -> c t p", t=2)
                        pool.tensor_tensor(low[:, u, :, :], source, high[:, u, :, :], ALU.subtract).then_inc(s["lowered"], 1)

            @block.scalar
            def _(act):
                act.activation(ew_high[:, :], ew[:, :], ACT.Copy).then_inc(s["cut"], 1)
                with act.Fori(0, G // 2) as i:
                    for u in range(2):
                        act.wait_ge(s["made"], i * 4 + (2 * u + 1))
                        act.activation(high[:, u, :, :].rearrange("c t p -> c (t p)"), XT[:, bass.ds((i * 2 + u) * 256, 256)], ACT.Copy).then_inc(s["staged"], 1)

            @block.tensor
            def _(pe):
                pe.sem_inc(s["made"], 3)
                pe.wait_ge(s["weights_ready"], 1)
                with pe.Fori(0, G // 2) as i:
                    for u in range(2):
                        pe.wait_ge(s["lowered"], i * 2 + (u + 1))
                        for t in range(2):
                            pe.wait_ge(s["added"], i * 4 + (2 * u + t + 1))
                            for n in range(2):
                                out = ps[:, 4 * u + 2 * t + n, :]
                                for turn, (x, m) in enumerate(((high, ew_high), (high, ew_low), (low, ew_high))):
                                    pe.matmul(out, x[:, u, t, :], m[:, n * 512:(n + 1) * 512], start=turn == 0, stop=False)
                                ins = pe.matmul(out, ones[:, :], eb[:, n * 512:(n + 1) * 512], start=False, stop=True)
                            ins.then_inc(s["made"], 1)

            @block.vector
            def _(dve):
                dve.sem_inc(s["added"], 4)
                ch = Chain(dve, s["own"])
                with dve.Fori(0, G // 2) as i:
                    ch.enter(i, 2 * (NX - 1))
                    for u in range(2):
                        dve.wait_ge(s["made"], i * 4 + (2 * u + 5))
                        for e in range(NX):
                            for t in range(2):
                                out = X[:, bass.ds(i * 2 + u, 1), t, :].rearrange("p g c -> p (g c)")
                                gate = gates[:, bass.ds(i * 4 + (2 * u + t), 1), e]
                                ins = dve.scalar_tensor_tensor(out, ps[:, 4 * u + 2 * t + e // 4, (e % 4) * C:(e % 4 + 1) * C], gate, out, ALU.mult, ALU.add)
                                if e == NX - 1:
                                    ins.then_inc(s["added"], 1)
                                elif t == 1:
                                    ch.link(ins)
        s.end()


def route(nc, gates):
    n = 2 * G
    with ExitStack() as ctx:
        def sb(name, shape):
            return ctx.enter_context(nc.sbuf_tensor("rt_" + name, shape, F32))
        rest, equal, count, mask, top, second = sb("rest", [P, n, NX]), sb("equal", [P, n, NX]), sb("count", [P, n, NX]), sb("mask", [P, n, NX]), sb("top", [P, n]), sb("second", [P, n])
        s = Signals(nc, "rt", "own centred exp_ready")

        def wide(ap):
            return bc(ap[:, :, None], [P, n, NX])

        with nc.Block() as block:
            @block.vector
            def _(dve):
                ch = Chain(dve, s["own"])

                def first_of(logits, peak):
                    ch.link(dve.tensor_tensor(equal[:, :, :], logits, wide(peak), ALU.is_equal))
                    ch.link(dve.tensor_copy(count[:, :, :], equal[:, :, :]))
                    for e in range(1, NX):
                        ch.link(dve.tensor_tensor(count[:, :, e], count[:, :, e], count[:, :, e - 1], ALU.add))
                    ch.link(dve.tensor_scalar(count[:, :, :], count[:, :, :], 1.0, None, ALU.is_equal))
                    ch.link(dve.tensor_tensor(equal[:, :, :], equal[:, :, :], count[:, :, :], ALU.mult))

                ch.link(dve.tensor_reduce(top[:, :], gates[:, :, :], AX.X, ALU.max))
                first_of(gates[:, :, :], top)
                ch.link(dve.tensor_copy(mask[:, :, :], equal[:, :, :]))
                ch.link(dve.scalar_tensor_tensor(rest[:, :, :], mask[:, :, :], LOWEST, gates[:, :, :], ALU.mult, ALU.add))
                ch.link(dve.tensor_reduce(second[:, :], rest[:, :, :], AX.X, ALU.max))
                first_of(rest[:, :, :], second)
                ch.link(dve.tensor_tensor(mask[:, :, :], mask[:, :, :], equal[:, :, :], ALU.add))
                dve.tensor_tensor(gates[:, :, :], gates[:, :, :], wide(top), ALU.subtract).then_inc(s["centred"], 1)
                dve.wait_ge(s["exp_ready"], 1)
                ch.link(dve.tensor_tensor(gates[:, :, :], gates[:, :, :], mask[:, :, :], ALU.mult))
                ch.link(dve.tensor_reduce(top[:, :], gates[:, :, :], AX.X, ALU.add))
                ch.link(dve.reciprocal(top[:, :], top[:, :]))
                ch.link(dve.tensor_tensor(gates[:, :, :], gates[:, :, :], wide(top), ALU.mult))

            @block.scalar
            def _(act):
                act.wait_ge(s["centred"], 1)
                act.activation(gates[:, :, :], gates[:, :, :], ACT.Exp).then_inc(s["exp_ready"], 1)
        s.end()


def metaformer(nc, w, out):
    def scratch(name, shape, dt=F32):
        return nc.dram_tensor(name, shape, dt, kind="Internal").ap()

    def tokens(ap):
        return ap.rearrange("(g p t) c -> p g t c", p=P, t=2)

    x1, x2, rows, channels, maxima = scratch("x1", [T, C]), scratch("x2", [T, C]), scratch("rows", [T, C]), scratch("channels", [P, T]), scratch("maxima", [2 * NT_, P], BF16)
    with nc.sbuf_tensor("m0_xt", [P, T], F32) as XT:
        with nc.sbuf_tensor("m0_x", [P, G, 2, C], F32) as X0, nc.sbuf_tensor("m0_xn", [P, G, 2, C], F32) as XN, nc.sbuf_tensor("m0_ident", [P, P], F32) as ident:
            load_all(nc, "m0_load", [(X0[:, :, :, :], tokens(w["x"])), (ident[:, :], w["ident"])])
            layer_norm(nc, "m0_ln", X0, XN, 1e-6)
            transpose_tokens(nc, "m0_tr", XN, lambda g: XT[:, bass.ds(g * 256, 256)].rearrange("c (p t) -> c t p", t=2), ident)
        selective_scan_mixer(nc, XT, w["x"], x1, w["l0_conv"])
    spectral_unit(nc, x1, x2, w["l0_ffn"])
    with nc.sbuf_tensor("x", [P, G, 2, C], F32) as X:
        load_all(nc, "m1_load", [(X[:, :, :, :], tokens(x2))])
        fourier_mixer(nc, X, rows, w["l1_conv"])
        expert_choice(nc, "c1", X, w["l1_ffn"])
        attention(nc, X, channels, maxima, w["l2_conv"])
        expert_choice(nc, "c2", X, w["l2_ffn"])
        triangle(nc, X, rows, w["l3_conv"])
        top2_experts(nc, X, w["l3_ffn"])
        load_all(nc, "m_store", [(tokens(out), X[:, :, :, :])])



def layout(inputs):
    def of(prefix):
        return lambda n: np.asarray(inputs[prefix + n])

    def turned(a, order, *shape):
        return np.ascontiguousarray(a.transpose(order)).reshape(shape)

    ident = np.eye(P, dtype=np.float32)
    out = {"x": np.asarray(inputs["x"]).reshape(T, C), "ident": ident}
    stage = {}

    f = of("L0_conv_")
    xp = f("x_proj_w")
    sel = np.zeros((3, 2 * NST, 2 * NST, P), np.float32)
    for n in range(2 * NST):
        sel[:, n, n] = 1
    stage["l0_conv"] = {
        "win": np.ascontiguousarray(f("in_proj_w").T),
        "convw": turned(f("conv_w").reshape(D2, P, 9), (1, 0, 2), P, D2, 9),
        "convb": np.ascontiguousarray(f("conv_b").reshape(D2, P).T),
        "xpw": turned(np.concatenate([xp[:, DTR:], xp[:, :DTR]], 1).reshape(4, 40, D2, P), (3, 2, 0, 1), P, D2, 4, 40),
        "dtw": turned(f("dt_proj_w"), (2, 0, 1), DTR, 4, 256),
        "dtb": turned(f("dt_proj_b").reshape(4, D2, P), (2, 0, 1), P, 4, D2),
        "a_log": turned(f("A_logs").reshape(4, D2, P, NST), (2, 0, 1, 3), P, 4, D2, NST),
        "ds": turned(f("Ds").reshape(4, D2, P), (2, 0, 1), P, 4, D2),
        "ng": np.ascontiguousarray(f("norm_g").reshape(D2, P).T),
        "nb": np.ascontiguousarray(f("norm_b").reshape(D2, P).T),
        "wout": turned(f("out_proj_w").T.reshape(D2, P, C), (1, 0, 2), P, D2, C),
        "sel": sel.reshape(96, 2 * NST, P).astype(mybir.dt.np(BF16)),
    }

    f = of("L0_ffn_")
    none = np.zeros((NK, P), np.float32)
    phi = f("phi")[:S].T
    stage["l0_ffn"] = {
        "phi_even": np.concatenate([phi[:, 0::2][:, ::-1], none], 1),
        "phi_odd": np.concatenate([phi[:, 1::2][:, ::-1], none], 1),
        "M_plus": turned(f("M_phi_plus"), (1, 2, 0, 3), NK, P, NEDGE, P),
        "M_minus": turned(f("M_phi_minus"), (1, 2, 0, 3), NK, P, NEDGE, P),
        "M_u": turned(f("M_u"), (1, 2, 0, 3), 3, P, NEDGE, P),
        "log_weights": f("log_weights"), "gumbel": f("gumbel"), "sigma": f("sigma"),
    }

    f = of("L1_conv_")
    turn = 2 * np.pi * (np.outer(np.arange(W), np.arange(NF)) % W) / W
    cos, sin = np.cos(turn), np.sin(turn)
    sin[:, [0, NF - 1]] = 0
    both = np.full(NF, 2.0)
    both[[0, NF - 1]] = 1
    stage["l1_conv"] = {
        "fw0": turned(f("fw0")[:, :, :NF], (2, 0, 3, 1), NF * P, 2 * C),
        "fw1": turned(f("fw1")[:, :, :NF], (2, 0, 3, 1), NF * P, 2 * C),
        "dft": (np.concatenate([sin, cos, -sin], 1) / np.sqrt(W)).astype(np.float32),
        "idft": np.ascontiguousarray((np.concatenate([cos * both, -sin * both], 1).T / np.sqrt(W)).astype(np.float32)),
        "w1": f("w1"), "w2": turned(f("w2").reshape(4, P, C), (1, 0, 2), P, 4, C),
        "b1": np.ascontiguousarray(f("b1").reshape(4, P).T), "b2": f("b2").reshape(1, C),
    }

    for layer in (1, 2):
        f = of(f"L{layer}_ffn_")
        w1, w2 = f("weight1"), f("weight2")
        stage[f"l{layer}_ffn"] = {
            "gate": np.ascontiguousarray(f("gate_w").T), "gate_b": f("gate_b").reshape(NE, 1),
            "w1": w1.reshape(NE * 129, 512), "w2": w2.reshape(NE * 513, C),
            "b1": turned(w1[:, P].reshape(NE, P, 4), (1, 0, 2), P, NE * 4), "b2": np.ascontiguousarray(w2[:, 512]),
        }

    f = of("L2_conv_")
    stage["l2_conv"] = {"wqkv": f("w_qkv"), "wout": f("w_out"), "bout": f("b_out").reshape(1, C)}

    f = of("L3_conv_")
    four = ("ga", "la", "gb", "lb")
    stage["l3_conv"] = {
        "wab": np.concatenate([f("W_" + n).T for n in four], 1), "bab": np.concatenate([f("b_" + n) for n in four]).reshape(1, 512),
        "wo": np.stack([f("W_go").T, f("W_lo").T], 1), "bo": np.stack([f("b_go"), f("b_lo")]).reshape(1, 2, C),
        "alpha_in": f("alpha_in"), "beta_in": f("beta_in"), "alpha_o": f("alpha_o"), "beta_o": f("beta_o"),
    }

    f = of("L3_ffn_")
    stage["l3_ffn"] = {
        "router": f("router_w"), "router_b": f("router_b").reshape(1, NX),
        "ew": turned(f("expert_w"), (1, 0, 2), P, NX * C), "eb": f("expert_b").reshape(1, NX * C),
    }
    for name, arrays in stage.items():
        for n, a in arrays.items():
            out[f"{name}.{n}"] = np.ascontiguousarray(a)
    return out


def kernel(**inputs):
    import concourse.bacc as bacc
    from concourse.bass_utils import run_bass_kernel_spmd

    nc = bacc.Bacc("TRN2", target_bir_lowering=False, num_devices=1)
    arrays, w = {}, {}
    for name, a in layout(inputs).items():
        dram = "in_" + name.replace(".", "_")
        arrays[dram] = a
        ap = nc.dram_tensor(dram, a.shape, mybir.dt.from_np(a.dtype), kind="ExternalInput").ap()
        if "." in name:
            group, n = name.split(".")
            w.setdefault(group, {})[n] = ap
        else:
            w[name] = ap
    for group in list(w):
        if group[0] == "l":
            w[group]["ident"] = w["ident"]
    w["l1_conv"]["fw"] = [w["l1_conv"]["fw0"], w["l1_conv"]["fw1"]]
    out = nc.dram_tensor("out", [T, C], F32, kind="ExternalOutput").ap()
    metaformer(nc, w, out)
    result = run_bass_kernel_spmd(nc, [arrays], core_ids=[0])
    return result.results[0]["out"].reshape(B, H, W, C)
```

```python
from contextlib import ExitStack

import numpy as np
import concourse.bass as bass
from concourse import mybir

P = 128
B, H, W, C = 4, 48, 48, 128
S = H * W
T = B * S
G = T // 256
GB = G // B
HALF = S // 2

F32 = mybir.dt.float32
BF16 = mybir.dt.bfloat16
F32R = mybir.dt.float32r
ALU = mybir.AluOpType
ACT = mybir.ActivationFunctionType
AX = mybir.AxisListType


class Chain:

    def __init__(self, eng, sem):
        self.eng, self.sem, self.base, self.n = eng, sem, 0, 0

    def link(self, ins):
        self.n += 1
        ins.then_inc(self.sem, 1)
        self.eng.wait_ge(self.sem, self.base + self.n)

    def enter(self, i, per):
        self.start, self.per, self.outer = self.base + self.n, per, (self.base, self.n)
        self.base, self.n = self.start + i * per, 0

    def leave(self, passes):
        assert self.n == self.per, (self.n, self.per)
        self.base, self.n = self.outer[0], self.outer[1] + passes * self.per


class Signals:

    def __init__(self, nc, stage, names):
        self.nc = nc
        self.named = {n: nc.alloc_semaphore(f"{stage}_{n}") for n in names.split()}
        self.all = list(self.named.values())

    def __getitem__(self, name):
        return self.named[name]

    def clear(self):
        for s in self.all:
            self.nc.gpsimd.sem_clear(s)
        self.nc.all_engine_barrier()

    def release(self):
        for s in self.all:
            self.nc.release_semaphore(s)

    def end(self):
        self.clear()
        self.release()


def bc(ap, shape):
    return ap.to_broadcast(shape)


def layer_norm(nc, name, X, XN, eps):
    NT = 2 * G
    BY_DVE, STEP = 36, 12
    with ExitStack() as ctx:
        st = ctx.enter_context(nc.sbuf_tensor(name + "_stats", [P, NT, 6], F32))
        mean = ctx.enter_context(nc.sbuf_tensor(name + "_mean", [P, NT], F32))
        var = ctx.enter_context(nc.sbuf_tensor(name + "_var", [P, NT], F32))
        std = ctx.enter_context(nc.sbuf_tensor(name + "_std", [P, NT], F32))
        rstd = ctx.enter_context(nc.sbuf_tensor(name + "_rstd", [P, NT], F32))
        shift = ctx.enter_context(nc.sbuf_tensor(name + "_shift", [P, NT], F32))
        epst = ctx.enter_context(nc.sbuf_tensor(name + "_eps", [P, 1], F32))
        s = Signals(nc, name, "own var_ready std_ready shift_ready")
        xf = X[:, :, :, :].rearrange("p g t c -> p (g t) c")
        nf = XN[:, :, :, :].rearrange("p g t c -> p (g t) c")
        block = ctx.enter_context(nc.Block())

        @block.vector
        def _(dve):
            ch = Chain(dve, s["own"])
            ch.link(dve.memset(epst[:, :], eps))
            with dve.Fori(0, NT // STEP) as i:
                for u in range(STEP):
                    ins = dve.bn_stats(st[:, i * STEP + u, :], xf[:, i * STEP + u, :])
                ch.enter(i, 1)
                ch.link(ins)
            ch.leave(NT // STEP)
            me, mo, ve, vo = (st[:, :, k] for k in (1, 4, 2, 5))
            ch.link(dve.tensor_tensor(mean[:, :], me, mo, ALU.add))
            ch.link(dve.tensor_tensor(std[:, :], me, mo, ALU.subtract))
            ch.link(dve.tensor_tensor(std[:, :], std[:, :], std[:, :], ALU.mult))
            ch.link(dve.tensor_tensor(var[:, :], ve, vo, ALU.add))
            ch.link(dve.tensor_scalar(mean[:, :], mean[:, :], 0.5, None, ALU.mult))
            ch.link(dve.tensor_scalar(var[:, :], var[:, :], 1.0 / C, None, ALU.mult))
            dve.scalar_tensor_tensor(var[:, :], std[:, :], 0.25, var[:, :], ALU.mult, ALU.add).then_inc(s["var_ready"], 1)
            dve.wait_ge(s["std_ready"], 1)
            ch.link(dve.reciprocal(rstd[:, :], std[:, :]))
            dve.scalar_tensor_tensor(shift[:, :], mean[:, :], -1.0, rstd[:, :], ALU.mult, ALU.mult).then_inc(s["shift_ready"], 1)
            with dve.Fori(0, BY_DVE // STEP) as i:
                for u in range(STEP):
                    n = bass.ds(i * STEP + u, 1)
                    dve.tensor_scalar(nf[:, n, :].rearrange("p n c -> p (n c)"), xf[:, n, :].rearrange("p n c -> p (n c)"), mean[:, n], rstd[:, n], ALU.subtract, ALU.mult)

        @block.scalar
        def _(act):
            act.wait_ge(s["var_ready"], 1)
            act.activation(std[:, :], var[:, :], ACT.Sqrt, bias=epst[:, :]).then_inc(s["std_ready"], 1)
            act.wait_ge(s["shift_ready"], 1)
            with act.Fori(BY_DVE // STEP, NT // STEP) as i:
                for u in range(STEP):
                    n = bass.ds(i * STEP + u, 1)
                    act.activation(nf[:, n, :].rearrange("p n c -> p (n c)"), xf[:, n, :].rearrange("p n c -> p (n c)"), ACT.Identity, scale=rstd[:, n], bias=shift[:, n])
    s.end()


def transpose_tokens(nc, name, XN, out_of, ident):
    with ExitStack() as ctx:
        stage = ctx.enter_context(nc.sbuf_tensor(name + "_stage", [P, 2, 4, C], F32))
        ps = ctx.enter_context(nc.psum_tensor(name + "_ps", [P, 2, 512], F32))
        s = Signals(nc, name, "staged turned stored")
        staged, turned, stored = s.all
        block = ctx.enter_context(nc.Block())

        @block.vector
        def _(dve):
            with dve.Fori(0, G // 4) as i:
                for u in range(2):
                    dve.wait_ge(turned, i * 2 + u + 1)
                    src = XN[:, bass.ds(i * 4 + 2 * u, 2), :, :].rearrange("p g t c -> p (g t) c")
                    dve.tensor_copy(stage[:, u, :, :], src).then_inc(staged, 1)

        @block.tensor
        def _(pe):
            pe.sem_inc(turned, 2)
            with pe.Fori(0, G // 4) as i:
                for u in range(2):
                    pe.wait_ge(staged, i * 2 + u + 1)
                    pe.wait_ge(stored, i * 2 + u + 1)
                    for t in range(4):
                        ins = pe.transpose(ps[:, u, t * 128:(t + 1) * 128], stage[:, u, t, :], ident[:, :])
                    ins.then_inc(turned, 1)

        @block.scalar
        def _(act):
            act.sem_inc(stored, 2)
            with act.Fori(0, G // 4) as i:
                for u in range(2):
                    act.wait_ge(turned, i * 2 + u + 3)
                    for g in range(2):
                        src = ps[:, u, g * 256:(g + 1) * 256].rearrange("c (t p) -> c t p", t=2)
                        ins = act.activation(out_of(i * 4 + 2 * u + g), src, ACT.Copy)
                    ins.then_inc(stored, 1)
    s.end()


def load_all(nc, name, pairs):
    s = Signals(nc, name, "loaded")
    with nc.Block() as block:
        @block.sync
        def _(sp):
            for dst, src in pairs:
                sp.dma_start(dst, src).then_inc(s["loaded"], 16)
            sp.wait_ge(s["loaded"], 16 * len(pairs))
    s.end()


def bias_rows(nc, ctx, name, biases):
    widths = [int(np.prod(b.shape)) for b in biases]
    total = sum(widths)
    rows = ctx.enter_context(nc.sbuf_tensor(name + "_bias", [P, total], F32R))
    ones = ctx.enter_context(nc.sbuf_tensor(name + "_ones", [P, P], F32R))
    with nc.sbuf_tensor(name + "_raw", [33, 2, total], F32) as raw, nc.sbuf_tensor(name + "_plain", [P, total], F32) as plain:
        at = [sum(widths[:i]) for i in range(len(widths))]
        load_all(nc, name + "_load", [(raw[r:r + 1, 0, a:a + n], b) for a, n, b in zip(at, widths, biases) for r in (0, 32)])
        s = Signals(nc, name, "cleared high kept")
        with nc.Block() as block:
            @block.vector
            def _(dve):
                dve.memset(plain[:, :], 0.0).then_inc(s["cleared"], 1)
                dve.wait_ge(s["cleared"], 1)
                dve.tensor_copy(rows[:, :], plain[:, :]).then_inc(s["cleared"], 1)
                dve.wait_ge(s["high"], 2)
                dve.tensor_tensor(rows[32:33, :], raw[32:33, 0, :], raw[32:33, 1, :].bitcast(F32R), ALU.subtract)
                n = min(P, total)
                for i in range(P // n):
                    dve.tensor_scalar(ones[:, i * n:(i + 1) * n], plain[:, 0:n], 1.0, None, ALU.add)

            @block.scalar
            def _(act):
                act.wait_ge(s["cleared"], 2)
                act.activation(rows[0:1, :], raw[0:1, 0, :], ACT.Copy).then_inc(s["high"], 1)
                act.activation(raw[32:33, 1, :].bitcast(F32R), raw[32:33, 0, :], ACT.Copy).then_inc(s["high"], 1)
        s.end()
    return ones, [rows[:, a:a + n] for a, n in zip(at, widths)]


R_ORDER = 384
NCH = S // R_ORDER
D2 = 2
NST = 16
DTR = 8
L2 = S // 2
SC = L2 // R_ORDER


def selective_scan_mixer(nc, xt_dram, x_in, x_out, w):
    with ExitStack() as ctx:
        def sb(name, shape, dt=F32):
            return ctx.enter_context(nc.sbuf_tensor("ss_" + name, shape, dt))

        win = sb("win", [P, 512])
        convw = sb("convw", [P, D2, 9])
        convb = sb("convb", [P, D2])
        xpw = sb("xpw", [P, D2, 4, 40])
        dtw = sb("dtw", [P, 4, 256])
        dtb = sb("dtb", [P, 4, D2])
        a_log = sb("a_log", [P, 4, D2, NST])
        a_neg = sb("a_neg", [P, 4, D2, NST])
        ds = sb("ds", [P, 4, D2])
        dsum = sb("dsum", [P, D2])
        ng = sb("ng", [P, D2])
        nb = sb("nb", [P, D2])
        wout = sb("wout", [P, D2, P])
        ident = sb("ident", [P, P])
        sel = sb("sel", [96, 32, P], BF16)
        warm = sb("warm", [P, 1])
        zero = sb("zero", [P, 512], BF16)
        over = sb("over", [P, P])
        eps = sb("eps", [P, 1])
        xb = sb("xb", [P, 18, C])
        xc = sb("xc", [P, 2, D2, S])
        y = sb("y", [P, D2, S])
        work = sb("work", [P, 22 * L2])
        XT = sb("xt", [P, S])
        bc3 = sb("bc3", [96, 2, L2], BF16)
        rest = sb("rest", [32, L2])
        mid = sb("mid", [32, L2], BF16)
        dtr = sb("dtr", [P, L2])
        last = sb("last", [P, D2, NST])
        ps = ctx.enter_context(nc.psum_tensor("ss_ps", [P, 8, 512], F32))

        def part(at, shape):
            n = int(np.prod(shape))
            names = "abcd"[:len(shape)]
            kw = {c: s for c, s in zip(names, shape)}
            return work[:, at * L2:at * L2 + n].rearrange(f"p ({' '.join(names)}) -> p {' '.join(names)}", **kw)

        xpad = part(0, [D2, 50, 50])
        decay, drive, hid, rep = part(0, [2, D2, L2]), part(4, [D2, L2]), part(6, [2, D2, L2]), part(10, [2, 2, L2])
        dt, dtu = part(14, [2, D2, L2]), part(18, [2, D2, L2])
        sq, sd, sz = part(0, [D2, S]), part(4, [S]), part(6, [D2, S])

        with nc.Block() as block:
            @block.vector
            def _(dve):
                dve.memset(dtw[:, :, :], 0.0)
                dve.memset(dtr[:, :], 0.0)

        load_all(nc, "ss_weights", [
            (win[:, :], w["win"]), (convw[:, :, :], w["convw"]), (convb[:, :], w["convb"]),
            (xpw[:, :, :, :], w["xpw"]), (dtw[0:DTR, :, :], w["dtw"]), (dtb[:, :, :], w["dtb"]),
            (a_log[:, :, :, :], w["a_log"]), (ds[:, :, :], w["ds"]), (ng[:, :], w["ng"]), (nb[:, :], w["nb"]),
            (wout[:, :, :], w["wout"]), (ident[:, :], w["ident"]), (sel[:, :, :], w["sel"])])

        s0 = Signals(nc, "ss0", "own exp_ready")
        own, exp_ready = s0["own"], s0["exp_ready"]
        with nc.Block() as block:

            @block.scalar
            def _(act):
                act.activation(a_neg[:, :, :, :], a_log[:, :, :, :], ACT.Exp).then_inc(exp_ready, 1)

            @block.vector
            def _(dve):
                ch = Chain(dve, own)
                dve.memset(zero[:, :], 0.0)
                dve.memset(over[:, :], 1.0 / 256)
                dve.memset(eps[:, :], 1e-5)
                ch.link(dve.tensor_tensor(dsum[:, :], ds[:, 0, :], ds[:, 1, :], ALU.add))
                for k in (2, 3):
                    ch.link(dve.tensor_tensor(dsum[:, :], dsum[:, :], ds[:, k, :], ALU.add))
                dve.wait_ge(exp_ready, 1)
                ch.link(dve.tensor_scalar(a_neg[:, :, :, :], a_neg[:, :, :, :], -1.0, None, ALU.mult))

        s0.end()
        s1 = Signals(nc, "ss1", "loaded projected padded cleared conv_own conv_done gated")
        sets = [Signals(nc, name, "bank_full bank_free dtr_ready split own exponent soft dt_ready decay_ready driven swept scanned weighted summed")
                for name in ("ssa", "ssb")]
        s3 = Signals(nc, "ss3", "mean centred squared varied sd_ready own normed affine zed zgated gated summed stored own_act")
        held = dict(ps=ps, xc=xc, y=y, xpw=xpw, dtw=dtw, dtb=dtb, a_neg=a_neg, sel=sel, zero=zero, warm=warm, ident=ident, decay=decay, drive=drive, hid=hid, rep=rep, dt=dt, dtu=dtu, bc3=bc3, rest=rest, mid=mid, dtr=dtr, last=last, xb=xb, over=over, eps=eps, ng=ng, nb=nb, win=win, wout=wout, XT=XT, x_out=x_out, sq=sq, sd=sd, sz=sz)

        with nc.Fori(0, B) as b:
            with nc.Block() as block:
                @block.sync
                def _(sp):
                    sp.dma_start(XT[:, :], xt_dram[:, bass.ds(b * S, S)]).then_inc(s1["loaded"], 16)
                    sp.dma_start(xb[:, :, :].rearrange("p n c -> p (n c)"), x_in[bass.ds(b * S, S), :].rearrange("(p n) c -> p (n c)", p=P)).then_inc(s1["loaded"], 16)
                    sp.wait_ge(s1["loaded"], 32)

                @block.gpsimd
                def _(pool):
                    pool.memset(xpad, 0.0).then_inc(s1["cleared"], 1)

                @block.tensor
                def _(pe):
                    pe.wait_ge(s1["loaded"], 32)
                    for n in range(D2 * NCH):
                        d, c = n // NCH, n % NCH
                        if n >= 8:
                            pe.wait_ge(s1["padded"], n - 7)
                        pe.matmul(ps[:, n % 8, 0:R_ORDER], win[:, d * P:(d + 1) * P],
                                  XT[:, c * R_ORDER:(c + 1) * R_ORDER], start=True, stop=True).then_inc(s1["projected"], 1)

                @block.scalar
                def _(act):
                    act.wait_ge(s1["cleared"], 1)
                    for n in range(D2 * NCH):
                        d, c = n // NCH, n % NCH
                        act.wait_ge(s1["projected"], n + 1)
                        act.activation(xpad[:, d, 1 + 8 * c:9 + 8 * c, 1:49],
                                       ps[:, n % 8, 0:R_ORDER].rearrange("p (h w) -> p h w", w=W), ACT.Copy).then_inc(s1["padded"], 1)
                    for d in range(D2):
                        act.wait_ge(s1["conv_done"], d + 1)
                        act.activation(xc[:, 0, d, :], y[:, d, :], ACT.Silu, bias=convb[:, d:d + 1]).then_inc(s1["gated"], 1)
                        act.wait_ge(s1["gated"], 2 * d + 1)
                        act.activation(xc[:, 1, d, :].rearrange("p (w h) -> p h w", h=H),
                                       xc[:, 0, d, :].rearrange("p (h w) -> p h w", w=W), ACT.Copy).then_inc(s1["gated"], 1)

                @block.vector
                def _(dve):
                    ch = Chain(dve, s1["conv_own"])
                    for d in range(D2):
                        dve.wait_ge(s1["padded"], NCH * (d + 1))
                        out = y[:, d, :].rearrange("p (h w) -> p h w", w=W)
                        for t in range(9):
                            tap = xpad[:, d, t // 3:t // 3 + H, t % 3:t % 3 + W]
                            if t == 0:
                                ch.link(dve.tensor_scalar(out, tap, convw[:, d, 0:1], None, ALU.mult))
                            else:
                                ins = dve.scalar_tensor_tensor(out, tap, convw[:, d, t:t + 1], out, ALU.mult, ALU.add)
                                if t < 8:
                                    ch.link(ins)
                        ins.then_inc(s1["conv_done"], 1)
                    for d in range(D2):
                        dve.wait_ge(s1["gated"], 2 * d + 1)
                        ins = dve.tensor_scalar(y[:, d, :], xc[:, 0, d, :], dsum[:, d:d + 1], None, ALU.mult)
            s1.clear()

            sections = [(k, half) for k in range(4) for half in ((0, 1) if k < 2 else (1, 0))]
            prepare_section(nc, sets[1], sections[0], held)
            for n, section in enumerate(sections):
                scan_section(nc, sets[n % 2], sets[1 - n % 2], n % 2, section, n % 2 == 0, sections[n + 1] if n + 1 < len(sections) else None, held)
            sets[1].clear()

            norm_gate_project(nc, s3, b, held)
            s3.clear()
        for s in (s1, *sets, s3):
            s.release()


def prepare_section(nc, s, section, v):
    ps, xc, xpw, dtw, dtb, dt, dtu = (v[n] for n in "ps xc xpw dtw dtb dt dtu".split())
    bc3, rest, mid, dtr = (v[n] for n in "bc3 rest mid dtr".split())
    k, half = section
    src = xc[:, k % 2, :, half * L2:(half + 1) * L2]
    R = R_ORDER

    with nc.Block() as block:
        @block.tensor
        def _(pe):
            for c in range(SC):
                for d in range(D2):
                    ins = pe.matmul(ps[0:40, c, 0:R], xpw[:, d, k, :], src[:, d, c * R:(c + 1) * R], start=d == 0, stop=d == 1)
                ins.then_inc(s["bank_full"], 1)
            for m in range(2 * SC):
                d, c = m // SC, m % SC
                pe.wait_ge(s["dtr_ready"], c + 1)
                if m >= 5:
                    pe.wait_ge(s["split"], SC)
                bank = 3 + m if m < 5 else 0
                pe.matmul(ps[:, bank, 0:R], dtw[:, k, d * P:(d + 1) * P], dtr[:, c * R:(c + 1) * R], start=True, stop=True).then_inc(s["bank_full"], 1)

        @block.scalar
        def _(act):
            for c in range(SC):
                act.wait_ge(s["bank_full"], c + 1)
                act.activation(dtr[0:DTR, c * R:(c + 1) * R], ps[32:40, c, 0:R], ACT.Copy).then_inc(s["dtr_ready"], 1)
            for m in range(2 * SC):
                d, c = m // SC, m % SC
                bank = 3 + m if m < 5 else 0
                act.wait_ge(s["bank_full"], SC + m + 1)
                act.activation(dtu[:, 0, d, c * R:(c + 1) * R], ps[:, bank, 0:R], ACT.Abs, bias=dtb[:, k, d:d + 1])
                act.activation(dt[:, 0, d, c * R:(c + 1) * R], ps[:, bank, 0:R], ACT.Relu, bias=dtb[:, k, d:d + 1]).then_inc(s["bank_free"], 1)
            act.wait_ge(s["bank_free"], 2 * SC)
            act.activation(dtu[:, 0, :, :], dtu[:, 0, :, :], ACT.Exp, scale=-1.0).then_inc(s["exponent"], 1)
            act.wait_ge(s["exponent"], 1)
            act.activation(dtu[:, 0, :, :], dtu[:, 0, :, :], ACT.Ln, bias=1.0).then_inc(s["soft"], 1)

        @block.vector
        def _(dve):
            ch = Chain(dve, s["own"])
            for c in range(SC):
                at = slice(c * R, (c + 1) * R)
                dve.wait_ge(s["bank_full"], c + 1)
                ch.link(dve.tensor_copy(bc3[0:32, 0, at], ps[0:32, c, 0:R]))
                dve.tensor_tensor(rest[:, at], ps[0:32, c, 0:R], bc3[0:32, 0, at], ALU.subtract).then_inc(s["split"], 1)
            dve.wait_ge(s["split"], SC)
            ch.link(dve.tensor_copy(mid[:, :], rest[:, :]))
            dve.tensor_copy(bc3[32:64, 0, :], mid[:, :])
            dve.tensor_tensor(bc3[64:96, 0, :], rest[:, :], mid[:, :], ALU.subtract)
            dve.wait_ge(s["soft"], 1)
            ch.link(dve.tensor_tensor(dt[:, 0, :, :], dt[:, 0, :, :], dtu[:, 0, :, :], ALU.add))
            dve.tensor_tensor(dtu[:, 0, :, :], dt[:, 0, :, :], src, ALU.mult)


def scan_section(nc, s, spent, slot, section, first, following, v):
    ps, xc, y, xpw, dtw, dtb, a_neg, sel, zero, ident = (v[n] for n in "ps xc y xpw dtw dtb a_neg sel zero ident".split())
    decay, drive, hid, rep, warm = (v[n] for n in "decay drive hid rep warm".split())
    bc3, rest, mid, dtr, last = (v[n] for n in "bc3 rest mid dtr last".split())
    dt, dtu, dt_next, dtu_next = v["dt"][:, slot], v["dtu"][:, slot], v["dt"][:, 1 - slot], v["dtu"][:, 1 - slot]
    k, half = section
    lo = half * L2
    step = -1 if k >= 2 else 1
    R = R_ORDER
    acc = ps[:, 0:5, :].rearrange("p b n -> p (b n)")
    bank = ps[:, 5:8, 0:R]
    cuts = sorted({0, L2, D2 * L2} | {n for n in range(0, D2 * L2, 512)})
    spans = list(zip(cuts, cuts[1:]))
    halves = [[(lo_, hi_) for lo_, hi_ in spans if lo_ // L2 == d] for d in range(D2)]
    whole_banks = [(n, min(n + 512, D2 * L2)) for n in range(0, D2 * L2, 512)]
    assert [len(h) for h in halves] == [SC, SC]
    if following:
        k_next, half_next = following
        src_next = xc[:, k_next % 2, :, half_next * L2:(half_next + 1) * L2]
    EXTRA = 3 if following else 0
    GROUPS = NST // 4
    assert GROUPS - 1 == SC

    def place(i, j, m):
        return i * (24 + EXTRA) + (6 * j + m + shift(i, j))

    def shift(i, j):
        return EXTRA // 3 if j == 3 and not (isinstance(i, int) and i == GROUPS - 1) else 0

    def chunk(ap, c):
        return ap[:, bass.ds(c * R, R)]

    with nc.Block() as block:
        @block.tensor
        def _(pe):
            pe.sem_inc(s["summed"], 4)
            for a, e in whole_banks:
                pe.matmul(acc[:, a:e], sel[:, 0, :], zero[0:96, 0:e - a], start=True, stop=False, skip_group_check=True)

            def rep_bank(i, j, m):
                pe.wait_ge(s["bank_free"], place(i, j, m) + 1)
                pe.matmul(bank[:, (m + shift(i, j)) % 3, :], sel[:, bass.ds(i * 4 + (j + 16 * (m // 3)), 1), :].rearrange("p a c -> p (a c)"),
                          bc3[:, slot, (m % 3) * R:(m % 3 + 1) * R], start=True, stop=True).then_inc(s["bank_full"], 1)

            def sum_bank(i, j, m):
                if m % SC == 0:
                    pe.wait_ge(s["weighted"], i * 8 + (2 * j + m // SC + 5))
                d, (a, e) = m // SC, halves[m // SC][m % SC]
                ins = pe.matmul(acc[:, a:e], ident[:, :], hid[:, j % 2, d, a - d * L2:e - d * L2], start=False, stop=False, skip_group_check=True)
                if m % SC == SC - 1:
                    ins.then_inc(s["summed"], 1)

            def rep_and_sum(i_rep, j_rep, i, j, after_split=False):
                for m in range(6):
                    rep_bank(i_rep, j_rep, m)
                    if m:
                        sum_bank(i, j, m - 1)
                    if after_split and m == 1:
                        pe.wait_ge(s["split"], i + 1)
                sum_bank(i, j, 5)

            def next_rows(i):
                pe.wait_ge(s["bank_free"], place(i, 2, 5) + 2)
                for d in range(D2):
                    ins = pe.matmul(bank[0:40, 0, :], xpw[:, d, k_next, :], chunk(src_next[:, d, :], i), start=d == 0, stop=d == 1)
                ins.then_inc(s["bank_full"], 1)

            def next_dt(i):
                pe.wait_ge(s["dtr_ready"], i + 1)
                for d in range(D2):
                    pe.wait_ge(s["bank_free"], place(i, 3, 5) + (2 + d))
                    pe.matmul(bank[:, 1 + d, :], dtw[:, k_next, d * P:(d + 1) * P], chunk(dtr, i), start=True, stop=True).then_inc(s["bank_full"], 1)

            for j in range(2):
                for m in range(6):
                    rep_bank(0, j, m)
            with pe.Fori(0, GROUPS - 1) as i:
                rep_and_sum(i, 2, i, 0)
                if following:
                    next_rows(i)
                rep_and_sum(i, 3, i, 1, after_split=bool(following))
                if following:
                    next_dt(i)
                rep_and_sum(i + 1, 0, i, 2)
                rep_and_sum(i + 1, 1, i, 3)
            rep_and_sum(GROUPS - 1, 2, GROUPS - 1, 0)
            rep_and_sum(GROUPS - 1, 3, GROUPS - 1, 1)
            for j in (2, 3):
                for m in range(6):
                    sum_bank(GROUPS - 1, j, m)
            for a, e in whole_banks:
                ins = pe.matmul(acc[:, a:e], sel[:, 0, :], zero[0:96, 0:e - a], start=False, stop=True, skip_group_check=True)
            ins.then_inc(s["summed"], 1)

        @block.scalar
        def _(act):
            act.sem_inc(s["bank_free"], 3)

            def rep_store(i, j, banks):
                for m in banks:
                    if m % 3 == 0:
                        act.wait_ge(s["weighted" if m else "scanned"], i * 8 + (2 * j + 2))
                    act.wait_ge(s["bank_full"], place(i, j, m) + 1)
                    act.activation(rep[:, j % 2, m // 3, (m % 3) * R:(m % 3 + 1) * R], bank[:, (m + shift(i, j)) % 3, :], ACT.Copy).then_inc(s["bank_free"], 1)

            def decays(i, j):
                for d in range(D2):
                    act.wait_ge(s["scanned"], i * 8 + (2 * j + d + 1))
                    act.activation(decay[:, j % 2, d, :], dt[:, d, :], ACT.Exp, scale=a_neg[:, k, d, bass.ds(i * 4 + j, 1)]).then_inc(s["decay_ready"], 1)

            def state(i, j):
                rep_store(i, j, (0, 1, 2))
                decays(i, j)
                rep_store(i, j, (3, 4, 5))
                if following and j == 2 and not (isinstance(i, int) and i == GROUPS - 1):
                    act.wait_ge(s["bank_full"], place(i, 2, 5) + 2)
                    act.activation(chunk(dtr[0:DTR, :], i), bank[32:40, 0, :], ACT.Copy).then_inc(s["dtr_ready"], 1)
                    act.wait_ge(s["dtr_ready"], i + 1)
                    act.sem_inc(s["bank_free"], 1)
                if following and j == 3 and not (isinstance(i, int) and i == GROUPS - 1):
                    for d in range(D2):
                        act.wait_ge(s["bank_full"], place(i, 3, 5) + (2 + d))
                        act.activation(chunk(dtu_next[:, d, :], i), bank[:, 1 + d, :], ACT.Abs, bias=dtb[:, k_next, d:d + 1])
                        act.activation(chunk(dt_next[:, d, :], i), bank[:, 1 + d, :], ACT.Relu, bias=dtb[:, k_next, d:d + 1]).then_inc(s["bank_free"], 1)

            act.activation(warm[:, :], zero[:, 0:1], ACT.Exp)
            with act.Fori(0, GROUPS - 1) as i:
                for j in range(4):
                    state(i, j)
            for j in range(4):
                state(GROUPS - 1, j)
                if following and j == 3:
                    act.wait_ge(s["bank_free"], 3 + place(GROUPS - 1, 0, 0))
                    act.activation(dtu_next, dtu_next, ACT.Exp, scale=-1.0).then_inc(s["exponent"], 1)
                    act.wait_ge(s["exponent"], 1)
                    act.activation(dtu_next, dtu_next, ACT.Ln, bias=1.0).then_inc(s["soft"], 1)

        @block.vector
        def _(dve):
            ch = Chain(dve, s["own"])
            dve.sem_inc(s["scanned"], 4)

            swept = s["swept"] if first else s["scanned"]
            if first:
                dve.sem_inc(swept, 4)

            def scan_state(i, j):
                dve.wait_ge(s["bank_free"], place(i, j, 2) + 4)
                for d in range(D2):
                    dve.wait_ge(swept, i * 8 + (2 * j + d + 3))
                    dve.tensor_tensor(drive[:, d, :], dtu[:, d, :], rep[:, j % 2, 0, :], ALU.mult).then_inc(s["driven"], 1)
                for d in range(D2):
                    dve.wait_ge(s["decay_ready"], i * 8 + (2 * j + d + 1))
                    dve.wait_ge(s["summed"], i * 8 + (2 * j + d + 1))
                    dve.wait_ge(s["driven"], i * 8 + (2 * j + d + 1))
                    start = 0.0 if first else last[:, d, bass.ds(i * 4 + j, 1)]
                    dve.tensor_tensor_scan(hid[:, j % 2, d, ::step], decay[:, j % 2, d, ::step], drive[:, d, ::step], start, ALU.mult, ALU.add).then_inc(swept, 1)
                if first:
                    for d in range(D2):
                        dve.wait_ge(swept, i * 8 + (2 * j + d + 5))
                        end = 0 if step < 0 else L2 - 1
                        dve.tensor_scalar(last[:, d, bass.ds(i * 4 + j, 1)], hid[:, j % 2, d, end:end + 1], 1.0, None, ALU.mult).then_inc(s["scanned"], 1)

            def split(i):
                dve.wait_ge(s["bank_full"], place(i, 2, 5) + 2)
                ch.link(dve.tensor_scalar(chunk(bc3[0:32, 1 - slot, :], i), bank[0:32, 0, :], 1.0, None, ALU.mult))
                ch.link(dve.tensor_tensor(chunk(rest, i), bank[0:32, 0, :], chunk(bc3[0:32, 1 - slot, :], i), ALU.subtract))
                dve.tensor_scalar(chunk(mid, i), chunk(rest, i), 1.0, None, ALU.mult).then_inc(s["split"], 1)

            with dve.Fori(0, GROUPS - 1) as i:
                if following:
                    ch.enter(i, 2)
                for j in range(4):
                    scan_state(i, j)
                    if following and j == 1:
                        split(i)
            for j in range(4):
                scan_state(GROUPS - 1, j)
                if following and j == 0:
                    dve.wait_ge(s["split"], SC)
                    dve.tensor_scalar(bc3[32:64, 1 - slot, :], mid[:, :], 1.0, None, ALU.mult)
                    dve.tensor_tensor(bc3[64:96, 1 - slot, :], rest[:, :], mid[:, :], ALU.subtract)
            if following:
                dve.wait_ge(s["soft"], 1)
                for d in range(D2):
                    dve.tensor_tensor(dt_next[:, d, :], dt_next[:, d, :], dtu_next[:, d, :], ALU.add).then_inc(s["dt_ready"], 1)
            dve.wait_ge(s["summed"], 2 * NST + 5)
            for d in range(D2):
                sums = acc[:, d * L2:(d + 1) * L2].rearrange("p (a b) -> p a b", b=48)
                if k % 2 == 0:
                    out = y[:, d, lo:lo + L2].rearrange("p (a b) -> p a b", b=48)
                else:
                    out = y[:, d, :].rearrange("p (h w) -> p w h", w=W)[:, lo // H:(lo + L2) // H, :]
                dve.tensor_tensor(out, out, sums, ALU.add)
            if following:
                dve.wait_ge(s["dt_ready"], 2)
                dve.tensor_tensor(dtu_next[:, 1, :], dt_next[:, 1, :], src_next[:, 1, :], ALU.mult)

        @block.gpsimd
        def _(pool):
            for signal in spent.all:
                pool.sem_clear(signal)
            pool.sem_inc(s["weighted"], 4)

            def weigh(i, j):
                pool.wait_ge(s["bank_free"], place(i, j, 5) + 4)
                for d in range(D2):
                    pool.wait_ge(s["scanned"], i * 8 + (2 * j + d + 5))
                    pool.tensor_tensor(hid[:, j % 2, d, :], hid[:, j % 2, d, :], rep[:, j % 2, 1, :], ALU.mult).then_inc(s["weighted"], 1)
            with pool.Fori(0, GROUPS - 1) as i:
                for j in range(4):
                    weigh(i, j)
            for j in range(4):
                weigh(GROUPS - 1, j)
            if following:
                pool.wait_ge(s["dt_ready"], 1)
                pool.tensor_tensor(dtu_next[:, 0, :], dt_next[:, 0, :], src_next[:, 0, :], ALU.mult)


def norm_gate_project(nc, s, b, v):
    ps, y, xb, over, eps, ng, nb, win, wout, XT, x_out = (v[n] for n in "ps y xb over eps ng nb win wout XT x_out".split())
    sq, sd, sz = v["sq"], v["sd"], v["sz"]
    R = R_ORDER
    flat = ps[:, 0:NCH, 0:R]

    def chunks(ap):
        return ap.rearrange("p (n r) -> p n r", r=R)

    with nc.Block() as block:
        @block.tensor
        def _(pe):
            for c in range(NCH):
                for d in range(D2):
                    ins = pe.matmul(flat[:, c, :], over[:, :], y[:, d, c * R:(c + 1) * R], start=d == 0, stop=d == 1)
            ins.then_inc(s["mean"], 1)
            pe.wait_ge(s["squared"], D2)
            for c in range(NCH):
                for d in range(D2):
                    ins = pe.matmul(flat[:, c, :], over[:, :], sq[:, d, c * R:(c + 1) * R], start=d == 0, stop=d == 1)
            ins.then_inc(s["varied"], 1)
            for d in range(D2):
                pe.wait_ge(s["sd_ready"], 1)
                if d:
                    pe.wait_ge(s["zgated"], 1)
                for c in range(NCH):
                    ins = pe.matmul(flat[:, c, :], win[:, (2 + d) * P:(3 + d) * P], XT[:, c * R:(c + 1) * R], start=True, stop=True)
                ins.then_inc(s["zed"], 1)
            pe.wait_ge(s["zgated"], 2)
            pe.wait_ge(s["gated"], 2)
            for n in range(18):
                for d in range(D2):
                    ins = pe.matmul(ps[:, n // 4, (n % 4) * P:(n % 4 + 1) * P], y[:, d, n::18], wout[:, d, :], start=d == 0, stop=d == 1)
            ins.then_inc(s["summed"], 1)

        @block.vector
        def _(dve):
            ch = Chain(dve, s["own"])
            dve.wait_ge(s["mean"], 1)
            for d in range(D2):
                dve.tensor_tensor(chunks(y[:, d, :]), chunks(y[:, d, :]), flat, ALU.subtract).then_inc(s["centred"], 1)
            dve.wait_ge(s["sd_ready"], 1)
            ch.link(dve.reciprocal(sd, sd))
            for d in range(D2):
                dve.tensor_tensor(y[:, d, :], y[:, d, :], sd, ALU.mult).then_inc(s["normed"], 1)
            for d in range(D2):
                dve.wait_ge(s["zgated"], d + 1)
                dve.wait_ge(s["affine"], d + 1)
                dve.tensor_tensor(y[:, d, :], y[:, d, :], sz[:, d, :], ALU.mult).then_inc(s["gated"], 1)
            dve.wait_ge(s["summed"], 1)
            for n in range(5):
                m = min(4, 18 - 4 * n)
                out = xb[:, 4 * n:4 * n + m, :]
                ins = dve.tensor_tensor(out, out, ps[:, n, 0:m * P].rearrange("p (n c) -> p n c", c=C), ALU.add)
                ins.then_inc(s["stored"], 1)

        @block.scalar
        def _(act):
            for d in range(D2):
                act.wait_ge(s["centred"], d + 1)
                act.activation(sq[:, d, :], y[:, d, :], ACT.Square).then_inc(s["squared"], 1)
            act.wait_ge(s["varied"], 1)
            act.activation(chunks(sd), flat, ACT.Sqrt, bias=eps[:, :]).then_inc(s["sd_ready"], 1)
            for d in range(D2):
                act.wait_ge(s["zed"], d + 1)
                act.activation(chunks(sz[:, d, :]), flat, ACT.Silu).then_inc(s["zgated"], 1)
            for d in range(D2):
                act.wait_ge(s["normed"], d + 1)
                act.activation(y[:, d, :], y[:, d, :], ACT.Identity, scale=ng[:, d:d + 1], bias=nb[:, d:d + 1]).then_inc(s["affine"], 1)

        @block.sync
        def _(sp):
            sp.wait_ge(s["stored"], 5)
            sp.dma_start(x_out[bass.ds(b * S, S), :].rearrange("(p n) c -> p (n c)", p=P), xb[:, :, :].rearrange("p n c -> p (n c)")).then_inc(s["mean"], 16)
            sp.wait_ge(s["mean"], 17)


def spread(ap, n):
    return bass.AP(ap.tensor, 0, [[0, P], [1, n]])


def add_channel_major(nc, name, X, Y, ident):
    with ExitStack() as ctx:
        stage = ctx.enter_context(nc.sbuf_tensor(name + "_stage", [P, 2, 4, P], F32))
        ps = ctx.enter_context(nc.psum_tensor(name + "_ps", [P, 2, 512], F32))
        s = Signals(nc, name, "staged turned added")
        with nc.Block() as block:
            @block.scalar
            def _(act):
                with act.Fori(0, G // 4) as i:
                    for u in range(2):
                        act.wait_ge(s["turned"], i * 2 + (u + 1))
                        act.activation(stage[:, u, :, :].rearrange("c (g t) p -> c t g p", t=2),
                                       Y[:, :, bass.ds((i * 4 + 2 * u) * P, 2 * P)].rearrange("c t (g p) -> c t g p", p=P),
                                       ACT.Copy).then_inc(s["staged"], 1)

            @block.tensor
            def _(pe):
                pe.sem_inc(s["turned"], 2)
                with pe.Fori(0, G // 4) as i:
                    for u in range(2):
                        pe.wait_ge(s["staged"], i * 2 + (u + 1))
                        pe.wait_ge(s["added"], i * 2 + (u + 1))
                        for t in range(4):
                            ins = pe.transpose(ps[:, u, t * P:(t + 1) * P], stage[:, u, t, :], ident[:, :])
                        ins.then_inc(s["turned"], 1)

            @block.vector
            def _(dve):
                dve.sem_inc(s["added"], 2)
                with dve.Fori(0, G // 4) as i:
                    for u in range(2):
                        dve.wait_ge(s["turned"], i * 2 + (u + 3))
                        out = X[:, bass.ds(i * 4 + 2 * u, 2), :, :].rearrange("p g t c -> p (g t c)")
                        dve.tensor_tensor(out, out, ps[:, u, :], ALU.add).then_inc(s["added"], 1)
        s.end()


NK = 16
CW = 384
NCW = HALF // CW
NEDGE = 4


def pieces(c):
    at, ends = c * CW, [HALF // 8, HALF // 4, HALF // 2, HALF]
    return [(max(lo, at) - at, min(hi, at + CW) - at, seg) for seg, (lo, hi) in enumerate(zip([0] + ends, ends)) if lo < at + CW and hi > at]


def spectral_unit(nc, x_dram, out_dram, w):
    def tokens(ap):
        return ap.rearrange("(g p t) c -> p g t c", p=P, t=2)

    with ExitStack() as ctx:
        def sb(name, shape, dt=F32):
            return ctx.enter_context(nc.sbuf_tensor("stu_" + name, shape, dt))

        ident = sb("ident", [P, P])
        wgt = sb("wgt", [P, NEDGE])
        wk = sb("wk", [P, NK, NEDGE])
        YT = sb("YT", [P, 2, G * P])
        with nc.sbuf_tensor("stu_u_high", [P, G, 2, C], F32R) as u_high, nc.sbuf_tensor("stu_u_low", [P, G, 2, C], F32R) as u_low:
            with nc.sbuf_tensor("stu_u", [P, G, 2, C], F32) as U:
                with nc.sbuf_tensor("stu_x", [P, G, 2, C], F32) as X:
                    load_all(nc, "stu_load", [(ident[:, :], w["ident"]), (X[:, :, :, :], tokens(x_dram))])
                    layer_norm(nc, "stu_ln", X, U, 1e-5)
                with nc.sbuf_tensor("stu_XT", [P, 2, G * P], F32) as XT:
                    transpose_tokens(nc, "stu_tr", U, lambda g: XT[:, :, bass.ds(g * P, P)], ident)
                    branch_weights(nc, w, wgt, wk)
                    autoregress(nc, w, XT, YT, wgt, U, u_high, u_low)
            convolve(nc, w, u_high, u_low, YT, wk)
        with nc.sbuf_tensor("stu_sum", [P, G, 2, C], F32) as X:
            load_all(nc, "stu_again", [(X[:, :, :, :], tokens(x_dram))])
            add_channel_major(nc, "stu_add", X, YT, ident)
            load_all(nc, "stu_store", [(tokens(out_dram), X[:, :, :, :])])


def branch_weights(nc, w, wgt, wk):
    with ExitStack() as ctx:
        def sb(name, shape):
            return ctx.enter_context(nc.sbuf_tensor("bw_" + name, shape, F32))
        lw, gum, sig, e = sb("lw", [P, 4]), sb("gum", [P, 4]), sb("sig", [P, NK]), sb("e", [P, 4])
        mx, total, hard, count = sb("mx", [P, 1]), sb("total", [P, 1]), sb("hard", [P, 4]), sb("count", [P, 4])
        ones = sb("ones", [P, 4])
        load_all(nc, "bw_load", [(lw[:, :], spread(w["log_weights"], 4)), (gum[:, :], spread(w["gumbel"], 4)),
                                 (sig[:, :], spread(w["sigma"], NK))])
        s = Signals(nc, "bw", "own max_ready exp_ready root")
        with nc.Block() as block:
            @block.vector
            def _(dve):
                ch = Chain(dve, s["own"])
                dve.memset(ones[:, :], 1.0)
                ch.link(dve.tensor_tensor(lw[:, :], lw[:, :], gum[:, :], ALU.add))
                dve.tensor_reduce(mx[:, :], lw[:, :], AX.X, ALU.max, negate=True).then_inc(s["max_ready"], 1)
                dve.wait_ge(s["exp_ready"], 1)
                ch.link(dve.reciprocal(total[:, :], total[:, :]))
                ch.link(dve.tensor_scalar(e[:, :], e[:, :], total[:, :], None, ALU.mult))
                ch.link(dve.tensor_reduce(mx[:, :], e[:, :], AX.X, ALU.max))
                ch.link(dve.tensor_scalar(hard[:, :], e[:, :], mx[:, :], None, ALU.is_equal))
                ch.link(dve.tensor_tensor_scan(count[:, :], ones[:, :], hard[:, :], 0.0, ALU.mult, ALU.add))
                ch.link(dve.tensor_scalar(count[:, :], count[:, :], 1.0, None, ALU.is_equal))
                ch.link(dve.tensor_tensor(hard[:, :], hard[:, :], count[:, :], ALU.mult))
                ch.link(dve.tensor_tensor(wgt[:, :], hard[:, :], e[:, :], ALU.subtract))
                ch.link(dve.tensor_tensor(wgt[:, :], wgt[:, :], e[:, :], ALU.add))
                dve.wait_ge(s["root"], 2)
                for n in range(NEDGE):
                    dve.tensor_scalar(wk[:, :, n], sig[:, :], wgt[:, n:n + 1], None, ALU.mult)

            @block.scalar
            def _(act):
                act.wait_ge(s["max_ready"], 1)
                act.activation(e[:, :], lw[:, :], ACT.Exp, bias=mx[:, :], accum_out=total[:, :]).then_inc(s["exp_ready"], 1)
                act.activation(sig[:, :], sig[:, :], ACT.Sqrt).then_inc(s["root"], 1)
                act.wait_ge(s["root"], 1)
                act.activation(sig[:, :], sig[:, :], ACT.Sqrt).then_inc(s["root"], 1)
        s.end()


def autoregress(nc, w, XT, YT, wgt, U, u_high, u_low):
    with ExitStack() as ctx:
        mu = ctx.enter_context(nc.sbuf_tensor("ar_mu", [P, 3, NEDGE, P], F32))
        eff = ctx.enter_context(nc.sbuf_tensor("ar_eff", [P, 3, NEDGE, P], F32))
        ps = ctx.enter_context(nc.psum_tensor("ar_ps", [P, 8, 512], F32))
        load_all(nc, "ar_load", [(mu[:, n, :, :], w["M_u"][n]) for n in range(3)])
        s = Signals(nc, "ar", "own ready made kept cut")
        with nc.Block() as block:
            @block.gpsimd
            def _(pool):
                pool.wait_ge(s["cut"], 1)
                pool.tensor_tensor(u_low[:, 0:G // 2, :, :], U[:, 0:G // 2, :, :], u_high[:, 0:G // 2, :, :], ALU.subtract)

            @block.vector
            def _(dve):
                ch = Chain(dve, s["own"])
                ch.link(dve.tensor_scalar(eff[:, :, 3, :], mu[:, :, 0, :], wgt[:, 0:1], None, ALU.mult))
                for n in (1, 2, 3):
                    ch.link(dve.scalar_tensor_tensor(eff[:, :, 3 - n, :], mu[:, :, n, :], wgt[:, n:n + 1], eff[:, :, 4 - n, :], ALU.mult, ALU.add))
                dve.sem_inc(s["ready"], 1)
                dve.wait_ge(s["cut"], 1)
                dve.tensor_tensor(u_low[:, G // 2:, :, :], U[:, G // 2:, :, :], u_high[:, G // 2:, :, :], ALU.subtract)

            @block.tensor
            def _(pe):
                pe.wait_ge(s["ready"], 1)
                with pe.Fori(0, B) as b:
                    for n in range(2 * NCW):
                        q, c = n % 2, n // 2
                        pe.wait_ge(s["kept"], b * (2 * NCW) + (n + 1))
                        for lo, hi, seg in pieces(c):
                            for back in range(3):
                                parity, shift = (q - back) % 2, -((q - back) // 2)
                                skip = shift if c == 0 and lo == 0 else 0
                                at = b * HALF + (c * CW + lo - shift + skip)
                                ins = pe.matmul(ps[:, n, lo + skip:hi], eff[:, back, seg, :],
                                                XT[:, parity, bass.ds(at, hi - lo - skip)],
                                                start=back == 0, stop=back == 2, skip_group_check=True)
                        ins.then_inc(s["made"], 1)

            @block.scalar
            def _(act):
                act.activation(u_high[:, :, :, :], U[:, :, :, :], ACT.Copy).then_inc(s["cut"], 1)
                act.sem_inc(s["kept"], 2 * NCW)
                with act.Fori(0, B) as b:
                    for n in range(2 * NCW):
                        act.wait_ge(s["made"], b * (2 * NCW) + (n + 1))
                        act.activation(YT[:, n % 2, bass.ds(b * HALF + (n // 2) * CW, CW)], ps[:, n, 0:CW], ACT.Copy).then_inc(s["kept"], 1)
        s.end()


def convolve(nc, w, u_high, u_low, YT, wk):
    UNITS = B * NCW * 2
    with ExitStack() as ctx:
        def sb(name, shape):
            return ctx.enter_context(nc.sbuf_tensor("cv_" + name, shape, F32))
        def sbr(name, shape):
            return ctx.enter_context(nc.sbuf_tensor("cv_" + name, shape, F32R))
        even, odd = sb("even", [P, HALF]), sb("odd", [P, HALF + 1])
        mp, mm = sb("mp", [P, 2, NEDGE, P]), sb("mm", [P, 2, NEDGE, P])
        even_high, odd_high = sbr("even_high", [P, 2, HALF]), sbr("odd_high", [P, 2, HALF + 1])
        even_low, odd_low = sbr("even_low", [P, 2, HALF]), sbr("odd_low", [P, 2, HALF + 1])
        total = sb("total", [P, NEDGE, P])
        one = sb("one", [P, 1])
        eff = sb("eff", [P, 2, NEDGE, P])
        eff_high, eff_low = sbr("eff_high", [P, 2, 2, NEDGE, P]), sbr("eff_low", [P, 2, 2, NEDGE, P])
        uk_high, uk_low = sbr("uk_high", [P, 3, 2, CW]), sbr("uk_low", [P, 3, 2, CW])
        ps = ctx.enter_context(nc.psum_tensor("cv_ps", [P, 8, 512], F32))
        s = Signals(nc, "cv", "filter0 filter1 matrix0 matrix1 filter_used matrix_used eff_ready own convolved kept lowered mixed added filter_halved filter_split filled")
        filt, matr = (s["filter0"], s["filter1"]), (s["matrix0"], s["matrix1"])
        rows = P + HALF
        units = [(b, c, q) for b in range(B) for c in reversed(range(NCW)) for q in range(2)]

        with nc.Block() as block:
            @block.sync
            def _(sp):
                with sp.Fori(0, NK // 2) as i:
                    for u in range(2):
                        k = i * 2 + u
                        sp.wait_ge(s["filter_split"], k * 2 + 2)
                        sp.dma_start(even[:, :], bass.AP(w["phi_even"].tensor, k * rows, [[1, P], [1, HALF]])).then_inc(filt[u], 16)
                        sp.dma_start(odd[:, :], bass.AP(w["phi_odd"].tensor, k * rows, [[1, P], [1, HALF + 1]])).then_inc(filt[u], 16)
                        sp.wait_ge(s["matrix_used"], k + 1)
                        sp.dma_start(mp[:, u, :, :].rearrange("d n e -> d (n e)"), w["M_plus"][bass.ds(k, 1)].rearrange("k d n e -> (k d) (n e)")).then_inc(matr[u], 16)
                        sp.dma_start(mm[:, u, :, :].rearrange("d n e -> d (n e)"), w["M_minus"][bass.ds(k, 1)].rearrange("k d n e -> (k d) (n e)")).then_inc(matr[u], 16)

            @block.tensor
            def _(pe):
                pe.sem_inc(s["filter_used"], 2)
                pe.sem_inc(s["mixed"], 3)
                with pe.Fori(0, NK // 2) as i:
                    for u in range(2):
                        k = i * 2 + u
                        pe.wait_ge(s["filter_split"], k * 2 + 4)

                        def conv(n):
                            b, c, q = units[n]
                            pe.wait_ge(s["kept"], k * UNITS + (n + 1))
                            pe.wait_ge(s["lowered"], k * UNITS + (n + 1))
                            blocks = [g for g in range(GB) if g * P < (c + 1) * CW]
                            for kind in range(2):
                                for g in blocks:
                                    off = max(0, g * P - c * CW)
                                    lag = c * CW + off - g * P
                                    filters = ((even_high, even_low), (odd_high, odd_low))[kind]
                                    from_, parity = (lag, q) if kind == 0 else (lag + q, 1 - q)
                                    for turn, (a, f) in enumerate(((0, 0), (0, 1), (1, 0))):
                                        ins = pe.matmul(ps[:, 2 * (n % 3) + kind, off:CW], (u_high, u_low)[a][:, b * GB + g, parity, :],
                                                        filters[f][:, u, ::-1][:, from_:from_ + CW - off],
                                                        start=g == 0 and turn == 0, stop=g == blocks[-1] and turn == 2, skip_group_check=True)
                            ins.then_inc(s["convolved"], 1)

                        def mix(n):
                            b, c, q = units[n]
                            if n == 0:
                                pe.wait_ge(s["eff_ready"], k + 1)
                            pe.wait_ge(s["kept"], k * UNITS + (n + 4))
                            pe.wait_ge(s["lowered"], k * UNITS + (n + 4))
                            pe.wait_ge(s["added"], k * UNITS + (n + 1))
                            for lo, hi, seg in pieces(c):
                                for kind in range(2):
                                    for turn, (m, x) in enumerate(((eff_high, uk_high), (eff_high, uk_low), (eff_low, uk_high))):
                                        ins = pe.matmul(ps[:, 6 + n % 2, lo:hi], m[:, u, kind, seg, :], x[:, n % 3, kind, lo:hi],
                                                        start=kind == 0 and turn == 0, stop=kind == 1 and turn == 2, skip_group_check=True)
                            ins.then_inc(s["mixed"], 1)
                            return ins

                        for n in range(UNITS):
                            conv(n)
                            if n >= 2:
                                mix(n - 2)
                        mix(UNITS - 2)
                        mix(UNITS - 1)
                        pe.wait_ge(s["mixed"], k * UNITS + (UNITS + 3))
                        pe.sem_inc(s["filter_used"], 1)

            @block.scalar
            def _(act):
                act.sem_inc(s["kept"], 3)
                with act.Fori(0, NK) as k:
                    for n in range(UNITS):
                        act.wait_ge(s["convolved"], k * UNITS + (n + 1))
                        act.wait_ge(s["mixed"], k * UNITS + (n + 1))
                        at = 2 * (n % 3)
                        act.activation(uk_high[:, n % 3, :, :], ps[:, at:at + 2, 0:CW], ACT.Copy).then_inc(s["kept"], 1)

            @block.gpsimd
            def _(pool):
                pool.memset(one[:, :], 1.0).then_inc(s["filled"], 1)
                pool.wait_ge(s["filled"], 1)
                pool.sem_inc(s["filter_split"], 2)
                with pool.Fori(0, NK // 2) as i:
                    for u in range(2):
                        k = i * 2 + u
                        pool.wait_ge(filt[u], i * 32 + 32)
                        pool.wait_ge(s["filter_used"], k + 1)
                        for n, (raw, high, low) in enumerate(((even, even_high, even_low), (odd, odd_high, odd_low))):
                            pool.tensor_tensor(high[:, u, :], raw[:, :], bc(one[:, :], [P, HALF + n]), ALU.mult).then_inc(s["filter_halved"], 1)
                            pool.wait_ge(s["filter_halved"], k * 2 + (n + 1))
                            pool.tensor_tensor(low[:, u, :], raw[:, :], high[:, u, :], ALU.subtract).then_inc(s["filter_split"], 1)

            @block.vector
            def _(dve):
                dve.sem_inc(s["matrix_used"], 2)
                dve.sem_inc(s["added"], 2)
                dve.sem_inc(s["lowered"], 3)
                ch = Chain(dve, s["own"])

                def sum_matrices(step, k, slot, loads):
                    both = tuple(enumerate((total[:, :, :], mm[:, slot, :, :])))
                    if step == 0:
                        dve.wait_ge(matr[slot], loads)
                        dve.wait_ge(s["filter_used"], k + 1)
                        dve.tensor_tensor(total[:, :, :], mp[:, slot, :, :], mm[:, slot, :, :], ALU.add)
                        ch.link(dve.tensor_tensor(mm[:, slot, :, :], mp[:, slot, :, :], mm[:, slot, :, :], ALU.subtract))
                    elif step == 1:
                        for kind, m in both:
                            ins = dve.tensor_scalar(eff[:, kind, 3, :], m[:, 0, :], wk[:, bass.ds(k, 1), 0], None, ALU.mult)
                        ch.link(ins)
                    elif step <= 4:
                        n = step - 1
                        for kind, m in both:
                            ins = dve.scalar_tensor_tensor(eff[:, kind, 3 - n, :], m[:, n, :], wk[:, bass.ds(k, 1), n],
                                                           eff[:, kind, 4 - n, :], ALU.mult, ALU.add)
                        ch.link(ins)
                    elif step == 5:
                        ch.link(dve.tensor_copy(eff_high[:, slot, :, :, :], eff[:, :, :, :]))
                    else:
                        ch.link(dve.tensor_tensor(eff_low[:, slot, :, :, :], eff[:, :, :, :], eff_high[:, slot, :, :, :], ALU.subtract))
                        dve.sem_inc(s["eff_ready"], 1)
                        dve.sem_inc(s["matrix_used"], 1)

                def add_units(k, u, following):
                    def lower(n):
                        dve.wait_ge(s["kept"], k * UNITS + (n + 4))
                        at = 2 * (n % 3)
                        dve.tensor_tensor(uk_low[:, n % 3, :, :], ps[:, at:at + 2, 0:CW], uk_high[:, n % 3, :, :], ALU.subtract).then_inc(s["lowered"], 1)

                    dve.wait_ge(s["added"], k * UNITS + 2)
                    lower(0)
                    lower(1)
                    for n in range(UNITS):
                        if n + 2 < UNITS:
                            lower(n + 2)
                        b, c, q = units[n]
                        dve.wait_ge(s["mixed"], k * UNITS + (n + 4))
                        out = YT[:, q, b * HALF + c * CW:b * HALF + (c + 1) * CW]
                        dve.tensor_tensor(out, out, ps[:, 6 + n % 2, 0:CW], ALU.add).then_inc(s["added"], 1)
                        if following is not None and n >= 8 and n % 2 == 0 and (n - 8) // 2 < 7:
                            sum_matrices((n - 8) // 2, k + 1, 1 - u, following)

                for step in range(7):
                    sum_matrices(step, 0, 0, 32)
                with dve.Fori(0, NK // 2 - 1) as i:
                    ch.enter(i, 14)
                    add_units(i * 2, 0, i * 32 + 32)
                    add_units(i * 2 + 1, 1, i * 32 + 64)
                ch.leave(NK // 2 - 1)
                add_units(NK - 2, 0, (NK // 2) * 32)
                add_units(NK - 1, 1, None)
        s.end()


NF = H // 2 + 1
NR = B * H
NW = 5


def fourier_mixer(nc, X, xn_dram, w):
    with ExitStack() as ctx:
        def sb(name, shape, dt=F32):
            return ctx.enter_context(nc.sbuf_tensor("ff_" + name, shape, dt))

        with nc.sbuf_tensor("ff_xn", [P, G, 2, C], F32) as XN:
            layer_norm(nc, "ff_ln", X, XN, 1e-6)
            load_all(nc, "ff_store", [(xn_dram.rearrange("(g p t) c -> p g t c", p=P, t=2), XN[:, :, :, :])])
        ident = sb("ident", [P, P])
        dft = sb("dft", [W, 3 * NF])
        idft = sb("idft", [P, W])
        HT = sb("HT", [P, T])
        with nc.Block() as block:
            @block.vector
            def _(dve):
                dve.memset(idft[:, :], 0.0)
        load_all(nc, "ff_load", [(ident[:, :], w["ident"]), (dft[:, :], w["dft"]), (idft[0:2 * NF, :], w["idft"])])
        with nc.sbuf_tensor("ff_mx", [P, NR, 2 * NF], F32) as mixed:
            for axis in range(2):
                with nc.sbuf_tensor(f"ff_fx{axis}", [P, 3, NF, NR], F32) as spectrum:
                    transform_rows(nc, f"ffa{axis}", axis, xn_dram, dft, spectrum)
                    mix_modes(nc, f"ffb{axis}", w["fw"][axis], spectrum, mixed)
                inverse_rows(nc, f"ffc{axis}", axis, idft, ident, mixed, HT)
        row_mlp(nc, w, HT, X)


def transform_rows(nc, name, axis, xn_dram, dft, spectrum):
    with ExitStack() as ctx:
        rows = ctx.enter_context(nc.sbuf_tensor(name + "_rows", [W, H, C], F32))
        ps = ctx.enter_context(nc.psum_tensor(name + "_ps", [P, 8, 512], F32))
        s = Signals(nc, name, "loaded0 loaded1 made kept")
        loaded = s.all[:2]
        flat = spectrum[:, :, :, :].rearrange("c m f r -> c (m f) r")
        with nc.Block() as block:
            @block.sync
            def _(sp):
                for b in range(B):
                    img = xn_dram[b * S:(b + 1) * S, :]
                    src = img.rearrange("(h w) c -> w h c", w=W) if axis == 0 else img.rearrange("(h w) c -> h w c", w=W)
                    for half in range(2):
                        if b:
                            sp.wait_ge(s["made"], 8 * b - 4 + 4 * half)
                        part = slice(half * H // 2, (half + 1) * H // 2)
                        sp.dma_start(rows[:, part, :], src[:, part, :]).then_inc(loaded[half], 16)

            @block.tensor
            def _(pe):
                with pe.Fori(0, B) as b:
                    for n in range(8):
                        if n % 4 == 0:
                            pe.wait_ge(loaded[n // 4], b * 16 + 16)
                        pe.wait_ge(s["kept"], b * 8 + (n + 1))
                        for r in range(6):
                            ins = pe.matmul(ps[:, n, r * 3 * NF:(r + 1) * 3 * NF], rows[:, 6 * n + r, :], dft[:, :], start=True, stop=True)
                        ins.then_inc(s["made"], 1)

            @block.scalar
            def _(act):
                act.sem_inc(s["kept"], 8)
                with act.Fori(0, B) as b:
                    for n in range(8):
                        act.wait_ge(s["made"], b * 8 + (n + 1))
                        act.activation(flat[:, :, bass.ds(b * H + 6 * n, 6)],
                                       ps[:, n, 0:18 * NF].rearrange("c (r m) -> c m r", r=6), ACT.Copy).then_inc(s["kept"], 1)
        s.end()


def mix_modes(nc, name, fw, spectrum, mixed):
    with ExitStack() as ctx:
        wt = ctx.enter_context(nc.sbuf_tensor(name + "_w", [P, NW, 2, C], F32))
        ps = ctx.enter_context(nc.psum_tensor(name + "_ps", [P, NW, 512], F32))
        s = Signals(nc, name, " ".join(f"loaded{u}" for u in range(NW)) + " made kept")
        loaded = s.all[:NW]
        with nc.Block() as block:
            @block.sync
            def _(sp):
                with sp.Fori(0, NF // NW) as i:
                    for u in range(NW):
                        sp.wait_ge(s["made"], i * NW + (u + 1))
                        sp.dma_start(wt[:, u, :, :].rearrange("c m o -> c (m o)"), fw[bass.ds((i * NW + u) * P, P), :]).then_inc(loaded[u], 16)

            @block.tensor
            def _(pe):
                pe.sem_inc(s["made"], NW)
                with pe.Fori(0, NF // NW) as i:
                    for u in range(NW):
                        pe.wait_ge(loaded[u], i * 16 + 16)
                        pe.wait_ge(s["kept"], i * NW + (u + 1))
                        for m in range(2):
                            rhs = spectrum[:, 1 - m:3 - m, bass.ds(i * NW + u, 1), :].rearrange("c m f r -> c m (f r)")
                            ins = pe.matmul(ps[:, u, 0:2 * NR].rearrange("c (m r) -> c m r", m=2), wt[:, u, m, :], rhs, start=m == 0, stop=m == 1)
                        ins.then_inc(s["made"], 1)

            @block.vector
            def _(dve):
                dve.sem_inc(s["kept"], NW)
                with dve.Fori(0, NF // NW) as i:
                    for u in range(NW):
                        dve.wait_ge(s["made"], i * NW + (NW + u + 1))
                        out = mixed[:, :, :].rearrange("c r (m f) -> c m f r", m=2)[:, :, bass.ds(i * NW + u, 1), :].rearrange("c m f r -> c m (f r)")
                        dve.tensor_copy(out, ps[:, u, 0:2 * NR].rearrange("c (m r) -> c m r", m=2)).then_inc(s["kept"], 1)
        s.end()


def inverse_rows(nc, name, axis, idft, ident, mixed, HT):
    with ExitStack() as ctx:
        stage = ctx.enter_context(nc.sbuf_tensor(name + "_stage", [P, H, P], F32))
        modes = ctx.enter_context(nc.sbuf_tensor(name + "_modes", [P, H, C], F32))
        ps = ctx.enter_context(nc.psum_tensor(name + "_ps", [P, 8, 512], F32))
        s = Signals(nc, name, "padded staged turned kept made added")
        with nc.Block() as block:
            @block.gpsimd
            def _(pool):
                pool.memset(stage[:, :, 2 * NF:], 0.0).then_inc(s["padded"], 1)

            @block.scalar
            def _(act):
                act.sem_inc(s["kept"], 2)
                with act.Fori(0, B) as b:
                    act.wait_ge(s["turned"], b * 12 + 1)
                    act.activation(stage[:, :, 0:2 * NF], mixed[:, bass.ds(b * H, H), :], ACT.Copy).then_inc(s["staged"], 1)
                    act.wait_ge(s["made"], b * 6 + 1)
                    for n in range(12):
                        act.wait_ge(s["turned"], b * 12 + (n + 2))
                        act.activation(modes[:, 4 * n:4 * n + 4, :], ps[:, n % 2, :].rearrange("m (r c) -> m r c", c=C), ACT.Copy).then_inc(s["kept"], 1)

            @block.tensor
            def _(pe):
                pe.sem_inc(s["turned"], 1)
                pe.sem_inc(s["made"], 1)
                pe.wait_ge(s["padded"], 1)
                with pe.Fori(0, B) as b:
                    pe.wait_ge(s["staged"], b + 1)
                    for n in range(13):
                        if n < 12:
                            pe.wait_ge(s["kept"], b * 12 + (n + 1))
                            for r in range(4):
                                ins = pe.transpose(ps[:, n % 2, r * P:(r + 1) * P], stage[:, 4 * n + r, :], ident[:, :])
                            ins.then_inc(s["turned"], 1)
                        if n >= 2 and n % 2 == 0:
                            j = n // 2 - 1
                            pe.wait_ge(s["kept"], b * 12 + (2 * j + 4))
                            pe.wait_ge(s["added"], b * 6 + (j + 1))
                            for r in range(8):
                                ins = pe.matmul(ps[:, 2 + j, r * W:(r + 1) * W], modes[:, 8 * j + r, :], idft[:, :], start=True, stop=True)
                            ins.then_inc(s["made"], 1)

            @block.vector
            def _(dve):
                dve.sem_inc(s["added"], 6)
                with dve.Fori(0, B) as b:
                    for j in range(6):
                        dve.wait_ge(s["made"], b * 6 + (j + 2))
                        if axis == 0:
                            dve.tensor_copy(HT[:, bass.ds(b * S + j * 384, 384)], ps[:, 2 + j, 0:384]).then_inc(s["added"], 1)
                        else:
                            out = HT[:, bass.ds(b * S, S)].rearrange("c (h w) -> c w h", w=W)[:, 8 * j:8 * j + 8, :]
                            dve.tensor_tensor(out, out, ps[:, 2 + j, 0:384].rearrange("c (w h) -> c w h", h=H), ALU.add).then_inc(s["added"], 1)
        s.end()


def row_mlp(nc, w, HT, X):
    with ExitStack() as ctx:
        def sb(name, shape):
            return ctx.enter_context(nc.sbuf_tensor("mlp_" + name, shape, F32))
        w1, w2, b1 = sb("w1", [P, 512]), sb("w2", [P, 4, C]), sb("b1", [P, 4])
        ones, (b2,) = bias_rows(nc, ctx, "mlp_b", [w["b2"]])
        hid = sb("hid", [P, 2, 4, 256])
        ps = ctx.enter_context(nc.psum_tensor("mlp_ps", [P, 8, 512], F32))
        load_all(nc, "mlp_load", [(w1[:, :], w["w1"]), (w2[:, :, :], w["w2"]), (b1[:, :], w["b1"])])
        s = Signals(nc, "mlp", "made hid_ready done added")
        with nc.Block() as block:
            @block.tensor
            def _(pe):
                pe.sem_inc(s["done"], 2)
                with pe.Fori(0, G // 2) as i:
                    for u in range(2):
                        pe.wait_ge(s["hid_ready"], i * 2 + (u + 1))
                        for n in range(4):
                            ins = pe.matmul(ps[:, 2 * u + n // 2, (n % 2) * 256:(n % 2) * 256 + 256], w1[:, n * P:(n + 1) * P],
                                            HT[:, bass.ds((i * 2 + u) * 256, 256)], start=True, stop=True)
                        ins.then_inc(s["made"], 1)
                    for u in range(2):
                        pe.wait_ge(s["hid_ready"], i * 2 + (u + 3))
                        pe.wait_ge(s["added"], i * 2 + (u + 1))
                        for t in range(2):
                            for n in range(4):
                                pe.matmul(ps[:, 4 + u, t * C:(t + 1) * C], hid[:, u, n, t::2], w2[:, n, :], start=n == 0, stop=False)
                            ins = pe.matmul(ps[:, 4 + u, t * C:(t + 1) * C], ones[:, :], b2, start=False, stop=True)
                        ins.then_inc(s["done"], 1)

            @block.scalar
            def _(act):
                act.sem_inc(s["hid_ready"], 2)
                with act.Fori(0, G // 2) as i:
                    for u in range(2):
                        act.wait_ge(s["made"], i * 2 + (u + 1))
                        act.wait_ge(s["done"], i * 2 + (u + 1))
                        for n in range(4):
                            ins = act.activation(hid[:, u, n, :], ps[:, 2 * u + n // 2, (n % 2) * 256:(n % 2) * 256 + 256], ACT.Relu, bias=b1[:, n:n + 1])
                        ins.then_inc(s["hid_ready"], 1)

            @block.vector
            def _(dve):
                dve.sem_inc(s["added"], 2)
                with dve.Fori(0, G // 2) as i:
                    for u in range(2):
                        dve.wait_ge(s["done"], i * 2 + (u + 3))
                        out = X[:, bass.ds(i * 2 + u, 1), :, :].rearrange("p g t c -> p (g t c)")
                        dve.tensor_tensor(out, out, ps[:, 4 + u, 0:256], ALU.add).then_inc(s["added"], 1)
        s.end()


NE = 64
GE = 4
LOWEST = -3.0e38


def expert_choice(nc, name, X, w):
    with ExitStack() as ctx:
        def sb(n, shape, dt=F32):
            return ctx.enter_context(nc.sbuf_tensor(f"{name}_{n}", shape, dt))

        ident = sb("ident", [P, P])
        weights = sb("weights", [NE, T])
        pooled = sb("pooled", [P, NE, B])
        load_all(nc, name + "_load", [(ident[:, :], w["ident"])])
        with nc.sbuf_tensor(name + "_xn", [P, G, 2, C], F32) as XN:
            layer_norm(nc, name + "_ln", X, XN, 1e-5)
            with nc.sbuf_tensor(name + "_xt", [P, T], F32) as XT:
                transpose_tokens(nc, name + "_tr", XN, lambda g: XT[:, bass.ds(g * 256, 256)].rearrange("c (p t) -> c t p", t=2), ident)
                expert_weights(nc, name + "w", w, XT, weights)
            pool_tokens(nc, name + "p", XN, weights, ident, pooled)
        outs = sb("outs", [B, NE, C])
        expert_layers(nc, name + "e", w, pooled, outs)
        scatter_tokens(nc, name + "s", w, weights, ident, outs, X)


def expert_weights(nc, name, w, XT, weights):
    with ExitStack() as ctx:
        def sb(n, shape):
            return ctx.enter_context(nc.sbuf_tensor(f"{name}_{n}", shape, F32))
        gate, gate_b = sb("gate", [P, NE]), sb("gate_b", [NE, 1])
        top, neg, total, probs, kept = sb("top", [NE, B, 8]), sb("neg", [NE, B]), sb("total", [NE, B]), sb("probs", [NE, B, S]), sb("kept", [NE, S])
        ps = ctx.enter_context(nc.psum_tensor(name + "_ps", [NE, 8, 512], F32))
        load_all(nc, name + "_load", [(gate[:, :], w["gate"]), (gate_b[:, :], w["gate_b"])])
        s = Signals(nc, name, "made stored own max_ready exp_ready")
        R = R_ORDER
        with nc.Block() as block:
            @block.tensor
            def _(pe):
                with pe.Fori(0, B * NCH // 8) as i:
                    for u in range(8):
                        pe.wait_ge(s["stored"], i * 8 + (u + 1))
                        pe.matmul(ps[:, u, 0:R], gate[:, :], XT[:, bass.ds((i * 8 + u) * R, R)], start=True, stop=True).then_inc(s["made"], 1)

            @block.scalar
            def _(act):
                act.sem_inc(s["stored"], 8)
                with act.Fori(0, B * NCH // 8) as i:
                    for u in range(8):
                        act.wait_ge(s["made"], i * 8 + (u + 1))
                        act.activation(weights[:, bass.ds((i * 8 + u) * R, R)], ps[:, u, 0:R], ACT.Identity, bias=gate_b[:, :]).then_inc(s["stored"], 1)
                for b in range(B):
                    act.wait_ge(s["max_ready"], b + 1)
                    act.activation(probs[:, b, :], weights[:, b * S:(b + 1) * S], ACT.Exp, bias=neg[:, b:b + 1],
                                   accum_out=total[:, b:b + 1]).then_inc(s["exp_ready"], 1)

            @block.vector
            def _(dve):
                ch = Chain(dve, s["own"])
                dve.wait_ge(s["stored"], 8 + B * NCH)
                for b in range(B):
                    logit = weights[:, b * S:(b + 1) * S]
                    ch.link(dve.max(top[:, b, :], logit))
                    dve.tensor_scalar(neg[:, b:b + 1], top[:, b, 0:1], -1.0, None, ALU.mult).then_inc(s["max_ready"], 1)
                for b in range(B):
                    logit = weights[:, b * S:(b + 1) * S]
                    ch.link(dve.match_replace(kept[:, :], top[:, b, :], logit, LOWEST))
                    ch.link(dve.tensor_tensor(kept[:, :], kept[:, :], logit, ALU.not_equal))
                    dve.wait_ge(s["exp_ready"], b + 1)
                    ch.link(dve.reciprocal(total[:, b:b + 1], total[:, b:b + 1]))
                    ch.link(dve.scalar_tensor_tensor(logit, probs[:, b, :], total[:, b:b + 1], kept[:, :], ALU.mult, ALU.mult))
        s.end()


def tile_of(stage, n):
    return stage[:, (n // 2) * 256 + n % 2:(n // 2 + 1) * 256:2]


def pool_tokens(nc, name, XN, weights, ident, pooled):
    with ExitStack() as ctx:
        def sb(n, shape):
            return ctx.enter_context(nc.sbuf_tensor(f"{name}_{n}", shape, F32))
        stage, wt, sums = sb("stage", [P, S]), sb("wt", [P, 20, P]), sb("sums", [P, C])
        ps = ctx.enter_context(nc.psum_tensor(name + "_ps", [P, 8, 512], F32))
        s = Signals(nc, name, "padded staged turned kept summed sums_ready sums_turned pooled")
        with nc.Block() as block:
            @block.gpsimd
            def _(pool):
                pool.memset(stage[NE:, :], 0.0).then_inc(s["padded"], 1)

            @block.scalar
            def _(act):
                with act.Fori(0, B) as b:
                    act.wait_ge(s["turned"], b * 5 + 1)
                    act.activation(stage[0:NE, :], weights[:, bass.ds(b * S, S)], ACT.Copy).then_inc(s["staged"], 1)
                    for n in range(5):
                        act.wait_ge(s["turned"], b * 5 + (n + 2))
                        m = 4 if n < 4 else 2
                        act.activation(wt[:, 4 * n:4 * n + m, :], ps[:, n, 0:m * P].rearrange("s (m e) -> s m e", e=P), ACT.Copy).then_inc(s["kept"], 1)

            @block.tensor
            def _(pe):
                pe.sem_inc(s["turned"], 1)
                pe.wait_ge(s["padded"], 1)
                with pe.Fori(0, B) as b:
                    pe.wait_ge(s["staged"], b + 1)
                    for n in range(18):
                        if n % 4 == 0:
                            pe.wait_ge(s["kept"], b * 5 + (n // 4 + 1))
                        ins = pe.transpose(ps[:, n // 4, (n % 4) * P:(n % 4 + 1) * P], tile_of(stage, n), ident[:, :])
                        if n % 4 == 3 or n == 17:
                            ins.then_inc(s["turned"], 1)
                    pe.wait_ge(s["kept"], b * 5 + 10)
                    pe.wait_ge(s["sums_ready"], b + 1)
                    for n in range(18):
                        ins = pe.matmul(ps[:, 5, 0:C], wt[:, n, :], XN[:, bass.ds(b * GB + n // 2, 1), n % 2, :].rearrange("p g c -> p (g c)"), start=n == 0, stop=n == 17)
                    ins.then_inc(s["summed"], 1)
                    pe.wait_ge(s["sums_ready"], b + 2)
                    pe.wait_ge(s["pooled"], b + 1)
                    pe.transpose(ps[:, 6, 0:P], sums[:, :], ident[:, :]).then_inc(s["sums_turned"], 1)

            @block.vector
            def _(dve):
                dve.sem_inc(s["kept"], 5)
                dve.sem_inc(s["sums_ready"], 1)
                dve.sem_inc(s["pooled"], 1)
                with dve.Fori(0, B) as b:
                    dve.wait_ge(s["summed"], b + 1)
                    dve.tensor_copy(sums[:, :], ps[:, 5, 0:C]).then_inc(s["sums_ready"], 1)
                    dve.wait_ge(s["sums_turned"], b + 1)
                    dve.tensor_copy(pooled[:, :, bass.ds(b, 1)].rearrange("d e b -> d (e b)"), ps[:, 6, 0:NE]).then_inc(s["pooled"], 1)
        s.end()


def expert_layers(nc, name, w, pooled, outs):
    SLOTS = 4
    NG = NE // GE
    with ExitStack() as ctx:
        def sb(n, shape):
            return ctx.enter_context(nc.sbuf_tensor(f"{name}_{n}", shape, F32))
        w1, w2 = sb("w1", [P, SLOTS, GE, 512]), sb("w2", [P, SLOTS, GE, 512])
        b1, pre, hid = sb("b1", [P, NE * 4]), sb("pre", [P, 2, GE * 4, B]), sb("hid", [P, 2, GE * 4, B])
        ps = ctx.enter_context(nc.psum_tensor(name + "_ps", [P, 4, 512], F32))
        load_all(nc, name + "_load", [(b1[:, :], w["b1"])])
        s = Signals(nc, name, " ".join(f"loaded{u}" for u in range(SLOTS)) + " made biased hid_ready done stored")
        loaded = s.all[:SLOTS]

        def skewed(eng, first, second):
            def step(i, u):
                first(i, u + 1) if u + 1 < SLOTS else first(i + 1, 0)
                second(i, u)

            last = NG // SLOTS - 1
            first(0, 0)
            with eng.Fori(0, last) as i:
                for u in range(SLOTS):
                    step(i, u)
            for u in range(SLOTS - 1):
                step(last, u)
            second(last, SLOTS - 1)

        with nc.Block() as block:
            @block.sync
            def _(sp):
                with sp.Fori(0, NG // SLOTS) as i:
                    for u in range(SLOTS):
                        sp.wait_ge(s["done"], i * SLOTS + (u + 1))
                        rows = bass.ds(i * (SLOTS * P) + u * P, P)
                        sp.dma_start(w1[:, u, :, :].rearrange("p n h -> p (n h)"), w["w1"][rows, :]).then_inc(loaded[u], 16)
                        sp.dma_start(w2[:, u, :, :].rearrange("p n o -> p (n o)"), w["w2"][rows, :]).then_inc(loaded[u], 16)

            @block.tensor
            def _(pe):
                pe.sem_inc(s["done"], SLOTS)

                def first(i, u):
                    pe.wait_ge(loaded[u], i * 32 + 32)
                    pe.wait_ge(s["biased"], i * SLOTS + (u + 1))
                    for n in range(GE):
                        for r in range(4):
                            ins = pe.matmul(ps[:, u % 2, (n * 4 + r) * B:(n * 4 + r + 1) * B], w1[:, u, n, r::4],
                                            pooled[:, bass.ds(i * (SLOTS * GE) + (u * GE + n), 1), :].rearrange("d e b -> d (e b)"), start=True, stop=True)
                    ins.then_inc(s["made"], 1)

                def second(i, u):
                    pe.wait_ge(s["hid_ready"], i * SLOTS + (u + 1))
                    pe.wait_ge(s["stored"], i * SLOTS + (u + 1))
                    for n in range(GE):
                        for r in range(4):
                            ins = pe.matmul(ps[0:B, 2 + u % 2, n * C:(n + 1) * C], hid[:, u % 2, n * 4 + r, :], w2[:, u, n, r * C:(r + 1) * C], start=r == 0, stop=r == 3)
                    ins.then_inc(s["done"], 1)

                skewed(pe, first, second)

            @block.vector
            def _(dve):
                dve.sem_inc(s["biased"], 2)
                dve.sem_inc(s["stored"], 2)

                def first(i, u):
                    dve.wait_ge(s["made"], i * SLOTS + (u + 1))
                    dve.wait_ge(s["done"], i * SLOTS + (u + 3))
                    bias = b1[:, bass.ds((i * SLOTS + u) * (GE * 4), GE * 4)]
                    dve.tensor_tensor(pre[:, u % 2, :, :], ps[:, u % 2, 0:GE * 4 * B].rearrange("p (n b) -> p n b", b=B),
                                      bc(bias[:, :, None], [P, GE * 4, B]), ALU.add).then_inc(s["biased"], 1)

                def second(i, u):
                    dve.wait_ge(s["done"], i * SLOTS + (u + 1 + SLOTS))
                    dve.tensor_copy(outs[:, bass.ds((i * SLOTS + u) * GE, GE), :].rearrange("b n c -> b (n c)"),
                                    ps[0:B, 2 + u % 2, 0:GE * C]).then_inc(s["stored"], 1)

                skewed(dve, first, second)

            @block.scalar
            def _(act):
                with act.Fori(0, NG // SLOTS) as i:
                    for u in range(SLOTS):
                        act.wait_ge(s["biased"], i * SLOTS + (u + 3))
                        act.activation(hid[:, u % 2, :, :], pre[:, u % 2, :, :], ACT.Gelu).then_inc(s["hid_ready"], 1)
        s.end()


def scatter_tokens(nc, name, w, weights, ident, outs, X):
    with ExitStack() as ctx:
        def sb(n, shape):
            return ctx.enter_context(nc.sbuf_tensor(f"{name}_{n}", shape, F32))
        stage, rows, b2 = sb("stage", [P, S]), sb("rows", [P, B, C]), sb("b2", [NE, C])
        ps = ctx.enter_context(nc.psum_tensor(name + "_ps", [P, 8, 512], F32))
        load_all(nc, name + "_load", [(b2[:, :], w["b2"])])
        s = Signals(nc, name, "padded moved rows_ready staged made added")
        with nc.Block() as block:
            @block.sync
            def _(sp):
                for b in range(B):
                    sp.dma_start(rows[0:NE, b, :], outs[b:b + 1, :, :]).then_inc(s["moved"], 16)

            @block.gpsimd
            def _(pool):
                pool.memset(stage[NE:, :], 0.0).then_inc(s["padded"], 1)
                pool.memset(rows[NE:, :, :], 0.0).then_inc(s["padded"], 1)

            @block.scalar
            def _(act):
                with act.Fori(0, B) as b:
                    act.wait_ge(s["made"], b * 5 + 1)
                    act.activation(stage[0:NE, :], weights[:, bass.ds(b * S, S)], ACT.Copy).then_inc(s["staged"], 1)

            @block.tensor
            def _(pe):
                pe.sem_inc(s["made"], 1)
                pe.wait_ge(s["padded"], 2)
                pe.wait_ge(s["rows_ready"], 1)
                with pe.Fori(0, B) as b:
                    pe.wait_ge(s["staged"], b + 1)
                    for n in range(18):
                        if n % 4 == 0:
                            pe.wait_ge(s["added"], b * 5 + (n // 4 + 1))
                        ins = pe.matmul(ps[:, n // 4, (n % 4) * C:(n % 4 + 1) * C], tile_of(stage, n),
                                        rows[:, bass.ds(b, 1), :].rearrange("e b c -> e (b c)"), start=True, stop=True)
                        if n % 4 == 3 or n == 17:
                            ins.then_inc(s["made"], 1)

            @block.vector
            def _(dve):
                dve.sem_inc(s["added"], 5)
                dve.wait_ge(s["moved"], 16 * B)
                for b in range(B):
                    ins = dve.tensor_tensor(rows[0:NE, b, :], rows[0:NE, b, :], b2[:, :], ALU.add)
                ins.then_inc(s["rows_ready"], 1)
                with dve.Fori(0, B) as b:
                    for n in range(5):
                        dve.wait_ge(s["made"], b * 5 + (n + 2))
                        m = 2 if n < 4 else 1
                        out = X[:, bass.ds(b * GB + 2 * n, m), :, :].rearrange("p g t c -> p (g t c)")
                        dve.tensor_tensor(out, out, ps[:, n, 0:m * 256], ALU.add).then_inc(s["added"], 1)
        s.end()


NH = 4
DH = 32
NT_ = S // P


def attention(nc, X, xt_dram, max_dram, w):
    with ExitStack() as ctx:
        def sb(n, shape, dt=F32):
            return ctx.enter_context(nc.sbuf_tensor("at_" + n, shape, dt))

        ident = sb("ident", [P, P])
        load_all(nc, "at_ident", [(ident[:, :], w["ident"])])
        with nc.sbuf_tensor("at_xn", [P, G, 2, C], F32) as XN, nc.sbuf_tensor("at_xt", [P, T], F32) as XT:
            layer_norm(nc, "at_ln", X, XN, 1e-6)
            transpose_tokens(nc, "at_tr", XN, lambda g: XT[:, bass.ds(g * 256, 256)].rearrange("c (t p) -> c t p", t=2), ident)
            load_all(nc, "at_store", [(xt_dram, XT[:, :])])
        wqkv, wout = sb("wqkv", [P, 3 * P]), sb("wout", [P, C])
        ones, (bout,) = bias_rows(nc, ctx, "at_b", [w["bout"]])
        packs = sb("packs", [P, 2, 4, 2, S], BF16)
        parts = sb("parts", [P, 2, 3, S], BF16)
        qk = sb("qk", [P, 2, S])
        probs = sb("probs", [P, 3, 2, R_ORDER])
        vn = sb("vn", [P, NT_, NH, DH])
        v = sb("v", [P, NT_, NH, 2, DH])
        ssq, scale = sb("ssq", [P, 2]), sb("scale", [P, 2])
        top, topT = sb("top", [P, 2 * NT_, NCH]), sb("topT", [P, P], BF16)
        neg = sb("neg", [P, P])
        kept, inv = sb("kept", [P, R_ORDER]), sb("inv", [P, R_ORDER])
        OT = sb("OT", [P, S])
        xb = probs[:, :, :, :].rearrange("p a h r -> p (a h r)")
        load_all(nc, "at_load", [(wqkv[:, :], w["wqkv"]), (wout[:, :], w["wout"])])

        ps = ctx.enter_context(nc.psum_tensor("at_ps", [P, 8, 512], F32))
        c0 = Signals(nc, "at0", "cleared")
        with nc.Block() as block:
            @block.vector
            def _(dve):
                dve.memset(v[:, :, :, 1, :], 1.0)
                dve.memset(neg[:, :], 0.0)
                dve.memset(inv[:, :], 1.0)

            @block.gpsimd
            def _(pool):
                for p in range(2):
                    pool.memset(packs[64:P, p, Q_SECOND, :, :], 0.0)
                    pool.memset(packs[64:P, p, K_SECOND, :, :], 0.0).then_inc(c0["cleared"], 1)
                pool.wait_ge(c0["cleared"], 2)
                for p in range(2):
                    pool.memset(packs[64:65, p, K_SECOND, :, :], 1.0)
        c0.end()

        s1 = Signals(nc, "at1", "loaded made kept own squared rooted lowered centred")
        s3 = Signals(nc, "at3", "packed mmade reduced negated turned copied stored placed "
                                "scored weighed used kept divided own")
        s4 = Signals(nc, "at4", "made")
        held = dict(ps=ps, packs=packs, parts=parts, top=top, neg=neg, topT=topT, ident=ident, max_dram=max_dram, v=v,
                    OT=OT, kept=kept, inv=inv, probs=probs, xb=xb, qk=qk, vn=vn, ssq=ssq, scale=scale, wqkv=wqkv, xt_dram=xt_dram)

        def output(b):
            with nc.Block() as block:
                @block.tensor
                def _(pe):
                    for n in range(NT_):
                        out = ps_bank(ps, n // 4)[:, (n % 4) * C:(n % 4 + 1) * C]
                        pe.matmul(out, OT[:, n * P:(n + 1) * P], wout[:, :], start=True, stop=False)
                        ins = pe.matmul(out, ones[:, :], bout, start=False, stop=True)
                        if n % 4 == 3 or n == NT_ - 1:
                            ins.then_inc(s4["made"], 1)

                @block.vector
                def _(dve):
                    for n in range(5):
                        dve.wait_ge(s4["made"], n + 1)
                        m = 2 if n < 4 else 1
                        out = X[:, bass.ds(b * GB + 2 * n, m), :, :].rearrange("p g t c -> p (g t c)")
                        dve.tensor_tensor(out, out, ps_bank(ps, n)[:, 0:m * 256], ALU.add)

                @block.scalar
                def _(act):
                    act.activation(v[:, :, :, 0, :], vn[:, :, :, :], ACT.Copy)
            s4.clear()

        def attend_pair(p, build):
            pair_of_heads(nc, s3, p, build, held)
            s3.clear()

        project_heads(nc, s1, 0, held)
        s1.clear()
        with nc.Block() as block:
            @block.scalar
            def _(act):
                act.activation(v[:, :, :, 0, :], vn[:, :, :, :], ACT.Copy)
        attend_pair(None, 0)
        with nc.Fori(0, B - 1) as b:
            attend_pair(0, 1)
            project_heads(nc, s1, b + 1, held)
            s1.clear()
            attend_pair(1, 0)
            output(b)
        attend_pair(0, 1)
        attend_pair(1, None)
        output(B - 1)
        for s in (s1, s3, s4):
            s.release()


Q_FIRST, K_FIRST, Q_SECOND, K_SECOND = range(4)
ROWS = {Q_FIRST: [(0, 0), (1, 0), (2, 1), (3, 1)], K_FIRST: [(0, 0), (1, 1), (2, 0), (3, 1)],
        Q_SECOND: [(0, 0), (1, 2)], K_SECOND: [(0, 2), (1, 0)]}


def ps_bank(ps, n):
    return ps[:, n, :]


def project_heads(nc, s, b, vv):
    ps, parts, xb, qk, vn, ssq, scale, wqkv, xt_dram = (vv[n] for n in "ps parts xb qk vn ssq scale wqkv xt_dram".split())
    R = R_ORDER
    with nc.Block() as block:
        @block.sync
        def _(sp):
            sp.dma_start(xb, xt_dram[:, bass.ds(b * S, S)]).then_inc(s["loaded"], 16)

        @block.tensor
        def _(pe):
            pe.wait_ge(s["loaded"], 16)
            for n in range(12):
                m, c = n // NCH, n % NCH
                if n >= 4:
                    pe.wait_ge(s["kept"], n - 3)
                pe.matmul(ps_bank(ps, n % 4)[:, 0:R], wqkv[:, m * P:(m + 1) * P], xb[:, c * R:(c + 1) * R], start=True, stop=True).then_inc(s["made"], 1)
            for n in range(NT_):
                if n >= 4:
                    pe.wait_ge(s["own"], n - 3)
                pe.matmul(ps_bank(ps, 4 + n % 4)[:, 0:P], xb[:, n * P:(n + 1) * P], wqkv[:, 2 * P:3 * P], start=True, stop=True).then_inc(s["made"], 1)

        @block.scalar
        def _(act):
            for n in range(12):
                act.wait_ge(s["made"], n + 1)
                act.activation(qk[:, n // NCH, (n % NCH) * R:(n % NCH + 1) * R], ps_bank(ps, n % 4)[:, 0:R], ACT.Copy).then_inc(s["kept"], 1)
                if n % NCH == NCH - 1:
                    m = n // NCH
                    act.wait_ge(s["kept"], n + 1)
                    act.activation(parts[:, m, 2, :], qk[:, m, :], ACT.Square, accum_out=ssq[:, m:m + 1]).then_inc(s["squared"], 1)
            act.wait_ge(s["squared"], 2)
            act.activation(scale[:, :], ssq[:, :], ACT.Sqrt).then_inc(s["rooted"], 1)
            for m in range(2):
                act.wait_ge(s["centred"], m + 1)
                act.activation(parts[:, m, 1, :], qk[:, m, :], ACT.Copy).then_inc(s["lowered"], 1)

        @block.vector
        def _(dve):
            for n in range(NT_):
                dve.wait_ge(s["made"], 13 + n)
                dve.tensor_copy(vn[:, n, :, :].rearrange("p h d -> p (h d)"), ps_bank(ps, 4 + n % 4)[:, 0:P]).then_inc(s["own"], 1)
            ch = Chain(dve, s["own"])
            ch.n = NT_
            dve.wait_ge(s["rooted"], 1)
            ch.link(dve.tensor_scalar(scale[:, :], scale[:, :], 1e-12, None, ALU.max))
            ch.link(dve.reciprocal(scale[:, :], scale[:, :]))
            ch.link(dve.tensor_scalar(scale[:, 0:1], scale[:, 0:1], 10.0, None, ALU.mult))
            for m in range(2):
                ch.link(dve.tensor_scalar(parts[:, m, 0, :], qk[:, m, :], scale[:, m:m + 1], None, ALU.mult))
                dve.scalar_tensor_tensor(qk[:, m, :], qk[:, m, :], scale[:, m:m + 1], parts[:, m, 0, :], ALU.mult, ALU.subtract).then_inc(s["centred"], 1)
            for m in range(2):
                dve.wait_ge(s["lowered"], m + 1)
                dve.tensor_tensor(parts[:, m, 2, :], qk[:, m, :], parts[:, m, 1, :], ALU.subtract)


def pair_of_heads(nc, s, pair, build, vv):
    ps, packs, parts, top, neg, topT, ident, max_dram = (vv[n] for n in "ps packs parts top neg topT ident max_dram".split())
    v, OT, kept, inv, probs = (vv[n] for n in "v OT kept inv probs".split())
    R = R_ORDER
    acc = ps_bank(ps, 4)
    STEPS = 4 * len(ROWS[Q_FIRST]) + 4 * len(ROWS[Q_SECOND])
    tiles = {c: [] for c in range(NCH)}
    if build is not None:
        tiles = {0: [], 5: [16, 17]}

    def at_least(eng, sem, n):
        if not isinstance(n, int) or n > 0:
            eng.wait_ge(sem, n)

    def maxima_groups(c):
        if build is None or (isinstance(c, int) and c == 0):
            return []
        if isinstance(c, int) and c == NCH - 1:
            return [((32 + 2 * t + h) * NCH + u, 16 + t, h, u) for t in range(2) for h in range(2) for u in range(NCH)]
        return [(c * (8 * NCH) + ((2 * t + h - 8) * NCH + u), c * 4 + (t - 4), h, u) for t in range(4) for h in range(2) for u in range(NCH)]

    def chunks(eng, body):
        body(0)
        with eng.Fori(1, NCH - 1) as c:
            body(c)
        body(NCH - 1)

    with nc.Block() as block:
        @block.tensor
        def _(pe):
            def maxima(group):
                g, tile, h, u = group
                pe.wait_ge(s["reduced"], g + 1)
                q = packs[:, build, Q_FIRST, h, bass.ds(tile * P, P)] if not isinstance(tile, int) else packs[:, build, Q_FIRST, h, tile * P:(tile + 1) * P]
                pe.matmul(ps_bank(ps, 5 + u % 3)[:, 0:R], q, packs[:, build, K_FIRST, h, u * R:(u + 1) * R], start=True, stop=True).then_inc(s["mmade"], 1)

            def turn():
                pe.wait_ge(s["negated"], 1)
                pe.transpose(ps_bank(ps, 5)[:, 0:P], neg[:, :], ident[:, :]).then_inc(s["turned"], 1)

            def attend(c):
                base = c * NT_
                groups = maxima_groups(c)
                if build is not None and isinstance(c, int) and c == NCH - 1 or groups:
                    pe.wait_ge(s["packed"], 16 * STEPS)

                def score(j):
                    at_least(pe, s["weighed"], base + (j - 1))
                    for h in range(2):
                        for q, k in ((Q_FIRST, K_FIRST), (Q_SECOND, K_SECOND)):
                            ins = pe.matmul(ps_bank(ps, 2 * (j % 2) + h)[:, 0:R], packs[:, pair, k, h, j * P:(j + 1) * P],
                                            packs[:, pair, q, h, bass.ds(c * R, R)], start=q == Q_FIRST, stop=q == Q_SECOND)
                    ins.then_inc(s["scored"], 1)

                def apply(j):
                    pe.wait_ge(s["weighed"], base + (j + 1))
                    for h in range(2):
                        ins = pe.matmul(acc[64 * h:64 * h + 64, 0:R], v[:, j, 2 * pair + h, :, :].rearrange("p a d -> p (a d)"), probs[:, j % 3, h, :],
                                        start=j == 0, stop=j == NT_ - 1, skip_group_check=True)
                    ins.then_inc(s["used"], 1)

                score(0)
                score(1)
                at_least(pe, s["kept"], c)
                for j in range(NT_):
                    apply(j)
                    at = 3 * (j - 2)
                    for group in groups[at:at + 1] if j >= 2 else []:
                        maxima(group)
                    if j + 2 < NT_:
                        score(j + 2)
                    for group in groups[at + 1:at + 3] if j >= 2 else []:
                        maxima(group)
                    if build is not None and isinstance(c, int) and c == NCH - 1 and j == 12:
                        turn()

            if pair is not None:
                chunks(pe, attend)
            else:
                pe.wait_ge(s["packed"], 16 * STEPS)
                for tile in range(NT_):
                    for h in range(2):
                        for u in range(NCH):
                            maxima(((2 * tile + h) * NCH + u, tile, h, u))
                turn()

        @block.scalar
        def _(act):
            def weigh(c):
                base = c * NT_
                for j in range(NT_):
                    act.wait_ge(s["scored"], base + (j + 1))
                    at_least(act, s["used"], base + (j - 2))
                    act.activation(probs[:, j % 3, :, :], ps[:, 2 * (j % 2):2 * (j % 2) + 2, 0:R], ACT.Exp).then_inc(s["weighed"], 1)
                act.wait_ge(s["used"], base + NT_)
                at_least(act, s["divided"], c)
                act.activation(kept[:, :], acc[:, 0:R], ACT.Copy).then_inc(s["kept"], 1)

            if pair is not None:
                chunks(act, weigh)

        @block.vector
        def _(dve):
            ch = Chain(dve, s["own"])

            dve.sem_inc(s["reduced"], 3)

            def reduce(group):
                g, tile, h, u = group
                dve.wait_ge(s["mmade"], g + 1)
                dve.tensor_reduce(top[:, bass.ds(tile + h * NT_, 1), u], ps_bank(ps, 5 + u % 3)[:, 0:R], AX.X, ALU.max).then_inc(s["reduced"], 1)

            def negate():
                dve.wait_ge(s["reduced"], 3 + 2 * NT_ * NCH)
                dve.tensor_reduce(neg[:, 0:2 * NT_], top[:, :, :], AX.X, ALU.max, negate=True).then_inc(s["negated"], 1)
                dve.wait_ge(s["turned"], 1)
                dve.tensor_copy(topT[:, :], ps_bank(ps, 5)[:, 0:P]).then_inc(s["copied"], 1)

            def divide(c):
                for group in maxima_groups(c):
                    reduce(group)
                if build is not None and isinstance(c, int) and c == NCH - 1:
                    negate()
                ch.enter(c, 2)
                dve.wait_ge(s["kept"], c + 1)
                for h in range(2):
                    ins = dve.tensor_copy(inv[64 * h:64 * h + DH, :], kept[64 * h + DH:64 * h + 2 * DH, :])
                ch.link(ins)
                ch.link(dve.reciprocal(inv[:, :], inv[:, :]))
                for h in range(2):
                    at = (2 * pair + h) * DH
                    ins = dve.tensor_tensor(OT[at:at + DH, bass.ds(c * R, R)], kept[64 * h:64 * h + DH, :], inv[64 * h:64 * h + DH, :], ALU.mult)
                ins.then_inc(s["divided"], 1)
                ch.base, ch.n = 0, 0

            if pair is not None:
                chunks(dve, divide)
            else:
                for tile in range(NT_):
                    for h in range(2):
                        for u in range(NCH):
                            reduce(((2 * tile + h) * NCH + u, tile, h, u))
                negate()

        @block.sync
        def _(sp):
            if build is not None:
                for h in range(2):
                    at = (2 * build + h) * DH
                    for kind, rows in ROWS.items():
                        for group, part in rows:
                            m = 0 if kind in (Q_FIRST, Q_SECOND) else 1
                            sp.dma_start(packs[32 * group:32 * group + DH, build, kind, h, :], parts[at:at + DH, m, part, :]).then_inc(s["packed"], 16)
                sp.wait_ge(s["copied"], 1)
                sp.dma_start(max_dram, topT[0:2 * NT_, :]).then_inc(s["stored"], 16)
                sp.wait_ge(s["stored"], 16)
                sp.dma_start(packs[64:65, build, Q_SECOND, :, :].rearrange("a h s -> a (h s)"), max_dram.rearrange("(a m) p -> a (m p)", a=1)).then_inc(s["placed"], 16)
                sp.wait_ge(s["placed"], 16)


def global_norm(nc, name, V, alpha, beta, scale, shift):
    with ExitStack() as ctx:
        def sb(n, shape):
            return ctx.enter_context(nc.sbuf_tensor(f"{name}_{n}", shape, F32))
        a, bt, sums, sq, total = sb("a", [P, 1]), sb("bt", [P, 1]), sb("sums", [P, 1]), sb("sq", [P, 4]), sb("total", [P, 1])
        mean, var, over, junk, eps = sb("mean", [P, 1]), sb("var", [P, 1]), sb("over", [P, P]), sb("junk", [P, T // 4]), sb("eps", [P, 1])
        neg = sb("neg", [P, 1])
        ps = ctx.enter_context(nc.psum_tensor(name + "_ps", [P, 2, 512], F32))
        load_all(nc, name + "_load", [(a[:, :], spread(alpha, 1)), (bt[:, :], spread(beta, 1))])
        s = Signals(nc, name, "own summed mean_ready squared total_ready var_ready rooted")
        flat = V[:, :, :, :].rearrange("p g t c -> p (g t c)")
        with nc.Block() as block:
            @block.vector
            def _(dve):
                ch = Chain(dve, s["own"])
                dve.memset(over[:, :], 1.0 / (T * C))
                dve.memset(eps[:, :], 1e-5)
                ch.link(dve.tensor_reduce(sums[:, :], flat, AX.X, ALU.add))
                dve.sem_inc(s["summed"], 1)
                dve.wait_ge(s["mean_ready"], 1)
                ch.link(dve.tensor_copy(mean[:, :], ps[:, 0, 0:1]))
                dve.tensor_scalar(neg[:, :], mean[:, :], -1.0, None, ALU.mult).then_inc(s["summed"], 1)
                dve.wait_ge(s["squared"], 4)
                dve.tensor_reduce(total[:, :], sq[:, :], AX.X, ALU.add).then_inc(s["total_ready"], 1)
                dve.wait_ge(s["var_ready"], 1)
                ch.link(dve.tensor_copy(var[:, :], ps[:, 1, 0:1]))
                dve.sem_inc(s["total_ready"], 1)
                dve.wait_ge(s["rooted"], 1)
                ch.link(dve.reciprocal(var[:, :], var[:, :]))
                ch.link(dve.tensor_tensor(scale[:, :], var[:, :], a[:, :], ALU.mult))
                ch.link(dve.scalar_tensor_tensor(shift[:, :], neg[:, :], scale[:, :], bt[:, :], ALU.mult, ALU.add))

            @block.tensor
            def _(pe):
                pe.wait_ge(s["summed"], 1)
                pe.matmul(ps[:, 0, 0:1], over[:, :], sums[:, :], start=True, stop=True).then_inc(s["mean_ready"], 1)
                pe.wait_ge(s["total_ready"], 1)
                pe.matmul(ps[:, 1, 0:1], over[:, :], total[:, :], start=True, stop=True).then_inc(s["var_ready"], 1)

            @block.scalar
            def _(act):
                act.wait_ge(s["summed"], 2)
                for n in range(4):
                    act.activation(junk[:, :], flat[:, n * (T // 4):(n + 1) * (T // 4)], ACT.Square, bias=neg[:, :], accum_out=sq[:, n:n + 1]).then_inc(s["squared"], 1)
                    act.wait_ge(s["squared"], n + 1)
                act.wait_ge(s["total_ready"], 2)
                act.activation(var[:, :], var[:, :], ACT.Sqrt, bias=eps[:, :]).then_inc(s["rooted"], 1)
        s.end()


def triangle(nc, X, k_dram, w):
    with ExitStack() as ctx:
        def sb(n, shape):
            return ctx.enter_context(nc.sbuf_tensor("tr_" + n, shape, F32))

        ident = sb("ident", [P, P])
        wab, wo = sb("wab", [P, 512]), sb("wo", [P, 2, C])
        zs, zb, ks, kb = sb("zs", [P, 1]), sb("zb", [P, 1]), sb("ks", [P, 1]), sb("kb", [P, 1])
        Z = sb("Z", [P, G, 2, C])
        load_all(nc, "tr_load", [(ident[:, :], w["ident"]), (wab[:, :], w["wab"]), (wo[:, :, :], w["wo"])])
        ones, (bab, bo) = bias_rows(nc, ctx, "tr_b", [w["bab"], w["bo"].rearrange("a n c -> a (n c)")])
        layer_norm(nc, "tr_ln", X, Z, 1e-6)
        global_norm(nc, "tr_gz", Z, w["alpha_in"], w["beta_in"], zs, zb)
        with nc.Block() as block:
            @block.vector
            def _(dve):
                zf = Z[:, :, :, :].rearrange("p g t c -> p (g t c)")
                dve.tensor_scalar(zf, zf, zs[:, :], zb[:, :], ALU.mult, ALU.add)
        with nc.sbuf_tensor("tr_zt", [P, T], F32) as ZT:
            transpose_tokens(nc, "tr_tr", Z, lambda g: ZT[:, bass.ds(g * 256, 256)].rearrange("c (p t) -> c t p", t=2), ident)
            triangle_products(nc, ZT, wab, bab, ones, k_dram)
        with nc.sbuf_tensor("tr_k", [P, G, 2, C], F32) as K:
            load_all(nc, "tr_kload", [(K[:, :, :, :], k_dram.rearrange("(g p t) c -> p g t c", p=P, t=2))])
            global_norm(nc, "tr_gk", K, w["alpha_o"], w["beta_o"], ks, kb)
            triangle_output(nc, Z, K, ks, kb, wo, bo, ones, ident, X)


def triangle_products(nc, ZT, wab, bab, ones, k_dram):
    with ExitStack() as ctx:
        def sb(n, shape):
            return ctx.enter_context(nc.sbuf_tensor("tp_" + n, shape, F32))
        zimg, gates = sb("zimg", [P, S]), sb("gates", [W, 4, 2, C])
        ab, kimg = sb("ab", [P, 2, H, C]), sb("kimg", [H, H, C])
        ps = ctx.enter_context(nc.psum_tensor("tp_ps", [P, 8, 512], F32))
        with nc.Block() as block:
            @block.vector
            def _(dve):
                dve.memset(ab[:, :, :, :], 0.0)
        s = Signals(nc, "tp", "staged projected gated multiplied made kept_act kept_dve stored")
        with nc.Fori(0, B) as b:
            with nc.Block() as block:
                @block.scalar
                def _(act):
                    act.activation(zimg[:, :], ZT[:, bass.ds(b * S, S)], ACT.Copy).then_inc(s["staged"], 1)
                    for r in range(H):
                        act.wait_ge(s["projected"], r + 1)
                        if r >= 4:
                            act.wait_ge(s["multiplied"], r - 3)
                        act.activation(gates[:, r % 4, :, :], ps[0:W, r % 4, :].rearrange("w (n m c) -> w n m c", n=2, m=2)[:, :, 0, :],
                                       ACT.Sigmoid).then_inc(s["gated"], 1)
                    for n in range(0, 16, 2):
                        act.wait_ge(s["made"], n + 1)
                        act.activation(kimg[:, :, 8 * n:8 * n + 8], ps[0:H, 4 + n % 4, 0:384].rearrange("i (c j) -> i j c", c=8), ACT.Copy).then_inc(s["kept_act"], 1)

                @block.vector
                def _(dve):
                    for r in range(H):
                        dve.wait_ge(s["gated"], r + 1)
                        dve.tensor_tensor(ab[0:W, :, r, :], gates[:, r % 4, :, :],
                                          ps[0:W, r % 4, :].rearrange("w (n m c) -> w n m c", n=2, m=2)[:, :, 1, :], ALU.mult).then_inc(s["multiplied"], 1)
                    for n in range(1, 16, 2):
                        dve.wait_ge(s["made"], n + 1)
                        dve.tensor_copy(kimg[:, :, 8 * n:8 * n + 8], ps[0:H, 4 + n % 4, 0:384].rearrange("i (c j) -> i j c", c=8)).then_inc(s["kept_dve"], 1)

                @block.tensor
                def _(pe):
                    pe.wait_ge(s["staged"], 1)
                    for r in range(H):
                        if r >= 4:
                            pe.wait_ge(s["multiplied"], r - 3)
                        pe.matmul(ps[0:W, r % 4, :], zimg[:, r * W:(r + 1) * W], wab[:, :], start=True, stop=False)
                        pe.matmul(ps[0:W, r % 4, :], ones[:, 0:W], bab, start=False, stop=True).then_inc(s["projected"], 1)
                    pe.wait_ge(s["multiplied"], H)
                    for n in range(16):
                        if n >= 4:
                            pe.wait_ge(s["kept_act"] if n % 2 == 0 else s["kept_dve"], n // 2 - 1)
                        for c in range(8):
                            ins = pe.matmul(ps[0:H, 4 + n % 4, c * H:(c + 1) * H], ab[:, 0, :, 8 * n + c], ab[:, 1, :, 8 * n + c], start=True, stop=True)
                        ins.then_inc(s["made"], 1)

                @block.sync
                def _(sp):
                    sp.wait_ge(s["kept_act"], 8)
                    sp.wait_ge(s["kept_dve"], 8)
                    sp.dma_start(k_dram[bass.ds(b * S, S), :].rearrange("(i j) c -> i (j c)", i=H), kimg[:, :, :].rearrange("i j c -> i (j c)")).then_inc(s["stored"], 16)
                    sp.wait_ge(s["stored"], 16)
            s.clear()
        s.release()


def triangle_output(nc, Z, K, ks, kb, wo, bo, ones, ident, X):
    with ExitStack() as ctx:
        def sb(n, shape):
            return ctx.enter_context(nc.sbuf_tensor("to_" + n, shape, F32))
        U = 4
        stage, turned, gate, prod = sb("stage", [P, U, 4, C]), sb("turned", [P, U, 4, P]), sb("gate", [P, U, 256]), sb("prod", [P, U, 256])
        ps = ctx.enter_context(nc.psum_tensor("to_ps", [P, 2 * U, 512], F32))
        s = Signals(nc, "to", "staged turned kept made gated own added")

        def tiles(V, g):
            return V[:, bass.ds(g, 1), :, :].rearrange("p g t c -> p (g t) c")

        with nc.Block() as block:
            @block.vector
            def _(dve):
                ch = Chain(dve, s["own"])
                dve.sem_inc(s["added"], U)
                with dve.Fori(0, G // U) as i:
                    ch.enter(i, U)
                    for u in range(U):
                        dve.wait_ge(s["turned"], i * U + (u + 1))
                        dve.tensor_copy(stage[:, u, 0:2, :], tiles(Z, i * U + u))
                        dve.tensor_scalar(stage[:, u, 2:4, :], tiles(K, i * U + u), ks[:, :], kb[:, :], ALU.mult, ALU.add).then_inc(s["staged"], 1)
                    for u in range(U):
                        dve.wait_ge(s["gated"], i * U + (u + 1))
                        ch.link(dve.tensor_tensor(prod[:, u, :], gate[:, u, :], ps[:, U + u, 256:512], ALU.mult))
                        out = X[:, bass.ds(i * U + u, 1), :, :].rearrange("p g t c -> p (g t c)")
                        dve.tensor_tensor(out, out, prod[:, u, :], ALU.add).then_inc(s["added"], 1)

            @block.tensor
            def _(pe):
                pe.sem_inc(s["turned"], U)
                with pe.Fori(0, G // U) as i:
                    for u in range(U):
                        pe.wait_ge(s["staged"], i * U + (u + 1))
                        pe.wait_ge(s["kept"], i * U + (u + 1))
                        for t in range(4):
                            ins = pe.transpose(ps[:, u, t * P:(t + 1) * P], stage[:, u, t, :], ident[:, :])
                        ins.then_inc(s["turned"], 1)
                    for u in range(U):
                        pe.wait_ge(s["kept"], i * U + (u + 1 + U))
                        pe.wait_ge(s["added"], i * U + (u + 1))
                        for t in range(4):
                            out = ps[:, U + u, t * C:(t + 1) * C]
                            pe.matmul(out, turned[:, u, t, :], wo[:, t // 2, :], start=True, stop=False)
                            ins = pe.matmul(out, ones[:, :], bo[:, (t // 2) * C:(t // 2 + 1) * C], start=False, stop=True)
                        ins.then_inc(s["made"], 1)

            @block.scalar
            def _(act):
                act.sem_inc(s["kept"], U)
                with act.Fori(0, G // U) as i:
                    for u in range(U):
                        act.wait_ge(s["turned"], i * U + (u + 1 + U))
                        act.wait_ge(s["added"], i * U + (u + 1))
                        act.activation(turned[:, u, :, :].rearrange("c t p -> c (t p)"), ps[:, u, :], ACT.Copy).then_inc(s["kept"], 1)
                    for u in range(U):
                        act.wait_ge(s["made"], i * U + (u + 1))
                        act.activation(gate[:, u, :], ps[:, U + u, 0:256], ACT.Sigmoid).then_inc(s["gated"], 1)
        s.end()


NX = 8


def top2_experts(nc, X, w):
    with ExitStack() as ctx:
        def sb(n, shape):
            return ctx.enter_context(nc.sbuf_tensor("moe_" + n, shape, F32))

        ident = sb("ident", [P, P])
        router, ew = sb("router", [P, NX]), sb("ew", [P, NX * C])
        ew_high, ew_low = (ctx.enter_context(nc.sbuf_tensor("moe_ew_" + n, [P, NX * C], F32R)) for n in ("high", "low"))
        gates = sb("gates", [P, 2 * G, NX])
        XT = sb("xt", [P, T])
        stage = sb("stage", [P, 2, 4, P])
        load_all(nc, "moe_load", [(ident[:, :], w["ident"]), (router[:, :], w["router"]), (ew[:, :], w["ew"])])
        ones, (router_b, eb) = bias_rows(nc, ctx, "moe_b", [w["router_b"], w["eb"]])
        with nc.sbuf_tensor("moe_xn", [P, G, 2, C], F32) as XN:
            layer_norm(nc, "moe_ln", X, XN, 1e-5)
            transpose_tokens(nc, "moe_tr", XN, lambda g: XT[:, bass.ds(g * 256, 256)].rearrange("c (t p) -> c t p", t=2), ident)
        ps = ctx.enter_context(nc.psum_tensor("moe_ps", [P, 8, 512], F32))

        s = Signals(nc, "mr", "staged made kept")
        with nc.Block() as block:
            @block.scalar
            def _(act):
                with act.Fori(0, G // 4) as i:
                    for u in range(2):
                        act.wait_ge(s["made"], i * 2 + (u + 1))
                        act.activation(stage[:, u, :, :].rearrange("c t p -> c (t p)"), XT[:, bass.ds((i * 2 + u) * 512, 512)], ACT.Copy).then_inc(s["staged"], 1)

            @block.tensor
            def _(pe):
                pe.sem_inc(s["made"], 2)
                with pe.Fori(0, G // 4) as i:
                    for u in range(2):
                        pe.wait_ge(s["staged"], i * 2 + (u + 1))
                        pe.wait_ge(s["kept"], i * 2 + (u + 1))
                        for t in range(4):
                            pe.matmul(ps[:, u, t * NX:(t + 1) * NX], stage[:, u, t, :], router[:, :], start=True, stop=False)
                            ins = pe.matmul(ps[:, u, t * NX:(t + 1) * NX], ones[:, :], router_b, start=False, stop=True)
                        ins.then_inc(s["made"], 1)

            @block.vector
            def _(dve):
                dve.sem_inc(s["kept"], 2)
                with dve.Fori(0, G // 4) as i:
                    for u in range(2):
                        dve.wait_ge(s["made"], i * 2 + (u + 3))
                        dve.tensor_copy(gates[:, bass.ds((i * 2 + u) * 4, 4), :], ps[:, u, 0:4 * NX].rearrange("p (t e) -> p t e", e=NX)).then_inc(s["kept"], 1)
        s.end()
        route(nc, gates)

        s = Signals(nc, "me", "cut weights_ready staged lowered made own added")
        high, low = (ctx.enter_context(nc.sbuf_tensor("moe_stage_" + n, [P, 2, 2, P], F32R)) for n in ("high", "low"))
        with nc.Block() as block:
            @block.gpsimd
            def _(pool):
                pool.wait_ge(s["cut"], 1)
                pool.tensor_tensor(ew_low[:, :], ew[:, :], ew_high[:, :], ALU.subtract).then_inc(s["weights_ready"], 1)
                with pool.Fori(0, G // 2) as i:
                    for u in range(2):
                        pool.wait_ge(s["staged"], i * 2 + (u + 1))
                        source = XT[:, bass.ds((i * 2 + u) * 256, 256)].rearrange("c (t p) -> c t p", t=2)
                        pool.tensor_tensor(low[:, u, :, :], source, high[:, u, :, :], ALU.subtract).then_inc(s["lowered"], 1)

            @block.scalar
            def _(act):
                act.activation(ew_high[:, :], ew[:, :], ACT.Copy).then_inc(s["cut"], 1)
                with act.Fori(0, G // 2) as i:
                    for u in range(2):
                        act.wait_ge(s["made"], i * 4 + (2 * u + 1))
                        act.activation(high[:, u, :, :].rearrange("c t p -> c (t p)"), XT[:, bass.ds((i * 2 + u) * 256, 256)], ACT.Copy).then_inc(s["staged"], 1)

            @block.tensor
            def _(pe):
                pe.sem_inc(s["made"], 3)
                pe.wait_ge(s["weights_ready"], 1)
                with pe.Fori(0, G // 2) as i:
                    for u in range(2):
                        pe.wait_ge(s["lowered"], i * 2 + (u + 1))
                        for t in range(2):
                            pe.wait_ge(s["added"], i * 4 + (2 * u + t + 1))
                            for n in range(2):
                                out = ps[:, 4 * u + 2 * t + n, :]
                                for turn, (x, m) in enumerate(((high, ew_high), (high, ew_low), (low, ew_high))):
                                    pe.matmul(out, x[:, u, t, :], m[:, n * 512:(n + 1) * 512], start=turn == 0, stop=False)
                                ins = pe.matmul(out, ones[:, :], eb[:, n * 512:(n + 1) * 512], start=False, stop=True)
                            ins.then_inc(s["made"], 1)

            @block.vector
            def _(dve):
                dve.sem_inc(s["added"], 4)
                dve.sem_inc(s["own"], 2)
                with dve.Fori(0, G // 2) as i:
                    for u in range(2):
                        dve.wait_ge(s["made"], i * 4 + (2 * u + 5))
                        for e in range(NX):
                            for t in range(2):
                                out = X[:, bass.ds(i * 2 + u, 1), t, :].rearrange("p g c -> p (g c)")
                                gate = gates[:, bass.ds(i * 4 + (2 * u + t), 1), e]
                                if e:
                                    dve.wait_ge(s["own"], i * (4 * (NX - 1)) + (u * 2 * (NX - 1) + 2 * (e - 1) + t + 3))
                                ins = dve.scalar_tensor_tensor(out, ps[:, 4 * u + 2 * t + e // 4, (e % 4) * C:(e % 4 + 1) * C], gate, out, ALU.mult, ALU.add)
                                if e == NX - 1:
                                    ins.then_inc(s["added"], 1)
                                else:
                                    ins.then_inc(s["own"], 1)
        s.end()


def route(nc, gates):
    n = 2 * G
    with ExitStack() as ctx:
        def sb(name, shape):
            return ctx.enter_context(nc.sbuf_tensor("rt_" + name, shape, F32))
        rest, equal, count, mask, top, second = sb("rest", [P, n, NX]), sb("equal", [P, n, NX]), sb("count", [P, n, NX]), sb("mask", [P, n, NX]), sb("top", [P, n]), sb("second", [P, n])
        s = Signals(nc, "rt", "own centred exp_ready")

        def wide(ap):
            return bc(ap[:, :, None], [P, n, NX])

        with nc.Block() as block:
            @block.vector
            def _(dve):
                ch = Chain(dve, s["own"])

                def first_of(logits, peak):
                    ch.link(dve.tensor_tensor(equal[:, :, :], logits, wide(peak), ALU.is_equal))
                    ch.link(dve.tensor_copy(count[:, :, :], equal[:, :, :]))
                    for e in range(1, NX):
                        ch.link(dve.tensor_tensor(count[:, :, e], count[:, :, e], count[:, :, e - 1], ALU.add))
                    ch.link(dve.tensor_scalar(count[:, :, :], count[:, :, :], 1.0, None, ALU.is_equal))
                    ch.link(dve.tensor_tensor(equal[:, :, :], equal[:, :, :], count[:, :, :], ALU.mult))

                ch.link(dve.tensor_reduce(top[:, :], gates[:, :, :], AX.X, ALU.max))
                first_of(gates[:, :, :], top)
                ch.link(dve.tensor_copy(mask[:, :, :], equal[:, :, :]))
                ch.link(dve.scalar_tensor_tensor(rest[:, :, :], mask[:, :, :], LOWEST, gates[:, :, :], ALU.mult, ALU.add))
                ch.link(dve.tensor_reduce(second[:, :], rest[:, :, :], AX.X, ALU.max))
                first_of(rest[:, :, :], second)
                ch.link(dve.tensor_tensor(mask[:, :, :], mask[:, :, :], equal[:, :, :], ALU.add))
                dve.tensor_tensor(gates[:, :, :], gates[:, :, :], wide(top), ALU.subtract).then_inc(s["centred"], 1)
                dve.wait_ge(s["exp_ready"], 1)
                ch.link(dve.tensor_tensor(gates[:, :, :], gates[:, :, :], mask[:, :, :], ALU.mult))
                ch.link(dve.tensor_reduce(top[:, :], gates[:, :, :], AX.X, ALU.add))
                ch.link(dve.reciprocal(top[:, :], top[:, :]))
                ch.link(dve.tensor_tensor(gates[:, :, :], gates[:, :, :], wide(top), ALU.mult))

            @block.scalar
            def _(act):
                act.wait_ge(s["centred"], 1)
                act.activation(gates[:, :, :], gates[:, :, :], ACT.Exp).then_inc(s["exp_ready"], 1)
        s.end()


def metaformer(nc, w, out):
    def scratch(name, shape, dt=F32):
        return nc.dram_tensor(name, shape, dt, kind="Internal").ap()

    def tokens(ap):
        return ap.rearrange("(g p t) c -> p g t c", p=P, t=2)

    x1, x2, rows, channels, maxima = scratch("x1", [T, C]), scratch("x2", [T, C]), scratch("rows", [T, C]), scratch("channels", [P, T]), scratch("maxima", [2 * NT_, P], BF16)
    with nc.sbuf_tensor("m0_xt", [P, T], F32) as XT:
        with nc.sbuf_tensor("m0_x", [P, G, 2, C], F32) as X0, nc.sbuf_tensor("m0_xn", [P, G, 2, C], F32) as XN, nc.sbuf_tensor("m0_ident", [P, P], F32) as ident:
            load_all(nc, "m0_load", [(X0[:, :, :, :], tokens(w["x"])), (ident[:, :], w["ident"])])
            layer_norm(nc, "m0_ln", X0, XN, 1e-6)
            transpose_tokens(nc, "m0_tr", XN, lambda g: XT[:, bass.ds(g * 256, 256)].rearrange("c (p t) -> c t p", t=2), ident)
        load_all(nc, "m0_store", [(channels, XT[:, :])])
    selective_scan_mixer(nc, channels, w["x"], x1, w["l0_conv"])
    spectral_unit(nc, x1, x2, w["l0_ffn"])
    with nc.sbuf_tensor("x", [P, G, 2, C], F32) as X:
        load_all(nc, "m1_load", [(X[:, :, :, :], tokens(x2))])
        fourier_mixer(nc, X, rows, w["l1_conv"])
        expert_choice(nc, "c1", X, w["l1_ffn"])
        attention(nc, X, channels, maxima, w["l2_conv"])
        expert_choice(nc, "c2", X, w["l2_ffn"])
        triangle(nc, X, rows, w["l3_conv"])
        top2_experts(nc, X, w["l3_ffn"])
        load_all(nc, "m_store", [(tokens(out), X[:, :, :, :])])



def layout(inputs):
    def of(prefix):
        return lambda n: np.asarray(inputs[prefix + n])

    def turned(a, order, *shape):
        return np.ascontiguousarray(a.transpose(order)).reshape(shape)

    ident = np.eye(P, dtype=np.float32)
    out = {"x": np.asarray(inputs["x"]).reshape(T, C), "ident": ident}
    stage = {}

    f = of("L0_conv_")
    xp = f("x_proj_w")
    sel = np.zeros((3, 2 * NST, 2 * NST, P), np.float32)
    for n in range(2 * NST):
        sel[:, n, n] = 1
    stage["l0_conv"] = {
        "win": np.ascontiguousarray(f("in_proj_w").T),
        "convw": turned(f("conv_w").reshape(D2, P, 9), (1, 0, 2), P, D2, 9),
        "convb": np.ascontiguousarray(f("conv_b").reshape(D2, P).T),
        "xpw": turned(np.concatenate([xp[:, DTR:], xp[:, :DTR]], 1).reshape(4, 40, D2, P), (3, 2, 0, 1), P, D2, 4, 40),
        "dtw": turned(f("dt_proj_w"), (2, 0, 1), DTR, 4, 256),
        "dtb": turned(f("dt_proj_b").reshape(4, D2, P), (2, 0, 1), P, 4, D2),
        "a_log": turned(f("A_logs").reshape(4, D2, P, NST), (2, 0, 1, 3), P, 4, D2, NST),
        "ds": turned(f("Ds").reshape(4, D2, P), (2, 0, 1), P, 4, D2),
        "ng": np.ascontiguousarray(f("norm_g").reshape(D2, P).T),
        "nb": np.ascontiguousarray(f("norm_b").reshape(D2, P).T),
        "wout": turned(f("out_proj_w").T.reshape(D2, P, C), (1, 0, 2), P, D2, C),
        "sel": sel.reshape(96, 2 * NST, P).astype(mybir.dt.np(BF16)),
    }

    f = of("L0_ffn_")
    none = np.zeros((NK, P), np.float32)
    phi = f("phi")[:S].T
    stage["l0_ffn"] = {
        "phi_even": np.concatenate([phi[:, 0::2][:, ::-1], none], 1),
        "phi_odd": np.concatenate([phi[:, 1::2][:, ::-1], none], 1),
        "M_plus": turned(f("M_phi_plus"), (1, 2, 0, 3), NK, P, NEDGE, P),
        "M_minus": turned(f("M_phi_minus"), (1, 2, 0, 3), NK, P, NEDGE, P),
        "M_u": turned(f("M_u"), (1, 2, 0, 3), 3, P, NEDGE, P),
        "log_weights": f("log_weights"), "gumbel": f("gumbel"), "sigma": f("sigma"),
    }

    f = of("L1_conv_")
    turn = 2 * np.pi * (np.outer(np.arange(W), np.arange(NF)) % W) / W
    cos, sin = np.cos(turn), np.sin(turn)
    sin[:, [0, NF - 1]] = 0
    both = np.full(NF, 2.0)
    both[[0, NF - 1]] = 1
    stage["l1_conv"] = {
        "fw0": turned(f("fw0")[:, :, :NF], (2, 0, 3, 1), NF * P, 2 * C),
        "fw1": turned(f("fw1")[:, :, :NF], (2, 0, 3, 1), NF * P, 2 * C),
        "dft": (np.concatenate([sin, cos, -sin], 1) / np.sqrt(W)).astype(np.float32),
        "idft": np.ascontiguousarray((np.concatenate([cos * both, -sin * both], 1).T / np.sqrt(W)).astype(np.float32)),
        "w1": f("w1"), "w2": turned(f("w2").reshape(4, P, C), (1, 0, 2), P, 4, C),
        "b1": np.ascontiguousarray(f("b1").reshape(4, P).T), "b2": f("b2").reshape(1, C),
    }

    for layer in (1, 2):
        f = of(f"L{layer}_ffn_")
        w1, w2 = f("weight1"), f("weight2")
        stage[f"l{layer}_ffn"] = {
            "gate": np.ascontiguousarray(f("gate_w").T), "gate_b": f("gate_b").reshape(NE, 1),
            "w1": turned(w1[:, :P].reshape(NE // GE, GE, P, 512), (0, 2, 1, 3), NE // GE * P, GE * 512),
            "w2": turned(w2[:, :512].reshape(NE // GE, GE, P, 4 * C), (0, 2, 1, 3), NE // GE * P, GE * 512),
            "b1": turned(w1[:, P].reshape(NE, P, 4), (1, 0, 2), P, NE * 4), "b2": np.ascontiguousarray(w2[:, 512]),
        }

    f = of("L2_conv_")
    stage["l2_conv"] = {"wqkv": f("w_qkv"), "wout": f("w_out"), "bout": f("b_out").reshape(1, C)}

    f = of("L3_conv_")
    four = ("ga", "la", "gb", "lb")
    stage["l3_conv"] = {
        "wab": np.concatenate([f("W_" + n).T for n in four], 1), "bab": np.concatenate([f("b_" + n) for n in four]).reshape(1, 512),
        "wo": np.stack([f("W_go").T, f("W_lo").T], 1), "bo": np.stack([f("b_go"), f("b_lo")]).reshape(1, 2, C),
        "alpha_in": f("alpha_in"), "beta_in": f("beta_in"), "alpha_o": f("alpha_o"), "beta_o": f("beta_o"),
    }

    f = of("L3_ffn_")
    stage["l3_ffn"] = {
        "router": f("router_w"), "router_b": f("router_b").reshape(1, NX),
        "ew": turned(f("expert_w"), (1, 0, 2), P, NX * C), "eb": f("expert_b").reshape(1, NX * C),
    }
    for name, arrays in stage.items():
        for n, a in arrays.items():
            out[f"{name}.{n}"] = np.ascontiguousarray(a)
    return out


def kernel(**inputs):
    import concourse.bacc as bacc
    from concourse.bass_utils import run_bass_kernel_spmd

    nc = bacc.Bacc("TRN2", target_bir_lowering=False, num_devices=1)
    arrays, w = {}, {}
    for name, a in layout(inputs).items():
        dram = "in_" + name.replace(".", "_")
        arrays[dram] = a
        ap = nc.dram_tensor(dram, a.shape, mybir.dt.from_np(a.dtype), kind="ExternalInput").ap()
        if "." in name:
            group, n = name.split(".")
            w.setdefault(group, {})[n] = ap
        else:
            w[name] = ap
    for group in list(w):
        if group[0] == "l":
            w[group]["ident"] = w["ident"]
    w["l1_conv"]["fw"] = [w["l1_conv"]["fw0"], w["l1_conv"]["fw1"]]
    out = nc.dram_tensor("out", [T, C], F32, kind="ExternalOutput").ap()
    metaformer(nc, w, out)
    result = run_bass_kernel_spmd(nc, [arrays], core_ids=[0])
    return result.results[0]["out"].reshape(B, H, W, C)
```
